# Optimizing a Trainium2 kernel written in Bass

```python
import numpy as np
import jax
import jax.numpy as jnp

def _softmax(x, axis=-1):
    return jax.nn.softmax(x, axis=axis)

def _gelu(x):
    return jax.nn.gelu(x, approximate=True)

def _silu(x):
    return jax.nn.silu(x)

def _sigmoid(x):
    return jax.nn.sigmoid(x)

def _layernorm(x, axis=-1, eps=1e-05):
    m = jnp.mean(x, axis=axis, keepdims=True)
    v = jnp.var(x, axis=axis, keepdims=True)
    return (x - m) / jnp.sqrt(v + eps)

def _scatter_add(tgt, idx, src, axis=0):
    return tgt.at[idx].add(src)

def _segment_sum(src, seg, n):
    return jax.ops.segment_sum(src, seg, n)
kernel_name = 'mk_decoder_postln_d4_seqx_r8_edcce3'

def setup_inputs(seed: int=0):
    np.random.seed(seed)
    _w = jnp.asarray

    def _rec_inputs():
        import jax
        import jax.numpy as jnp
        _rk = jax.random.key(seed)
        x = 7.22e-05 + 1 * jax.random.normal(jax.random.fold_in(_rk, 1), (4, 256, 128), jnp.float32)
        _lenS = 256 - jax.random.randint(jax.random.fold_in(_rk, 7), (4,), 0, max(1, 256 // 4) + 1, jnp.int32)
        _lenS2 = 256 - jax.random.randint(jax.random.fold_in(_rk, 8), (4,), 0, max(1, 256 // 4) + 1, jnp.int32)
        _ctx_1024P = jax.random.normal(jax.random.fold_in(_rk, 11), (4, 16, 128), jnp.float32)
        _ctx_1024c = jax.random.dirichlet(jax.random.fold_in(_rk, 511), 0.3 * jnp.ones((16,), jnp.float32), (4, 256))
        _ctx_1024t = jnp.einsum('bsk,bkd->bsd', _ctx_1024c, _ctx_1024P)
        _ctx_1024t = _ctx_1024t * jax.lax.rsqrt(jnp.mean(jnp.square(_ctx_1024t)) + 1e-12) * 0.953939
        ctx_1024 = 4.13588e-05 + 0.999923 * (_ctx_1024t + 0.3 * jax.random.normal(jax.random.fold_in(_rk, 611), (4, 256, 128), jnp.float32))
        _validS = jnp.arange(256)[None, :] < _lenS[:, None]
        _validS2 = jnp.arange(256)[None, :] < _lenS2[:, None]
        _causal = jnp.tril(jnp.ones((256, 256), dtype=bool))
        mask_1x1xSxS2_ik0 = jnp.where(jnp.broadcast_to(_validS2[0:1, None, None, :], (1, 1, 256, 256)), 0, 1).astype(jnp.int32)
        return (x, ctx_1024, mask_1x1xSxS2_ik0)
    x, ctx_1024, mask_1x1xSxS2_ik0 = _rec_inputs()

    def _L0_attn_setup():
        import jax, jax.numpy as jnp
        import numpy as np
        D = 128
        key = jax.random.key(seed)
        ks = jax.random.split(key, 9)
        s = 1.0 / np.sqrt(D)
        x = jax.random.normal(ks[0], (8, 512, D), dtype=jnp.float32)
        Wq = jax.random.uniform(ks[1], (D, D), jnp.float32, -s, s)
        bq = jax.random.uniform(ks[2], (D,), jnp.float32, -s, s)
        Wk = jax.random.uniform(ks[3], (D, D), jnp.float32, -s, s)
        bk = jax.random.uniform(ks[4], (D,), jnp.float32, -s, s)
        Wv = jax.random.uniform(ks[5], (D, D), jnp.float32, -s, s)
        bv = jax.random.uniform(ks[6], (D,), jnp.float32, -s, s)
        Wo = jax.random.uniform(ks[7], (D, D), jnp.float32, -s, s)
        bo = jax.random.uniform(ks[8], (D,), jnp.float32, -s, s)
        return {'x': x, 'Wq': Wq, 'bq': bq, 'Wk': Wk, 'bk': bk, 'Wv': Wv, 'bv': bv, 'Wo': Wo, 'bo': bo}
    _L0_attn_all = _L0_attn_setup()
    _L0_attn_in = {k: v for k, v in _L0_attn_all.items() if k in ('Wq', 'bq', 'Wk', 'bk', 'Wv', 'bv', 'Wo', 'bo')}
    del _L0_attn_all

    def _L0_xattn_setup():
        import jax, jax.numpy as jnp
        import numpy as np
        EMBED_DIM = 128
        NUM_HEADS = 16
        HEAD_DIM = EMBED_DIM // NUM_HEADS
        key = jax.random.key(seed)
        ks = jax.random.split(key, 11)
        B, S, D = (4, 256, EMBED_DIM)
        scale = 1.0 / np.sqrt(D)
        inp = {'Q': jax.random.normal(ks[0], (B, S, D), jnp.float32), 'K': jax.random.normal(ks[1], (B, S, D), jnp.float32), 'V': jax.random.normal(ks[2], (B, S, D), jnp.float32), 'Wq': jax.random.normal(ks[3], (D, D), jnp.float32) * scale, 'bq': jax.random.normal(ks[4], (D,), jnp.float32) * 0.01, 'Wk': jax.random.normal(ks[5], (D, D), jnp.float32) * scale, 'bk': jax.random.normal(ks[6], (D,), jnp.float32) * 0.01, 'Wv': jax.random.normal(ks[7], (D, D), jnp.float32) * scale, 'bv': jax.random.normal(ks[8], (D,), jnp.float32) * 0.01, 'Wo': jax.random.normal(ks[9], (D, D), jnp.float32) * scale, 'bo': jax.random.normal(ks[10], (D,), jnp.float32) * 0.01}
        return inp
    _L0_xattn_all = _L0_xattn_setup()
    _L0_xattn_in = {k: v for k, v in _L0_xattn_all.items() if k in ('Wq', 'bq', 'Wk', 'bk', 'Wv', 'bv', 'Wo', 'bo')}
    del _L0_xattn_all

    def _L0_ffn_setup():
        import jax, jax.numpy as jnp
        import numpy as np
        D_MODEL = 128
        N_EXPERTS = 16
        TOP_K = 2
        EXPERT_DIM = 128
        SHARED_DIM = 256
        B, T = (2, 128)
        key = jax.random.key(seed)
        ks = jax.random.split(key, 7)
        std = 0.02
        return {'x': jax.random.normal(ks[0], (B, T, D_MODEL), dtype=jnp.float32), 'router_w': jax.random.normal(ks[1], (N_EXPERTS, D_MODEL), dtype=jnp.float32) * std, 'gate_up_w': jax.random.normal(ks[2], (N_EXPERTS, D_MODEL, 2 * EXPERT_DIM), dtype=jnp.float32) * std, 'down_w': jax.random.normal(ks[3], (N_EXPERTS, EXPERT_DIM, D_MODEL), dtype=jnp.float32) * std, 'shared_gate_w': jax.random.normal(ks[4], (SHARED_DIM, D_MODEL), dtype=jnp.float32) * std, 'shared_up_w': jax.random.normal(ks[5], (SHARED_DIM, D_MODEL), dtype=jnp.float32) * std, 'shared_down_w': jax.random.normal(ks[6], (D_MODEL, SHARED_DIM), dtype=jnp.float32) * std}
    _L0_ffn_all = _L0_ffn_setup()
    _L0_ffn_in = {k: v for k, v in _L0_ffn_all.items() if k in ('router_w', 'gate_up_w', 'down_w', 'shared_gate_w', 'shared_up_w', 'shared_down_w')}
    del _L0_ffn_all

    def _L1_attn_setup():
        import jax, jax.numpy as jnp
        from jax import lax
        import numpy as np
        D_MODEL = 128
        D_STATE = 16
        D_CONV = 4
        EXPAND = 2
        D_INNER = EXPAND * D_MODEL
        DT_RANK = (D_MODEL + 15) // 16
        B_SZ, SEQ = (4, 128)
        LN_EPS = 1e-05

        def _mamba(x, in_w, conv_w, conv_b, xproj_w, dt_w, dt_b, A_log, D, out_w):
            Bn, L, _ = x.shape
            xz = x @ in_w.T
            xi, z = jnp.split(xz, 2, axis=-1)
            xc = lax.conv_general_dilated(xi.transpose(0, 2, 1), conv_w, window_strides=(1,), padding=[(D_CONV - 1, 0)], feature_group_count=D_INNER)
            xc = jax.nn.silu(xc + conv_b[None, :, None]).transpose(0, 2, 1)
            dbl = xc @ xproj_w.T
            dt, Bm, Cm = jnp.split(dbl, [DT_RANK, DT_RANK + D_STATE], axis=-1)
            delta = jax.nn.softplus(dt @ dt_w.T + dt_b)
            A = -jnp.exp(A_log)

            def step(h, inputs):
                d_t, B_t, C_t, u_t = inputs
                dA = jnp.exp(d_t[..., None] * A)
                h = h * dA + (d_t * u_t)[..., None] * B_t[:, None, :]
                y = jnp.einsum('bds,bs->bd', h, C_t)
                return (h, y)
            h0 = jnp.zeros((Bn, D_INNER, D_STATE), x.dtype)
            xs = (delta.transpose(1, 0, 2), Bm.transpose(1, 0, 2), Cm.transpose(1, 0, 2), xc.transpose(1, 0, 2))
            _, ys = lax.scan(step, h0, xs)
            y = ys.transpose(1, 0, 2) + xc * D
            y = y * jax.nn.silu(z)
            return y @ out_w.T
        key = jax.random.key(seed)
        ks = iter(jax.random.split(key, 32))
        inp = {'x': jax.random.normal(next(ks), (B_SZ, SEQ, D_MODEL), jnp.float32), 'ln_g': jnp.ones((D_MODEL,), jnp.float32), 'ln_b': jnp.zeros((D_MODEL,), jnp.float32), 'fus_w': jax.random.normal(next(ks), (D_MODEL, 2 * D_MODEL), jnp.float32) * 0.02, 'fus_b': jnp.zeros((D_MODEL,), jnp.float32)}
        for p in ('f', 'b'):
            inp[p + '_in_w'] = jax.random.normal(next(ks), (2 * D_INNER, D_MODEL), jnp.float32) * 0.02
            inp[p + '_conv_w'] = jax.random.normal(next(ks), (D_INNER, 1, D_CONV), jnp.float32) * 0.2
            inp[p + '_conv_b'] = jnp.zeros((D_INNER,), jnp.float32)
            inp[p + '_xproj_w'] = jax.random.normal(next(ks), (DT_RANK + 2 * D_STATE, D_INNER), jnp.float32) * 0.02
            inp[p + '_dt_w'] = jax.random.normal(next(ks), (D_INNER, DT_RANK), jnp.float32) * 0.02
            inp[p + '_dt_b'] = jax.random.normal(next(ks), (D_INNER,), jnp.float32) * 0.5 - 4.0
            inp[p + '_A_log'] = jnp.log(jax.random.uniform(next(ks), (D_INNER, D_STATE), jnp.float32, 1.0, 16.0))
            inp[p + '_D'] = jnp.ones((D_INNER,), jnp.float32)
            inp[p + '_out_w'] = jax.random.normal(next(ks), (D_MODEL, D_INNER), jnp.float32) * 0.02
        return inp
    _L1_attn_all = _L1_attn_setup()
    _L1_attn_in = {k: v for k, v in _L1_attn_all.items() if k in ('ln_g', 'ln_b', 'fus_w', 'fus_b', 'f_in_w', 'f_conv_w', 'f_conv_b', 'f_xproj_w', 'f_dt_w', 'f_dt_b', 'f_A_log', 'f_D', 'f_out_w', 'b_in_w', 'b_conv_w', 'b_conv_b', 'b_xproj_w', 'b_dt_w', 'b_dt_b', 'b_A_log', 'b_D', 'b_out_w')}
    del _L1_attn_all

    def _L1_xattn_setup():
        import jax, jax.numpy as jnp
        import numpy as np
        B, S, D, H = (2, 256, 128, 16)
        DK = D // H
        key = jax.random.key(seed)
        ks = jax.random.split(key, 12)
        std = 1.0 / np.sqrt(D)
        inp = {'query': jax.random.normal(ks[0], (B, S, D), jnp.float32), 'key': jax.random.normal(ks[1], (B, S, D), jnp.float32), 'value': jax.random.normal(ks[2], (B, S, D), jnp.float32), 'mask': jnp.tril(jnp.ones((S, S), jnp.int32))[None, None, :, :], 'Wq': jax.random.normal(ks[3], (D, D), jnp.float32) * std, 'bq': jax.random.normal(ks[4], (D,), jnp.float32) * std, 'Wk': jax.random.normal(ks[5], (D, D), jnp.float32) * std, 'bk': jax.random.normal(ks[6], (D,), jnp.float32) * std, 'Wv': jax.random.normal(ks[7], (D, D), jnp.float32) * std, 'bv': jax.random.normal(ks[8], (D,), jnp.float32) * std, 'Wo': jax.random.normal(ks[9], (D, D), jnp.float32) * std, 'bo': jax.random.normal(ks[10], (D,), jnp.float32) * std}
        return inp
    _L1_xattn_all = _L1_xattn_setup()
    _L1_xattn_in = {k: v for k, v in _L1_xattn_all.items() if k in ('Wq', 'bq', 'Wk', 'bk', 'Wv', 'bv', 'Wo', 'bo')}
    del _L1_xattn_all

    def _L1_ffn_setup():
        import jax, jax.numpy as jnp
        import numpy as np
        E, K, D, F = (8, 2, 128, 512)
        EPS = 1e-06
        B, S = (2, 128)
        key = jax.random.key(seed)
        ks = jax.random.split(key, 6)
        s_in = 1.0 / np.sqrt(D)
        s_mid = 1.0 / np.sqrt(F)
        return {'x': jax.random.normal(ks[0], (B, S, D), dtype=jnp.float32), 'Wg': jax.random.normal(ks[1], (D, E), dtype=jnp.float32) * s_in, 'gamma': jnp.ones((E, D), dtype=jnp.float32), 'beta': jnp.zeros((E, D), dtype=jnp.float32), 'W1': jax.random.normal(ks[2], (E, D, F), dtype=jnp.float32) * s_in, 'b1': jnp.zeros((E, F), dtype=jnp.float32), 'W2': jax.random.normal(ks[3], (E, F, D), dtype=jnp.float32) * s_mid, 'b2': jnp.zeros((E, D), dtype=jnp.float32)}
    _L1_ffn_all = _L1_ffn_setup()
    _L1_ffn_in = {k: v for k, v in _L1_ffn_all.items() if k in ('Wg', 'gamma', 'beta', 'W1', 'b1', 'W2', 'b2')}
    del _L1_ffn_all

    def _L2_attn_setup():
        import jax, jax.numpy as jnp
        import numpy as np
        import math
        D_MODEL = 128
        LAYER_ID = 6
        NUM_LAYERS = 12
        B = 8
        T = 256

        def _wkv(w, u, k, v):
            wn = -jnp.exp(w)

            def step(carry, kv):
                aa, bb, pp = carry
                kt, vt = kv
                ww = u + kt
                p = jnp.maximum(pp, ww)
                e1 = jnp.exp(pp - p)
                e2 = jnp.exp(ww - p)
                y = (e1 * aa + e2 * vt) / (e1 * bb + e2)
                ww2 = pp + wn
                p2 = jnp.maximum(ww2, kt)
                e1b = jnp.exp(ww2 - p2)
                e2b = jnp.exp(kt - p2)
                return ((e1b * aa + e2b * vt, e1b * bb + e2b, p2), y)
            Bd, Td, Cd = k.shape
            init = (jnp.zeros((Bd, Cd), k.dtype), jnp.zeros((Bd, Cd), k.dtype), jnp.full((Bd, Cd), -1e+38, k.dtype))
            kT = jnp.swapaxes(k, 0, 1)
            vT = jnp.swapaxes(v, 0, 1)
            _, ys = jax.lax.scan(step, init, (kT, vT))
            return jnp.swapaxes(ys, 0, 1)
        key = jax.random.key(seed)
        ks = jax.random.split(key, 5)
        r01 = LAYER_ID / (NUM_LAYERS - 1)
        r1a0 = 1.0 - LAYER_ID / NUM_LAYERS
        h = np.arange(D_MODEL, dtype=np.float32)
        w = (-5.0 + 8.0 * (h / (D_MODEL - 1)) ** (0.7 + 1.3 * r01)).astype(np.float32)
        zigzag = np.array([(i + 1) % 3 - 1 for i in range(D_MODEL)], np.float32) * 0.5
        u = (np.ones(D_MODEL, np.float32) * math.log(0.3) + zigzag).astype(np.float32)
        xinit = (h / D_MODEL).astype(np.float32)
        tmk = (xinit ** r1a0).reshape(1, 1, D_MODEL).astype(np.float32)
        tmv = (tmk + 0.3 * r01).astype(np.float32)
        tmr = (xinit ** (0.5 * r1a0)).reshape(1, 1, D_MODEL).astype(np.float32)
        s = 1.0 / math.sqrt(D_MODEL)
        Wk = jax.random.normal(ks[0], (D_MODEL, D_MODEL), jnp.float32) * s
        Wv = jax.random.normal(ks[1], (D_MODEL, D_MODEL), jnp.float32) * s
        Wr = jax.random.normal(ks[2], (D_MODEL, D_MODEL), jnp.float32) * s
        Wo = jax.random.normal(ks[3], (D_MODEL, D_MODEL), jnp.float32) * s
        x = jax.random.normal(ks[4], (B, T, D_MODEL), jnp.float32)
        return dict(x=x, w=jnp.asarray(w), u=jnp.asarray(u), time_mix_k=jnp.asarray(tmk), time_mix_v=jnpp if False else jnp.asarray(tmv), time_mix_r=jnp.asarray(tmr), Wk=Wk, Wv=Wv, Wr=Wr, Wo=Wo)
    _L2_attn_all = _L2_attn_setup()
    _L2_attn_in = {k: v for k, v in _L2_attn_all.items() if k in ('w', 'u', 'time_mix_k', 'time_mix_v', 'time_mix_r', 'Wk', 'Wv', 'Wr', 'Wo')}
    del _L2_attn_all

    def _L2_xattn_setup():
        import jax, jax.numpy as jnp
        import numpy as np
        D_MODEL = 128
        N_HEADS = 16
        HEAD_DIM = D_MODEL // N_HEADS
        key = jax.random.key(seed)
        k1, k2, k3, k4, k5, k6 = jax.random.split(key, 6)
        B, T_q, T_kv = (4, 128, 512)
        s = 1.0 / np.sqrt(D_MODEL)
        return {'query': jax.random.normal(k1, (B, T_q, D_MODEL), dtype=jnp.float32), 'kv_source': jax.random.normal(k2, (B, T_kv, D_MODEL), dtype=jnp.float32), 'w_q': jax.random.normal(k3, (D_MODEL, D_MODEL), dtype=jnp.float32) * s, 'w_k': jax.random.normal(k4, (D_MODEL, D_MODEL), dtype=jnp.float32) * s, 'w_v': jax.random.normal(k5, (D_MODEL, D_MODEL), dtype=jnp.float32) * s, 'w_o': jax.random.normal(k6, (D_MODEL, D_MODEL), dtype=jnp.float32) * s}
    _L2_xattn_all = _L2_xattn_setup()
    _L2_xattn_in = {k: v for k, v in _L2_xattn_all.items() if k in ('w_q', 'w_k', 'w_v', 'w_o')}
    del _L2_xattn_all

    def _L2_ffn_setup():
        import jax, jax.numpy as jnp
        import numpy as np
        E, H, I, K = (8, 128, 256, 2)
        B, S = (4, 256)
        key = jax.random.key(seed)
        k1, k2, k3, k4 = jax.random.split(key, 4)
        x = jax.random.normal(k1, (B, S, H), dtype=jnp.float32)
        router_w = jax.random.uniform(k2, (E, H), dtype=jnp.float32, minval=-1.0, maxval=1.0) / np.sqrt(H).astype(np.float32)
        w13 = jax.random.normal(k3, (E, H, 2 * I), dtype=jnp.float32) * 0.02
        w2 = jax.random.normal(k4, (E, I, H), dtype=jnp.float32) * 0.02
        return {'x': x, 'router_w': router_w, 'w13': w13, 'w2': w2}
    _L2_ffn_all = _L2_ffn_setup()
    _L2_ffn_in = {k: v for k, v in _L2_ffn_all.items() if k in ('router_w', 'w13', 'w2')}
    del _L2_ffn_all

    def _L3_attn_setup():
        import jax, jax.numpy as jnp
        import numpy as np
        HEADS = 8
        K_SIZE = 64
        key = jax.random.key(seed)
        k1, k2, k3, k4 = jax.random.split(key, 4)
        B, C, D = (4, 256, 128)
        return {'x': jax.random.normal(k1, (B, C, D), dtype=jnp.float32), 'Mq': jax.random.normal(k2, (D, HEADS * K_SIZE), dtype=jnp.float32) * 0.02, 'Mk': jax.random.normal(k3, (D, HEADS * K_SIZE), dtype=jnp.float32) * 0.02, 'Mv': jax.random.normal(k4, (D, 128), dtype=jnp.float32) * 0.02}
    _L3_attn_all = _L3_attn_setup()
    _L3_attn_in = {k: v for k, v in _L3_attn_all.items() if k in ('Mq', 'Mk', 'Mv')}
    del _L3_attn_all

    def _L3_xattn_setup():
        import jax, jax.numpy as jnp
        import numpy as np
        H, S, D_MODEL, D_HEAD = (16, 512, 128, 64)
        key = jax.random.key(seed)
        ks = jax.random.split(key, 7)
        s = 0.02
        return {'Q': jax.random.normal(ks[0], (1, S, D_MODEL), dtype=jnp.float32), 'K': jax.random.normal(ks[1], (1, S, D_MODEL), dtype=jnp.float32), 'V': jax.random.normal(ks[2], (1, S, D_MODEL), dtype=jnp.float32), 'WQ': jax.random.normal(ks[3], (H, D_MODEL, D_HEAD), dtype=jnp.float32) * s, 'WK': jax.random.normal(ks[4], (H, D_MODEL, D_HEAD), dtype=jnp.float32) * s, 'WV': jax.random.normal(ks[5], (H, D_MODEL, D_HEAD), dtype=jnp.float32) * s, 'WO': jax.random.normal(ks[6], (H * D_HEAD, D_MODEL), dtype=jnp.float32) * s}
    _L3_xattn_all = _L3_xattn_setup()
    _L3_xattn_in = {k: v for k, v in _L3_xattn_all.items() if k in ('WQ', 'WK', 'WV', 'WO')}
    del _L3_xattn_all

    def _L3_ffn_setup():
        import jax, jax.numpy as jnp
        import numpy as np
        EXPERTS = 8
        TOP_K = 2

        def swiglu(x, w1, w2, w3):
            h = x @ w1
            return h * jax.nn.sigmoid(h) * (x @ w2) @ w3
        key = jax.random.key(seed)
        ks = jax.random.split(key, 9)
        B, S, D = (4, 256, 128)
        H = 2 * D
        s = 0.02
        x = jax.random.normal(ks[0], (B, S, D), dtype=jnp.float32)
        gate_w = jax.random.normal(ks[1], (D, EXPERTS), dtype=jnp.float32) * s
        ew1 = jax.random.normal(ks[2], (EXPERTS, D, H), dtype=jnp.float32) * s
        ew2 = jax.random.normal(ks[3], (EXPERTS, D, H), dtype=jnp.float32) * s
        ew3 = jax.random.normal(ks[4], (EXPERTS, H, D), dtype=jnp.float32) * s
        sw1 = jax.random.normal(ks[5], (D, H), dtype=jnp.float32) * s
        sw2 = jax.random.normal(ks[6], (D, H), dtype=jnp.float32) * s
        sw3 = jax.random.normal(ks[7], (H, D), dtype=jnp.float32) * s
        return {'x': x, 'gate_w': gate_w, 'ew1': ew1, 'ew2': ew2, 'ew3': ew3, 'sw1': sw1, 'sw2': sw2, 'sw3': sw3}
    _L3_ffn_all = _L3_ffn_setup()
    _L3_ffn_in = {k: v for k, v in _L3_ffn_all.items() if k in ('gate_w', 'ew1', 'ew2', 'ew3', 'sw1', 'sw2', 'sw3')}
    del _L3_ffn_all
    return {'x': x, 'ctx_1024': ctx_1024, 'mask_1x1xSxS2_ik0': mask_1x1xSxS2_ik0, 'L0_attn_Wq': _L0_attn_in['Wq'], 'L0_attn_bq': _L0_attn_in['bq'], 'L0_attn_Wk': _L0_attn_in['Wk'], 'L0_attn_bk': _L0_attn_in['bk'], 'L0_attn_Wv': _L0_attn_in['Wv'], 'L0_attn_bv': _L0_attn_in['bv'], 'L0_attn_Wo': _L0_attn_in['Wo'], 'L0_attn_bo': _L0_attn_in['bo'], 'L0_xattn_Wq': _L0_xattn_in['Wq'], 'L0_xattn_bq': _L0_xattn_in['bq'], 'L0_xattn_Wk': _L0_xattn_in['Wk'], 'L0_xattn_bk': _L0_xattn_in['bk'], 'L0_xattn_Wv': _L0_xattn_in['Wv'], 'L0_xattn_bv': _L0_xattn_in['bv'], 'L0_xattn_Wo': _L0_xattn_in['Wo'], 'L0_xattn_bo': _L0_xattn_in['bo'], 'L0_ffn_router_w': _L0_ffn_in['router_w'], 'L0_ffn_gate_up_w': _L0_ffn_in['gate_up_w'], 'L0_ffn_down_w': _L0_ffn_in['down_w'], 'L0_ffn_shared_gate_w': _L0_ffn_in['shared_gate_w'], 'L0_ffn_shared_up_w': _L0_ffn_in['shared_up_w'], 'L0_ffn_shared_down_w': _L0_ffn_in['shared_down_w'], 'L1_attn_ln_g': _L1_attn_in['ln_g'], 'L1_attn_ln_b': _L1_attn_in['ln_b'], 'L1_attn_fus_w': _L1_attn_in['fus_w'], 'L1_attn_fus_b': _L1_attn_in['fus_b'], 'L1_attn_f_in_w': _L1_attn_in['f_in_w'], 'L1_attn_f_conv_w': _L1_attn_in['f_conv_w'], 'L1_attn_f_conv_b': _L1_attn_in['f_conv_b'], 'L1_attn_f_xproj_w': _L1_attn_in['f_xproj_w'], 'L1_attn_f_dt_w': _L1_attn_in['f_dt_w'], 'L1_attn_f_dt_b': _L1_attn_in['f_dt_b'], 'L1_attn_f_A_log': _L1_attn_in['f_A_log'], 'L1_attn_f_D': _L1_attn_in['f_D'], 'L1_attn_f_out_w': _L1_attn_in['f_out_w'], 'L1_attn_b_in_w': _L1_attn_in['b_in_w'], 'L1_attn_b_conv_w': _L1_attn_in['b_conv_w'], 'L1_attn_b_conv_b': _L1_attn_in['b_conv_b'], 'L1_attn_b_xproj_w': _L1_attn_in['b_xproj_w'], 'L1_attn_b_dt_w': _L1_attn_in['b_dt_w'], 'L1_attn_b_dt_b': _L1_attn_in['b_dt_b'], 'L1_attn_b_A_log': _L1_attn_in['b_A_log'], 'L1_attn_b_D': _L1_attn_in['b_D'], 'L1_attn_b_out_w': _L1_attn_in['b_out_w'], 'L1_xattn_Wq': _L1_xattn_in['Wq'], 'L1_xattn_bq': _L1_xattn_in['bq'], 'L1_xattn_Wk': _L1_xattn_in['Wk'], 'L1_xattn_bk': _L1_xattn_in['bk'], 'L1_xattn_Wv': _L1_xattn_in['Wv'], 'L1_xattn_bv': _L1_xattn_in['bv'], 'L1_xattn_Wo': _L1_xattn_in['Wo'], 'L1_xattn_bo': _L1_xattn_in['bo'], 'L1_ffn_Wg': _L1_ffn_in['Wg'], 'L1_ffn_gamma': _L1_ffn_in['gamma'], 'L1_ffn_beta': _L1_ffn_in['beta'], 'L1_ffn_W1': _L1_ffn_in['W1'], 'L1_ffn_b1': _L1_ffn_in['b1'], 'L1_ffn_W2': _L1_ffn_in['W2'], 'L1_ffn_b2': _L1_ffn_in['b2'], 'L2_attn_w': _L2_attn_in['w'], 'L2_attn_u': _L2_attn_in['u'], 'L2_attn_time_mix_k': _L2_attn_in['time_mix_k'], 'L2_attn_time_mix_v': _L2_attn_in['time_mix_v'], 'L2_attn_time_mix_r': _L2_attn_in['time_mix_r'], 'L2_attn_Wk': _L2_attn_in['Wk'], 'L2_attn_Wv': _L2_attn_in['Wv'], 'L2_attn_Wr': _L2_attn_in['Wr'], 'L2_attn_Wo': _L2_attn_in['Wo'], 'L2_xattn_w_q': _L2_xattn_in['w_q'], 'L2_xattn_w_k': _L2_xattn_in['w_k'], 'L2_xattn_w_v': _L2_xattn_in['w_v'], 'L2_xattn_w_o': _L2_xattn_in['w_o'], 'L2_ffn_router_w': _L2_ffn_in['router_w'], 'L2_ffn_w13': _L2_ffn_in['w13'], 'L2_ffn_w2': _L2_ffn_in['w2'], 'L3_attn_Mq': _L3_attn_in['Mq'], 'L3_attn_Mk': _L3_attn_in['Mk'], 'L3_attn_Mv': _L3_attn_in['Mv'], 'L3_xattn_WQ': _L3_xattn_in['WQ'], 'L3_xattn_WK': _L3_xattn_in['WK'], 'L3_xattn_WV': _L3_xattn_in['WV'], 'L3_xattn_WO': _L3_xattn_in['WO'], 'L3_ffn_gate_w': _L3_ffn_in['gate_w'], 'L3_ffn_ew1': _L3_ffn_in['ew1'], 'L3_ffn_ew2': _L3_ffn_in['ew2'], 'L3_ffn_ew3': _L3_ffn_in['ew3'], 'L3_ffn_sw1': _L3_ffn_in['sw1'], 'L3_ffn_sw2': _L3_ffn_in['sw2'], 'L3_ffn_sw3': _L3_ffn_in['sw3']}

def reference(x, ctx_1024, mask_1x1xSxS2_ik0, L0_attn_Wq, L0_attn_bq, L0_attn_Wk, L0_attn_bk, L0_attn_Wv, L0_attn_bv, L0_attn_Wo, L0_attn_bo, L0_xattn_Wq, L0_xattn_bq, L0_xattn_Wk, L0_xattn_bk, L0_xattn_Wv, L0_xattn_bv, L0_xattn_Wo, L0_xattn_bo, L0_ffn_router_w, L0_ffn_gate_up_w, L0_ffn_down_w, L0_ffn_shared_gate_w, L0_ffn_shared_up_w, L0_ffn_shared_down_w, L1_attn_ln_g, L1_attn_ln_b, L1_attn_fus_w, L1_attn_fus_b, L1_attn_f_in_w, L1_attn_f_conv_w, L1_attn_f_conv_b, L1_attn_f_xproj_w, L1_attn_f_dt_w, L1_attn_f_dt_b, L1_attn_f_A_log, L1_attn_f_D, L1_attn_f_out_w, L1_attn_b_in_w, L1_attn_b_conv_w, L1_attn_b_conv_b, L1_attn_b_xproj_w, L1_attn_b_dt_w, L1_attn_b_dt_b, L1_attn_b_A_log, L1_attn_b_D, L1_attn_b_out_w, L1_xattn_Wq, L1_xattn_bq, L1_xattn_Wk, L1_xattn_bk, L1_xattn_Wv, L1_xattn_bv, L1_xattn_Wo, L1_xattn_bo, L1_ffn_Wg, L1_ffn_gamma, L1_ffn_beta, L1_ffn_W1, L1_ffn_b1, L1_ffn_W2, L1_ffn_b2, L2_attn_w, L2_attn_u, L2_attn_time_mix_k, L2_attn_time_mix_v, L2_attn_time_mix_r, L2_attn_Wk, L2_attn_Wv, L2_attn_Wr, L2_attn_Wo, L2_xattn_w_q, L2_xattn_w_k, L2_xattn_w_v, L2_xattn_w_o, L2_ffn_router_w, L2_ffn_w13, L2_ffn_w2, L3_attn_Mq, L3_attn_Mk, L3_attn_Mv, L3_xattn_WQ, L3_xattn_WK, L3_xattn_WV, L3_xattn_WO, L3_ffn_gate_w, L3_ffn_ew1, L3_ffn_ew2, L3_ffn_ew3, L3_ffn_sw1, L3_ffn_sw2, L3_ffn_sw3):
    import jax
    import jax.numpy as jnp

    def _L0_attn_ref(x, Wq, bq, Wk, bk, Wv, bv, Wo, bo):
        import jax, jax.numpy as jnp
        import numpy as np
        D = 128
        Q = x @ Wq.T + bq
        K = x @ Wk.T + bk
        V = x @ Wv.T + bv
        Q = jax.nn.elu(Q) + 1.0
        K = jax.nn.elu(K) + 1.0
        KV = jnp.einsum('bnd,bne->bde', K, V)
        Z = jnp.einsum('bnd,bd->bn', Q, K.sum(axis=1) + 1e-06)
        context = jnp.einsum('bnd,bde->bne', Q, KV) / Z[..., None]
        return context @ Wo.T + bo

    def _L0_xattn_ref(Q, K, V, Wq, bq, Wk, bk, Wv, bv, Wo, bo):
        import jax, jax.numpy as jnp
        import numpy as np
        EMBED_DIM = 128
        NUM_HEADS = 16
        HEAD_DIM = EMBED_DIM // NUM_HEADS
        B, S, D = Q.shape
        H, Hd = (NUM_HEADS, HEAD_DIM)
        q = Q @ Wq.T + bq
        k = K @ Wk.T + bk
        v = V @ Wv.T + bv
        q = q.reshape(B, S, H, Hd).transpose(0, 2, 1, 3)
        k = k.reshape(B, S, H, Hd).transpose(0, 2, 1, 3)
        v = v.reshape(B, S, H, Hd).transpose(0, 2, 1, 3)
        scores = jnp.einsum('bhqd,bhkd->bhqk', q, k) / jnp.sqrt(jnp.float32(Hd))
        attn = jax.nn.softmax(scores, axis=-1)
        out = jnp.einsum('bhqk,bhkd->bhqd', attn, v)
        out = out.transpose(0, 2, 1, 3).reshape(B, S, D)
        return out @ Wo.T + bo

    def _L0_ffn_ref(x, router_w, gate_up_w, down_w, shared_gate_w, shared_up_w, shared_down_w):
        import jax, jax.numpy as jnp
        import numpy as np
        D_MODEL = 128
        N_EXPERTS = 16
        TOP_K = 2
        EXPERT_DIM = 128
        SHARED_DIM = 256
        B, T = (2, 128)
        Bb, Tt, C = x.shape
        N = Bb * Tt
        E = gate_up_w.shape[0]
        logits = jnp.einsum('btc,ec->bte', x, router_w)
        top_vals, top_idx = jax.lax.top_k(logits, TOP_K)
        gates = jax.nn.sigmoid(top_vals)
        xf = x.reshape(N, C)
        sel = top_idx.reshape(N, TOP_K)
        gw = gates.reshape(N, TOP_K)
        w_full = jnp.zeros((N, E), dtype=x.dtype).at[jnp.arange(N)[:, None], sel].add(gw)
        gu = jnp.einsum('nc,ech->neh', xf, gate_up_w)
        gate, up = jnp.split(gu, 2, axis=-1)
        h = jax.nn.silu(gate) * up
        out_all = jnp.einsum('neh,ehc->nec', h, down_w)
        moe = jnp.einsum('ne,nec->nc', w_full, out_all).reshape(Bb, Tt, C)
        sg = jnp.einsum('btc,sc->bts', x, shared_gate_w)
        su = jnp.einsum('btc,sc->bts', x, shared_up_w)
        shared = jnp.einsum('bts,cs->btc', jax.nn.silu(sg) * su, shared_down_w)
        return moe + shared

    def _L1_attn_ref(x, ln_g, ln_b, fus_w, fus_b, f_in_w, f_conv_w, f_conv_b, f_xproj_w, f_dt_w, f_dt_b, f_A_log, f_D, f_out_w, b_in_w, b_conv_w, b_conv_b, b_xproj_w, b_dt_w, b_dt_b, b_A_log, b_D, b_out_w):
        import jax, jax.numpy as jnp
        from jax import lax
        import numpy as np
        D_MODEL = 128
        D_STATE = 16
        D_CONV = 4
        EXPAND = 2
        D_INNER = EXPAND * D_MODEL
        DT_RANK = (D_MODEL + 15) // 16
        B_SZ, SEQ = (4, 128)
        LN_EPS = 1e-05

        def _mamba(x, in_w, conv_w, conv_b, xproj_w, dt_w, dt_b, A_log, D, out_w):
            Bn, L, _ = x.shape
            xz = x @ in_w.T
            xi, z = jnp.split(xz, 2, axis=-1)
            xc = lax.conv_general_dilated(xi.transpose(0, 2, 1), conv_w, window_strides=(1,), padding=[(D_CONV - 1, 0)], feature_group_count=D_INNER)
            xc = jax.nn.silu(xc + conv_b[None, :, None]).transpose(0, 2, 1)
            dbl = xc @ xproj_w.T
            dt, Bm, Cm = jnp.split(dbl, [DT_RANK, DT_RANK + D_STATE], axis=-1)
            delta = jax.nn.softplus(dt @ dt_w.T + dt_b)
            A = -jnp.exp(A_log)

            def step(h, inputs):
                d_t, B_t, C_t, u_t = inputs
                dA = jnp.exp(d_t[..., None] * A)
                h = h * dA + (d_t * u_t)[..., None] * B_t[:, None, :]
                y = jnp.einsum('bds,bs->bd', h, C_t)
                return (h, y)
            h0 = jnp.zeros((Bn, D_INNER, D_STATE), x.dtype)
            xs = (delta.transpose(1, 0, 2), Bm.transpose(1, 0, 2), Cm.transpose(1, 0, 2), xc.transpose(1, 0, 2))
            _, ys = lax.scan(step, h0, xs)
            y = ys.transpose(1, 0, 2) + xc * D
            y = y * jax.nn.silu(z)
            return y @ out_w.T
        residual = x
        mu = jnp.mean(x, -1, keepdims=True)
        var = jnp.var(x, -1, keepdims=True)
        xn = (x - mu) * lax.rsqrt(var + LN_EPS) * ln_g + ln_b
        feat_fwd = _mamba(xn, f_in_w, f_conv_w, f_conv_b, f_xproj_w, f_dt_w, f_dt_b, f_A_log, f_D, f_out_w)
        xf = jnp.flip(xn, axis=1)
        feat_bwd = jnp.flip(_mamba(xf, b_in_w, b_conv_w, b_conv_b, b_xproj_w, b_dt_w, b_dt_b, b_A_log, b_D, b_out_w), axis=1)
        feat = jnp.concatenate([feat_fwd, feat_bwd], axis=-1)
        fused = feat @ fus_w.T + fus_b
        return fused + residual

    def _L1_xattn_ref(query, key, value, mask, Wq, bq, Wk, bk, Wv, bv, Wo, bo):
        import jax, jax.numpy as jnp
        import numpy as np
        B, S, D, H = (2, 256, 128, 16)
        DK = D // H
        b = query.shape[0]
        Q = query @ Wq.T + bq
        K = key @ Wk.T + bk
        V = value @ Wv.T + bv
        Q = Q.reshape(b, -1, H, DK).transpose(0, 2, 1, 3)
        K = K.reshape(b, -1, H, DK).transpose(0, 2, 1, 3)
        V = V.reshape(b, -1, H, DK).transpose(0, 2, 1, 3)
        scores = jnp.einsum('bhqd,bhkd->bhqk', Q, K) / jnp.sqrt(jnp.float32(DK))
        scores = jnp.where(mask == 0, -jnp.inf, scores)
        weights = jax.nn.softmax(scores, axis=-1)
        attn = jnp.einsum('bhqk,bhkd->bhqd', weights, V)
        attn = attn.transpose(0, 2, 1, 3).reshape(b, -1, D)
        return attn @ Wo.T + bo

    def _L1_ffn_ref(x, Wg, gamma, beta, W1, b1, W2, b2):
        import jax, jax.numpy as jnp
        import numpy as np
        E, K, D, F = (8, 2, 128, 512)
        EPS = 1e-06
        B, S = (2, 128)
        orig_shape = x.shape
        xf = x.reshape(-1, orig_shape[-1])
        scores = xf @ Wg
        w, idx = jax.lax.top_k(scores, K)
        w = jax.nn.softmax(w, axis=-1)
        mu = jnp.mean(xf, axis=-1, keepdims=True)
        var = jnp.var(xf, axis=-1, keepdims=True)
        xhat = (xf - mu) * jax.lax.rsqrt(var + EPS)
        normed = xhat[None, :, :] * gamma[:, None, :] + beta[:, None, :]
        h = jax.nn.relu(jnp.einsum('end,edf->enf', normed, W1) + b1[:, None, :])
        out = jnp.einsum('enf,efd->end', h, W2) + b2[:, None, :] + xf[None, :, :]
        cw = jnp.sum(w[..., None] * jax.nn.one_hot(idx, E, dtype=w.dtype), axis=1)
        y = jnp.einsum('ne,end->nd', cw, out)
        return y.reshape(orig_shape)

    def _L2_attn_ref(x, w, u, time_mix_k, time_mix_v, time_mix_r, Wk, Wv, Wr, Wo):
        import jax, jax.numpy as jnp
        import numpy as np
        import math
        D_MODEL = 128
        LAYER_ID = 6
        NUM_LAYERS = 12
        B = 8
        T = 256

        def _wkv(w, u, k, v):
            wn = -jnp.exp(w)

            def step(carry, kv):
                aa, bb, pp = carry
                kt, vt = kv
                ww = u + kt
                p = jnp.maximum(pp, ww)
                e1 = jnp.exp(pp - p)
                e2 = jnp.exp(ww - p)
                y = (e1 * aa + e2 * vt) / (e1 * bb + e2)
                ww2 = pp + wn
                p2 = jnp.maximum(ww2, kt)
                e1b = jnp.exp(ww2 - p2)
                e2b = jnp.exp(kt - p2)
                return ((e1b * aa + e2b * vt, e1b * bb + e2b, p2), y)
            Bd, Td, Cd = k.shape
            init = (jnp.zeros((Bd, Cd), k.dtype), jnp.zeros((Bd, Cd), k.dtype), jnp.full((Bd, Cd), -1e+38, k.dtype))
            kT = jnp.swapaxes(k, 0, 1)
            vT = jnp.swapaxes(v, 0, 1)
            _, ys = jax.lax.scan(step, init, (kT, vT))
            return jnp.swapaxes(ys, 0, 1)
        xs = jnp.pad(x, ((0, 0), (1, 0), (0, 0)))[:, :-1]
        xk = x * time_mix_k + xs * (1.0 - time_mix_k)
        xv = x * time_mix_v + xs * (1.0 - time_mix_v)
        xr = x * time_mix_r + xs * (1.0 - time_mix_r)
        k = jnp.einsum('btc,dc->btd', xk, Wk)
        v = jnp.einsum('btc,dc->btd', xv, Wv)
        r = jnp.einsum('btc,dc->btd', xr, Wr)
        wkv = _wkv(w, u, k, v)
        rwkv = jax.nn.sigmoid(r) * wkv
        return jnp.einsum('btc,dc->btd', rwkv, Wo)

    def _L2_xattn_ref(query, kv_source, w_q, w_k, w_v, w_o):
        import jax, jax.numpy as jnp
        import numpy as np
        D_MODEL = 128
        N_HEADS = 16
        HEAD_DIM = D_MODEL // N_HEADS
        B, T_q, _ = query.shape
        T_kv = kv_source.shape[1]
        q = (query @ w_q.T).reshape(B, T_q, N_HEADS, HEAD_DIM)
        k = (kv_source @ w_k.T).reshape(B, T_kv, N_HEADS, HEAD_DIM)
        v = (kv_source @ w_v.T).reshape(B, T_kv, N_HEADS, HEAD_DIM)
        scale = HEAD_DIM ** (-0.5)
        attn = jax.nn.softmax(jnp.einsum('bqhd,bkhd->bhqk', q, k) * scale, axis=-1)
        out = jnp.einsum('bhqk,bkhd->bqhd', attn, v).reshape(B, T_q, D_MODEL)
        return out @ w_o.T

    def _L2_ffn_ref(x, router_w, w13, w2):
        import jax, jax.numpy as jnp
        import numpy as np
        E, H, I, K = (8, 128, 256, 2)
        B, S = (4, 256)
        logits = jnp.einsum('bsh,eh->bse', x, router_w)
        probs = jax.nn.softmax(logits, axis=-1)
        weights, indices = jax.lax.top_k(probs, K)
        weights = weights / (weights.sum(axis=-1, keepdims=True) + 1e-06)
        h13 = jnp.einsum('bsh,ehi->bsei', x, w13)
        gate, up = jnp.split(h13, 2, axis=-1)
        h = jax.nn.silu(gate) * up
        y = jnp.einsum('bsei,eih->bseh', h, w2)
        y_sel = jnp.take_along_axis(y, indices[..., None], axis=2)
        return (y_sel * weights[..., None]).sum(axis=2)

    def _L3_attn_ref(x, Mq, Mk, Mv):
        import jax, jax.numpy as jnp
        import numpy as np
        HEADS = 8
        K_SIZE = 64
        B, C, _ = x.shape
        H, K = (HEADS, K_SIZE)
        V = Mv.shape[1] // H
        q = (x @ Mq).reshape(B, H, C, K)
        k = (x @ Mk).reshape(B, H, C, K)
        v = (x @ Mv).reshape(B, H, C, V)
        scores = jnp.einsum('bhqk,bhck->bhqc', q, k).reshape(B * H, C, C)
        att = jax.nn.softmax(scores / jnp.sqrt(jnp.float32(K)), axis=1)
        att4 = att.reshape(B, C, H, C)
        out = jnp.einsum('bqhc,bhcd->bqhd', att4, v)
        return out.reshape(B, C, H * V)

    def _L3_xattn_ref(Q, K, V, WQ, WK, WV, WO):
        import jax, jax.numpy as jnp
        import numpy as np
        H, S, D_MODEL, D_HEAD = (16, 512, 128, 64)
        q = jnp.einsum('bsd,hde->bhse', Q, WQ)
        k = jnp.einsum('btd,hde->bhte', K, WK)
        v = jnp.einsum('btd,hde->bhte', V, WV)
        scale = q.shape[-1] ** (-0.5)
        scores = jnp.einsum('bhse,bhte->bhst', q, k) * scale
        s_q, s_kv = (scores.shape[-2], scores.shape[-1])
        causal = jnp.tril(jnp.ones((s_q, s_kv), dtype=bool))
        scores = jnp.where(causal, scores, -jnp.inf)
        wei = jax.nn.softmax(scores, axis=-1)
        out = jnp.einsum('bhst,bhte->bhse', wei, v)
        b = out.shape[0]
        out = out.transpose(0, 2, 1, 3).reshape(b, s_q, -1)
        return out @ WO

    def _L3_ffn_ref(x, gate_w, ew1, ew2, ew3, sw1, sw2, sw3):
        import jax, jax.numpy as jnp
        import numpy as np
        EXPERTS = 8
        TOP_K = 2

        def swiglu(x, w1, w2, w3):
            h = x @ w1
            return h * jax.nn.sigmoid(h) * (x @ w2) @ w3
        B, S, D = x.shape
        gate_out = x @ gate_w
        top_v, top_i = jax.lax.top_k(gate_out, TOP_K)
        masked = jnp.full_like(gate_out, -1e+20)
        bi = jnp.arange(B)[:, None, None]
        si = jnp.arange(S)[None, :, None]
        masked = masked.at[bi, si, top_i].set(top_v)
        probs = jax.nn.softmax(masked, axis=-1)
        chosen = jnp.zeros_like(gate_out, dtype=bool).at[bi, si, top_i].set(True)
        w = jnp.where(chosen, probs, 0.0)

        def one_expert(w1, w2, w3, we):
            return swiglu(x, w1, w2, w3) * we[..., None]
        out = jax.vmap(one_expert, in_axes=(0, 0, 0, 2))(ew1, ew2, ew3, w).sum(0)
        out = out + swiglu(x, sw1, sw2, sw3)
        return out
    x = _layernorm(x + _L0_attn_ref(x, L0_attn_Wq, L0_attn_bq, L0_attn_Wk, L0_attn_bk, L0_attn_Wv, L0_attn_bv, L0_attn_Wo, L0_attn_bo), axis=-1)
    x = _layernorm(x + _L0_xattn_ref(x, ctx_1024, ctx_1024, L0_xattn_Wq, L0_xattn_bq, L0_xattn_Wk, L0_xattn_bk, L0_xattn_Wv, L0_xattn_bv, L0_xattn_Wo, L0_xattn_bo), axis=-1)
    x = _layernorm(x + _L0_ffn_ref(x, L0_ffn_router_w, L0_ffn_gate_up_w, L0_ffn_down_w, L0_ffn_shared_gate_w, L0_ffn_shared_up_w, L0_ffn_shared_down_w), axis=-1)
    x = _layernorm(x + _L1_attn_ref(x, L1_attn_ln_g, L1_attn_ln_b, L1_attn_fus_w, L1_attn_fus_b, L1_attn_f_in_w, L1_attn_f_conv_w, L1_attn_f_conv_b, L1_attn_f_xproj_w, L1_attn_f_dt_w, L1_attn_f_dt_b, L1_attn_f_A_log, L1_attn_f_D, L1_attn_f_out_w, L1_attn_b_in_w, L1_attn_b_conv_w, L1_attn_b_conv_b, L1_attn_b_xproj_w, L1_attn_b_dt_w, L1_attn_b_dt_b, L1_attn_b_A_log, L1_attn_b_D, L1_attn_b_out_w), axis=-1)
    x = _layernorm(x + _L1_xattn_ref(x, ctx_1024, ctx_1024, mask_1x1xSxS2_ik0, L1_xattn_Wq, L1_xattn_bq, L1_xattn_Wk, L1_xattn_bk, L1_xattn_Wv, L1_xattn_bv, L1_xattn_Wo, L1_xattn_bo), axis=-1)
    x = _layernorm(x + _L1_ffn_ref(x, L1_ffn_Wg, L1_ffn_gamma, L1_ffn_beta, L1_ffn_W1, L1_ffn_b1, L1_ffn_W2, L1_ffn_b2), axis=-1)
    x = _layernorm(x + _L2_attn_ref(x, L2_attn_w, L2_attn_u, L2_attn_time_mix_k, L2_attn_time_mix_v, L2_attn_time_mix_r, L2_attn_Wk, L2_attn_Wv, L2_attn_Wr, L2_attn_Wo), axis=-1)
    x = _layernorm(x + _L2_xattn_ref(x, ctx_1024, L2_xattn_w_q, L2_xattn_w_k, L2_xattn_w_v, L2_xattn_w_o), axis=-1)
    x = _layernorm(x + _L2_ffn_ref(x, L2_ffn_router_w, L2_ffn_w13, L2_ffn_w2), axis=-1)
    x = _layernorm(x + _L3_attn_ref(x, L3_attn_Mq, L3_attn_Mk, L3_attn_Mv), axis=-1)
    x = _layernorm(x + _L3_xattn_ref(x, ctx_1024, ctx_1024, L3_xattn_WQ, L3_xattn_WK, L3_xattn_WV, L3_xattn_WO), axis=-1)
    x = _layernorm(x + _L3_ffn_ref(x, L3_ffn_gate_w, L3_ffn_ew1, L3_ffn_ew2, L3_ffn_ew3, L3_ffn_sw1, L3_ffn_sw2, L3_ffn_sw3), axis=-1)
    return x

_drawn_inputs = setup_inputs


def setup_inputs(seed=0):
    import zlib

    import numpy as np

    out = dict(_drawn_inputs(seed))
    spreads = {'L1_attn_ln_g': (1.0, 0.6),
     'L1_attn_ln_b': (0.0, 0.8),
     'L1_attn_fus_b': (0.0, 0.1),
     'L1_attn_f_conv_b': (0.0, 0.8),
     'L1_attn_f_D': (1.0, 0.6),
     'L1_attn_b_conv_b': (0.0, 0.8),
     'L1_attn_b_D': (1.0, 0.6),
     'L1_ffn_gamma': (1.0, 0.2),
     'L1_ffn_beta': (0.0, 0.342),
     'L1_ffn_b1': (0.0, 0.341),
     'L1_ffn_b2': (0.0, 0.1)}
    factors = {'L0_attn_Wq': 8.0,
     'L0_attn_bq': 8.0,
     'L0_attn_Wk': 8.0,
     'L0_attn_bk': 8.0,
     'L0_xattn_bq': 8.0,
     'L0_xattn_bk': 8.0,
     'L0_xattn_bv': 3.481,
     'L0_xattn_bo': 3.261,
     'L0_ffn_router_w': 5.772,
     'L0_ffn_gate_up_w': 5.933,
     'L0_ffn_down_w': 4.744,
     'L0_ffn_shared_gate_w': 4.283,
     'L0_ffn_shared_up_w': 4.019,
     'L0_ffn_shared_down_w': 3.931,
     'L1_attn_fus_w': 8.0,
     'L1_attn_f_in_w': 8.0,
     'L1_attn_f_conv_w': 8.0,
     'L1_attn_f_xproj_w': 8.0,
     'L1_attn_f_dt_w': 8.0,
     'L1_attn_f_dt_b': 8.0,
     'L1_attn_f_A_log': 8.0,
     'L1_attn_f_out_w': 8.0,
     'L1_attn_b_in_w': 8.0,
     'L1_attn_b_conv_w': 8.0,
     'L1_attn_b_xproj_w': 8.0,
     'L1_attn_b_dt_w': 8.0,
     'L1_attn_b_dt_b': 8.0,
     'L1_attn_b_A_log': 8.0,
     'L1_attn_b_out_w': 8.0,
     'L1_xattn_bk': 8.0,
     'L2_attn_u': 2.736,
     'L2_ffn_router_w': 8.0,
     'L2_ffn_w13': 8.0,
     'L2_ffn_w2': 8.0,
     'L3_attn_Mq': 8.0,
     'L3_attn_Mk': 8.0,
     'L3_xattn_WQ': 8.0,
     'L3_xattn_WK': 8.0,
     'L3_ffn_gate_w': 8.0,
     'L3_ffn_ew1': 8.0,
     'L3_ffn_ew2': 8.0,
     'L3_ffn_ew3': 8.0,
     'L3_ffn_sw1': 6.967,
     'L3_ffn_sw2': 6.545,
     'L3_ffn_sw3': 6.942}
    for name, (base, spread) in spreads.items():
        noise = np.random.default_rng([zlib.crc32(name.encode()), seed]).standard_normal(out[name].shape)
        drawn = base * np.exp(spread * noise) if base else spread * noise
        out[name] = jnp.asarray(drawn.astype(out[name].dtype))
    for name, factor in factors.items():
        out[name] = (out[name] * factor).astype(out[name].dtype)
    return out
```

```python
import numpy as np

import concourse.bass as bass
from concourse import mybir
from contextlib import ExitStack

FP32 = mybir.dt.float32
BF16 = mybir.dt.bfloat16
I32 = mybir.dt.int32
ALU = mybir.AluOpType
ACT = mybir.ActivationFunctionType
AX = mybir.AxisListType

P = 128
B, S = 4, 256
TOK = B * S
NT = TOK // P
TPB = S // P
HALF = 512
HEADS = 16


class Signal:

    def __init__(self, ctx, nc, name):
        self.sem = ctx.enter_context(nc.semaphore(name))
        self.base = 0

    def __call__(self, n):
        return self.sem, n + self.base

    def past(self, total):
        self.base += total


class Steps:

    def __init__(self, signal, start=0):
        self.counter, self.count = signal, start

    def done(self, ins):
        self.count = self.count + 1
        ins.then_inc(self.counter.sem, 1)

    def last(self):
        return self.counter(self.count)


class Core:

    def __init__(self, ctx, nc):
        self.nc = nc

        def sb(name, shape, dt):
            return ctx.enter_context(nc.sbuf_tensor(name, shape, dt))

        self.x_tok = sb("x_tok", [P, NT, P], FP32)
        self.x_feat = sb("x_feat", [P, TOK], FP32)
        self.c_feat = sb("c_feat", [P, TOK], FP32)
        self.ident = sb("ident", [P, P], FP32)
        self.ident16 = sb("ident16", [P, P], BF16)
        self.ps = ctx.enter_context(nc.psum_tensor("ps", [P, 8, HALF], FP32))
        self.kept, self.number = {}, 0
        self.named = {}
        self.ctx = ctx

    def tensor(self, ctx, name, shape, dt):
        self.named[name] = self.named.get(name, 0) + 1
        return ctx.enter_context(self.nc.sbuf_tensor(f"{name}_{self.named[name]}", shape, dt))

    def counter(self, name, kept=False):
        if kept:
            if name not in self.kept:
                self.kept[name] = Signal(self.ctx, self.nc, name)
            return self.kept[name]
        signal = Signal(self.stage, self.nc, f"{name}_{self.number}")
        self.to_clear.append(signal.sem)
        return signal

    def new_stage(self, ctx):
        self.stage, self.number, self.to_clear = ctx, self.number + 1, []


def col(ap, n, size):
    return ap[:, bass.ds(n * size, size)]


class TokenNorm:

    STEPS = 2 * NT + 7

    def __init__(self, core, ctx, name, eps, steps, rooted):
        self.core, self.eps, self.steps, self.rooted = core, eps, steps, rooted
        self.stats = core.tensor(ctx, name + "_stats", [P, NT * 6], FP32)
        self.mv = core.tensor(ctx, name + "_mv", [P, NT, 2], FP32)
        self.var = core.tensor(ctx, name + "_var", [P, NT], FP32)
        self.rstd = core.tensor(ctx, name + "_rstd", [P, NT], FP32)
        self.root = core.tensor(ctx, name + "_root", [P, NT], FP32)

    def on_scalar(self, act):
        act.wait_ge(*self.steps(2 * NT + 1))
        act.activation(self.root[:, :], self.var[:, :], ACT.Sqrt).then_inc(self.rooted.sem, 1)

    def on_vector(self, dve):
        steps, stats, mv, var, rstd, root = self.steps, self.stats, self.mv, self.var, self.rstd, self.root
        for t in range(NT):
            dve.bn_stats(stats[:, 6 * t:6 * t + 6], self.core.x_tok[:, t, :]).then_inc(steps.sem, 1)
        for t in range(NT):
            dve.wait_ge(*steps(t + 1))
            dve.bn_aggr(mv[:, t, :], stats[:, 6 * t:6 * t + 6]).then_inc(steps.sem, 1)
        dve.wait_ge(*steps(2 * NT))
        dve.tensor_scalar(var[:, :], mv[:, :, 1], self.eps, None, ALU.add).then_inc(steps.sem, 1)
        dve.wait_ge(*self.rooted(1))
        dve.reciprocal(rstd[:, :], root[:, :]).then_inc(steps.sem, 1)
        dve.wait_ge(*steps(2 * NT + 2))
        dve.tensor_tensor(root[:, :], rstd[:, :], rstd[:, :], ALU.mult).then_inc(steps.sem, 1)
        dve.wait_ge(*steps(2 * NT + 3))
        dve.tensor_tensor(root[:, :], root[:, :], var[:, :], ALU.mult).then_inc(steps.sem, 1)
        dve.wait_ge(*steps(2 * NT + 4))
        dve.tensor_scalar(root[:, :], root[:, :], 1.0, -0.5, ALU.subtract, ALU.mult).then_inc(steps.sem, 1)
        dve.wait_ge(*steps(2 * NT + 5))
        dve.tensor_tensor(root[:, :], root[:, :], rstd[:, :], ALU.mult).then_inc(steps.sem, 1)
        dve.wait_ge(*steps(2 * NT + 6))
        dve.tensor_tensor(rstd[:, :], rstd[:, :], root[:, :], ALU.add).then_inc(steps.sem, 1)
        dve.wait_ge(*steps(2 * NT + 7))

    def normalise(self, dve, out, t):
        return dve.tensor_scalar(out, self.core.x_tok[:, t, :], self.mv[:, t, 0:1], self.rstd[:, t:t + 1],
                                 ALU.subtract, ALU.mult)


def load_stage(core, x, context, ident, ident16):
    nc = core.nc
    loaded = core.counter("io_loaded", kept=True)
    turned = core.counter("io_turned", kept=True)
    copied = core.counter("io_copied", kept=True)
    with ExitStack() as ctx:
        c_tok = core.tensor(ctx, "c_tok", [P, NT, P], FP32)
        with nc.Block(no_gpsimd_drain=True) as block:
            @block.sync
            def _(sp):
                sp.dma_start(core.x_tok[:, :, :], x.rearrange("(t p) d -> p t d", p=P)).then_inc(loaded.sem, 16)
                sp.dma_start(c_tok[:, :, :], context.rearrange("(t p) d -> p t d", p=P)).then_inc(loaded.sem, 16)
                sp.dma_start(core.ident[:, :], ident).then_inc(loaded.sem, 16)
                sp.dma_start(core.ident16[:, :], ident16).then_inc(loaded.sem, 16)

            @block.tensor
            def _(pe):
                pe.wait_ge(*loaded(64))
                for n, src in enumerate((core.x_tok, c_tok)):
                    for t in range(NT):
                        pe.transpose(core.ps[:, 2 * n + t // 4, t % 4 * P:(t % 4 + 1) * P], src[:, t, :],
                                     core.ident[:, :]).then_inc(turned.sem, 1)

            @block.scalar
            def _(act):
                for n, dst in enumerate((core.x_feat, core.c_feat)):
                    act.wait_ge(*turned(NT * (n + 1)))
                    act.copy(dst[:, :].rearrange("p (k c) -> p k c", k=2),
                             core.ps[:, 2 * n:2 * n + 2, :]).then_inc(copied.sem, 1)


def post_norm(core, out=None):
    nc, x_tok, x_feat, ps = core.nc, core.x_tok, core.x_feat, core.ps
    steps = core.counter("norm_steps", kept=True)
    normed = core.counter("norm_tile_ready", kept=True)
    turned = core.counter("norm_tile_turned", kept=True)
    copied = core.counter("norm_copied", kept=True)
    rooted = core.counter("norm_rooted", kept=True)
    with ExitStack() as ctx:
        norm = TokenNorm(core, ctx, "norm", 1e-5, steps, rooted)
        with nc.Block(no_gpsimd_drain=True) as block:
            @block.gpsimd
            def _(pool):
                for sem in core.to_clear:
                    pool.sem_clear(sem)

            @block.vector
            def _(dve):
                norm.on_vector(dve)
                for t in range(NT):
                    norm.normalise(dve, x_tok[:, t, :], t).then_inc(normed.sem, 1)

            if out is None:
                @block.tensor
                def _(pe):
                    for t in range(NT):
                        pe.wait_ge(*normed(t + 1))
                        pe.transpose(ps[:, t // 4, t % 4 * P:(t % 4 + 1) * P], x_tok[:, t, :],
                                     core.ident[:, :]).then_inc(turned.sem, 1)

                @block.scalar
                def _(act):
                    norm.on_scalar(act)
                    for k in range(2):
                        act.wait_ge(*turned(4 * k + 4))
                        act.copy(x_feat[:, k * HALF:(k + 1) * HALF], ps[:, k, :]).then_inc(copied.sem, 1)
            else:
                @block.scalar
                def _(act):
                    norm.on_scalar(act)

                @block.sync
                def _(sp):
                    dst = out.rearrange("(t p) d -> p t d", p=P)
                    for k in range(2):
                        sp.wait_ge(*normed(4 * k + 4))
                        sp.dma_start(dst[:, 4 * k:4 * k + 4, :], x_tok[:, 4 * k:4 * k + 4, :]).then_inc(copied.sem, 16)
                    sp.wait_ge(*copied(32))
    for s, total in ((steps, TokenNorm.STEPS), (rooted, 1), (normed, NT), (turned, NT), (copied, 2)):
        s.past(total)


def cross_attention(core, w, dim, scale, biased, masked):
    nc, ps = core.nc, core.ps
    HT = P // dim
    NQ = HEADS // HT
    HG = min(HT, 4)
    NG = HEADS // HG
    VD = HEADS * dim
    VB = (VD + HALF - 1) // HALF
    NC = VD // P
    names = ("slice_ready bias_added high_ready qk_ready q_taken k_taken v_ready v_taken low_ready max_ready max_taken "
             "shift_ready shift_turned shift_taken scores_ready probs_ready sums_inverted mixed_ready mixed_taken "
             "mixed_turned turned_taken y_ready y_taken consts mask_turned pool_held").split()
    sig = {n: core.counter("xa_" + n) for n in names}
    loaded = core.counter("xa_loaded")
    wq, wk, wv, wo = w["wq"], w["wk"], w["wv"], w["wo"]
    with ExitStack() as ctx:
        def sb(name, shape, dt=FP32):
            return core.tensor(ctx, "xa_" + name, shape, dt)

        wq_s, wk_s = sb("wq", [P, NQ * P]), sb("wk", [P, NQ * P])
        head_rows = sb("head_rows", [P, HT])
        wv_s, wo_s = sb("wv", [P, VD]), sb("wo", [P, NC * P])
        sel = sb("sel", [2 * HG, HG * P], BF16)
        xb, cb = sb("xb", [P, S]), sb("cb", [P, S])
        qT, kT = sb("qT", [P, NQ, S]), sb("kT", [P, HEADS, S])
        q16, k16 = sb("q16", [P, NQ, S], BF16), sb("k16", [P, HEADS, S], BF16)
        v = sb("v", [P, NG, TPB, HG, dim + 1])
        mx = sb("mx", [P, NG, TPB, HG])
        shift = sb("shift", [P, NG, TPB, 2, HG], BF16)
        shiftT = sb("shiftT", [2 * HG, NG * S], BF16)
        probs = sb("probs", [P, 2, TPB, HG, S])
        rec = sb("rec", [P, 2, TPB, HG])
        mixed = sb("mixed", [P, TPB, NG, HG * dim])
        mixedT = sb("mixedT", [P, TPB, NC, P])
        if biased:
            bq, bk = sb("bq", [P, NQ]), sb("bk", [P, NQ])
            bv, bo = sb("bv", [P, VD]), sb("bo", [P, P])
        if masked:
            mask_i = sb("mask_i", [P, TPB, S], I32)
            mask_f = sb("mask_f", [P, TPB, S])
            mask_q = sb("mask_q", [P, TPB, S], BF16)
            mask_k = sb("mask_k", [P, TPB, S], BF16)
        loads = [(wq_s[:, :], wq), (wk_s[:, :], wk), (wv_s[:, :], wv), (wo_s[:, :], wo), (sel[:, :], w["sel"]),
                 (head_rows[:, :], w["rows"])]
        if biased:
            loads += [(bq[:, :], w["bq"]), (bk[:, :], w["bk"]), (bv[:, :], w["bv"].partition_broadcast(P)),
                      (bo[:, :], w["bo"].partition_broadcast(P))]
        if masked:
            loads += [(mask_i[:, :, :], w["mask"].rearrange("(t p) k -> p t k", p=P))]
        ALL = 16 * len(loads)
        SH = S * NG
        mask_turns = TPB * TPB if masked else 0

        def scores_cols(h):
            return h * S // HALF, h * S % HALF

        with nc.Block(no_gpsimd_drain=True) as block:
            @block.sync
            def _(sp):
                for dst, src in loads:
                    sp.dma_start(dst, src).then_inc(loaded.sem, 16)

            @block.gpsimd
            def _(pool):
                pool.memset(v[:, :, :, :, dim:dim + 1], 1.0).then_inc(sig["consts"].sem, 1)
                if masked:
                    pool.wait_ge(*loaded(ALL))
                    pool.tensor_copy(mask_f[:, :, :], mask_i[:, :, :]).then_inc(sig["consts"].sem, 1)
                with pool.Fori(0, B) as b:
                    pool.wait_ge(*sig["v_ready"](TPB * b + 1))
                    pool.sem_inc(sig["pool_held"].sem, 1)
                    pool.tensor_copy(xb[:, :], col(core.x_feat, b, S)).then_inc(sig["slice_ready"].sem, 1)
                    pool.tensor_copy(cb[:, :], col(core.c_feat, b, S)).then_inc(sig["slice_ready"].sem, 1)
                    for n in range(NQ):
                        pool.wait_ge(*sig["q_taken"](b * NQ + n + 3))
                        pool.sem_inc(sig["pool_held"].sem, 1)
                        pool.tensor_copy(q16[:, n, :], qT[:, n, :]).then_inc(sig["low_ready"].sem, 1)
                        pool.wait_ge(*sig["k_taken"](b * NQ + n + 3))
                        pool.sem_inc(sig["pool_held"].sem, 1)
                        pool.tensor_copy(k16[:, n * HT:(n + 1) * HT, :],
                                         kT[:, n * HT:(n + 1) * HT, :]).then_inc(sig["low_ready"].sem, 1)

            @block.tensor
            def _(pe):
                pe.sem_inc(sig["v_ready"].sem, 1)
                pe.wait_ge(*loaded(ALL))
                if masked:
                    pe.wait_ge(*sig["consts"](3))
                    for t in range(TPB):
                        for k in range(TPB):
                            m_ps = ps[:, 7, :].bitcast(BF16)
                            pe.transpose(m_ps[:, (t * TPB + k) * P:(t * TPB + k + 1) * P],
                                         mask_q[:, t, k * P:(k + 1) * P],
                                         core.ident16[:, :]).then_inc(sig["mask_turned"].sem, 1)
                    pe.wait_ge(*sig["consts"](4))
                with pe.Fori(0, B) as b:
                    pe.wait_ge(*sig["slice_ready"](2 * b + 2))
                    pe.wait_ge(*sig["y_taken"](b + 1))
                    for n in range(NQ):
                        pe.wait_ge(*sig["q_taken"](b * NQ + n + 1))
                        pe.wait_ge(*sig["k_taken"](b * NQ + n + 1))
                        pe.matmul(ps[:, n % 2, 0:S], wq_s[:, n * P:(n + 1) * P], xb[:, :], start=True, stop=True)
                        pe.matmul(ps[:, 2 + n % 2, 0:S], wk_s[:, n * P:(n + 1) * P], cb[:, :],
                                  start=True, stop=True).then_inc(sig["qk_ready"].sem, 1)
                    for t in range(TPB):
                        for n in range(VB):
                            width = min(HALF, VD)
                            last = pe.matmul(ps[:, 4 + 2 * t + n, 0:width], cb[:, t * P:(t + 1) * P],
                                             wv_s[:, n * width:(n + 1) * width], start=True, stop=True)
                        last.then_inc(sig["v_ready"].sem, 1)
                    for g in range(NG):
                        if g == 0:
                            pe.wait_ge(*sig["low_ready"](b * 2 * NQ + 2 * NQ))
                            pe.wait_ge(*sig["v_taken"](TPB * b + TPB))
                            pe.wait_ge(*sig["q_taken"](b * NQ + NQ + 2))
                            pe.wait_ge(*sig["k_taken"](b * NQ + NQ + 2))
                        for t in range(TPB):
                            pe.wait_ge(*sig["max_taken"]((b * NG + g) * TPB + t + 1))
                            for h in range(0, HG, 2):
                                dst = ps[:, 4 + 2 * t + h // 2, :]
                                head = g * HG + h
                                last = pe.matmul(dst, q16[:, head // HT, t * P:(t + 1) * P],
                                                 k16[:, head:head + 2, :].rearrange("p h s -> p (h s)"),
                                                 start=True, stop=not masked)
                                if masked:
                                    last = pe.matmul(dst.rearrange("p (h s) -> p h s", h=2), core.ident16[:, :],
                                                     mask_q[:, t, :].unsqueeze(1).to_broadcast([P, 2, S]),
                                                     start=False, stop=True)
                            last.then_inc(sig["max_ready"].sem, 1)
                    pe.wait_ge(*sig["shift_ready"](b + 1))
                    for g in range(NG):
                        for t in range(TPB):
                            o = (g * TPB + t) * P
                            last = pe.transpose(ps[0:2 * HG, o // 1024, :].bitcast(BF16)[:, o % 1024:o % 1024 + P],
                                                shift[:, g, t, :, :].rearrange("p a h -> p (a h)"),
                                                core.ident16[:, :])
                    last.then_inc(sig["shift_turned"].sem, 1)

                    def make_scores(g):
                        for t in range(TPB):
                            if g >= 1:
                                pe.wait_ge(*sig["probs_ready"]((b * NG + g - 1) * TPB + t + 1))
                            for h in range(HG):
                                bank, c = scores_cols(h)
                                dst = ps[:, 2 * t + bank, c:c + S]
                                head = g * HG + h
                                pe.matmul(dst, kT[:, head, t * P:(t + 1) * P], qT[:, head // HT, :],
                                          start=True, stop=False)
                                if masked:
                                    pe.matmul(dst, core.ident16[:, :], mask_k[:, t, :], start=False, stop=False)
                                last = pe.matmul(dst, sel[:, h * P:(h + 1) * P], shiftT[:, g * S:(g + 1) * S],
                                                 start=False, stop=True)
                            last.then_inc(sig["scores_ready"].sem, 1)

                    pe.wait_ge(*sig["shift_taken"](b + 1))
                    make_scores(0)
                    for g in range(NG):
                        if g + 1 < NG:
                            make_scores(g + 1)
                        pe.wait_ge(*sig["probs_ready"]((b * NG + g) * TPB + TPB))
                        pe.wait_ge(*sig["mixed_taken"](b * NG + g + 1))
                        for q in range(TPB):
                            for h in range(HG):
                                o = (q * HG + h) * (dim + 1)
                                for t in range(TPB):
                                    last = pe.matmul(ps[:, 4 + g % 2, o:o + dim + 1],
                                                     probs[:, g % 2, t, h, q * P:(q + 1) * P], v[:, g, t, h, :],
                                                     start=t == 0, stop=t == TPB - 1)
                        last.then_inc(sig["mixed_ready"].sem, 1)
                    pe.wait_ge(*sig["mixed_taken"](b * NG + NG + 2))
                    for q in range(TPB):
                        if q:
                            pe.wait_ge(*sig["turned_taken"](TPB * b + q))
                        for c in range(NC):
                            if VD == P:
                                src = mixed[:, q, :, :].rearrange("p g f -> p (g f)")
                            else:
                                src = mixed[:, q, c, :]
                            last = pe.transpose(ps[:, 6 + c // 4, c % 4 * P:(c % 4 + 1) * P], src, core.ident[:, :])
                        last.then_inc(sig["mixed_turned"].sem, 1)
                    for q in range(TPB):
                        pe.wait_ge(*sig["turned_taken"](TPB * b + q + 1))
                        for c in range(NC):
                            last = pe.matmul(ps[:, 4, q * P:(q + 1) * P], mixedT[:, q, c, :],
                                             wo_s[:, c * P:(c + 1) * P], start=c == 0, stop=c == NC - 1)
                    last.then_inc(sig["y_ready"].sem, 1)

            @block.scalar
            def _(act):
                act.sem_inc(sig["q_taken"].sem, 2)
                act.wait_ge(*loaded(ALL))
                with act.Fori(0, B) as b:
                    for n in range(NQ):
                        act.wait_ge(*sig["qk_ready"](b * NQ + n + 1))
                        if biased:
                            act.activation(qT[:, n, :], ps[:, n % 2, 0:S], ACT.Identity,
                                           bias=bq[:, n:n + 1]).then_inc(sig["q_taken"].sem, 1)
                        else:
                            act.copy(qT[:, n, :], ps[:, n % 2, 0:S]).then_inc(sig["q_taken"].sem, 1)
                    for g in range(NG):
                        if g >= 2:
                            act.wait_ge(*sig["mixed_ready"](b * NG + g - 1))
                        for t in range(TPB):
                            act.wait_ge(*sig["scores_ready"]((b * NG + g) * TPB + t + 1))
                            nb = HG * S // HALF
                            act.activation(probs[:, g % 2, t, :, :].rearrange("p h s -> p (h s)")
                                           .rearrange("p (n c) -> p n c", n=nb),
                                           ps[:, 2 * t:2 * t + nb, :], ACT.Exp,
                                           scale=scale).then_inc(sig["probs_ready"].sem, 1)
                    for q in range(TPB):
                        act.wait_ge(*sig["mixed_turned"](TPB * b + q + 1))
                        if NC == 1:
                            act.copy(mixedT[:, q, 0, :], ps[:, 6, 0:P]).then_inc(sig["turned_taken"].sem, 1)
                        else:
                            act.copy(mixedT[:, q, :, :].rearrange("p c f -> p (c f)").rearrange("p (n c) -> p n c", n=NC // 4),
                                     ps[:, 6:6 + NC // 4, :]).then_inc(sig["turned_taken"].sem, 1)

            @block.vector
            def _(dve):
                dve.sem_inc(sig["k_taken"].sem, 2)
                dve.sem_inc(sig["max_taken"].sem, 2)
                dve.sem_inc(sig["mixed_taken"].sem, 2)
                dve.sem_inc(sig["y_taken"].sem, 1)
                dve.wait_ge(*loaded(ALL))
                if biased:
                    dve.tensor_tensor(core.x_tok[:, :, :], core.x_tok[:, :, :],
                                      bo[:, :].unsqueeze(1).to_broadcast([P, NT, P]), ALU.add)\
                       .then_inc(sig["bias_added"].sem, 1)
                if masked:
                    dve.wait_ge(*sig["consts"](2))
                    dve.tensor_scalar(mask_q[:, :, :], mask_f[:, :, :], 0.0, -1e30, ALU.is_equal, ALU.mult)\
                       .then_inc(sig["consts"].sem, 1)
                    dve.wait_ge(*sig["mask_turned"](mask_turns))
                    m_ps = ps[:, 7, :].bitcast(BF16)
                    dve.tensor_copy(mask_k[:, :, :].rearrange("p k (t q) -> p k t q", t=TPB),
                                    m_ps[:, 0:TPB * TPB * P].rearrange("p (t k q) -> p k t q", t=TPB, k=TPB))\
                       .then_inc(sig["consts"].sem, 1)
                with dve.Fori(0, B) as b:
                    for n in range(NQ):
                        dve.wait_ge(*sig["qk_ready"](b * NQ + n + 1))
                        dst = kT[:, n * HT:(n + 1) * HT, :]
                        src = ps[:, 2 + n % 2, 0:S].unsqueeze(1).to_broadcast([P, HT, S])
                        rows = head_rows[:, :].unsqueeze(2).to_broadcast([P, HT, S])
                        if biased:
                            dve.scalar_tensor_tensor(dst, src, bk[:, n:n + 1], rows, ALU.add,
                                                     ALU.mult).then_inc(sig["k_taken"].sem, 1)
                        else:
                            dve.tensor_tensor(dst, src, rows, ALU.mult).then_inc(sig["k_taken"].sem, 1)
                    dve.wait_ge(*sig["consts"](1))
                    for t in range(TPB):
                        dve.wait_ge(*sig["v_ready"](TPB * b + t + 2))
                        for n in range(VB):
                            gs = NG // VB
                            dst = v[:, n * gs:(n + 1) * gs, t, :, 0:dim]
                            src = ps[:, 4 + 2 * t + n, 0:min(HALF, VD)].rearrange("p (g h d) -> p g h d", g=gs, h=HG)
                            if biased:
                                last = dve.tensor_tensor(dst, src, bv[:, n * HALF:n * HALF + min(HALF, VD)]
                                                         .rearrange("p (g h d) -> p g h d", g=gs, h=HG), ALU.add)
                            else:
                                last = dve.tensor_copy(dst, src)
                        last.then_inc(sig["v_taken"].sem, 1)
                    for g in range(NG):
                        for t in range(TPB):
                            dve.wait_ge(*sig["max_ready"]((b * NG + g) * TPB + t + 1))
                            nb = HG * S // HALF
                            dve.tensor_reduce(mx[:, g, t, :], ps[:, 4 + 2 * t:4 + 2 * t + nb, :]
                                              .rearrange("p n (h s) -> p (n h) s", s=S), AX.X, ALU.max)\
                               .then_inc(sig["max_taken"].sem, 1)
                    dve.wait_ge(*sig["max_taken"]((b + 1) * NG * TPB + 2))
                    hi = shift[:, :, :, 0, :].rearrange("p g t h -> p (g t) h")
                    lo = shift[:, :, :, 1, :].rearrange("p g t h -> p (g t) h")
                    m3 = mx[:, :, :, :].rearrange("p g t h -> p (g t) h")
                    dve.tensor_scalar(hi, m3, -1.0, None, ALU.mult).then_inc(sig["high_ready"].sem, 1)
                    dve.wait_ge(*sig["high_ready"](b + 1))
                    dve.scalar_tensor_tensor(lo, m3, -1.0, hi, ALU.mult, ALU.subtract).then_inc(sig["shift_ready"].sem, 1)
                    dve.wait_ge(*sig["shift_turned"](b + 1))
                    for n in range((SH + 1023) // 1024):
                        last = dve.tensor_copy(shiftT[:, n * 1024:(n + 1) * 1024],
                                               ps[0:2 * HG, n, :].bitcast(BF16))
                    last.then_inc(sig["shift_taken"].sem, 1)
                    for g in range(NG):
                        dve.wait_ge(*sig["mixed_ready"](b * NG + g + 1))
                        acc = ps[:, 4 + g % 2, 0:TPB * HG * (dim + 1)].rearrange("p (q h d) -> p q h d", q=TPB, h=HG)
                        dve.reciprocal(rec[:, g % 2, :, :], acc[:, :, :, dim]).then_inc(sig["sums_inverted"].sem, 1)
                        dve.wait_ge(*sig["sums_inverted"](b * NG + g + 1))
                        dve.tensor_tensor(mixed[:, :, g, :].rearrange("p q (h d) -> p q h d", h=HG),
                                          acc[:, :, :, 0:dim],
                                          rec[:, g % 2, :, :].unsqueeze(3).to_broadcast([P, TPB, HG, dim]),
                                          ALU.mult).then_inc(sig["mixed_taken"].sem, 1)
                    dve.wait_ge(*sig["y_ready"](b + 1))
                    if biased:
                        dve.wait_ge(*sig["bias_added"](1))
                    xs = core.x_tok[:, bass.ds(b * TPB, TPB), :]
                    dve.tensor_tensor(xs, xs, ps[:, 4, 0:TPB * P].rearrange("p (q f) -> p q f", q=TPB),
                                      ALU.add).then_inc(sig["y_taken"].sem, 1)


ROUTE_SIGNALS = "logits_ready steps exps_ready parts_ready parts_turned parts_taken zeroed".split()


class Routing:

    def __init__(self, core, sb, sig, scores, NE, rule):
        self.core, self.sig, self.scores, self.NE, self.rule = core, sig, scores, NE, rule
        self.K3 = 3 * NE
        self.router = sb("router", [P, scores])
        self.sel = sb("sel", [P, NE * P], BF16)
        self.top = sb("top", [P, NT, 8])
        self.lg = sb("lg", [P, NT, scores])
        self.ex = sb("ex", [P, NT, scores])
        self.ch = sb("ch", [P, NT, scores])
        self.den = sb("den", [P, NT, 2])
        self.wt = sb("wt", [P, NT, NE])
        self.rest = sb("rest", [P, NT, NE])
        self.parts = sb("parts", [P, NT, 3, NE], BF16)
        self.partsT = sb("partsT", [P, TOK], BF16)

    def on_tensor(self, pe):
        core, sig, ps = self.core, self.sig, self.core.ps
        for t in range(NT):
            last = pe.matmul(ps[:, 0, t * self.scores:(t + 1) * self.scores], core.x_feat[:, t * P:(t + 1) * P],
                             self.router[:, :], start=True, stop=True)
        last.then_inc(sig["logits_ready"].sem, 1)
        pe.wait_ge(*sig["parts_ready"](1))
        for t in range(NT):
            last = pe.transpose(ps[0:self.K3, 1, :].bitcast(BF16)[:, t * P:(t + 1) * P],
                                self.parts[:, t, :, :].rearrange("p a e -> p (a e)"), core.ident16[:, :])
        last.then_inc(sig["parts_turned"].sem, 1)

    def on_scalar(self, act):
        act.wait_ge(*self.sig["steps"](2))
        act.activation(self.ex[:, :, :], self.lg[:, :, :], ACT.Exp, scale=-1.0 if self.rule == "sigmoid" else 1.0)\
           .then_inc(self.sig["exps_ready"].sem, 1)

    def on_vector(self, dve):
        sig, ps, scores, rule, NE, K3 = self.sig, self.core.ps, self.scores, self.rule, self.NE, self.K3
        top, lg, ex, ch, den, wt, rest = self.top, self.lg, self.ex, self.ch, self.den, self.wt, self.rest
        parts, partsT, shared = self.parts, self.partsT, NE > scores
        route = Steps(sig["steps"], 0)
        dve.wait_ge(*sig["logits_ready"](1))
        logits = ps[:, 0, 0:NT * scores].rearrange("p (t e) -> p t e", t=NT)
        for t in range(NT):
            last = dve.max(top[:, t, :], logits[:, t, :])
        route.done(last)
        dve.wait_ge(*route.last())
        first = top[:, :, 0:1].to_broadcast([P, NT, scores])
        second = top[:, :, 1:2].to_broadcast([P, NT, scores])
        if rule == "sigmoid":
            route.done(dve.tensor_copy(lg[:, :, :], logits))
        else:
            route.done(dve.tensor_tensor(lg[:, :, :], logits, first, ALU.subtract))
        route.done(dve.tensor_tensor(ch[:, :, :], logits, second, ALU.is_ge))
        dve.wait_ge(*sig["exps_ready"](1))
        dve.wait_ge(*route.last())
        if rule == "sigmoid":
            route.done(dve.tensor_scalar(ex[:, :, :], ex[:, :, :], 1.0, None, ALU.add))
            dve.wait_ge(*route.last())
            route.done(dve.reciprocal(ex[:, :, :], ex[:, :, :]))
            dve.wait_ge(*route.last())
            if shared:
                dve.wait_ge(*sig["zeroed"](3))
            route.done(dve.tensor_tensor(wt[:, :, 0:scores], ex[:, :, :], ch[:, :, :], ALU.mult))
        else:
            if rule == "renormalised":
                route.done(dve.tensor_reduce(den[:, :, 1], ex[:, :, :], AX.X, ALU.add))
            route.done(dve.tensor_tensor(ch[:, :, :], ex[:, :, :], ch[:, :, :], ALU.mult))
            dve.wait_ge(*route.last())
            route.done(dve.tensor_reduce(den[:, :, 0], ch[:, :, :], AX.X, ALU.add))
            dve.wait_ge(*route.last())
            if rule == "renormalised":
                route.done(dve.scalar_tensor_tensor(den[:, :, 0], den[:, :, 1], 1e-6, den[:, :, 0],
                                                    ALU.mult, ALU.add))
                dve.wait_ge(*route.last())
            route.done(dve.reciprocal(den[:, :, 0], den[:, :, 0]))
            dve.wait_ge(*route.last())
            if shared:
                dve.wait_ge(*sig["zeroed"](3))
            route.done(dve.tensor_tensor(wt[:, :, 0:scores], ch[:, :, :],
                                         den[:, :, 0:1].to_broadcast([P, NT, scores]), ALU.mult))
        dve.wait_ge(*route.last())
        route.done(dve.tensor_copy(parts[:, :, 0, :], wt[:, :, :]))
        dve.wait_ge(*route.last())
        route.done(dve.tensor_tensor(rest[:, :, :], wt[:, :, :], parts[:, :, 0, :], ALU.subtract))
        dve.wait_ge(*route.last())
        route.done(dve.tensor_copy(parts[:, :, 1, :], rest[:, :, :]))
        dve.wait_ge(*route.last())
        dve.tensor_tensor(parts[:, :, 2, :], rest[:, :, :], parts[:, :, 1, :], ALU.subtract)\
           .then_inc(sig["parts_ready"].sem, 1)
        dve.wait_ge(*sig["parts_turned"](1))
        dve.wait_ge(*sig["zeroed"](1))
        dve.tensor_copy(partsT[0:K3, :], ps[0:K3, 1, :].bitcast(BF16)).then_inc(sig["parts_taken"].sem, 1)


def gated_experts(core, w, units, per_expert, scores, rule):
    nc, ps, x_tok, x_feat = core.nc, core.ps, core.x_tok, core.x_feat
    NE = units // per_expert
    shared = NE > scores
    names = ROUTE_SIGNALS + ("even_unit_loaded odd_unit_loaded gate_ready gate_taken up_ready up_taken spread_ready hidden_ready "
                             "hidden_used y_copied y_turned").split()
    sig = {n: core.counter("ff_" + n) for n in names}
    unit_loaded = sig["even_unit_loaded"], sig["odd_unit_loaded"]
    loaded = core.counter("ff_loaded")
    with ExitStack() as ctx:
        def sb(name, shape, dt=FP32):
            return core.tensor(ctx, "ff_" + name, shape, dt)

        routing = Routing(core, sb, sig, scores, NE, rule)
        ring = sb("ring", [P, 2, 3 * P])
        gate = sb("gate", [P, 2, 2, HALF])
        up = sb("up", [P, 2, 2, HALF])
        hid = sb("hid", [P, 2, 2, HALF])
        yT = sb("yT", [P, TOK])
        zero = sb("zero", [P, HALF], BF16)
        GATE, UP, SPREAD, Y = 0, 2, 4, 6

        with nc.Block(no_gpsimd_drain=True) as block:
            @block.sync
            def _(sp):
                sp.dma_start(routing.router[:, :], w["router"]).then_inc(loaded.sem, 16)
                sp.dma_start(routing.sel[:, :], w["sel"]).then_inc(loaded.sem, 16)
                for s in range(2):
                    sp.dma_start(ring[:, s, :], w["units"][s, :, :]).then_inc(unit_loaded[s].sem, 16)
                with sp.Fori(0, units // 2 - 1) as i:
                    for s in range(2):
                        sp.wait_ge(*sig["hidden_used"](2 * i + s + 3))
                        sp.dma_start(ring[:, s, :], w["units"][bass.ds(2 * i + s + 2, 1), :, :]
                                     .rearrange("u p n -> p (u n)")).then_inc(unit_loaded[s].sem, 16)

            @block.gpsimd
            def _(pool):
                pool.memset(routing.partsT[:, :], 0.0).then_inc(sig["zeroed"].sem, 1)
                pool.memset(zero[:, :], 0.0).then_inc(sig["zeroed"].sem, 1)
                if shared:
                    pool.memset(routing.wt[:, :, scores:NE], 1.0).then_inc(sig["zeroed"].sem, 1)

            def products_up(pe, n, s, turn, e):
                pe.wait_ge(*unit_loaded[s](16 * turn + 16))
                for h in range(2):
                    cols = x_feat[:, h * HALF:(h + 1) * HALF]
                    pe.wait_ge(*sig["gate_taken"](2 * n + h + 1))
                    pe.matmul(ps[:, GATE + h, :], ring[:, s, 0:P], cols, start=True, stop=True)\
                      .then_inc(sig["gate_ready"].sem, 1)
                    pe.wait_ge(*sig["up_taken"](2 * n + h + 3))
                    pe.matmul(ps[:, UP + h, :], ring[:, s, P:2 * P], cols, start=True, stop=True)\
                      .then_inc(sig["up_ready"].sem, 1)
                for h in range(2):
                    pe.wait_ge(*sig["hidden_ready"](2 * n + h + 1))
                    pe.matmul(ps[:, SPREAD + h, :], routing.sel[:, bass.ds(e * P, P)],
                              routing.partsT[:, h * HALF:(h + 1) * HALF],
                              start=True, stop=True).then_inc(sig["spread_ready"].sem, 1)

            def products_down(pe, n, s, last=False):
                for h in range(2):
                    pe.wait_ge(*sig["hidden_ready"](2 * n + h + 3))
                    ins = pe.matmul(ps[:, Y + h, :], ring[:, s, 2 * P:3 * P], hid[:, s, h, :], start=False, stop=last)
                    if h == 1:
                        ins.then_inc(sig["hidden_used"].sem, 1)

            @block.tensor
            def _(pe):
                pe.sem_inc(sig["hidden_used"].sem, 2)
                pe.wait_ge(*loaded(32))
                pe.wait_ge(*sig["zeroed"](2))
                for h in range(2):
                    pe.matmul(ps[:, Y + h, :], zero[:, 0:P], zero[:, :], start=True, stop=False)
                routing.on_tensor(pe)
                pe.wait_ge(*sig["parts_taken"](1))
                products_up(pe, 0, 0, 0, 0)
                with pe.Fori(0, units // 2 - 1) as i:
                    n = 2 * i
                    products_up(pe, n + 1, 1, i, n + 1 if per_expert == 1 else i)
                    products_down(pe, n, 0)
                    products_up(pe, n + 2, 0, i + 1, n + 2 if per_expert == 1 else i + 1)
                    products_down(pe, n + 1, 1)
                products_up(pe, units - 1, 1, units // 2 - 1, NE - 1)
                products_down(pe, units - 2, 0)
                products_down(pe, units - 1, 1, last=True)
                pe.wait_ge(*sig["y_copied"](1))
                for t in range(NT):
                    pe.transpose(ps[:, t // 4, t % 4 * P:(t % 4 + 1) * P], yT[:, t * P:(t + 1) * P],
                                 core.ident[:, :]).then_inc(sig["y_turned"].sem, 1)

            @block.scalar
            def _(act):
                act.sem_inc(sig["gate_taken"].sem, 2)
                routing.on_scalar(act)
                with act.Fori(0, units // 2) as i:
                    for s in range(2):
                        for h in range(2):
                            n = 2 * i + s
                            act.wait_ge(*sig["gate_ready"](2 * n + h + 1))
                            act.wait_ge(*sig["up_taken"](2 * n + h + 1))
                            act.activation(gate[:, s, h, :], ps[:, GATE + h, :], ACT.Silu)\
                               .then_inc(sig["gate_taken"].sem, 1)
                act.wait_ge(*sig["hidden_used"](units + 2))
                act.copy(yT[:, :].rearrange("p (n c) -> p n c", n=2), ps[:, Y:Y + 2, :]).then_inc(sig["y_copied"].sem, 1)

            @block.vector
            def _(dve):
                dve.sem_inc(sig["up_taken"].sem, 4)
                dve.sem_inc(sig["hidden_ready"].sem, 2)
                dve.wait_ge(*loaded(32))
                routing.on_vector(dve)
                with dve.Fori(0, units // 2) as i:
                    for s in range(2):
                        for h in range(2):
                            n = 2 * i + s
                            dve.wait_ge(*sig["gate_taken"](2 * n + h + 3))
                            dve.wait_ge(*sig["up_ready"](2 * n + h + 1))
                            dve.tensor_tensor(up[:, s, h, :], gate[:, s, h, :], ps[:, UP + h, :], ALU.mult)\
                               .then_inc(sig["up_taken"].sem, 1)
                        for h in range(2):
                            dve.wait_ge(*sig["up_taken"](2 * n + h + 5))
                            dve.wait_ge(*sig["hidden_used"](n + 1))
                            dve.wait_ge(*sig["spread_ready"](2 * n + h + 1))
                            dve.tensor_tensor(hid[:, s, h, :], up[:, s, h, :], ps[:, SPREAD + h, :], ALU.mult)\
                               .then_inc(sig["hidden_ready"].sem, 1)
                for t in range(2):
                    dve.wait_ge(*sig["y_turned"](4 * t + 4))
                    xs = x_tok[:, 4 * t:4 * t + 4, :]
                    dve.tensor_tensor(xs, xs, ps[:, t, :].rearrange("p (t f) -> p t f", t=4), ALU.add)


def normed_experts(core, w):
    nc, ps, x_tok, x_feat = core.nc, core.ps, core.x_tok, core.x_feat
    NE, U = 8, 4
    names = ROUTE_SIGNALS + ("even_loaded odd_loaded tile_ready tile_turned xhat_ready normed_ready hid_ready "
                             "relu_taken spread_ready spread_taken hidden_ready hidden_used wt_turned wt_taken "
                             "held own norm_steps rooted y_copied y_turned").split()
    sig = {n: core.counter("ne_" + n) for n in names}
    loaded = core.counter("ne_loaded")
    mats_loaded = sig["even_loaded"], sig["odd_loaded"]
    with ExitStack() as ctx:
        def sb(name, shape, dt=FP32):
            return core.tensor(ctx, "ne_" + name, shape, dt)

        routing = Routing(core, sb, sig, NE, NE, "softmax")
        ring = sb("ring", [P, 2, 2, U, P])
        gamma, beta, b1 = sb("gamma", [P, NE]), sb("beta", [P, NE]), sb("b1", [P, NE * U])
        b2 = sb("b2", [NE, P])
        norm = TokenNorm(core, ctx, "ne", 1e-6, sig["norm_steps"], sig["rooted"])
        xhat = sb("xhat", [P, NT, P])
        xhatT = sb("xhatT", [P, TOK])
        normed = sb("normed", [P, 2, TOK])
        relu = sb("relu", [P, 2, 2, HALF])
        hid = sb("hid", [P, 2, 2, HALF])
        spread = sb("spread", [P, 2, TOK])
        wtT = sb("wtT", [NE, TOK])
        total = sb("total", [P, NT])
        yT = sb("yT", [P, TOK])
        HID, SPREAD, Y = 0, 4, 6

        with nc.Block(no_gpsimd_drain=True) as block:
            @block.sync
            def _(sp):
                for dst, src in ((routing.router, "router"), (routing.sel, "sel"), (gamma, "gamma"), (beta, "beta"),
                                 (b1, "b1"), (b2, "b2")):
                    sp.dma_start(dst[:, :], w[src]).then_inc(loaded.sem, 16)
                for s in range(2):
                    sp.dma_start(ring[:, s, :, :, :].rearrange("p a u f -> p (a u f)"), w["mats"][s, :, :])\
                      .then_inc(mats_loaded[s].sem, 16)
                with sp.Fori(0, NE // 2 - 1) as i:
                    for s in range(2):
                        sp.wait_ge(*sig["hidden_used"](U * (2 * i + s) + U + 2))
                        sp.dma_start(ring[:, s, :, :, :].rearrange("p a u f -> p (a u f)"),
                                     w["mats"][bass.ds(2 * i + s + 2, 1), :, :].rearrange("e p n -> p (e n)"))\
                          .then_inc(mats_loaded[s].sem, 16)

            @block.gpsimd
            def _(pool):
                pool.memset(routing.partsT[:, :], 0.0).then_inc(sig["zeroed"].sem, 1)

            def products_up(pe, n, s, u):
                for h in range(2):
                    pe.wait_ge(*sig["relu_taken"](2 * n + h + 1))
                    pe.matmul(ps[:, HID + 2 * (u % 2) + h, :], ring[:, s, 0, u, :],
                              normed[:, s, h * HALF:(h + 1) * HALF], start=True, stop=True)\
                      .then_inc(sig["hid_ready"].sem, 1)

            def enter_expert(pe, e, s, turn):
                for h in range(2):
                    pe.wait_ge(*sig["spread_taken"](2 * e + h + 1))
                    pe.matmul(ps[:, SPREAD + h, :], routing.sel[:, bass.ds(e * P, P)],
                              routing.partsT[:, h * HALF:(h + 1) * HALF], start=True, stop=True)\
                      .then_inc(sig["spread_ready"].sem, 1)
                pe.wait_ge(*mats_loaded[s](16 * turn + 16))
                pe.wait_ge(*sig["normed_ready"](e + 1))

            def products_down(pe, n, s, u, last=False):
                for h in range(2):
                    pe.wait_ge(*sig["hidden_ready"](2 * n + h + 5))
                    ins = pe.matmul(ps[:, Y + h, :], ring[:, s, 1, u, :], hid[:, u % 2, h, :], start=False, stop=last)
                    if h == 1:
                        ins.then_inc(sig["hidden_used"].sem, 1)

            @block.tensor
            def _(pe):
                pe.sem_inc(sig["hidden_used"].sem, 2)
                pe.wait_ge(*loaded(96))
                for t in range(NT):
                    pe.wait_ge(*sig["tile_ready"](t + 1))
                    pe.transpose(ps[:, 2 + t // 4, t % 4 * P:(t % 4 + 1) * P], xhat[:, t, :],
                                 core.ident[:, :]).then_inc(sig["tile_turned"].sem, 1)
                routing.on_tensor(pe)
                for t in range(NT):
                    last = pe.transpose(ps[0:NE, 4 + t // 4, t % 4 * P:(t % 4 + 1) * P], routing.wt[:, t, :],
                                        core.ident[:, :])
                last.then_inc(sig["wt_turned"].sem, 1)
                pe.wait_ge(*sig["wt_taken"](1))
                for h in range(2):
                    pe.matmul(ps[:, Y + h, :], b2[:, :], wtT[:, h * HALF:(h + 1) * HALF], start=True, stop=False)
                pe.wait_ge(*sig["parts_taken"](1))
                pe.wait_ge(*sig["xhat_ready"](2))
                enter_expert(pe, 0, 0, 0)
                products_up(pe, 0, 0, 0)

                def pair(i, final):
                    for k in range(2 * U):
                        n = 2 * U * i + k
                        if k + 1 == U:
                            enter_expert(pe, 2 * i + 1, 1, i)
                        if k + 1 == 2 * U and not final:
                            enter_expert(pe, 2 * i + 2, 0, i + 1)
                        if not (final and k + 1 == 2 * U):
                            products_up(pe, n + 1, (k + 1) // U % 2, (k + 1) % U)
                        products_down(pe, n, k // U, k % U, last=final and k + 1 == 2 * U)

                with pe.Fori(0, NE // 2 - 1) as i:
                    pair(i, False)
                pair(NE // 2 - 1, True)
                pe.wait_ge(*sig["y_copied"](1))
                for t in range(NT):
                    pe.transpose(ps[:, t // 4, t % 4 * P:(t % 4 + 1) * P], yT[:, t * P:(t + 1) * P],
                                 core.ident[:, :]).then_inc(sig["y_turned"].sem, 1)

            @block.scalar
            def _(act):
                norm.on_scalar(act)
                for h in range(2):
                    act.wait_ge(*sig["tile_turned"](4 * h + 4))
                    act.copy(xhatT[:, h * HALF:(h + 1) * HALF], ps[:, 2 + h, :]).then_inc(sig["xhat_ready"].sem, 1)
                act.sem_inc(sig["relu_taken"].sem, 4)
                act.sem_inc(sig["spread_taken"].sem, 2)
                routing.on_scalar(act)
                act.wait_ge(*loaded(96))
                with act.Fori(0, NE // 2) as i:
                    for k in range(2 * U):
                        n, s, u = 2 * U * i + k, k // U, k % U
                        if u == 0:
                            for h in range(2):
                                e = 2 * i + s
                                act.wait_ge(*sig["spread_ready"](2 * e + h + 1))
                                act.copy(spread[:, s, h * HALF:(h + 1) * HALF], ps[:, SPREAD + h, :])\
                                   .then_inc(sig["spread_taken"].sem, 1)
                        for h in range(2):
                            act.wait_ge(*sig["hid_ready"](2 * n + h + 1))
                            act.wait_ge(*sig["hidden_ready"](2 * n + h + 1))
                            act.sem_inc(sig["held"].sem, 1)
                            act.activation(relu[:, u % 2, h, :], ps[:, HID + 2 * (u % 2) + h, :], ACT.Relu,
                                           bias=b1[:, bass.ds(n, 1)]).then_inc(sig["relu_taken"].sem, 1)
                act.wait_ge(*sig["hidden_used"](NE * U + 2))
                act.copy(yT[:, :].rearrange("p (n c) -> p n c", n=2), ps[:, Y:Y + 2, :]).then_inc(sig["y_copied"].sem, 1)

            @block.vector
            def _(dve):
                norm.on_vector(dve)
                for t in range(NT):
                    norm.normalise(dve, xhat[:, t, :], t).then_inc(sig["tile_ready"].sem, 1)
                dve.wait_ge(*loaded(96))
                routing.on_vector(dve)
                own = sig["own"]
                dve.tensor_reduce(total[:, :], routing.wt[:, :, :], AX.X, ALU.add).then_inc(own.sem, 1)
                dve.wait_ge(*own(1))
                dve.tensor_scalar(total[:, :], total[:, :], 1.0, None, ALU.add).then_inc(own.sem, 1)
                dve.wait_ge(*own(2))
                dve.tensor_tensor(x_tok[:, :, :], x_tok[:, :, :], total[:, :].unsqueeze(2).to_broadcast([P, NT, P]),
                                  ALU.mult).then_inc(own.sem, 1)
                dve.wait_ge(*sig["wt_turned"](1))
                dve.tensor_copy(wtT[:, :].rearrange("e (n c) -> e n c", n=2), ps[0:NE, 4:6, :])\
                   .then_inc(sig["wt_taken"].sem, 1)
                dve.wait_ge(*sig["xhat_ready"](2))

                def normalise(e, s):
                    dve.tensor_scalar(normed[:, s, :], xhatT[:, :], gamma[:, bass.ds(e, 1)], beta[:, bass.ds(e, 1)],
                                      ALU.mult, ALU.add).then_inc(sig["normed_ready"].sem, 1)

                normalise(0, 0)
                dve.sem_inc(sig["hidden_ready"].sem, 4)

                def pair(i, final):
                    for k in range(2 * U):
                        n, s, u = 2 * U * i + k, k // U, k % U
                        if u == 1 and not (final and s == 1):
                            dve.wait_ge(*sig["hid_ready"](2 * (n - u) + 1))
                            normalise(2 * i + s + 1, 1 - s)
                        for h in range(2):
                            dve.wait_ge(*sig["relu_taken"](2 * n + h + 5))
                            dve.wait_ge(*sig["hidden_used"](n + 1))
                            dve.tensor_tensor(hid[:, u % 2, h, :], relu[:, u % 2, h, :],
                                              spread[:, s, h * HALF:(h + 1) * HALF], ALU.mult)\
                               .then_inc(sig["hidden_ready"].sem, 1)

                with dve.Fori(0, NE // 2 - 1) as i:
                    pair(i, False)
                pair(NE // 2 - 1, True)
                dve.wait_ge(*own(3))
                for t in range(2):
                    dve.wait_ge(*sig["y_turned"](4 * t + 4))
                    xs = x_tok[:, 4 * t:4 * t + 4, :]
                    dve.tensor_tensor(xs, xs, ps[:, t, :].rearrange("p (t f) -> p t f", t=4), ALU.add)


def linear_attention(core, w):
    nc, ps, x_tok, x_feat = core.nc, core.ps, core.x_tok, core.x_feat
    VW = P + 1
    names = ("steps q_ready k_ready v_ready q_under k_under q_exp k_exp q_mapped k_mapped v_taken kv_ready kv_taken "
             "mixed_ready mixed_taken mixed_turned turned_taken y_ready ones").split()
    sig = {n: core.counter("la_" + n) for n in names}
    loaded = core.counter("la_loaded")
    with ExitStack() as ctx:
        def sb(name, shape, dt=FP32):
            return core.tensor(ctx, "la_" + name, shape, dt)

        mats = sb("mats", [P, 4, P])
        bq = sb("bq", [P, 1])
        rows = sb("rows", [P, 3, P])
        q, q_min, q_max = sb("q", [P, TOK]), sb("q_min", [P, TOK]), sb("q_max", [P, TOK])
        k, k_min, k_max = sb("k", [P, NT, P]), sb("k_min", [P, NT, P]), sb("k_max", [P, NT, P])
        v = sb("v", [P, NT, VW])
        kv = sb("kv", [P, B, VW])
        rec = sb("rec", [P, NT])
        mixed = sb("mixed", [P, NT, P])
        mixedT = sb("mixedT", [P, NT, P])

        def halves(t):
            return t.rearrange("p (n c) -> p n c", n=2)

        with nc.Block(no_gpsimd_drain=True) as block:
            @block.sync
            def _(sp):
                sp.dma_start(mats[:, :, :], w["mats"]).then_inc(loaded.sem, 16)
                sp.dma_start(bq[:, :], w["bq"]).then_inc(loaded.sem, 16)
                sp.dma_start(rows[:, :, :], w["rows"].partition_broadcast(P)).then_inc(loaded.sem, 16)

            @block.gpsimd
            def _(pool):
                pool.memset(v[:, :, P:VW], 1.0).then_inc(sig["ones"].sem, 1)

            @block.tensor
            def _(pe):
                pe.wait_ge(*loaded(48))
                for n in range(2):
                    last = pe.matmul(ps[:, n, :], mats[:, 0, :], x_feat[:, n * HALF:(n + 1) * HALF],
                                     start=True, stop=True)
                last.then_inc(sig["q_ready"].sem, 1)
                for bank, m, done in ((2, 1, "k_ready"), (4, 2, "v_ready")):
                    for t in range(NT):
                        last = pe.matmul(ps[:, bank + t // 4, t % 4 * P:(t % 4 + 1) * P],
                                         x_feat[:, t * P:(t + 1) * P], mats[:, m, :], start=True, stop=True)
                    last.then_inc(sig[done].sem, 1)
                pe.wait_ge(*sig["k_mapped"](1))
                pe.wait_ge(*sig["v_taken"](1))
                for b in range(B):
                    for t in range(TPB):
                        last = pe.matmul(ps[:, 6 + b // 2, b % 2 * 256:b % 2 * 256 + VW], k[:, TPB * b + t, :],
                                         v[:, TPB * b + t, :], start=t == 0, stop=t == TPB - 1)
                last.then_inc(sig["kv_ready"].sem, 1)
                pe.wait_ge(*sig["kv_taken"](1))
                pe.wait_ge(*sig["q_mapped"](1))
                for t in range(NT):
                    last = pe.matmul(ps[:, t // 2, t % 2 * 256:t % 2 * 256 + VW], q[:, t * P:(t + 1) * P],
                                     kv[:, t // TPB, :], start=True, stop=True)
                last.then_inc(sig["mixed_ready"].sem, 1)
                pe.wait_ge(*sig["mixed_taken"](1))
                for t in range(NT):
                    last = pe.transpose(ps[:, 4 + t // 4, t % 4 * P:(t % 4 + 1) * P], mixed[:, t, :],
                                        core.ident[:, :])
                last.then_inc(sig["mixed_turned"].sem, 1)
                pe.wait_ge(*sig["turned_taken"](1))
                for t in range(NT):
                    last = pe.matmul(ps[:, 6 + t // 4, t % 4 * P:(t % 4 + 1) * P], mixedT[:, t, :], mats[:, 3, :],
                                     start=True, stop=True)
                last.then_inc(sig["y_ready"].sem, 1)

            @block.scalar
            def _(act):
                act.wait_ge(*sig["q_under"](1))
                act.activation(q_min[:, :], q_min[:, :], ACT.Exp).then_inc(sig["q_exp"].sem, 1)
                act.wait_ge(*sig["k_under"](1))
                act.activation(k_min[:, :, :], k_min[:, :, :], ACT.Exp).then_inc(sig["k_exp"].sem, 1)
                act.wait_ge(*sig["mixed_turned"](1))
                act.copy(halves(mixedT[:, :, :].rearrange("p t f -> p (t f)")), ps[:, 4:6, :])\
                   .then_inc(sig["turned_taken"].sem, 1)

            @block.vector
            def _(dve):
                own = Steps(sig["steps"])
                dve.wait_ge(*loaded(48))
                own.done(dve.tensor_tensor(x_tok[:, :, :], x_tok[:, :, :],
                                           rows[:, 2:3, :].to_broadcast([P, NT, P]), ALU.add))
                dve.wait_ge(*sig["q_ready"](1))
                dve.tensor_scalar(halves(q_min[:, :]), ps[:, 0:2, :], bq[:, 0:1], 0.0, ALU.add, ALU.min)\
                   .then_inc(sig["q_under"].sem, 1)
                own.done(dve.tensor_scalar(halves(q_max[:, :]), ps[:, 0:2, :], bq[:, 0:1], 0.0, ALU.add, ALU.max))
                dve.wait_ge(*sig["k_ready"](1))
                own.done(dve.tensor_tensor(k_max[:, :, :], ps[:, 2:4, :].rearrange("p n (t f) -> p (n t) f", f=P),
                                           rows[:, 0:1, :].to_broadcast([P, NT, P]), ALU.add))
                dve.wait_ge(*own.last())
                dve.tensor_scalar(k_min[:, :, :], k_max[:, :, :], 0.0, None, ALU.min).then_inc(sig["k_under"].sem, 1)
                dve.wait_ge(*sig["k_under"](1))
                own.done(dve.tensor_scalar(k_max[:, :, :], k_max[:, :, :], 0.0, None, ALU.max))
                dve.wait_ge(*sig["v_ready"](1))
                dve.tensor_tensor(v[:, :, 0:P], ps[:, 4:6, :].rearrange("p n (t f) -> p (n t) f", f=P),
                                  rows[:, 1:2, :].to_broadcast([P, NT, P]), ALU.add)\
                   .then_inc(sig["v_taken"].sem, 1)
                dve.wait_ge(*sig["ones"](1))
                dve.wait_ge(*sig["k_exp"](1))
                dve.wait_ge(*own.last())
                dve.tensor_tensor(k[:, :, :], k_min[:, :, :], k_max[:, :, :], ALU.add)\
                   .then_inc(sig["k_mapped"].sem, 1)
                dve.wait_ge(*sig["q_exp"](1))
                dve.tensor_tensor(q[:, :], q_min[:, :], q_max[:, :], ALU.add).then_inc(sig["q_mapped"].sem, 1)
                dve.wait_ge(*sig["kv_ready"](1))
                src = ps[:, 6:8, :].rearrange("p n (b c) -> p (n b) c", b=2)
                own.done(dve.tensor_copy(kv[:, :, 0:P], src[:, :, 0:P]))
                dve.tensor_scalar(kv[:, :, P:VW], src[:, :, P:VW], 1e-6, None, ALU.add)\
                   .then_inc(sig["kv_taken"].sem, 1)
                dve.wait_ge(*sig["mixed_ready"](1))
                src = ps[:, 0:4, :].rearrange("p n (t c) -> p (n t) c", t=2)
                own.done(dve.reciprocal(rec[:, :], src[:, :, P]))
                dve.wait_ge(*own.last())
                dve.tensor_tensor(mixed[:, :, :], src[:, :, 0:P], rec[:, :].unsqueeze(2).to_broadcast([P, NT, P]),
                                  ALU.mult).then_inc(sig["mixed_taken"].sem, 1)
                dve.wait_ge(*sig["y_ready"](1))
                dve.tensor_tensor(x_tok[:, :, :], x_tok[:, :, :],
                                  ps[:, 6:8, :].rearrange("p n (t f) -> p (n t) f", f=P), ALU.add)


def rwkv_mixer(core, w):
    nc, ps, x_tok, x_feat = core.nc, core.ps, core.x_tok, core.x_feat
    names = "own own_act k_ready v_ready r_ready mixed taken y_ready expo scanned gated filled".split()
    sig = {n: core.counter("rw_" + n) for n in names}
    loaded = core.counter("rw_loaded")
    with ExitStack() as ctx:
        def sb(name, shape, dt=FP32):
            return core.tensor(ctx, "rw_" + name, shape, dt)

        mats = sb("mats", [P, 4, P])
        cols = sb("cols", [P, 5])
        keep = sb("keep", [P, 3])
        wn = sb("wn", [P, 1])
        xm = sb("xm", [P, 3, B, S])
        k, v = sb("k", [P, B, S]), sb("v", [P, B, S])
        pp, aa, bb = (sb(n, [P, B, S + 1]) for n in ("pp", "aa", "bb"))
        uk, top = sb("uk", [P, B, S]), sb("top", [P, B, S])
        e1, e2, e1b, e2b = (sb(n, [P, B, S]) for n in ("e1", "e2", "e1b", "e2b"))
        er = sb("er", [P, B, S])
        num, den = sb("num", [P, B, S]), sb("den", [P, B, S])

        def banks(n):
            return ps[:, n:n + 2, :].rearrange("p n (b s) -> p (n b) s", s=S)

        with nc.Block(no_gpsimd_drain=True) as block:
            @block.sync
            def _(sp):
                sp.dma_start(mats[:, :, :], w["mats"]).then_inc(loaded.sem, 16)
                sp.dma_start(cols[:, :], w["cols"]).then_inc(loaded.sem, 16)

            @block.gpsimd
            def _(pool):
                pool.memset(pp[:, :, 0:1], -1e38).then_inc(sig["filled"].sem, 1)
                pool.memset(aa[:, :, 0:1], 0.0).then_inc(sig["filled"].sem, 1)
                pool.memset(bb[:, :, 0:1], 0.0).then_inc(sig["filled"].sem, 1)

            @block.tensor
            def _(pe):
                pe.wait_ge(*loaded(32))
                for m, done in enumerate(("k_ready", "v_ready", "r_ready")):
                    pe.wait_ge(*sig["mixed"](m + 1))
                    for n in range(2):
                        last = pe.matmul(ps[:, 2 * m + n, :], mats[:, m, :],
                                         xm[:, m, 2 * n:2 * n + 2, :].rearrange("p b s -> p (b s)"),
                                         start=True, stop=True)
                    last.then_inc(sig[done].sem, 1)
                for b in range(B):
                    pe.wait_ge(*sig["gated"](b + 1))
                    for t in range(TPB):
                        n = TPB * b + t
                        last = pe.matmul(ps[:, 6 + n // 4, n % 4 * P:(n % 4 + 1) * P], num[:, b, t * P:(t + 1) * P],
                                         mats[:, 3, :], start=True, stop=True)
                    if b % 2:
                        last.then_inc(sig["y_ready"].sem, 1)

            @block.scalar
            def _(act):
                act.wait_ge(*loaded(32))
                act.activation(wn[:, :], cols[:, 3:4], ACT.Exp).then_inc(sig["own_act"].sem, 1)
                act.wait_ge(*sig["own_act"](1))
                act.mul(wn[:, :], wn[:, :], -1.0).then_inc(sig["own_act"].sem, 1)
                act.wait_ge(*sig["v_ready"](1))
                act.copy(v[:, :, :], banks(2)).then_inc(sig["taken"].sem, 1)
                act.wait_ge(*sig["r_ready"](1))
                act.activation(er[:, :, :], banks(4), ACT.Exp, scale=-1.0).then_inc(sig["taken"].sem, 1)
                for n, e in enumerate((e1b, e2b, e1, e2)):
                    act.wait_ge(*sig["expo"](n + 1))
                    act.activation(e[:, :, :], e[:, :, :], ACT.Exp).then_inc(sig["own_act"].sem, 1)

            @block.vector
            def _(dve):
                own = Steps(sig["own"])
                dve.wait_ge(*loaded(32))
                own.done(dve.tensor_scalar(keep[:, :], cols[:, 0:3], -1.0, 1.0, ALU.mult, ALU.add))
                xb = x_feat[:, :].rearrange("p (b s) -> p b s", s=S)
                for m in range(3):
                    own.done(dve.tensor_scalar(xm[:, m, :, :], xb, cols[:, m:m + 1], None, ALU.mult))
                    dve.wait_ge(*own.last())
                    dve.scalar_tensor_tensor(xm[:, m, :, 1:S], xb[:, :, 0:S - 1], keep[:, m:m + 1],
                                             xm[:, m, :, 1:S], ALU.mult, ALU.add).then_inc(sig["mixed"].sem, 1)
                dve.wait_ge(*sig["k_ready"](1))
                own.done(dve.tensor_copy(k[:, :, :], banks(0)))
                dve.wait_ge(*own.last())
                dve.wait_ge(*sig["filled"](3))
                dve.wait_ge(*sig["own_act"](2))
                for b in range(B):
                    own.done(dve.tensor_tensor_scan(pp[:, b, 1:S + 1], wn[:, 0:1].to_broadcast([P, S]), k[:, b, :],
                                                    -1e38, ALU.add, ALU.max))
                own.done(dve.tensor_scalar(uk[:, :, :], k[:, :, :], cols[:, 4:5], None, ALU.add))
                dve.wait_ge(*own.last())
                old, new = pp[:, :, 0:S], pp[:, :, 1:S + 1]
                dve.scalar_tensor_tensor(e1b[:, :, :], old, wn[:, 0:1], new, ALU.add, ALU.subtract)\
                   .then_inc(sig["expo"].sem, 1)
                dve.tensor_tensor(e2b[:, :, :], k[:, :, :], new, ALU.subtract).then_inc(sig["expo"].sem, 1)
                own.done(dve.tensor_tensor(top[:, :, :], old, uk[:, :, :], ALU.max))
                dve.wait_ge(*own.last())
                dve.tensor_tensor(e1[:, :, :], old, top[:, :, :], ALU.subtract).then_inc(sig["expo"].sem, 1)
                dve.tensor_tensor(e2[:, :, :], uk[:, :, :], top[:, :, :], ALU.subtract).then_inc(sig["expo"].sem, 1)
                dve.wait_ge(*sig["taken"](1))
                dve.wait_ge(*sig["own_act"](4))
                dve.wait_ge(*sig["expo"](4))
                own.done(dve.tensor_tensor(top[:, :, :], e2b[:, :, :], v[:, :, :], ALU.mult))
                dve.wait_ge(*own.last())
                for b in range(B):
                    own.done(dve.tensor_tensor_scan(aa[:, b, 1:S + 1], e1b[:, b, :], top[:, b, :], 0.0,
                                                    ALU.mult, ALU.add))
                    own.done(dve.tensor_tensor_scan(bb[:, b, 1:S + 1], e1b[:, b, :], e2b[:, b, :], 0.0,
                                                    ALU.mult, ALU.add))
                dve.wait_ge(*sig["own_act"](6))
                dve.wait_ge(*own.last())
                own.done(dve.tensor_tensor(num[:, :, :], e1[:, :, :], aa[:, :, 0:S], ALU.mult))
                own.done(dve.tensor_tensor(den[:, :, :], e1[:, :, :], bb[:, :, 0:S], ALU.mult))
                own.done(dve.tensor_tensor(v[:, :, :], e2[:, :, :], v[:, :, :], ALU.mult))
                dve.wait_ge(*own.last())
                own.done(dve.tensor_tensor(num[:, :, :], num[:, :, :], v[:, :, :], ALU.add))
                own.done(dve.tensor_tensor(den[:, :, :], den[:, :, :], e2[:, :, :], ALU.add))
                dve.wait_ge(*sig["taken"](2))
                dve.wait_ge(*own.last())
                own.done(dve.scalar_tensor_tensor(den[:, :, :], er[:, :, :], 1.0, den[:, :, :], ALU.add, ALU.mult))
                dve.wait_ge(*own.last())
                for b in range(B):
                    own.done(dve.reciprocal(den[:, b, :], den[:, b, :]))
                    dve.wait_ge(*own.last())
                    dve.tensor_tensor(num[:, b, :], num[:, b, :], den[:, b, :], ALU.mult)\
                       .then_inc(sig["gated"].sem, 1)
                for n in range(2):
                    dve.wait_ge(*sig["y_ready"](n + 1))
                    xs = x_tok[:, 4 * n:4 * n + 4, :]
                    dve.tensor_tensor(xs, xs, ps[:, 6 + n, :].rearrange("p (t f) -> p t f", f=P), ALU.add)


def reshaped_attention(core, w):
    nc, ps, x_tok, x_feat = core.nc, core.ps, core.x_tok, core.x_feat
    H, K, V = 8, 64, 16
    BL = 8
    ROWS = S * BL
    names = ("steps qk_ready q_taken k_taken v_ready v_taken vt_ready vt_taken scores_ready max_ready scores_used "
             "exp_ready rec_ready probs_ready mixed_ready mixed_taken held").split()
    sig = {n: core.counter("ra_" + n) for n in names}
    loaded = core.counter("ra_loaded")
    with ExitStack() as ctx:
        def sb(name, shape, dt=FP32):
            return core.tensor(ctx, "ra_" + name, shape, dt)

        mq, mk, mv = sb("mq", [P, BL * K]), sb("mk", [P, BL * K]), sb("mv", [P, P])
        qT, kT = sb("qT", [K, S, BL]), sb("kT", [K, S, BL])
        vT = sb("vT", [V, S, BL])
        v = sb("v", [P, 2, H, V])
        probs = sb("probs", [P, 2, H, S])
        xb = sb("xb", [P, S])
        nmax = sb("nmax", [P, 2, H])
        sums = sb("sums", [P, 2, H])
        rec = sb("rec", [P, 2, H])
        with nc.Block(no_gpsimd_drain=True) as block:
            @block.sync
            def _(sp):
                for dst, src in ((mq, "mq"), (mk, "mk"), (mv, "mv")):
                    sp.dma_start(dst[:, :], w[src]).then_inc(loaded.sem, 16)

            @block.tensor
            def _(pe):
                pe.wait_ge(*loaded(48))
                with pe.Fori(0, B) as b:
                    pe.wait_ge(*sig["mixed_taken"](b + 1))
                    for j in range(BL):
                        pe.wait_ge(*sig["q_taken"](b * BL + j + 1))
                        pe.wait_ge(*sig["k_taken"](b * BL + j + 1))
                        pe.sem_inc(sig["held"].sem, 1)
                        xs = x_feat[:, bass.ds(b * S, S)]
                        pe.matmul(ps[0:K, j % 2, 0:S], mq[:, j * K:(j + 1) * K], xs, start=True, stop=True)
                        pe.matmul(ps[0:K, 2 + j % 2, 0:S], mk[:, j * K:(j + 1) * K], xs,
                                  start=True, stop=True).then_inc(sig["qk_ready"].sem, 1)
                    for j in range(BL):
                        last = pe.matmul(ps[0:V, 4 + j // 2, j % 2 * S:j % 2 * S + S], mv[:, j * V:(j + 1) * V], xs,
                                         start=True, stop=True)
                    last.then_inc(sig["v_ready"].sem, 1)
                    pe.wait_ge(*sig["v_taken"](b + 1))
                    pe.sem_inc(sig["held"].sem, 1)
                    for n in range(2):
                        for h in range(H):
                            src = vT[:, h * 32 + n * 16:h * 32 + n * 16 + 16, :].rearrange("d t j -> d (t j)")
                            last = pe.transpose(ps[:, 4, (n * H + h) * V:(n * H + h + 1) * V], src,
                                                core.ident[0:V, 0:V])
                    last.then_inc(sig["vt_ready"].sem, 1)
                    pe.wait_ge(*sig["q_taken"](b * BL + BL + 2))
                    pe.wait_ge(*sig["k_taken"](b * BL + BL + 2))
                    for h in range(H):
                        for n in range(2):
                            i = 2 * h + n
                            pe.wait_ge(*sig["scores_used"](b * 16 + i + 1))
                            ks = kT[:, h * 32 + n * 16:h * 32 + n * 16 + 16, :].rearrange("d t j -> d (t j)")
                            qs = qT[:, h * 32:h * 32 + 32, :].rearrange("d t j -> d (t j)")
                            pe.matmul(ps[:, i % 4, 0:S], ks, qs, start=True, stop=True)\
                              .then_inc(sig["scores_ready"].sem, 1)
                    pe.wait_ge(*sig["vt_taken"](b + 1))
                    pe.wait_ge(*sig["probs_ready"](16 * b + 16))
                    for t in range(TPB):
                        for r in range(BL):
                            for n in range(2):
                                src = probs[:, n, 4 * t:4 * t + 4, :].rearrange("c h (i r) -> c r (h i)", r=BL)
                                last = pe.matmul(ps[:, 5, t * P + r * V:t * P + r * V + V], src[:, r, :],
                                                 v[:, n, r, :], start=n == 0, stop=n == 1)
                    last.then_inc(sig["mixed_ready"].sem, 1)

            @block.scalar
            def _(act):
                act.sem_inc(sig["q_taken"].sem, 2)
                act.sem_inc(sig["scores_used"].sem, 4)
                with act.Fori(0, B) as b:
                    for j in range(BL):
                        act.wait_ge(*sig["qk_ready"](b * BL + j + 1))
                        act.copy(qT[:, :, j], ps[0:K, j % 2, 0:S]).then_inc(sig["q_taken"].sem, 1)
                    for h in range(H):
                        for n in range(2):
                            i = 2 * h + n
                            act.wait_ge(*sig["max_ready"](b * 16 + i + 1))
                            act.activation(probs[:, n, h, :], ps[:, i % 4, 0:S], ACT.Exp, bias=nmax[:, n, h:h + 1],
                                           scale=K ** -0.5, accum_out=sums[:, n, h:h + 1])\
                               .then_inc(sig["scores_used"].sem, 1)

            @block.vector
            def _(dve):
                dve.sem_inc(sig["k_taken"].sem, 2)
                dve.sem_inc(sig["mixed_taken"].sem, 1)
                with dve.Fori(0, B) as b:
                    for j in range(BL):
                        dve.wait_ge(*sig["qk_ready"](b * BL + j + 1))
                        dve.tensor_copy(kT[:, :, j], ps[0:K, 2 + j % 2, 0:S]).then_inc(sig["k_taken"].sem, 1)
                    dve.wait_ge(*sig["v_ready"](b + 1))
                    dve.tensor_copy(vT[:, :, :].rearrange("d t (n k) -> d n k t", n=4),
                                    ps[0:V, 4:8, :].rearrange("d n (k t) -> d n k t", k=2))\
                       .then_inc(sig["v_taken"].sem, 1)
                    dve.wait_ge(*sig["vt_ready"](b + 1))
                    dve.tensor_copy(v[:, :, :, :].rearrange("p n h d -> p (n h d)"), ps[:, 4, 0:2 * H * V])\
                       .then_inc(sig["vt_taken"].sem, 1)

                    def scale_by_sum(i):
                        h, n = i // 2, i % 2
                        dve.wait_ge(*sig["scores_used"](b * 16 + i + 5))
                        dve.reciprocal(rec[:, n, h:h + 1], sums[:, n, h:h + 1]).then_inc(sig["rec_ready"].sem, 1)
                        dve.wait_ge(*sig["rec_ready"](b * 16 + i + 1))
                        dve.tensor_scalar(probs[:, n, h, :], probs[:, n, h, :], rec[:, n, h:h + 1], None,
                                          ALU.mult).then_inc(sig["probs_ready"].sem, 1)

                    for i in range(2 * H):
                        h, n = i // 2, i % 2
                        dve.wait_ge(*sig["scores_ready"](b * 16 + i + 1))
                        dve.tensor_reduce(nmax[:, n, h:h + 1], ps[:, i % 4, 0:S], AX.X, ALU.max)\
                           .then_inc(sig["steps"].sem, 1)
                        dve.wait_ge(*sig["steps"](b * 16 + i + 1))
                        dve.tensor_scalar(nmax[:, n, h:h + 1], nmax[:, n, h:h + 1], -K ** -0.5, None,
                                          ALU.mult).then_inc(sig["max_ready"].sem, 1)
                        if i >= 2:
                            scale_by_sum(i - 2)
                    scale_by_sum(2 * H - 2)
                    scale_by_sum(2 * H - 1)
                    dve.wait_ge(*sig["mixed_ready"](b + 1))
                    xs = x_tok[:, bass.ds(b * TPB, TPB), :]
                    dve.tensor_tensor(xs, xs, ps[:, 5, 0:TPB * P].rearrange("p (t f) -> p t f", t=TPB),
                                      ALU.add).then_inc(sig["mixed_taken"].sem, 1)


def two_way_mamba(core, w):
    nc, ps, x_tok = core.nc, core.ps, core.x_tok
    N, T, PAD, R = 16, 4, 3, 8
    HALVES, WAYS = 2, 2
    names = ("norm_steps rooted tile_ready tile_turned norm_ready weights_scaled a_exp a_ready diag_ready conv_ready z_ready "
             "xc_tanh xc_half xc_ready sz_tanh sz_half sz_ready half_ready bc_ready dt_ready dt_taken bc_taken bc_steps pre_ready abs_ready pos_ready exp_ready "
             "log_ready log_joined soft_steps delta_ready du_ready restart b_ready b_taken c_ready da_ready dbu_ready scanned "
             "hc_ready y_added y_gated join_ready join_taken out_ready act_held zeroed doubled").split()
    sig = {n: core.counter("mb_" + n) for n in names}
    loaded = core.counter("mb_loaded")
    with ExitStack() as ctx:
        def sb(name, shape, dt=FP32):
            return core.tensor(ctx, "mb_" + name, shape, dt)

        cols = sb("cols", [P, 2 + 4 * WAYS * HALVES])
        in_w = sb("in_w", [P, WAYS, 4 * P])
        taps = sb("taps", [P, WAYS, T, 2 * P])
        a = sb("a", [P, WAYS, HALVES, N])
        xp_bc = sb("xp_bc", [P, WAYS, HALVES, 96])
        xp_dt = sb("xp_dt", [P, WAYS, HALVES, R])
        dt_w = sb("dt_w", [R, WAYS, 2 * P])
        out_w = sb("out_w", [P, WAYS, 2 * P])
        fus = sb("fus", [P, WAYS, P])
        fus_b = sb("fus_b", [P, P])
        sel = sb("sel", [P, 2 * N * P], BF16)
        norm = TokenNorm(core, ctx, "mb", 1e-5, sig["norm_steps"], sig["rooted"])
        half_b = sb("half_b", [P, WAYS * HALVES])
        xn = sb("xn", [P, NT, P])
        xn_feat = sb("xn_feat", [P, B, S + 2 * PAD])
        conv_w = sb("conv_w", [P, WAYS, T, 2 * P])
        diag = sb("diag", [P, WAYS, HALVES, P])
        xc, sz, delta, du = (sb(n, [P, WAYS, HALVES, TOK]) for n in ("xc", "sz", "delta", "du"))
        dts = sb("dts", [R, WAYS, TOK])
        parts = sb("parts", [P, WAYS, TOK], BF16)
        da, dbu, hs, hc = (sb(n, [P, HALVES, TOK]) for n in ("da", "dbu", "hs", "hc"))
        bs = sb("bs", [P, 2, TOK])
        join = sb("join", [P, WAYS, HALVES, P])
        high = hc[:, 0, 0:TOK // 2].bitcast(BF16)
        middle = hc[:, 0, TOK // 2:TOK].bitcast(BF16)
        rest = hs[:, 0, :]

        SERIES = [1 / 7, -1 / 6, 1 / 5, -1 / 4, 1 / 3, -1 / 2, 1.0]
        SOFT = len(SERIES) + 2

        def col_of(r, h, n):
            c = 2 + 4 * (HALVES * r + h) + n
            return cols[:, c:c + 1]

        CONV_B, DT_B, D = 0, 1, 2

        def pair(n):
            return ps[:, 2 * n:2 * n + 2, :]

        def two(t):
            return t.rearrange("p (n c) -> p n c", n=2)

        loads = [(cols[:, :], "cols"), (in_w[:, :, :], "in_w"), (taps[:, :, :, :], "taps"), (a[:, :, :, :], "a_log"),
                 (xp_bc[:, :, :, :], "xp_bc"), (xp_dt[:, :, :, :], "xp_dt"), (dt_w[:, :, :], "dt_w"),
                 (out_w[:, :, :], "out_w"), (fus[:, :, :], "fus"), (fus_b[:, :], "fus_b"), (sel[:, :], "sel")]
        ALL = 16 * len(loads)

        with nc.Block(no_gpsimd_drain=True) as block:
            @block.sync
            def _(sp):
                for dst, name in loads:
                    src = w[name].partition_broadcast(P) if name in ("taps", "fus_b") else w[name]
                    sp.dma_start(dst, src).then_inc(loaded.sem, 16)

            @block.gpsimd
            def _(pool):
                pool.memset(xn_feat[:, :, 0:PAD], 0.0).then_inc(sig["zeroed"].sem, 1)
                pool.memset(xn_feat[:, :, PAD + S:], 0.0).then_inc(sig["zeroed"].sem, 1)
                pool.wait_ge(*sig["zeroed"](2))
                pool.memset(parts[96:P, :, :], 0.0).then_inc(sig["zeroed"].sem, 1)
                pool.wait_ge(*sig["zeroed"](3))
                pool.wait_ge(*loaded(ALL))
                for r in range(WAYS):
                    pool.tensor_tensor(conv_w[:, r, :, :], taps[:, r, :, :],
                                       in_w[:, r, 0:2 * P].unsqueeze(1).to_broadcast([P, T, 2 * P]),
                                       ALU.mult).then_inc(sig["weights_scaled"].sem, 1)
                for r in range(WAYS):
                    for h in range(HALVES):
                        pool.tensor_scalar(diag[:, r, h, :], core.ident[:, :], col_of(r, h, D), None, ALU.mult)\
                            .then_inc(sig["diag_ready"].sem, 1)
                for r in range(WAYS):
                    for h in range(HALVES):
                        n = HALVES * r + h
                        pool.wait_ge(*sig["soft_steps"](SOFT * n + SOFT))
                        pool.tensor_tensor(bs[:, h, :], bs[:, h, :], dbu[:, h, :], ALU.add)\
                            .then_inc(sig["log_joined"].sem, 1)
                        pool.wait_ge(*sig["log_joined"](n + 1))
                        pool.wait_ge(*sig["pos_ready"](n + 1))
                        pool.tensor_tensor(delta[:, r, h, :], delta[:, r, h, :], bs[:, h, :], ALU.add)\
                            .then_inc(sig["delta_ready"].sem, 1)
                        pool.wait_ge(*sig["delta_ready"](n + 1))
                        pool.tensor_tensor(du[:, r, h, :], delta[:, r, h, :], xc[:, r, h, :], ALU.mult)\
                            .then_inc(sig["du_ready"].sem, 1)
                pool.wait_ge(*sig["du_ready"](WAYS * HALVES))
                for r in range(WAYS):
                    if r:
                        pool.wait_ge(*sig["scanned"](2 + 2 * N * r))
                    edge = 0 if r == 0 else S - 1
                    for h in range(HALVES):
                        pool.memset(da[:, h, :].rearrange("p (b s) -> p b s", s=S)[:, :, edge:edge + 1], 0.0)\
                            .then_inc(sig["restart"].sem, 1)
                    with pool.Fori(0, N // 2) as i:
                        for u in range(2):
                            n = N * r + 2 * i + u
                            for h in range(HALVES):
                                pool.wait_ge(*sig["b_taken"](n + 2))
                                pool.wait_ge(*sig["scanned"](2 * n + h + 1))
                                pool.tensor_tensor(dbu[:, h, :], du[:, r, h, :], bs[:, u, :], ALU.mult)\
                                    .then_inc(sig["dbu_ready"].sem, 1)

            @block.tensor
            def _(pe):
                pe.wait_ge(*loaded(ALL))
                for t in range(NT):
                    pe.wait_ge(*sig["tile_ready"](t + 1))
                    pe.transpose(ps[:, t // 4, t % 4 * P:(t % 4 + 1) * P], xn[:, t, :], core.ident[:, :])\
                      .then_inc(sig["tile_turned"].sem, 1)
                pe.wait_ge(*sig["norm_ready"](2))
                pe.wait_ge(*sig["zeroed"](3))
                for r in range(WAYS):
                    pe.wait_ge(*sig["weights_scaled"](r + 1))
                    if r:
                        pe.wait_ge(*sig["bc_taken"](r))
                        pe.wait_ge(*sig["dt_taken"](r))
                        pe.wait_ge(*sig["pos_ready"](HALVES * r))
                    for h in range(HALVES):
                        for n in range(2):
                            for j in range(T):
                                at = j if r == 0 else 2 * PAD - j
                                last = pe.matmul(ps[:, 2 * h + n, :], conv_w[:, r, j, h * P:(h + 1) * P],
                                                 xn_feat[:, 2 * n:2 * n + 2, at:at + S], start=j == 0, stop=j == T - 1)
                        last.then_inc(sig["conv_ready"].sem, 1)
                    for h in range(HALVES):
                        for n in range(2):
                            last = pe.matmul(ps[:, 4 + 2 * h + n, :], in_w[:, r, (2 + h) * P:(3 + h) * P],
                                             xn_feat[:, 2 * n:2 * n + 2, PAD:PAD + S], start=True, stop=True)
                        last.then_inc(sig["z_ready"].sem, 1)
                    pe.wait_ge(*sig["xc_ready"](HALVES * (r + 1)))
                    for out, mat, bank, done in ((96, xp_bc, 0, "bc_ready"), (R, xp_dt, 2, "dt_ready")):
                        for n in range(2):
                            for h in range(HALVES):
                                last = pe.matmul(ps[0:out, bank + n, :], mat[:, r, h, :],
                                                 xc[:, r, h, n * HALF:(n + 1) * HALF], start=h == 0, stop=h == 1)
                        last.then_inc(sig[done].sem, 1)
                    pe.wait_ge(*sig["dt_taken"](r + 1))
                    pe.wait_ge(*sig["sz_ready"](HALVES * (r + 1)))
                    for h in range(HALVES):
                        for n in range(2):
                            last = pe.matmul(ps[:, 4 + 2 * h + n, :], dt_w[:, r, h * P:(h + 1) * P],
                                             dts[:, r, n * HALF:(n + 1) * HALF], start=True, stop=True)
                        last.then_inc(sig["pre_ready"].sem, 1)
                pe.wait_ge(*sig["bc_taken"](WAYS))
                pe.wait_ge(*sig["pos_ready"](WAYS * HALVES))
                pe.wait_ge(*sig["diag_ready"](WAYS * HALVES))

                def spread(r, s, bank, row, done):
                    for n in range(2):
                        last = pe.matmul(ps[:, bank + n, :], sel[:, bass.ds(row * P, P)],
                                         parts[:, r, n * HALF:(n + 1) * HALF], start=True, stop=True)
                    last.then_inc(sig[done].sem, 1)

                def spread_b(r, s):
                    pe.wait_ge(*sig["b_taken"](N * r + s + 1))
                    spread(r, s, 0, s, "b_ready")

                def spread_c(r, s):
                    pe.wait_ge(*sig["hc_ready"](2 * (N * r + s) + 2))
                    spread(r, s, 2, s + N, "c_ready")

                def add_state(r, s, last_state=False):
                    for h in range(HALVES):
                        pe.wait_ge(*sig["hc_ready"](2 * (N * r + s) + h + 3))
                        for n in range(2):
                            last = pe.matmul(ps[:, 4 + 2 * h + n, :], core.ident[:, :],
                                             hc[:, h, n * HALF:(n + 1) * HALF], start=False, stop=last_state)
                        last.then_inc(sig["y_added"].sem, 1)

                for r in range(WAYS):
                    if r:
                        pe.wait_ge(*sig["y_gated"](HALVES * r))
                    for h in range(HALVES):
                        for n in range(2):
                            pe.matmul(ps[:, 4 + 2 * h + n, :], diag[:, r, h, :],
                                      xc[:, r, h, n * HALF:(n + 1) * HALF], start=True, stop=False)
                    spread_b(r, 0)
                    spread_c(r, 0)
                    with pe.Fori(0, N // 2 - 1) as i:
                        for u in range(2):
                            spread_b(r, 2 * i + u + 1)
                            add_state(r, 2 * i + u)
                            spread_c(r, 2 * i + u + 1)
                    spread_b(r, N - 1)
                    add_state(r, N - 2)
                    spread_c(r, N - 1)
                    add_state(r, N - 1, last_state=True)
                for r in range(WAYS):
                    for h in range(HALVES):
                        if r == h == 0:
                            pe.wait_ge(*sig["b_taken"](WAYS * N + 1))
                        c = (HALVES * r + h) * P
                        last = pe.matmul(ps[:, 0, c:c + P], out_w[:, r, h * P:(h + 1) * P], fus[:, r, :],
                                         start=True, stop=True)
                last.then_inc(sig["join_ready"].sem, 1)
                pe.wait_ge(*sig["join_taken"](1))
                pe.wait_ge(*sig["y_gated"](WAYS * HALVES))
                pe.wait_ge(*sig["hc_ready"](2 * WAYS * N + 2))
                for t in range(NT):
                    for r in range(WAYS):
                        for h in range(HALVES):
                            last = pe.matmul(ps[:, 2 + t // 4, t % 4 * P:(t % 4 + 1) * P],
                                             sz[:, r, h, t * P:(t + 1) * P], join[:, r, h, :],
                                             start=r == h == 0, stop=r == h == 1)
                    if t % 4 == 3:
                        last.then_inc(sig["out_ready"].sem, 1)

            @block.scalar
            def _(act):
                norm.on_scalar(act)
                act.wait_ge(*loaded(ALL))
                act.activation(a[:, :, :, :], a[:, :, :, :], ACT.Exp).then_inc(sig["a_exp"].sem, 1)
                act.wait_ge(*sig["a_exp"](1))
                act.mul(a[:, :, :, :], a[:, :, :, :], -1.0).then_inc(sig["a_ready"].sem, 1)
                for n in range(WAYS * HALVES):
                    c = 2 + 4 * n
                    act.mul(half_b[:, n:n + 1], cols[:, c:c + 1], 0.5).then_inc(sig["half_ready"].sem, 1)
                for n in range(2):
                    act.wait_ge(*sig["tile_turned"](4 * n + 4))
                    act.activation(xn_feat[:, 2 * n:2 * n + 2, PAD:PAD + S],
                                   ps[:, n, :].rearrange("p (b s) -> p b s", s=S), ACT.Identity,
                                   scale=cols[:, 0:1], bias=cols[:, 1:2]).then_inc(sig["norm_ready"].sem, 1)
                act.wait_ge(*sig["half_ready"](WAYS * HALVES))
                for r in range(WAYS):
                    for h in range(HALVES):
                        act.wait_ge(*sig["conv_ready"](HALVES * r + h + 1))
                        act.activation(two(xc[:, r, h, :]), pair(h), ACT.Tanh, scale=0.5,
                                       bias=half_b[:, HALVES * r + h:HALVES * r + h + 1])\
                           .then_inc(sig["xc_tanh"].sem, 1)
                    for h in range(HALVES):
                        act.wait_ge(*sig["z_ready"](HALVES * r + h + 1))
                        act.activation(two(sz[:, r, h, :]), pair(2 + h), ACT.Tanh, scale=0.5)\
                           .then_inc(sig["sz_tanh"].sem, 1)
                    for h in range(HALVES):
                        n = HALVES * r + h
                        e = da[:, h, :]
                        act.wait_ge(*sig["pre_ready"](n + 1))
                        if r:
                            act.wait_ge(*sig["soft_steps"](SOFT * (n - 2) + SOFT))
                        act.activation(two(e), pair(2 + h), ACT.Abs, bias=col_of(r, h, DT_B))\
                           .then_inc(sig["abs_ready"].sem, 1)
                    for h in range(HALVES):
                        n = HALVES * r + h
                        e = da[:, h, :]
                        act.wait_ge(*sig["abs_ready"](n + 1))
                        act.activation(e, e, ACT.Exp, scale=-1.0).then_inc(sig["exp_ready"].sem, 1)
                    for h in range(HALVES):
                        n = HALVES * r + h
                        act.wait_ge(*sig["exp_ready"](n + 1))
                        if r:
                            act.wait_ge(*sig["log_joined"](n - 1))
                        act.activation(dbu[:, h, :], da[:, h, :], ACT.Ln, bias=1.0).then_inc(sig["log_ready"].sem, 1)
                act.sem_inc(sig["b_taken"].sem, 1)
                act.wait_ge(*sig["a_ready"](1))
                act.wait_ge(*sig["du_ready"](WAYS * HALVES))
                for r in range(WAYS):
                    act.wait_ge(*sig["restart"](HALVES * (r + 1)))
                    with act.Fori(0, N // 2) as i:
                        for u in range(2):
                            s = 2 * i + u
                            n = N * r + s
                            act.wait_ge(*sig["b_ready"](n + 1))
                            act.wait_ge(*sig["dbu_ready"](2 * n + 2))
                            act.copy(two(bs[:, u, :]), pair(0)).then_inc(sig["b_taken"].sem, 1)
                            for h in range(HALVES):
                                act.wait_ge(*sig["scanned"](2 * n + h + 1))
                                act.sem_inc(sig["act_held"].sem, 1)
                                lo = 1 - r
                                act.activation(da[:, h, :].rearrange("p (b s) -> p b s", s=S)[:, :, lo:lo + S - 1],
                                               delta[:, r, h, :].rearrange("p (b s) -> p b s", s=S)[:, :, lo:lo + S - 1],
                                               ACT.Exp, scale=a[:, r, h, bass.ds(s, 1)])\
                                   .then_inc(sig["da_ready"].sem, 1)

            def softplus_tail(r, h):
                dve, n, steps = nc.vector, HALVES * r + h, sig["soft_steps"]
                e, series, log = da[:, h, :], bs[:, h, :], dbu[:, h, :]
                dve.wait_ge(*sig["exp_ready"](n + 1))
                if r:
                    dve.wait_ge(*sig["delta_ready"](n - 1))
                dve.tensor_scalar(series, e, SERIES[0], None, ALU.mult).then_inc(steps.sem, 1)
                for m, c in enumerate(SERIES[1:]):
                    dve.wait_ge(*steps(SOFT * n + m + 1))
                    dve.scalar_tensor_tensor(series, series, c, e, ALU.add, ALU.mult).then_inc(steps.sem, 1)
                dve.wait_ge(*steps(SOFT * n + len(SERIES)))
                dve.wait_ge(*sig["log_ready"](n + 1))
                dve.tensor_tensor(log, log, series, ALU.subtract).then_inc(steps.sem, 1)
                dve.wait_ge(*steps(SOFT * n + len(SERIES) + 1))
                dve.scalar_tensor_tensor(log, e, 1 / 16, log, ALU.is_ge, ALU.mult).then_inc(steps.sem, 1)

            @block.vector
            def _(dve):
                norm.on_vector(dve)
                for t in range(NT):
                    norm.normalise(dve, xn[:, t, :], t).then_inc(sig["tile_ready"].sem, 1)
                dve.wait_ge(*loaded(ALL))
                dve.wait_ge(*sig["tile_ready"](NT))
                dve.scalar_tensor_tensor(x_tok[:, :, :], x_tok[:, :, :], 2.0,
                                         fus_b[:, :].unsqueeze(1).to_broadcast([P, NT, P]), ALU.mult, ALU.add)\
                   .then_inc(sig["doubled"].sem, 1)
                for r in range(WAYS):
                    for name, dst, first, bias in (("xc", xc, 0, True), ("sz", sz, 2, False)):
                        for h in range(HALVES):
                            n = HALVES * r + h
                            half = hs[:, h, :]
                            dve.wait_ge(*sig[name + "_tanh"](n + 1))
                            if name == "sz":
                                dve.wait_ge(*sig["xc_ready"](n + 1))
                            elif r:
                                dve.wait_ge(*sig["sz_ready"](n - 1))
                                dve.wait_ge(*sig["bc_taken"](r))
                            dve.tensor_scalar(two(half), pair(first + h), col_of(r, h, CONV_B) if bias else 0.0,
                                              0.5, ALU.add, ALU.mult).then_inc(sig[name + "_half"].sem, 1)
                            dve.wait_ge(*sig[name + "_half"](n + 1))
                            dve.scalar_tensor_tensor(dst[:, r, h, :], dst[:, r, h, :], 1.0, half, ALU.add,
                                                     ALU.mult).then_inc(sig[name + "_ready"].sem, 1)
                    dve.wait_ge(*sig["sz_ready"](HALVES * (r + 1)))
                    dve.wait_ge(*sig["dt_ready"](r + 1))
                    dve.tensor_copy(two(dts[:, r, :]), ps[0:R, 2:4, :]).then_inc(sig["dt_taken"].sem, 1)
                    dve.wait_ge(*sig["bc_ready"](r + 1))
                    bc, steps = ps[0:96, 0:2, :], sig["bc_steps"]
                    if r:
                        dve.wait_ge(*sig["bc_taken"](r))
                    dve.tensor_copy(two(high[0:96, :]), bc).then_inc(steps.sem, 1)
                    dve.wait_ge(*steps(4 * r + 1))
                    dve.tensor_tensor(two(rest[0:96, :]), bc, two(high[0:96, :]), ALU.subtract).then_inc(steps.sem, 1)
                    dve.tensor_copy(parts[0:32, r, :], high[0:32, :]).then_inc(steps.sem, 1)
                    dve.wait_ge(*steps(4 * r + 3))
                    dve.tensor_copy(middle[0:96, :], rest[0:96, :]).then_inc(steps.sem, 1)
                    dve.wait_ge(*steps(4 * r + 4))
                    dve.tensor_copy(parts[32:64, r, :], middle[32:64, :])
                    dve.tensor_tensor(parts[64:96, r, :], rest[64:96, :], middle[64:96, :], ALU.subtract)\
                       .then_inc(sig["bc_taken"].sem, 1)
                    for h in range(HALVES):
                        n = HALVES * r + h
                        dve.wait_ge(*sig["abs_ready"](n + 1))
                        dve.tensor_scalar(two(delta[:, r, h, :]), pair(2 + h), col_of(r, h, DT_B), 0.0,
                                          ALU.add, ALU.max).then_inc(sig["pos_ready"].sem, 1)
                    for h in range(HALVES):
                        softplus_tail(r, h)
                dve.sem_inc(sig["scanned"].sem, 2)
                dve.sem_inc(sig["hc_ready"].sem, 2)
                dve.sem_inc(sig["y_added"].sem, 2)
                dve.sem_inc(sig["dbu_ready"].sem, 4)

                def way(t, r):
                    return t if r == 0 else t[:, ::-1]

                dve.wait_ge(*sig["bc_taken"](WAYS))
                for r in range(WAYS):
                    with dve.Fori(0, N) as s:
                        n = N * r + s
                        for h in range(HALVES):
                            dve.wait_ge(*sig["da_ready"](2 * n + h + 1))
                            dve.wait_ge(*sig["dbu_ready"](2 * n + h + 5))
                            dve.wait_ge(*sig["hc_ready"](2 * n + h + 1))
                            dve.tensor_tensor_scan(way(hs[:, h, :], r), way(da[:, h, :], r), way(dbu[:, h, :], r), 0.0,
                                                   ALU.mult, ALU.add).then_inc(sig["scanned"].sem, 1)
                        for h in range(HALVES):
                            dve.wait_ge(*sig["scanned"](2 * n + h + 3))
                            dve.wait_ge(*sig["c_ready"](n + 1))
                            dve.wait_ge(*sig["y_added"](2 * n + h + 1))
                            dve.tensor_tensor(two(hc[:, h, :]), two(hs[:, h, :]), pair(1), ALU.mult)\
                               .then_inc(sig["hc_ready"].sem, 1)
                    dve.wait_ge(*sig["y_added"](2 + 2 * N * (r + 1)))
                    dve.wait_ge(*sig["sz_ready"](WAYS * HALVES))
                    for h in range(HALVES):
                        dve.tensor_tensor(two(sz[:, r, h, :]), pair(2 + h), two(sz[:, r, h, :]), ALU.mult)\
                           .then_inc(sig["y_gated"].sem, 1)
                dve.wait_ge(*sig["join_ready"](1))
                dve.tensor_copy(join[:, :, :, :].rearrange("p r h f -> p (r h f)"), ps[:, 0, :])\
                   .then_inc(sig["join_taken"].sem, 1)
                dve.wait_ge(*sig["doubled"](1))
                for n in range(2):
                    dve.wait_ge(*sig["out_ready"](n + 1))
                    xs = x_tok[:, 4 * n:4 * n + 4, :]
                    dve.tensor_tensor(xs, xs, ps[:, 2 + n, :].rearrange("p (t f) -> p t f", f=P), ALU.add)


def selector(parts, n, rows=None):
    t = np.zeros((rows or parts * n, n, P), "bfloat16")
    for r in range(parts * n):
        t[r, r % n, :] = 1
    return t.reshape(-1, n * P)


def layout(i):
    a = {k: np.asarray(v) for k, v in i.items()}
    d = {"x": a["x"].reshape(TOK, P), "context": a["ctx_1024"].reshape(TOK, P),
         "ident": np.eye(P, dtype=np.float32), "ident16": np.eye(P, dtype="bfloat16")}
    for s, dim, q, k, v, o in (("L0x", 8, "L0_xattn_Wq", "L0_xattn_Wk", "L0_xattn_Wv", "L0_xattn_Wo"),
                               ("L1x", 8, "L1_xattn_Wq", "L1_xattn_Wk", "L1_xattn_Wv", "L1_xattn_Wo"),
                               ("L2x", 8, "L2_xattn_w_q", "L2_xattn_w_k", "L2_xattn_w_v", "L2_xattn_w_o")):
        d[s + "_wq"], d[s + "_wk"] = a[q].T, a[k].T
        d[s + "_wv"], d[s + "_wo"] = a[v].T, a[o].T
        d[s + "_sel"] = selector(2, 4)
        d[s + "_rows"] = np.repeat(np.eye(HEADS, dtype=np.float32), dim, axis=0)
    for s in ("L0", "L1"):
        d[s + "x_bq"], d[s + "x_bk"] = a[s + "_xattn_bq"].reshape(P, 1), a[s + "_xattn_bk"].reshape(P, 1)
        d[s + "x_bv"], d[s + "x_bo"] = a[s + "_xattn_bv"], a[s + "_xattn_bo"]
    d["L1x_mask"] = a["mask_1x1xSxS2_ik0"].reshape(S, S)

    def heads64(w):
        return w.transpose(1, 0, 2).reshape(P, HEADS * 64)

    d["L3x_wq"], d["L3x_wk"], d["L3x_wv"] = (heads64(a["L3_xattn_" + n]) for n in ("WQ", "WK", "WV"))
    d["L3x_wo"] = a["L3_xattn_WO"].reshape(8, P, P).transpose(1, 0, 2).reshape(P, 8 * P)
    d["L3x_sel"] = selector(2, 2)
    d["L3x_rows"] = np.repeat(np.eye(2, dtype=np.float32), 64, axis=0)
    d["L3x_mask"] = np.tril(np.ones((S, S), np.int32))

    def units(gate, up, down):
        return np.concatenate([gate, up, down], axis=2)

    def cut(w):
        e, m, n = w.shape
        return w.reshape(e, m, n // P, P).transpose(0, 2, 1, 3).reshape(-1, m, P)

    gu, dn = a["L0_ffn_gate_up_w"], a["L0_ffn_down_w"]
    sg, su, sd = (a["L0_ffn_shared_" + n] for n in ("gate_w", "up_w", "down_w"))
    d["L0f_units"] = np.concatenate([
        units(gu[:, :, :P], gu[:, :, P:], dn),
        units(cut(sg.T[None]), cut(su.T[None]), sd.T.reshape(2, P, P))])
    d["L0f_router"], d["L0f_sel"] = a["L0_ffn_router_w"].T, selector(3, 18, P)
    w13, w2 = a["L2_ffn_w13"], a["L2_ffn_w2"]
    d["L2f_units"] = units(cut(w13[:, :, :256]), cut(w13[:, :, 256:]), w2.reshape(16, P, P))
    d["L2f_router"], d["L2f_sel"] = a["L2_ffn_router_w"].T, selector(3, 8, P)
    e1, e2, e3, s1, s2, s3 = (a["L3_ffn_" + n] for n in ("ew1", "ew2", "ew3", "sw1", "sw2", "sw3"))
    d["L3f_units"] = np.concatenate([units(cut(e1), cut(e2), e3.reshape(16, P, P)),
                                     units(cut(s1[None]), cut(s2[None]), s3.reshape(2, P, P))])
    d["L3f_router"], d["L3f_sel"] = a["L3_ffn_gate_w"], selector(3, 9, P)
    d["L0a_mats"] = np.stack([a["L0_attn_" + n].T for n in ("Wq", "Wk", "Wv", "Wo")], axis=1)
    d["L0a_bq"] = a["L0_attn_bq"].reshape(P, 1)
    d["L0a_rows"] = np.stack([a["L0_attn_" + n] for n in ("bk", "bv", "bo")])
    d["L3a_mq"], d["L3a_mk"], d["L3a_mv"] = a["L3_attn_Mq"], a["L3_attn_Mk"], a["L3_attn_Mv"]
    w1, w2 = a["L1_ffn_W1"], a["L1_ffn_W2"]
    d["L1f_mats"] = np.concatenate([w1, w2.reshape(8, 4, P, P).transpose(0, 2, 1, 3).reshape(8, P, 4 * P)], axis=2)
    d["L1f_router"], d["L1f_sel"] = a["L1_ffn_Wg"], selector(3, 8, P)
    d["L1f_gamma"], d["L1f_beta"] = a["L1_ffn_gamma"].T, a["L1_ffn_beta"].T
    d["L1f_b1"], d["L1f_b2"] = a["L1_ffn_b1"].reshape(32, P).T, a["L1_ffn_b2"]
    d["L2a_mats"] = np.stack([a["L2_attn_" + n].T for n in ("Wk", "Wv", "Wr", "Wo")], axis=1)
    d["L2a_cols"] = np.stack([a["L2_attn_" + n].reshape(P) for n in
                              ("time_mix_k", "time_mix_v", "time_mix_r", "w", "u")], axis=1)
    ways = [{n[len("L1_attn_f_"):]: v for n, v in a.items() if n.startswith(f"L1_attn_{way}_")} for way in "fb"]
    cols = [a["L1_attn_ln_g"], a["L1_attn_ln_b"]]
    for m in ways:
        for h in range(2):
            cols += [m[n][h * P:(h + 1) * P] for n in ("conv_b", "dt_b", "D", "D")]
    d["L1a_cols"] = np.stack(cols, axis=1)

    def both(f):
        return np.stack([f(m) for m in ways], axis=1)

    def halved(t):
        return t.reshape(2, P, -1).transpose(1, 0, 2)

    d["L1a_in_w"] = both(lambda m: m["in_w"].T)
    d["L1a_taps"] = np.stack([m["conv_w"][:, 0, :].T for m in ways])
    d["L1a_a_log"] = both(lambda m: halved(m["A_log"]))
    d["L1a_xp_bc"] = both(lambda m: halved(np.tile(m["xproj_w"][8:].T, (1, 3))))
    d["L1a_xp_dt"] = both(lambda m: halved(m["xproj_w"][:8].T))
    d["L1a_dt_w"] = both(lambda m: m["dt_w"].T)
    d["L1a_out_w"] = both(lambda m: m["out_w"])
    d["L1a_fus"] = a["L1_attn_fus_w"].T.reshape(2, P, P).transpose(1, 0, 2)
    d["L1a_fus_b"] = a["L1_attn_fus_b"]
    d["L1a_sel"] = selector(3, 32, P)
    return {k: np.ascontiguousarray(v) for k, v in d.items()}


STAGES = (0, 12)


def build(nc, d, out):
    ctx = ExitStack()
    with ctx:
        core = Core(ctx, nc)

        def of(stage):
            return {n[len(stage) + 1:]: v for n, v in d.items() if n.startswith(stage + "_")}

        stages = [
            lambda: linear_attention(core, of("L0a")),
            lambda: cross_attention(core, of("L0x"), dim=8, scale=8 ** -0.5, biased=True, masked=False),
            lambda: gated_experts(core, of("L0f"), units=18, per_expert=1, scores=16, rule="sigmoid"),
            lambda: two_way_mamba(core, of("L1a")),
            lambda: cross_attention(core, of("L1x"), dim=8, scale=8 ** -0.5, biased=True, masked=True),
            lambda: normed_experts(core, of("L1f")),
            lambda: rwkv_mixer(core, of("L2a")),
            lambda: cross_attention(core, of("L2x"), dim=8, scale=8 ** -0.5, biased=False, masked=False),
            lambda: gated_experts(core, of("L2f"), units=16, per_expert=2, scores=8, rule="renormalised"),
            lambda: reshaped_attention(core, of("L3a")),
            lambda: cross_attention(core, of("L3x"), dim=64, scale=64 ** -0.5, biased=False, masked=True),
            lambda: gated_experts(core, of("L3f"), units=18, per_expert=2, scores=8, rule="softmax"),
        ]
        load_stage(core, d["x"], d["context"], d["ident"], d["ident16"])
        for n in range(*STAGES):
            with ExitStack() as stage:
                core.new_stage(stage)
                stages[n]()
                post_norm(core, out if n == STAGES[1] - 1 else None)


def kernel(**inputs):
    import concourse.bacc as _bacc
    from concourse.bass_utils import run_bass_kernel_spmd as _run

    nc = _bacc.Bacc("TRN2", target_bir_lowering=False, num_devices=1)
    arrays, d = {}, {}
    for name, a in layout(inputs).items():
        arrays[f"in_{name}"] = a
        d[name] = nc.dram_tensor(f"in_{name}", a.shape, mybir.dt.from_np(a.dtype), kind="ExternalInput").ap()
    out = nc.dram_tensor("out_x", (TOK, P), FP32, kind="ExternalOutput").ap()
    build(nc, d, out)
    r = _run(nc, [arrays], core_ids=[0])
    return r.results[0]["out_x"].reshape(B, S, P)
```

```python
import numpy as np

import concourse.bass as bass
from concourse import mybir
from contextlib import ExitStack

FP32 = mybir.dt.float32
BF16 = mybir.dt.bfloat16
I32 = mybir.dt.int32
ALU = mybir.AluOpType
ACT = mybir.ActivationFunctionType
AX = mybir.AxisListType

P = 128
B, S = 4, 256
TOK = B * S
NT = TOK // P
TPB = S // P
HALF = 512
HEADS = 16


class Signal:

    def __init__(self, ctx, nc, name):
        self.sem = ctx.enter_context(nc.semaphore(name))
        self.base = 0

    def __call__(self, n):
        return self.sem, n + self.base

    def past(self, total):
        self.base += total


class Steps:

    def __init__(self, signal, start=0):
        self.counter, self.count = signal, start

    def done(self, ins):
        self.count = self.count + 1
        ins.then_inc(self.counter.sem, 1)

    def last(self):
        return self.counter(self.count)


class Core:

    def __init__(self, ctx, nc):
        self.nc = nc

        def sb(name, shape, dt):
            return ctx.enter_context(nc.sbuf_tensor(name, shape, dt))

        self.x_tok = sb("x_tok", [P, NT, P], FP32)
        self.x_feat = sb("x_feat", [P, TOK], FP32)
        self.c_feat = sb("c_feat", [P, TOK], FP32)
        self.ident = sb("ident", [P, P], FP32)
        self.ident16 = sb("ident16", [P, P], BF16)
        self.ps = ctx.enter_context(nc.psum_tensor("ps", [P, 8, HALF], FP32))
        self.kept, self.number = {}, 0
        self.named = {}
        self.ctx = ctx

    def tensor(self, ctx, name, shape, dt):
        self.named[name] = self.named.get(name, 0) + 1
        return ctx.enter_context(self.nc.sbuf_tensor(f"{name}_{self.named[name]}", shape, dt))

    def counter(self, name, kept=False):
        if kept:
            if name not in self.kept:
                self.kept[name] = Signal(self.ctx, self.nc, name)
            return self.kept[name]
        signal = Signal(self.stage, self.nc, f"{name}_{self.number}")
        self.to_clear.append(signal.sem)
        return signal

    def new_stage(self, ctx):
        self.stage, self.number, self.to_clear = ctx, self.number + 1, []


def col(ap, n, size):
    return ap[:, bass.ds(n * size, size)]


class TokenNorm:

    STEPS = 2 * NT + 7

    def __init__(self, core, ctx, name, eps, steps, rooted):
        self.core, self.eps, self.steps, self.rooted = core, eps, steps, rooted
        self.stats = core.tensor(ctx, name + "_stats", [P, NT * 6], FP32)
        self.mv = core.tensor(ctx, name + "_mv", [P, NT, 2], FP32)
        self.var = core.tensor(ctx, name + "_var", [P, NT], FP32)
        self.rstd = core.tensor(ctx, name + "_rstd", [P, NT], FP32)
        self.root = core.tensor(ctx, name + "_root", [P, NT], FP32)

    def on_scalar(self, act):
        act.wait_ge(*self.steps(2 * NT + 1))
        act.activation(self.root[:, :], self.var[:, :], ACT.Sqrt).then_inc(self.rooted.sem, 1)

    def on_vector(self, dve):
        steps, stats, mv, var, rstd, root = self.steps, self.stats, self.mv, self.var, self.rstd, self.root
        for t in range(NT):
            dve.bn_stats(stats[:, 6 * t:6 * t + 6], self.core.x_tok[:, t, :]).then_inc(steps.sem, 1)
        for t in range(NT):
            dve.wait_ge(*steps(t + 1))
            dve.bn_aggr(mv[:, t, :], stats[:, 6 * t:6 * t + 6]).then_inc(steps.sem, 1)
        dve.wait_ge(*steps(2 * NT))
        dve.tensor_scalar(var[:, :], mv[:, :, 1], self.eps, None, ALU.add).then_inc(steps.sem, 1)
        dve.wait_ge(*self.rooted(1))
        dve.reciprocal(rstd[:, :], root[:, :]).then_inc(steps.sem, 1)
        dve.wait_ge(*steps(2 * NT + 2))
        dve.tensor_tensor(root[:, :], rstd[:, :], rstd[:, :], ALU.mult).then_inc(steps.sem, 1)
        dve.wait_ge(*steps(2 * NT + 3))
        dve.tensor_tensor(root[:, :], root[:, :], var[:, :], ALU.mult).then_inc(steps.sem, 1)
        dve.wait_ge(*steps(2 * NT + 4))
        dve.tensor_scalar(root[:, :], root[:, :], 1.0, -0.5, ALU.subtract, ALU.mult).then_inc(steps.sem, 1)
        dve.wait_ge(*steps(2 * NT + 5))
        dve.tensor_tensor(root[:, :], root[:, :], rstd[:, :], ALU.mult).then_inc(steps.sem, 1)
        dve.wait_ge(*steps(2 * NT + 6))
        dve.tensor_tensor(rstd[:, :], rstd[:, :], root[:, :], ALU.add).then_inc(steps.sem, 1)
        dve.wait_ge(*steps(2 * NT + 7))

    def normalise(self, dve, out, t):
        return dve.tensor_scalar(out, self.core.x_tok[:, t, :], self.mv[:, t, 0:1], self.rstd[:, t:t + 1],
                                 ALU.subtract, ALU.mult)


def load_stage(core, x, context, ident, ident16):
    nc = core.nc
    loaded = core.counter("io_loaded", kept=True)
    turned = core.counter("io_turned", kept=True)
    copied = core.counter("io_copied", kept=True)
    with ExitStack() as ctx:
        c_tok = core.tensor(ctx, "c_tok", [P, NT, P], FP32)
        with nc.Block(no_gpsimd_drain=True) as block:
            @block.sync
            def _(sp):
                sp.dma_start(core.x_tok[:, :, :], x.rearrange("(t p) d -> p t d", p=P)).then_inc(loaded.sem, 16)
                sp.dma_start(c_tok[:, :, :], context.rearrange("(t p) d -> p t d", p=P)).then_inc(loaded.sem, 16)
                sp.dma_start(core.ident[:, :], ident).then_inc(loaded.sem, 16)
                sp.dma_start(core.ident16[:, :], ident16).then_inc(loaded.sem, 16)

            @block.tensor
            def _(pe):
                pe.wait_ge(*loaded(64))
                for n, src in enumerate((core.x_tok, c_tok)):
                    for t in range(NT):
                        pe.transpose(core.ps[:, 2 * n + t // 4, t % 4 * P:(t % 4 + 1) * P], src[:, t, :],
                                     core.ident[:, :]).then_inc(turned.sem, 1)

            @block.scalar
            def _(act):
                for n, dst in enumerate((core.x_feat, core.c_feat)):
                    act.wait_ge(*turned(NT * (n + 1)))
                    act.copy(dst[:, :].rearrange("p (k c) -> p k c", k=2),
                             core.ps[:, 2 * n:2 * n + 2, :]).then_inc(copied.sem, 1)


def post_norm(core, out=None):
    nc, x_tok, x_feat, ps = core.nc, core.x_tok, core.x_feat, core.ps
    steps = core.counter("norm_steps", kept=True)
    normed = core.counter("norm_tile_ready", kept=True)
    turned = core.counter("norm_tile_turned", kept=True)
    copied = core.counter("norm_copied", kept=True)
    rooted = core.counter("norm_rooted", kept=True)
    with ExitStack() as ctx:
        norm = TokenNorm(core, ctx, "norm", 1e-5, steps, rooted)
        with nc.Block(no_gpsimd_drain=True) as block:
            @block.gpsimd
            def _(pool):
                for sem in core.to_clear:
                    pool.sem_clear(sem)

            @block.vector
            def _(dve):
                norm.on_vector(dve)
                for t in range(NT):
                    norm.normalise(dve, x_tok[:, t, :], t).then_inc(normed.sem, 1)

            if out is None:
                @block.tensor
                def _(pe):
                    for t in range(NT):
                        pe.wait_ge(*normed(t + 1))
                        pe.transpose(ps[:, t // 4, t % 4 * P:(t % 4 + 1) * P], x_tok[:, t, :],
                                     core.ident[:, :]).then_inc(turned.sem, 1)

                @block.scalar
                def _(act):
                    norm.on_scalar(act)
                    for k in range(2):
                        act.wait_ge(*turned(4 * k + 4))
                        act.copy(x_feat[:, k * HALF:(k + 1) * HALF], ps[:, k, :]).then_inc(copied.sem, 1)
            else:
                @block.scalar
                def _(act):
                    norm.on_scalar(act)

                @block.sync
                def _(sp):
                    dst = out.rearrange("(t p) d -> p t d", p=P)
                    for k in range(2):
                        sp.wait_ge(*normed(4 * k + 4))
                        sp.dma_start(dst[:, 4 * k:4 * k + 4, :], x_tok[:, 4 * k:4 * k + 4, :]).then_inc(copied.sem, 16)
                    sp.wait_ge(*copied(32))
    for s, total in ((steps, TokenNorm.STEPS), (rooted, 1), (normed, NT), (turned, NT), (copied, 2)):
        s.past(total)


def cross_attention(core, w, dim, scale, biased, masked):
    nc, ps = core.nc, core.ps
    HT = P // dim
    NQ = HEADS // HT
    HG = min(HT, 4)
    NG = HEADS // HG
    VD = HEADS * dim
    VW = min(HALF, VD)
    VB = VD // VW
    NC = VD // P
    NB = HG * S // HALF
    DV = dim + 1
    MS = 2 // NB
    KS = 4
    RING = 6
    PS_MAX, PS_MIX, PS_OUT = 4, 6, 7
    names = ("item_ready q_taken kv_taken bias_added k_laid k_cast max_ready max_taken high_ready shift_ready "
             "shift_turned shift_taken scores_ready probs_ready mixed_ready sums_inverted mixed_taken mixed_turned "
             "turned_taken y_ready y_taken consts mask_turned pe_held").split()
    sig = {n: core.counter("xa_" + n) for n in names}
    loaded = core.counter("xa_loaded")
    items = [(kind, n, half) for half in range(2) for n in range(NQ) for kind in "qk"]
    items += [("v", n, t) for t in range(NT) for n in range(VB)]

    def taken(i):
        q = sum(kind == "q" for kind, _, _ in items[:i])
        return 2 * q, i - q

    with ExitStack() as ctx:
        def sb(name, shape, dt=FP32):
            return core.tensor(ctx, "xa_" + name, shape, dt)

        wq_s, wk_s = sb("wq", [P, NQ * P]), sb("wk", [P, NQ * P])
        head_rows = sb("head_rows", [P, HT])
        wv_s, wo_s = sb("wv", [P, VD]), sb("wo", [P, NC * P])
        sel = sb("sel", [2 * HG, HG * P], BF16)
        qT, k_raw = sb("qT", [P, NQ * TOK]), sb("k_raw", [P, NQ * TOK])
        q16 = sb("q16", [P, NQ * TOK], BF16)
        kT, k16 = sb("kT", [P, KS, HG, S]), sb("k16", [P, 2, HG, S], BF16)
        v = sb("v", [P, NT * HEADS * DV])
        mx = sb("mx", [P, TPB, HG])
        shift = sb("shift", [P, TPB, 2, HG], BF16)
        shiftT = sb("shiftT", [2 * HG, S], BF16)
        probs = sb("probs", [P, 2, TPB, HG, S])
        rec = sb("rec", [P, 2, TPB, HG])
        mixed = sb("mixed", [P, TPB, VD])
        mixedT = sb("mixedT", [P, TPB, NC, P])
        if biased:
            bq, bk = sb("bq", [P, NQ]), sb("bk", [P, NQ])
            bv, bo = sb("bv", [P, VD]), sb("bo", [P, P])
        if masked:
            mask_i = sb("mask_i", [P, TPB, S], I32)
            mask_f = sb("mask_f", [P, TPB, S])
            mask_q = sb("mask_q", [P, TPB, S], BF16)
            mask_k = sb("mask_k", [P, TPB, S], BF16)
        loads = [(wq_s[:, :], w["wq"]), (wk_s[:, :], w["wk"]), (wv_s[:, :], w["wv"]), (wo_s[:, :], w["wo"]),
                 (sel[:, :], w["sel"]), (head_rows[:, :], w["rows"])]
        if biased:
            loads += [(bq[:, :], w["bq"]), (bk[:, :], w["bk"]), (bv[:, :], w["bv"].partition_broadcast(P)),
                      (bo[:, :], w["bo"].partition_broadcast(P))]
        if masked:
            loads += [(mask_i[:, :, :], w["mask"].rearrange("(t p) k -> p t k", p=P))]
        ALL = 16 * len(loads)
        v5 = v[:, :].rearrange("p (t h d) -> p t h d", t=NT, h=HEADS)
        turned_mask = ps[:, PS_OUT, :].bitcast(BF16)
        mixed_ps = ps[:, PS_MIX, 0:TPB * HG * DV].rearrange("p (q h d) -> p q h d", q=TPB, h=HG)

        def after(b, g, ahead):
            b, g = b + (g + ahead) // NG, (g + ahead) % NG
            return None if isinstance(b, int) and b >= B else (b, g, b * NG + g)

        with nc.Block(no_gpsimd_drain=True) as block:
            @block.sync
            def _(sp):
                for dst, src in loads:
                    sp.dma_start(dst, src).then_inc(loaded.sem, 16)

            @block.gpsimd
            def _(pool):
                pool.memset(v5[:, :, :, dim:DV], 1.0).then_inc(sig["consts"].sem, 1)
                if masked:
                    pool.wait_ge(*loaded(ALL))
                    pool.tensor_copy(mask_f[:, :, :], mask_i[:, :, :]).then_inc(sig["consts"].sem, 1)

            @block.tensor
            def _(pe):
                pe.sem_inc(sig["max_ready"].sem, 3)
                pe.sem_inc(sig["mixed_ready"].sem, 2)
                pe.wait_ge(*loaded(ALL))
                for i, (kind, n, part) in enumerate(items):
                    if i >= RING:
                        q_count, kv_count = taken(i - RING + 1)
                        pe.wait_ge(*sig["q_taken"](q_count))
                        if kv_count:
                            pe.wait_ge(*sig["kv_taken"](kv_count))
                    if kind == "v":
                        ins = pe.matmul(ps[:, i % RING, 0:VW], core.c_feat[:, part * P:(part + 1) * P],
                                        wv_s[:, n * VW:(n + 1) * VW], start=True, stop=True)
                    else:
                        wt, src = (wq_s, core.x_feat) if kind == "q" else (wk_s, core.c_feat)
                        ins = pe.matmul(ps[:, i % RING, :], wt[:, n * P:(n + 1) * P],
                                        src[:, part * HALF:(part + 1) * HALF], start=True, stop=True)
                    ins.then_inc(sig["item_ready"].sem, 1)
                if masked:
                    pe.wait_ge(*sig["consts"](3))
                    for t in range(TPB):
                        for k in range(TPB):
                            pe.transpose(turned_mask[:, (t * TPB + k) * P:(t * TPB + k + 1) * P],
                                         mask_q[:, t, k * P:(k + 1) * P],
                                         core.ident16[:, :]).then_inc(sig["mask_turned"].sem, 1)
                    pe.wait_ge(*sig["consts"](4))
                pe.wait_ge(*sig["q_taken"](taken(len(items))[0]))
                pe.wait_ge(*sig["kv_taken"](taken(len(items))[1]))

                def max_scores(unit, t):
                    if unit is None:
                        return
                    b, g, u = unit
                    if t == 0:
                        pe.wait_ge(*sig["k_cast"](u + 1))
                    pe.wait_ge(*sig["max_taken"](u * TPB + t + 1))
                    pe.sem_inc(sig["pe_held"].sem, 1)
                    for n in range(NB):
                        dst = ps[:, PS_MAX + (n if NB == 2 else t), :]
                        q_tile = (g * HG // HT) * TOK
                        last = pe.matmul(dst, q16[:, bass.ds(b * S + (q_tile + t * P), P)],
                                         k16[:, g % 2, 2 * n:2 * n + 2, :].rearrange("p h s -> p (h s)"),
                                         start=True, stop=not masked)
                        if masked:
                            last = pe.matmul(dst.rearrange("p (h s) -> p h s", h=2), core.ident16[:, :],
                                             mask_q[:, t, :].unsqueeze(1).to_broadcast([P, 2, S]),
                                             start=False, stop=True)
                    last.then_inc(sig["max_ready"].sem, 1)

                def turn_shift(unit):
                    if unit is None:
                        return
                    b, g, u = unit
                    pe.wait_ge(*sig["shift_ready"](u + 1))
                    pe.wait_ge(*sig["shift_taken"](u + 1))
                    if g == 2:
                        pe.wait_ge(*sig["y_taken"](b + 1))
                    for t in range(TPB):
                        last = pe.transpose(ps[0:2 * HG, PS_OUT, :].bitcast(BF16)[:, t * P:(t + 1) * P],
                                            shift[:, t, :, :].rearrange("p a h -> p (a h)"), core.ident16[:, :])
                    last.then_inc(sig["shift_turned"].sem, 1)

                def scores(unit, t):
                    if unit is None:
                        return
                    b, g, u = unit
                    pe.wait_ge(*sig["probs_ready"](u * TPB + t + 1))
                    if t == 0:
                        pe.wait_ge(*sig["shift_taken"](u + 2))
                    pe.sem_inc(sig["pe_held"].sem, 1)
                    for h in range(HG):
                        dst = ps[:, NB * t + h // 2, h % 2 * S:(h % 2 + 1) * S]
                        q_tile = (g * HG // HT) * TOK
                        pe.matmul(dst, kT[:, g % KS, h, t * P:(t + 1) * P], qT[:, bass.ds(b * S + q_tile, S)],
                                  start=True, stop=False)
                        if masked:
                            pe.matmul(dst, core.ident16[:, :], mask_k[:, t, :], start=False, stop=False)
                        last = pe.matmul(dst, sel[:, h * P:(h + 1) * P], shiftT[:, :], start=False, stop=True)
                    last.then_inc(sig["scores_ready"].sem, 1)

                def mix(unit):
                    b, g, u = unit
                    pe.wait_ge(*sig["probs_ready"](u * TPB + 2 * TPB))
                    pe.wait_ge(*sig["mixed_taken"](u + 1))
                    pe.sem_inc(sig["pe_held"].sem, 1)
                    for q in range(TPB):
                        for h in range(HG):
                            for t in range(TPB):
                                o = (t * HEADS + g * HG + h) * DV
                                last = pe.matmul(mixed_ps[:, q, h, :], probs[:, g % 2, t, h, q * P:(q + 1) * P],
                                                 v[:, bass.ds(b * (TPB * HEADS * DV) + o, DV)],
                                                 start=t == 0, stop=t == TPB - 1)
                    last.then_inc(sig["mixed_ready"].sem, 1)

                def turn_mixed(b, q):
                    if q == 0:
                        pe.wait_ge(*sig["mixed_taken"](b * NG + NG + 1))
                    else:
                        pe.wait_ge(*sig["turned_taken"](TPB * b + q))
                    for c in range(NC):
                        bank, o = (PS_OUT, HALF // 2) if NC == 1 else (2 + c // 4, c % 4 * P)
                        last = pe.transpose(ps[:, bank, o:o + P], mixed[:, q, c * P:(c + 1) * P], core.ident[:, :])
                    last.then_inc(sig["mixed_turned"].sem, 1)

                def output(b):
                    pe.wait_ge(*sig["turned_taken"](TPB * b + TPB))
                    for q in range(TPB):
                        for c in range(NC):
                            last = pe.matmul(ps[:, PS_OUT, q * P:(q + 1) * P], mixedT[:, q, c, :],
                                             wo_s[:, c * P:(c + 1) * P], start=c == 0, stop=c == NC - 1)
                    last.then_inc(sig["y_ready"].sem, 1)

                def step(b, g):
                    turn_shift(after(b, g, 1))
                    for t in range(TPB):
                        max_scores(after(b, g, 2), t)
                        scores(after(b, g, 1), t)
                        if g == NG:
                            turn_mixed(b, t)
                    mix(after(b, g, 0))
                    if g == NG:
                        output(b)

                for t in range(TPB):
                    max_scores((0, 0, 0), t)
                max_scores((0, 1, 1), 0)
                turn_shift((0, 0, 0))
                max_scores((0, 1, 1), 1)
                for t in range(TPB):
                    scores((0, 0, 0), t)
                step(0, 0)
                with pe.Fori(0, B - 1) as b:
                    for g in range(1, NG + 1):
                        step(b, g)
                for g in range(1, NG):
                    step(B - 1, g)
                for q in range(TPB):
                    turn_mixed(B - 1, q)
                output(B - 1)

            @block.scalar
            def _(act):
                act.sem_inc(sig["probs_ready"].sem, TPB)
                act.wait_ge(*loaded(ALL))
                for i, (kind, n, half) in enumerate(items):
                    if kind == "q":
                        act.wait_ge(*sig["item_ready"](i + 1))
                        o = n * TOK + half * HALF
                        for dst in (qT[:, o:o + HALF], q16[:, o:o + HALF]):
                            if biased:
                                ins = act.activation(dst, ps[:, i % RING, :], ACT.Identity, bias=bq[:, n:n + 1])
                            else:
                                ins = act.copy(dst, ps[:, i % RING, :])
                            ins.then_inc(sig["q_taken"].sem, 1)

                def cast_keys(unit):
                    if unit is None:
                        return
                    b, g, u = unit
                    act.wait_ge(*sig["k_laid"](u + 1))
                    act.wait_ge(*sig["max_ready"](u * TPB + 1))
                    act.copy(k16[:, g % 2, :, :], kT[:, g % KS, :, :]).then_inc(sig["k_cast"].sem, 1)

                def exps(unit, t):
                    if unit is None:
                        return
                    b, g, u = unit
                    act.wait_ge(*sig["scores_ready"](u * TPB + t + 1))
                    act.wait_ge(*sig["mixed_ready"](u + 1))
                    act.activation(probs[:, g % 2, t, :, :].rearrange("p h s -> p (h s)")
                                   .rearrange("p (n c) -> p n c", n=NB),
                                   ps[:, NB * t:NB * t + NB, :], ACT.Exp,
                                   scale=scale).then_inc(sig["probs_ready"].sem, 1)

                def take_turned(b, q):
                    act.wait_ge(*sig["mixed_turned"](TPB * b + q + 1))
                    if NC == 1:
                        act.copy(mixedT[:, q, 0, :], ps[:, PS_OUT, HALF // 2:HALF // 2 + P])\
                           .then_inc(sig["turned_taken"].sem, 1)
                    else:
                        act.copy(mixedT[:, q, :, :].rearrange("p c f -> p (c f)").rearrange("p (n c) -> p n c", n=NC // 4),
                                 ps[:, 2:2 + NC // 4, :]).then_inc(sig["turned_taken"].sem, 1)

                def step(b, g):
                    cast_keys(after(b, g, 3))
                    for t in range(TPB):
                        exps(after(b, g, 1), t)
                        if g == NG:
                            take_turned(b, t)

                for u in range(3):
                    cast_keys((0, u, u))
                for t in range(TPB):
                    exps((0, 0, 0), t)
                step(0, 0)
                with act.Fori(0, B - 1) as b:
                    for g in range(1, NG + 1):
                        step(b, g)
                for g in range(1, NG):
                    step(B - 1, g)
                for q in range(TPB):
                    take_turned(B - 1, q)

            @block.vector
            def _(dve):
                dve.sem_inc(sig["max_taken"].sem, MS)
                dve.sem_inc(sig["shift_taken"].sem, 1)
                dve.sem_inc(sig["mixed_taken"].sem, 1)
                dve.sem_inc(sig["y_taken"].sem, 1)
                dve.wait_ge(*loaded(ALL))
                if masked:
                    dve.wait_ge(*sig["consts"](2))
                    dve.tensor_scalar(mask_q[:, :, :], mask_f[:, :, :], 0.0, -1e30, ALU.is_equal, ALU.mult)\
                       .then_inc(sig["consts"].sem, 1)
                dve.wait_ge(*sig["consts"](1))
                for i, (kind, n, part) in enumerate(items):
                    if kind == "q":
                        continue
                    dve.wait_ge(*sig["item_ready"](i + 1))
                    if kind == "k":
                        o = n * TOK + part * HALF
                        if biased:
                            ins = dve.tensor_scalar(k_raw[:, o:o + HALF], ps[:, i % RING, :], bk[:, n:n + 1], None, ALU.add)
                        else:
                            ins = dve.tensor_copy(k_raw[:, o:o + HALF], ps[:, i % RING, :])
                    else:
                        heads = VW // dim
                        dst = v5[:, part, n * heads:(n + 1) * heads, 0:dim]
                        src = ps[:, i % RING, 0:VW].rearrange("p (h d) -> p h d", d=dim)
                        if biased:
                            ins = dve.tensor_tensor(dst, src, bv[:, n * VW:(n + 1) * VW]
                                                    .rearrange("p (h d) -> p h d", d=dim), ALU.add)
                        else:
                            ins = dve.tensor_copy(dst, src)
                    ins.then_inc(sig["kv_taken"].sem, 1)
                if biased:
                    dve.tensor_tensor(core.x_tok[:, :, :], core.x_tok[:, :, :],
                                      bo[:, :].unsqueeze(1).to_broadcast([P, NT, P]), ALU.add)\
                       .then_inc(sig["bias_added"].sem, 1)
                if masked:
                    dve.wait_ge(*sig["mask_turned"](TPB * TPB))
                    dve.tensor_copy(mask_k[:, :, :].rearrange("p k (t q) -> p k t q", t=TPB),
                                    turned_mask[:, 0:TPB * TPB * P].rearrange("p (t k q) -> p k t q", t=TPB, k=TPB))\
                       .then_inc(sig["consts"].sem, 1)
                dve.wait_ge(*sig["kv_taken"](taken(len(items))[1]))

                def lay_keys(unit):
                    if unit is None:
                        return
                    b, g, u = unit
                    if not isinstance(u, int) or u >= KS:
                        dve.wait_ge(*sig["scores_ready"]((u - KS) * TPB + TPB))
                    n, h0 = g * HG // HT, g * HG % HT
                    src = k_raw[:, bass.ds(b * S + n * TOK, S)].unsqueeze(1).to_broadcast([P, HG, S])
                    rows = head_rows[:, h0:h0 + HG].unsqueeze(2).to_broadcast([P, HG, S])
                    dve.tensor_tensor(kT[:, g % KS, :, :], src, rows, ALU.mult).then_inc(sig["k_laid"].sem, 1)

                def reduce(unit):
                    if unit is None:
                        return
                    b, g, u = unit
                    if not isinstance(u, int) or u > 0:
                        dve.wait_ge(*sig["shift_ready"](u))
                    for t in range(TPB):
                        dve.wait_ge(*sig["max_ready"](u * TPB + t + 4))
                        banks = ps[:, PS_MAX:PS_MAX + 2, :] if NB == 2 else ps[:, PS_MAX + t:PS_MAX + t + 1, :]
                        dve.tensor_reduce(mx[:, t, :], banks.rearrange("p n (h s) -> p (n h) s", s=S), AX.X, ALU.max)\
                           .then_inc(sig["max_taken"].sem, 1)
                    dve.wait_ge(*sig["max_taken"](u * TPB + TPB + MS))
                    dve.tensor_scalar(shift[:, :, 0, :], mx[:, :, :], -1.0, None, ALU.mult)\
                       .then_inc(sig["high_ready"].sem, 1)
                    dve.wait_ge(*sig["high_ready"](u + 1))
                    dve.scalar_tensor_tensor(shift[:, :, 1, :], mx[:, :, :], -1.0, shift[:, :, 0, :],
                                             ALU.mult, ALU.subtract).then_inc(sig["shift_ready"].sem, 1)

                def take_shift(unit):
                    if unit is None:
                        return
                    b, g, u = unit
                    dve.wait_ge(*sig["shift_turned"](u + 1))
                    dve.tensor_copy(shiftT[:, :], ps[0:2 * HG, PS_OUT, :].bitcast(BF16)[:, 0:S])\
                       .then_inc(sig["shift_taken"].sem, 1)

                def take_mixed(unit):
                    b, g, u = unit
                    dve.wait_ge(*sig["mixed_ready"](u + 3))
                    dve.wait_ge(*sig["mixed_taken"](u + 1))
                    dve.reciprocal(rec[:, g % 2, :, :], mixed_ps[:, :, :, dim]).then_inc(sig["sums_inverted"].sem, 1)
                    dve.wait_ge(*sig["sums_inverted"](u + 1))
                    dve.tensor_tensor(mixed[:, :, g * HG * dim:(g + 1) * HG * dim].rearrange("p q (h d) -> p q h d", h=HG),
                                      mixed_ps[:, :, :, 0:dim],
                                      rec[:, g % 2, :, :].unsqueeze(3).to_broadcast([P, TPB, HG, dim]),
                                      ALU.mult).then_inc(sig["mixed_taken"].sem, 1)

                def add_output(b):
                    dve.wait_ge(*sig["y_ready"](b + 1))
                    if biased:
                        dve.wait_ge(*sig["bias_added"](1))
                    xs = core.x_tok[:, bass.ds(b * TPB, TPB), :]
                    dve.tensor_tensor(xs, xs, ps[:, PS_OUT, 0:TPB * P].rearrange("p (q f) -> p q f", q=TPB),
                                      ALU.add).then_inc(sig["y_taken"].sem, 1)

                def step(b, g):
                    lay_keys(after(b, g, 3))
                    if g == NG:
                        add_output(b)
                    take_shift(after(b, g, 2))
                    take_mixed(after(b, g, 0))
                    reduce(after(b, g, 3))

                for u in range(3):
                    lay_keys((0, u, u))
                reduce((0, 0, 0))
                take_shift((0, 0, 0))
                reduce((0, 1, 1))
                take_shift((0, 1, 1))
                reduce((0, 2, 2))
                step(0, 0)
                with dve.Fori(0, B - 1) as b:
                    for g in range(1, NG + 1):
                        step(b, g)
                for g in range(1, NG):
                    step(B - 1, g)
                add_output(B - 1)




ROUTE_SIGNALS = "logits_ready steps exps_ready parts_ready parts_turned parts_taken zeroed".split()


class Routing:

    def __init__(self, core, sb, sig, scores, NE, rule):
        self.core, self.sig, self.scores, self.NE, self.rule = core, sig, scores, NE, rule
        self.K3 = 3 * NE
        self.router = sb("router", [P, scores])
        self.sel = sb("sel", [P, NE * P], BF16)
        self.top = sb("top", [P, NT, 8])
        self.lg = sb("lg", [P, NT, scores])
        self.ex = sb("ex", [P, NT, scores])
        self.ch = sb("ch", [P, NT, scores])
        self.den = sb("den", [P, NT, 2])
        self.wt = sb("wt", [P, NT, NE])
        self.rest = sb("rest", [P, NT, NE])
        self.parts = sb("parts", [P, NT, 3, NE], BF16)
        self.partsT = sb("partsT", [P, TOK], BF16)

    def on_tensor(self, pe):
        core, sig, ps = self.core, self.sig, self.core.ps
        for t in range(NT):
            last = pe.matmul(ps[:, 0, t * self.scores:(t + 1) * self.scores], core.x_feat[:, t * P:(t + 1) * P],
                             self.router[:, :], start=True, stop=True)
        last.then_inc(sig["logits_ready"].sem, 1)
        pe.wait_ge(*sig["parts_ready"](1))
        for t in range(NT):
            last = pe.transpose(ps[0:self.K3, 1, :].bitcast(BF16)[:, t * P:(t + 1) * P],
                                self.parts[:, t, :, :].rearrange("p a e -> p (a e)"), core.ident16[:, :])
        last.then_inc(sig["parts_turned"].sem, 1)

    def on_scalar(self, act):
        act.wait_ge(*self.sig["steps"](2))
        act.activation(self.ex[:, :, :], self.lg[:, :, :], ACT.Exp, scale=-1.0 if self.rule == "sigmoid" else 1.0)\
           .then_inc(self.sig["exps_ready"].sem, 1)

    def on_vector(self, dve):
        sig, ps, scores, rule, NE, K3 = self.sig, self.core.ps, self.scores, self.rule, self.NE, self.K3
        top, lg, ex, ch, den, wt, rest = self.top, self.lg, self.ex, self.ch, self.den, self.wt, self.rest
        parts, partsT, shared = self.parts, self.partsT, NE > scores
        route = Steps(sig["steps"], 0)
        dve.wait_ge(*sig["logits_ready"](1))
        logits = ps[:, 0, 0:NT * scores].rearrange("p (t e) -> p t e", t=NT)
        for t in range(NT):
            last = dve.max(top[:, t, :], logits[:, t, :])
        route.done(last)
        dve.wait_ge(*route.last())
        first = top[:, :, 0:1].to_broadcast([P, NT, scores])
        second = top[:, :, 1:2].to_broadcast([P, NT, scores])
        if rule == "sigmoid":
            route.done(dve.tensor_copy(lg[:, :, :], logits))
        else:
            route.done(dve.tensor_tensor(lg[:, :, :], logits, first, ALU.subtract))
        route.done(dve.tensor_tensor(ch[:, :, :], logits, second, ALU.is_ge))
        dve.wait_ge(*sig["exps_ready"](1))
        dve.wait_ge(*route.last())
        if rule == "sigmoid":
            route.done(dve.tensor_scalar(ex[:, :, :], ex[:, :, :], 1.0, None, ALU.add))
            dve.wait_ge(*route.last())
            route.done(dve.reciprocal(ex[:, :, :], ex[:, :, :]))
            dve.wait_ge(*route.last())
            if shared:
                dve.wait_ge(*sig["zeroed"](3))
            route.done(dve.tensor_tensor(wt[:, :, 0:scores], ex[:, :, :], ch[:, :, :], ALU.mult))
        else:
            if rule == "renormalised":
                route.done(dve.tensor_reduce(den[:, :, 1], ex[:, :, :], AX.X, ALU.add))
            route.done(dve.tensor_tensor(ch[:, :, :], ex[:, :, :], ch[:, :, :], ALU.mult))
            dve.wait_ge(*route.last())
            route.done(dve.tensor_reduce(den[:, :, 0], ch[:, :, :], AX.X, ALU.add))
            dve.wait_ge(*route.last())
            if rule == "renormalised":
                route.done(dve.scalar_tensor_tensor(den[:, :, 0], den[:, :, 1], 1e-6, den[:, :, 0],
                                                    ALU.mult, ALU.add))
                dve.wait_ge(*route.last())
            route.done(dve.reciprocal(den[:, :, 0], den[:, :, 0]))
            dve.wait_ge(*route.last())
            if shared:
                dve.wait_ge(*sig["zeroed"](3))
            route.done(dve.tensor_tensor(wt[:, :, 0:scores], ch[:, :, :],
                                         den[:, :, 0:1].to_broadcast([P, NT, scores]), ALU.mult))
        dve.wait_ge(*route.last())
        route.done(dve.tensor_copy(parts[:, :, 0, :], wt[:, :, :]))
        dve.wait_ge(*route.last())
        route.done(dve.tensor_tensor(rest[:, :, :], wt[:, :, :], parts[:, :, 0, :], ALU.subtract))
        dve.wait_ge(*route.last())
        route.done(dve.tensor_copy(parts[:, :, 1, :], rest[:, :, :]))
        dve.wait_ge(*route.last())
        dve.tensor_tensor(parts[:, :, 2, :], rest[:, :, :], parts[:, :, 1, :], ALU.subtract)\
           .then_inc(sig["parts_ready"].sem, 1)
        dve.wait_ge(*sig["parts_turned"](1))
        dve.wait_ge(*sig["zeroed"](1))
        dve.tensor_copy(partsT[0:K3, :], ps[0:K3, 1, :].bitcast(BF16)).then_inc(sig["parts_taken"].sem, 1)


def gated_experts(core, w, units, per_expert, scores, rule):
    nc, ps, x_tok, x_feat = core.nc, core.ps, core.x_tok, core.x_feat
    NE = units // per_expert
    shared = NE > scores
    names = ROUTE_SIGNALS + ("even_unit_loaded odd_unit_loaded gate_ready gate_taken up_ready up_taken spread_ready hidden_ready "
                             "hidden_used y_copied y_turned").split()
    sig = {n: core.counter("ff_" + n) for n in names}
    unit_loaded = sig["even_unit_loaded"], sig["odd_unit_loaded"]
    loaded = core.counter("ff_loaded")
    with ExitStack() as ctx:
        def sb(name, shape, dt=FP32):
            return core.tensor(ctx, "ff_" + name, shape, dt)

        routing = Routing(core, sb, sig, scores, NE, rule)
        ring = sb("ring", [P, 2, 3 * P])
        gate = sb("gate", [P, 2, 2, HALF])
        up = sb("up", [P, 2, 2, HALF])
        hid = sb("hid", [P, 2, 2, HALF])
        yT = sb("yT", [P, TOK])
        zero = sb("zero", [P, HALF], BF16)
        GATE, UP, SPREAD, Y = 0, 2, 4, 6

        with nc.Block(no_gpsimd_drain=True) as block:
            @block.sync
            def _(sp):
                sp.dma_start(routing.router[:, :], w["router"]).then_inc(loaded.sem, 16)
                sp.dma_start(routing.sel[:, :], w["sel"]).then_inc(loaded.sem, 16)
                for s in range(2):
                    sp.dma_start(ring[:, s, :], w["units"][s, :, :]).then_inc(unit_loaded[s].sem, 16)
                with sp.Fori(0, units // 2 - 1) as i:
                    for s in range(2):
                        sp.wait_ge(*sig["hidden_used"](2 * i + s + 3))
                        sp.dma_start(ring[:, s, :], w["units"][bass.ds(2 * i + s + 2, 1), :, :]
                                     .rearrange("u p n -> p (u n)")).then_inc(unit_loaded[s].sem, 16)

            @block.gpsimd
            def _(pool):
                pool.memset(routing.partsT[:, :], 0.0).then_inc(sig["zeroed"].sem, 1)
                pool.memset(zero[:, :], 0.0).then_inc(sig["zeroed"].sem, 1)
                if shared:
                    pool.memset(routing.wt[:, :, scores:NE], 1.0).then_inc(sig["zeroed"].sem, 1)

            def products_up(pe, n, s, turn, e):
                pe.wait_ge(*unit_loaded[s](16 * turn + 16))
                for h in range(2):
                    cols = x_feat[:, h * HALF:(h + 1) * HALF]
                    pe.wait_ge(*sig["gate_taken"](2 * n + h + 1))
                    pe.matmul(ps[:, GATE + h, :], ring[:, s, 0:P], cols, start=True, stop=True)\
                      .then_inc(sig["gate_ready"].sem, 1)
                    pe.wait_ge(*sig["up_taken"](2 * n + h + 3))
                    pe.matmul(ps[:, UP + h, :], ring[:, s, P:2 * P], cols, start=True, stop=True)\
                      .then_inc(sig["up_ready"].sem, 1)
                for h in range(2):
                    pe.wait_ge(*sig["hidden_ready"](2 * n + h + 1))
                    pe.matmul(ps[:, SPREAD + h, :], routing.sel[:, bass.ds(e * P, P)],
                              routing.partsT[:, h * HALF:(h + 1) * HALF],
                              start=True, stop=True).then_inc(sig["spread_ready"].sem, 1)

            def products_down(pe, n, s, last=False):
                for h in range(2):
                    pe.wait_ge(*sig["hidden_ready"](2 * n + h + 3))
                    ins = pe.matmul(ps[:, Y + h, :], ring[:, s, 2 * P:3 * P], hid[:, s, h, :], start=False, stop=last)
                    if h == 1:
                        ins.then_inc(sig["hidden_used"].sem, 1)

            @block.tensor
            def _(pe):
                pe.sem_inc(sig["hidden_used"].sem, 2)
                pe.wait_ge(*loaded(32))
                pe.wait_ge(*sig["zeroed"](2))
                for h in range(2):
                    pe.matmul(ps[:, Y + h, :], zero[:, 0:P], zero[:, :], start=True, stop=False)
                routing.on_tensor(pe)
                pe.wait_ge(*sig["parts_taken"](1))
                products_up(pe, 0, 0, 0, 0)
                with pe.Fori(0, units // 2 - 1) as i:
                    n = 2 * i
                    products_up(pe, n + 1, 1, i, n + 1 if per_expert == 1 else i)
                    products_down(pe, n, 0)
                    products_up(pe, n + 2, 0, i + 1, n + 2 if per_expert == 1 else i + 1)
                    products_down(pe, n + 1, 1)
                products_up(pe, units - 1, 1, units // 2 - 1, NE - 1)
                products_down(pe, units - 2, 0)
                products_down(pe, units - 1, 1, last=True)
                pe.wait_ge(*sig["y_copied"](1))
                for t in range(NT):
                    pe.transpose(ps[:, t // 4, t % 4 * P:(t % 4 + 1) * P], yT[:, t * P:(t + 1) * P],
                                 core.ident[:, :]).then_inc(sig["y_turned"].sem, 1)

            @block.scalar
            def _(act):
                act.sem_inc(sig["gate_taken"].sem, 2)
                routing.on_scalar(act)
                with act.Fori(0, units // 2) as i:
                    for s in range(2):
                        for h in range(2):
                            n = 2 * i + s
                            act.wait_ge(*sig["gate_ready"](2 * n + h + 1))
                            act.wait_ge(*sig["up_taken"](2 * n + h + 1))
                            act.activation(gate[:, s, h, :], ps[:, GATE + h, :], ACT.Silu)\
                               .then_inc(sig["gate_taken"].sem, 1)
                act.wait_ge(*sig["hidden_used"](units + 2))
                act.copy(yT[:, :].rearrange("p (n c) -> p n c", n=2), ps[:, Y:Y + 2, :]).then_inc(sig["y_copied"].sem, 1)

            @block.vector
            def _(dve):
                dve.sem_inc(sig["up_taken"].sem, 4)
                dve.sem_inc(sig["hidden_ready"].sem, 2)
                dve.wait_ge(*loaded(32))
                routing.on_vector(dve)
                with dve.Fori(0, units // 2) as i:
                    for s in range(2):
                        for h in range(2):
                            n = 2 * i + s
                            dve.wait_ge(*sig["gate_taken"](2 * n + h + 3))
                            dve.wait_ge(*sig["up_ready"](2 * n + h + 1))
                            dve.tensor_tensor(up[:, s, h, :], gate[:, s, h, :], ps[:, UP + h, :], ALU.mult)\
                               .then_inc(sig["up_taken"].sem, 1)
                        for h in range(2):
                            dve.wait_ge(*sig["up_taken"](2 * n + h + 5))
                            dve.wait_ge(*sig["hidden_used"](n + 1))
                            dve.wait_ge(*sig["spread_ready"](2 * n + h + 1))
                            dve.tensor_tensor(hid[:, s, h, :], up[:, s, h, :], ps[:, SPREAD + h, :], ALU.mult)\
                               .then_inc(sig["hidden_ready"].sem, 1)
                for t in range(2):
                    dve.wait_ge(*sig["y_turned"](4 * t + 4))
                    xs = x_tok[:, 4 * t:4 * t + 4, :]
                    dve.tensor_tensor(xs, xs, ps[:, t, :].rearrange("p (t f) -> p t f", t=4), ALU.add)


def normed_experts(core, w):
    nc, ps, x_tok, x_feat = core.nc, core.ps, core.x_tok, core.x_feat
    NE, U = 8, 4
    names = ROUTE_SIGNALS + ("even_loaded odd_loaded tile_ready tile_turned xhat_ready normed_ready hid_ready "
                             "relu_taken spread_ready spread_taken hidden_ready hidden_used wt_turned wt_taken "
                             "held own norm_steps rooted y_copied y_turned").split()
    sig = {n: core.counter("ne_" + n) for n in names}
    loaded = core.counter("ne_loaded")
    mats_loaded = sig["even_loaded"], sig["odd_loaded"]
    with ExitStack() as ctx:
        def sb(name, shape, dt=FP32):
            return core.tensor(ctx, "ne_" + name, shape, dt)

        routing = Routing(core, sb, sig, NE, NE, "softmax")
        ring = sb("ring", [P, 2, 2, U, P])
        gamma, beta, b1 = sb("gamma", [P, NE]), sb("beta", [P, NE]), sb("b1", [P, NE * U])
        b2 = sb("b2", [NE, P])
        norm = TokenNorm(core, ctx, "ne", 1e-6, sig["norm_steps"], sig["rooted"])
        xhat = sb("xhat", [P, NT, P])
        xhatT = sb("xhatT", [P, TOK])
        normed = sb("normed", [P, 2, TOK])
        relu = sb("relu", [P, 2, 2, HALF])
        hid = sb("hid", [P, 2, 2, HALF])
        spread = sb("spread", [P, 2, TOK])
        wtT = sb("wtT", [NE, TOK])
        total = sb("total", [P, NT])
        yT = sb("yT", [P, TOK])
        HID, SPREAD, Y = 0, 4, 6

        with nc.Block(no_gpsimd_drain=True) as block:
            @block.sync
            def _(sp):
                for dst, src in ((routing.router, "router"), (routing.sel, "sel"), (gamma, "gamma"), (beta, "beta"),
                                 (b1, "b1"), (b2, "b2")):
                    sp.dma_start(dst[:, :], w[src]).then_inc(loaded.sem, 16)
                for s in range(2):
                    sp.dma_start(ring[:, s, :, :, :].rearrange("p a u f -> p (a u f)"), w["mats"][s, :, :])\
                      .then_inc(mats_loaded[s].sem, 16)
                with sp.Fori(0, NE // 2 - 1) as i:
                    for s in range(2):
                        sp.wait_ge(*sig["hidden_used"](U * (2 * i + s) + U + 2))
                        sp.dma_start(ring[:, s, :, :, :].rearrange("p a u f -> p (a u f)"),
                                     w["mats"][bass.ds(2 * i + s + 2, 1), :, :].rearrange("e p n -> p (e n)"))\
                          .then_inc(mats_loaded[s].sem, 16)

            @block.gpsimd
            def _(pool):
                pool.memset(routing.partsT[:, :], 0.0).then_inc(sig["zeroed"].sem, 1)

            def products_up(pe, n, s, u):
                for h in range(2):
                    pe.wait_ge(*sig["relu_taken"](2 * n + h + 1))
                    pe.matmul(ps[:, HID + 2 * (u % 2) + h, :], ring[:, s, 0, u, :],
                              normed[:, s, h * HALF:(h + 1) * HALF], start=True, stop=True)\
                      .then_inc(sig["hid_ready"].sem, 1)

            def enter_expert(pe, e, s, turn):
                for h in range(2):
                    pe.wait_ge(*sig["spread_taken"](2 * e + h + 1))
                    pe.matmul(ps[:, SPREAD + h, :], routing.sel[:, bass.ds(e * P, P)],
                              routing.partsT[:, h * HALF:(h + 1) * HALF], start=True, stop=True)\
                      .then_inc(sig["spread_ready"].sem, 1)
                pe.wait_ge(*mats_loaded[s](16 * turn + 16))
                pe.wait_ge(*sig["normed_ready"](e + 1))

            def products_down(pe, n, s, u, last=False):
                for h in range(2):
                    pe.wait_ge(*sig["hidden_ready"](2 * n + h + 5))
                    ins = pe.matmul(ps[:, Y + h, :], ring[:, s, 1, u, :], hid[:, u % 2, h, :], start=False, stop=last)
                    if h == 1:
                        ins.then_inc(sig["hidden_used"].sem, 1)

            @block.tensor
            def _(pe):
                pe.sem_inc(sig["hidden_used"].sem, 2)
                pe.wait_ge(*loaded(96))
                for t in range(NT):
                    pe.wait_ge(*sig["tile_ready"](t + 1))
                    pe.transpose(ps[:, 2 + t // 4, t % 4 * P:(t % 4 + 1) * P], xhat[:, t, :],
                                 core.ident[:, :]).then_inc(sig["tile_turned"].sem, 1)
                routing.on_tensor(pe)
                for t in range(NT):
                    last = pe.transpose(ps[0:NE, 4 + t // 4, t % 4 * P:(t % 4 + 1) * P], routing.wt[:, t, :],
                                        core.ident[:, :])
                last.then_inc(sig["wt_turned"].sem, 1)
                pe.wait_ge(*sig["wt_taken"](1))
                for h in range(2):
                    pe.matmul(ps[:, Y + h, :], b2[:, :], wtT[:, h * HALF:(h + 1) * HALF], start=True, stop=False)
                pe.wait_ge(*sig["parts_taken"](1))
                pe.wait_ge(*sig["xhat_ready"](2))
                enter_expert(pe, 0, 0, 0)
                products_up(pe, 0, 0, 0)

                def pair(i, final):
                    for k in range(2 * U):
                        n = 2 * U * i + k
                        if k + 1 == U:
                            enter_expert(pe, 2 * i + 1, 1, i)
                        if k + 1 == 2 * U and not final:
                            enter_expert(pe, 2 * i + 2, 0, i + 1)
                        if not (final and k + 1 == 2 * U):
                            products_up(pe, n + 1, (k + 1) // U % 2, (k + 1) % U)
                        products_down(pe, n, k // U, k % U, last=final and k + 1 == 2 * U)

                with pe.Fori(0, NE // 2 - 1) as i:
                    pair(i, False)
                pair(NE // 2 - 1, True)
                pe.wait_ge(*sig["y_copied"](1))
                for t in range(NT):
                    pe.transpose(ps[:, t // 4, t % 4 * P:(t % 4 + 1) * P], yT[:, t * P:(t + 1) * P],
                                 core.ident[:, :]).then_inc(sig["y_turned"].sem, 1)

            @block.scalar
            def _(act):
                norm.on_scalar(act)
                for h in range(2):
                    act.wait_ge(*sig["tile_turned"](4 * h + 4))
                    act.copy(xhatT[:, h * HALF:(h + 1) * HALF], ps[:, 2 + h, :]).then_inc(sig["xhat_ready"].sem, 1)
                act.sem_inc(sig["relu_taken"].sem, 4)
                act.sem_inc(sig["spread_taken"].sem, 2)
                routing.on_scalar(act)
                act.wait_ge(*loaded(96))
                with act.Fori(0, NE // 2) as i:
                    for k in range(2 * U):
                        n, s, u = 2 * U * i + k, k // U, k % U
                        if u == 0:
                            for h in range(2):
                                e = 2 * i + s
                                act.wait_ge(*sig["spread_ready"](2 * e + h + 1))
                                act.copy(spread[:, s, h * HALF:(h + 1) * HALF], ps[:, SPREAD + h, :])\
                                   .then_inc(sig["spread_taken"].sem, 1)
                        for h in range(2):
                            act.wait_ge(*sig["hid_ready"](2 * n + h + 1))
                            act.wait_ge(*sig["hidden_ready"](2 * n + h + 1))
                            act.sem_inc(sig["held"].sem, 1)
                            act.activation(relu[:, u % 2, h, :], ps[:, HID + 2 * (u % 2) + h, :], ACT.Relu,
                                           bias=b1[:, bass.ds(n, 1)]).then_inc(sig["relu_taken"].sem, 1)
                act.wait_ge(*sig["hidden_used"](NE * U + 2))
                act.copy(yT[:, :].rearrange("p (n c) -> p n c", n=2), ps[:, Y:Y + 2, :]).then_inc(sig["y_copied"].sem, 1)

            @block.vector
            def _(dve):
                norm.on_vector(dve)
                for t in range(NT):
                    norm.normalise(dve, xhat[:, t, :], t).then_inc(sig["tile_ready"].sem, 1)
                dve.wait_ge(*loaded(96))
                routing.on_vector(dve)
                own = sig["own"]
                dve.tensor_reduce(total[:, :], routing.wt[:, :, :], AX.X, ALU.add).then_inc(own.sem, 1)
                dve.wait_ge(*own(1))
                dve.tensor_scalar(total[:, :], total[:, :], 1.0, None, ALU.add).then_inc(own.sem, 1)
                dve.wait_ge(*own(2))
                dve.tensor_tensor(x_tok[:, :, :], x_tok[:, :, :], total[:, :].unsqueeze(2).to_broadcast([P, NT, P]),
                                  ALU.mult).then_inc(own.sem, 1)
                dve.wait_ge(*sig["wt_turned"](1))
                dve.tensor_copy(wtT[:, :].rearrange("e (n c) -> e n c", n=2), ps[0:NE, 4:6, :])\
                   .then_inc(sig["wt_taken"].sem, 1)
                dve.wait_ge(*sig["xhat_ready"](2))

                def normalise(e, s):
                    dve.tensor_scalar(normed[:, s, :], xhatT[:, :], gamma[:, bass.ds(e, 1)], beta[:, bass.ds(e, 1)],
                                      ALU.mult, ALU.add).then_inc(sig["normed_ready"].sem, 1)

                normalise(0, 0)
                dve.sem_inc(sig["hidden_ready"].sem, 4)

                def pair(i, final):
                    for k in range(2 * U):
                        n, s, u = 2 * U * i + k, k // U, k % U
                        if u == 1 and not (final and s == 1):
                            dve.wait_ge(*sig["hid_ready"](2 * (n - u) + 1))
                            normalise(2 * i + s + 1, 1 - s)
                        for h in range(2):
                            dve.wait_ge(*sig["relu_taken"](2 * n + h + 5))
                            dve.wait_ge(*sig["hidden_used"](n + 1))
                            dve.tensor_tensor(hid[:, u % 2, h, :], relu[:, u % 2, h, :],
                                              spread[:, s, h * HALF:(h + 1) * HALF], ALU.mult)\
                               .then_inc(sig["hidden_ready"].sem, 1)

                with dve.Fori(0, NE // 2 - 1) as i:
                    pair(i, False)
                pair(NE // 2 - 1, True)
                dve.wait_ge(*own(3))
                for t in range(2):
                    dve.wait_ge(*sig["y_turned"](4 * t + 4))
                    xs = x_tok[:, 4 * t:4 * t + 4, :]
                    dve.tensor_tensor(xs, xs, ps[:, t, :].rearrange("p (t f) -> p t f", t=4), ALU.add)


def linear_attention(core, w):
    nc, ps, x_tok, x_feat = core.nc, core.ps, core.x_tok, core.x_feat
    VW = P + 1
    names = ("steps q_ready k_ready v_ready q_under k_under q_exp k_exp q_mapped k_mapped v_taken kv_ready kv_taken "
             "mixed_ready mixed_taken mixed_turned turned_taken y_ready ones").split()
    sig = {n: core.counter("la_" + n) for n in names}
    loaded = core.counter("la_loaded")
    with ExitStack() as ctx:
        def sb(name, shape, dt=FP32):
            return core.tensor(ctx, "la_" + name, shape, dt)

        mats = sb("mats", [P, 4, P])
        bq = sb("bq", [P, 1])
        rows = sb("rows", [P, 3, P])
        q, q_min, q_max = sb("q", [P, TOK]), sb("q_min", [P, TOK]), sb("q_max", [P, TOK])
        k, k_min, k_max = sb("k", [P, NT, P]), sb("k_min", [P, NT, P]), sb("k_max", [P, NT, P])
        v = sb("v", [P, NT, VW])
        kv = sb("kv", [P, B, VW])
        rec = sb("rec", [P, NT])
        mixed = sb("mixed", [P, NT, P])
        mixedT = sb("mixedT", [P, NT, P])

        def halves(t):
            return t.rearrange("p (n c) -> p n c", n=2)

        with nc.Block(no_gpsimd_drain=True) as block:
            @block.sync
            def _(sp):
                sp.dma_start(mats[:, :, :], w["mats"]).then_inc(loaded.sem, 16)
                sp.dma_start(bq[:, :], w["bq"]).then_inc(loaded.sem, 16)
                sp.dma_start(rows[:, :, :], w["rows"].partition_broadcast(P)).then_inc(loaded.sem, 16)

            @block.gpsimd
            def _(pool):
                pool.memset(v[:, :, P:VW], 1.0).then_inc(sig["ones"].sem, 1)

            @block.tensor
            def _(pe):
                pe.wait_ge(*loaded(48))
                for n in range(2):
                    last = pe.matmul(ps[:, n, :], mats[:, 0, :], x_feat[:, n * HALF:(n + 1) * HALF],
                                     start=True, stop=True)
                last.then_inc(sig["q_ready"].sem, 1)
                for bank, m, done in ((2, 1, "k_ready"), (4, 2, "v_ready")):
                    for t in range(NT):
                        last = pe.matmul(ps[:, bank + t // 4, t % 4 * P:(t % 4 + 1) * P],
                                         x_feat[:, t * P:(t + 1) * P], mats[:, m, :], start=True, stop=True)
                    last.then_inc(sig[done].sem, 1)
                pe.wait_ge(*sig["k_mapped"](1))
                pe.wait_ge(*sig["v_taken"](1))
                for b in range(B):
                    for t in range(TPB):
                        last = pe.matmul(ps[:, 6 + b // 2, b % 2 * 256:b % 2 * 256 + VW], k[:, TPB * b + t, :],
                                         v[:, TPB * b + t, :], start=t == 0, stop=t == TPB - 1)
                last.then_inc(sig["kv_ready"].sem, 1)
                pe.wait_ge(*sig["kv_taken"](1))
                pe.wait_ge(*sig["q_mapped"](1))
                for t in range(NT):
                    last = pe.matmul(ps[:, t // 2, t % 2 * 256:t % 2 * 256 + VW], q[:, t * P:(t + 1) * P],
                                     kv[:, t // TPB, :], start=True, stop=True)
                last.then_inc(sig["mixed_ready"].sem, 1)
                pe.wait_ge(*sig["mixed_taken"](1))
                for t in range(NT):
                    last = pe.transpose(ps[:, 4 + t // 4, t % 4 * P:(t % 4 + 1) * P], mixed[:, t, :],
                                        core.ident[:, :])
                last.then_inc(sig["mixed_turned"].sem, 1)
                pe.wait_ge(*sig["turned_taken"](1))
                for t in range(NT):
                    last = pe.matmul(ps[:, 6 + t // 4, t % 4 * P:(t % 4 + 1) * P], mixedT[:, t, :], mats[:, 3, :],
                                     start=True, stop=True)
                last.then_inc(sig["y_ready"].sem, 1)

            @block.scalar
            def _(act):
                act.wait_ge(*sig["q_under"](1))
                act.activation(q_min[:, :], q_min[:, :], ACT.Exp).then_inc(sig["q_exp"].sem, 1)
                act.wait_ge(*sig["k_under"](1))
                act.activation(k_min[:, :, :], k_min[:, :, :], ACT.Exp).then_inc(sig["k_exp"].sem, 1)
                act.wait_ge(*sig["mixed_turned"](1))
                act.copy(halves(mixedT[:, :, :].rearrange("p t f -> p (t f)")), ps[:, 4:6, :])\
                   .then_inc(sig["turned_taken"].sem, 1)

            @block.vector
            def _(dve):
                own = Steps(sig["steps"])
                dve.wait_ge(*loaded(48))
                own.done(dve.tensor_tensor(x_tok[:, :, :], x_tok[:, :, :],
                                           rows[:, 2:3, :].to_broadcast([P, NT, P]), ALU.add))
                dve.wait_ge(*sig["q_ready"](1))
                dve.tensor_scalar(halves(q_min[:, :]), ps[:, 0:2, :], bq[:, 0:1], 0.0, ALU.add, ALU.min)\
                   .then_inc(sig["q_under"].sem, 1)
                own.done(dve.tensor_scalar(halves(q_max[:, :]), ps[:, 0:2, :], bq[:, 0:1], 0.0, ALU.add, ALU.max))
                dve.wait_ge(*sig["k_ready"](1))
                own.done(dve.tensor_tensor(k_max[:, :, :], ps[:, 2:4, :].rearrange("p n (t f) -> p (n t) f", f=P),
                                           rows[:, 0:1, :].to_broadcast([P, NT, P]), ALU.add))
                dve.wait_ge(*own.last())
                dve.tensor_scalar(k_min[:, :, :], k_max[:, :, :], 0.0, None, ALU.min).then_inc(sig["k_under"].sem, 1)
                dve.wait_ge(*sig["k_under"](1))
                own.done(dve.tensor_scalar(k_max[:, :, :], k_max[:, :, :], 0.0, None, ALU.max))
                dve.wait_ge(*sig["v_ready"](1))
                dve.tensor_tensor(v[:, :, 0:P], ps[:, 4:6, :].rearrange("p n (t f) -> p (n t) f", f=P),
                                  rows[:, 1:2, :].to_broadcast([P, NT, P]), ALU.add)\
                   .then_inc(sig["v_taken"].sem, 1)
                dve.wait_ge(*sig["ones"](1))
                dve.wait_ge(*sig["k_exp"](1))
                dve.wait_ge(*own.last())
                dve.tensor_tensor(k[:, :, :], k_min[:, :, :], k_max[:, :, :], ALU.add)\
                   .then_inc(sig["k_mapped"].sem, 1)
                dve.wait_ge(*sig["q_exp"](1))
                dve.tensor_tensor(q[:, :], q_min[:, :], q_max[:, :], ALU.add).then_inc(sig["q_mapped"].sem, 1)
                dve.wait_ge(*sig["kv_ready"](1))
                src = ps[:, 6:8, :].rearrange("p n (b c) -> p (n b) c", b=2)
                own.done(dve.tensor_copy(kv[:, :, 0:P], src[:, :, 0:P]))
                dve.tensor_scalar(kv[:, :, P:VW], src[:, :, P:VW], 1e-6, None, ALU.add)\
                   .then_inc(sig["kv_taken"].sem, 1)
                dve.wait_ge(*sig["mixed_ready"](1))
                src = ps[:, 0:4, :].rearrange("p n (t c) -> p (n t) c", t=2)
                own.done(dve.reciprocal(rec[:, :], src[:, :, P]))
                dve.wait_ge(*own.last())
                dve.tensor_tensor(mixed[:, :, :], src[:, :, 0:P], rec[:, :].unsqueeze(2).to_broadcast([P, NT, P]),
                                  ALU.mult).then_inc(sig["mixed_taken"].sem, 1)
                dve.wait_ge(*sig["y_ready"](1))
                dve.tensor_tensor(x_tok[:, :, :], x_tok[:, :, :],
                                  ps[:, 6:8, :].rearrange("p n (t f) -> p (n t) f", f=P), ALU.add)


def rwkv_mixer(core, w):
    nc, ps, x_tok, x_feat = core.nc, core.ps, core.x_tok, core.x_feat
    names = "own own_act k_ready v_ready r_ready mixed taken y_ready expo scanned gated filled".split()
    sig = {n: core.counter("rw_" + n) for n in names}
    loaded = core.counter("rw_loaded")
    with ExitStack() as ctx:
        def sb(name, shape, dt=FP32):
            return core.tensor(ctx, "rw_" + name, shape, dt)

        mats = sb("mats", [P, 4, P])
        cols = sb("cols", [P, 5])
        keep = sb("keep", [P, 3])
        wn = sb("wn", [P, 1])
        xm = sb("xm", [P, 3, B, S])
        k, v = sb("k", [P, B, S]), sb("v", [P, B, S])
        pp, aa, bb = (sb(n, [P, B, S + 1]) for n in ("pp", "aa", "bb"))
        uk, top = sb("uk", [P, B, S]), sb("top", [P, B, S])
        e1, e2, e1b, e2b = (sb(n, [P, B, S]) for n in ("e1", "e2", "e1b", "e2b"))
        er = sb("er", [P, B, S])
        num, den = sb("num", [P, B, S]), sb("den", [P, B, S])

        def banks(n):
            return ps[:, n:n + 2, :].rearrange("p n (b s) -> p (n b) s", s=S)

        with nc.Block(no_gpsimd_drain=True) as block:
            @block.sync
            def _(sp):
                sp.dma_start(mats[:, :, :], w["mats"]).then_inc(loaded.sem, 16)
                sp.dma_start(cols[:, :], w["cols"]).then_inc(loaded.sem, 16)

            @block.gpsimd
            def _(pool):
                pool.memset(pp[:, :, 0:1], -1e38).then_inc(sig["filled"].sem, 1)
                pool.memset(aa[:, :, 0:1], 0.0).then_inc(sig["filled"].sem, 1)
                pool.memset(bb[:, :, 0:1], 0.0).then_inc(sig["filled"].sem, 1)

            @block.tensor
            def _(pe):
                pe.wait_ge(*loaded(32))
                for m, done in enumerate(("k_ready", "v_ready", "r_ready")):
                    pe.wait_ge(*sig["mixed"](m + 1))
                    for n in range(2):
                        last = pe.matmul(ps[:, 2 * m + n, :], mats[:, m, :],
                                         xm[:, m, 2 * n:2 * n + 2, :].rearrange("p b s -> p (b s)"),
                                         start=True, stop=True)
                    last.then_inc(sig[done].sem, 1)
                for b in range(B):
                    pe.wait_ge(*sig["gated"](b + 1))
                    for t in range(TPB):
                        n = TPB * b + t
                        last = pe.matmul(ps[:, 6 + n // 4, n % 4 * P:(n % 4 + 1) * P], num[:, b, t * P:(t + 1) * P],
                                         mats[:, 3, :], start=True, stop=True)
                    if b % 2:
                        last.then_inc(sig["y_ready"].sem, 1)

            @block.scalar
            def _(act):
                act.wait_ge(*loaded(32))
                act.activation(wn[:, :], cols[:, 3:4], ACT.Exp).then_inc(sig["own_act"].sem, 1)
                act.wait_ge(*sig["own_act"](1))
                act.mul(wn[:, :], wn[:, :], -1.0).then_inc(sig["own_act"].sem, 1)
                act.wait_ge(*sig["v_ready"](1))
                act.copy(v[:, :, :], banks(2)).then_inc(sig["taken"].sem, 1)
                act.wait_ge(*sig["r_ready"](1))
                act.activation(er[:, :, :], banks(4), ACT.Exp, scale=-1.0).then_inc(sig["taken"].sem, 1)
                for n, e in enumerate((e1b, e2b, e1, e2)):
                    act.wait_ge(*sig["expo"](n + 1))
                    act.activation(e[:, :, :], e[:, :, :], ACT.Exp).then_inc(sig["own_act"].sem, 1)

            @block.vector
            def _(dve):
                own = Steps(sig["own"])
                dve.wait_ge(*loaded(32))
                own.done(dve.tensor_scalar(keep[:, :], cols[:, 0:3], -1.0, 1.0, ALU.mult, ALU.add))
                xb = x_feat[:, :].rearrange("p (b s) -> p b s", s=S)
                for m in range(3):
                    own.done(dve.tensor_scalar(xm[:, m, :, :], xb, cols[:, m:m + 1], None, ALU.mult))
                    dve.wait_ge(*own.last())
                    dve.scalar_tensor_tensor(xm[:, m, :, 1:S], xb[:, :, 0:S - 1], keep[:, m:m + 1],
                                             xm[:, m, :, 1:S], ALU.mult, ALU.add).then_inc(sig["mixed"].sem, 1)
                dve.wait_ge(*sig["k_ready"](1))
                own.done(dve.tensor_copy(k[:, :, :], banks(0)))
                dve.wait_ge(*own.last())
                dve.wait_ge(*sig["filled"](3))
                dve.wait_ge(*sig["own_act"](2))
                for b in range(B):
                    own.done(dve.tensor_tensor_scan(pp[:, b, 1:S + 1], wn[:, 0:1].to_broadcast([P, S]), k[:, b, :],
                                                    -1e38, ALU.add, ALU.max))
                own.done(dve.tensor_scalar(uk[:, :, :], k[:, :, :], cols[:, 4:5], None, ALU.add))
                dve.wait_ge(*own.last())
                old, new = pp[:, :, 0:S], pp[:, :, 1:S + 1]
                dve.scalar_tensor_tensor(e1b[:, :, :], old, wn[:, 0:1], new, ALU.add, ALU.subtract)\
                   .then_inc(sig["expo"].sem, 1)
                dve.tensor_tensor(e2b[:, :, :], k[:, :, :], new, ALU.subtract).then_inc(sig["expo"].sem, 1)
                own.done(dve.tensor_tensor(top[:, :, :], old, uk[:, :, :], ALU.max))
                dve.wait_ge(*own.last())
                dve.tensor_tensor(e1[:, :, :], old, top[:, :, :], ALU.subtract).then_inc(sig["expo"].sem, 1)
                dve.tensor_tensor(e2[:, :, :], uk[:, :, :], top[:, :, :], ALU.subtract).then_inc(sig["expo"].sem, 1)
                dve.wait_ge(*sig["taken"](1))
                dve.wait_ge(*sig["own_act"](4))
                dve.wait_ge(*sig["expo"](4))
                own.done(dve.tensor_tensor(top[:, :, :], e2b[:, :, :], v[:, :, :], ALU.mult))
                dve.wait_ge(*own.last())
                for b in range(B):
                    own.done(dve.tensor_tensor_scan(aa[:, b, 1:S + 1], e1b[:, b, :], top[:, b, :], 0.0,
                                                    ALU.mult, ALU.add))
                    own.done(dve.tensor_tensor_scan(bb[:, b, 1:S + 1], e1b[:, b, :], e2b[:, b, :], 0.0,
                                                    ALU.mult, ALU.add))
                dve.wait_ge(*sig["own_act"](6))
                dve.wait_ge(*own.last())
                own.done(dve.tensor_tensor(num[:, :, :], e1[:, :, :], aa[:, :, 0:S], ALU.mult))
                own.done(dve.tensor_tensor(den[:, :, :], e1[:, :, :], bb[:, :, 0:S], ALU.mult))
                own.done(dve.tensor_tensor(v[:, :, :], e2[:, :, :], v[:, :, :], ALU.mult))
                dve.wait_ge(*own.last())
                own.done(dve.tensor_tensor(num[:, :, :], num[:, :, :], v[:, :, :], ALU.add))
                own.done(dve.tensor_tensor(den[:, :, :], den[:, :, :], e2[:, :, :], ALU.add))
                dve.wait_ge(*sig["taken"](2))
                dve.wait_ge(*own.last())
                own.done(dve.scalar_tensor_tensor(den[:, :, :], er[:, :, :], 1.0, den[:, :, :], ALU.add, ALU.mult))
                dve.wait_ge(*own.last())
                for b in range(B):
                    own.done(dve.reciprocal(den[:, b, :], den[:, b, :]))
                    dve.wait_ge(*own.last())
                    dve.tensor_tensor(num[:, b, :], num[:, b, :], den[:, b, :], ALU.mult)\
                       .then_inc(sig["gated"].sem, 1)
                for n in range(2):
                    dve.wait_ge(*sig["y_ready"](n + 1))
                    xs = x_tok[:, 4 * n:4 * n + 4, :]
                    dve.tensor_tensor(xs, xs, ps[:, 6 + n, :].rearrange("p (t f) -> p t f", f=P), ALU.add)


def reshaped_attention(core, w):
    nc, ps, x_tok, x_feat = core.nc, core.ps, core.x_tok, core.x_feat
    H, K, V = 8, 64, 16
    BL = 8
    ROWS = S * BL
    names = ("steps qk_ready q_taken k_taken v_ready v_taken vt_ready vt_taken scores_ready max_ready scores_used "
             "exp_ready rec_ready probs_ready mixed_ready mixed_taken held").split()
    sig = {n: core.counter("ra_" + n) for n in names}
    loaded = core.counter("ra_loaded")
    with ExitStack() as ctx:
        def sb(name, shape, dt=FP32):
            return core.tensor(ctx, "ra_" + name, shape, dt)

        mq, mk, mv = sb("mq", [P, BL * K]), sb("mk", [P, BL * K]), sb("mv", [P, P])
        qT, kT = sb("qT", [K, S, BL]), sb("kT", [K, S, BL])
        vT = sb("vT", [V, S, BL])
        v = sb("v", [P, 2, H, V])
        probs = sb("probs", [P, 2, H, S])
        xb = sb("xb", [P, S])
        nmax = sb("nmax", [P, 2, H])
        sums = sb("sums", [P, 2, H])
        rec = sb("rec", [P, 2, H])
        with nc.Block(no_gpsimd_drain=True) as block:
            @block.sync
            def _(sp):
                for dst, src in ((mq, "mq"), (mk, "mk"), (mv, "mv")):
                    sp.dma_start(dst[:, :], w[src]).then_inc(loaded.sem, 16)

            @block.tensor
            def _(pe):
                pe.wait_ge(*loaded(48))
                with pe.Fori(0, B) as b:
                    pe.wait_ge(*sig["mixed_taken"](b + 1))
                    for j in range(BL):
                        pe.wait_ge(*sig["q_taken"](b * BL + j + 1))
                        pe.wait_ge(*sig["k_taken"](b * BL + j + 1))
                        pe.sem_inc(sig["held"].sem, 1)
                        xs = x_feat[:, bass.ds(b * S, S)]
                        pe.matmul(ps[0:K, j % 2, 0:S], mq[:, j * K:(j + 1) * K], xs, start=True, stop=True)
                        pe.matmul(ps[0:K, 2 + j % 2, 0:S], mk[:, j * K:(j + 1) * K], xs,
                                  start=True, stop=True).then_inc(sig["qk_ready"].sem, 1)
                    for j in range(BL):
                        last = pe.matmul(ps[0:V, 4 + j // 2, j % 2 * S:j % 2 * S + S], mv[:, j * V:(j + 1) * V], xs,
                                         start=True, stop=True)
                    last.then_inc(sig["v_ready"].sem, 1)
                    pe.wait_ge(*sig["v_taken"](b + 1))
                    pe.sem_inc(sig["held"].sem, 1)
                    for n in range(2):
                        for h in range(H):
                            src = vT[:, h * 32 + n * 16:h * 32 + n * 16 + 16, :].rearrange("d t j -> d (t j)")
                            last = pe.transpose(ps[:, 4, (n * H + h) * V:(n * H + h + 1) * V], src,
                                                core.ident[0:V, 0:V])
                    last.then_inc(sig["vt_ready"].sem, 1)
                    pe.wait_ge(*sig["q_taken"](b * BL + BL + 2))
                    pe.wait_ge(*sig["k_taken"](b * BL + BL + 2))
                    for h in range(H):
                        for n in range(2):
                            i = 2 * h + n
                            pe.wait_ge(*sig["scores_used"](b * 16 + i + 1))
                            ks = kT[:, h * 32 + n * 16:h * 32 + n * 16 + 16, :].rearrange("d t j -> d (t j)")
                            qs = qT[:, h * 32:h * 32 + 32, :].rearrange("d t j -> d (t j)")
                            pe.matmul(ps[:, i % 4, 0:S], ks, qs, start=True, stop=True)\
                              .then_inc(sig["scores_ready"].sem, 1)
                    pe.wait_ge(*sig["vt_taken"](b + 1))
                    pe.wait_ge(*sig["probs_ready"](16 * b + 16))
                    for t in range(TPB):
                        for r in range(BL):
                            for n in range(2):
                                src = probs[:, n, 4 * t:4 * t + 4, :].rearrange("c h (i r) -> c r (h i)", r=BL)
                                last = pe.matmul(ps[:, 5, t * P + r * V:t * P + r * V + V], src[:, r, :],
                                                 v[:, n, r, :], start=n == 0, stop=n == 1)
                    last.then_inc(sig["mixed_ready"].sem, 1)

            @block.scalar
            def _(act):
                act.sem_inc(sig["q_taken"].sem, 2)
                act.sem_inc(sig["scores_used"].sem, 4)
                with act.Fori(0, B) as b:
                    for j in range(BL):
                        act.wait_ge(*sig["qk_ready"](b * BL + j + 1))
                        act.copy(qT[:, :, j], ps[0:K, j % 2, 0:S]).then_inc(sig["q_taken"].sem, 1)
                    for h in range(H):
                        for n in range(2):
                            i = 2 * h + n
                            act.wait_ge(*sig["max_ready"](b * 16 + i + 1))
                            act.activation(probs[:, n, h, :], ps[:, i % 4, 0:S], ACT.Exp, bias=nmax[:, n, h:h + 1],
                                           scale=K ** -0.5, accum_out=sums[:, n, h:h + 1])\
                               .then_inc(sig["scores_used"].sem, 1)

            @block.vector
            def _(dve):
                dve.sem_inc(sig["k_taken"].sem, 2)
                dve.sem_inc(sig["mixed_taken"].sem, 1)
                with dve.Fori(0, B) as b:
                    for j in range(BL):
                        dve.wait_ge(*sig["qk_ready"](b * BL + j + 1))
                        dve.tensor_copy(kT[:, :, j], ps[0:K, 2 + j % 2, 0:S]).then_inc(sig["k_taken"].sem, 1)
                    dve.wait_ge(*sig["v_ready"](b + 1))
                    dve.tensor_copy(vT[:, :, :].rearrange("d t (n k) -> d n k t", n=4),
                                    ps[0:V, 4:8, :].rearrange("d n (k t) -> d n k t", k=2))\
                       .then_inc(sig["v_taken"].sem, 1)
                    dve.wait_ge(*sig["vt_ready"](b + 1))
                    dve.tensor_copy(v[:, :, :, :].rearrange("p n h d -> p (n h d)"), ps[:, 4, 0:2 * H * V])\
                       .then_inc(sig["vt_taken"].sem, 1)

                    def scale_by_sum(i):
                        h, n = i // 2, i % 2
                        dve.wait_ge(*sig["scores_used"](b * 16 + i + 5))
                        dve.reciprocal(rec[:, n, h:h + 1], sums[:, n, h:h + 1]).then_inc(sig["rec_ready"].sem, 1)
                        dve.wait_ge(*sig["rec_ready"](b * 16 + i + 1))
                        dve.tensor_scalar(probs[:, n, h, :], probs[:, n, h, :], rec[:, n, h:h + 1], None,
                                          ALU.mult).then_inc(sig["probs_ready"].sem, 1)

                    for i in range(2 * H):
                        h, n = i // 2, i % 2
                        dve.wait_ge(*sig["scores_ready"](b * 16 + i + 1))
                        dve.tensor_reduce(nmax[:, n, h:h + 1], ps[:, i % 4, 0:S], AX.X, ALU.max)\
                           .then_inc(sig["steps"].sem, 1)
                        dve.wait_ge(*sig["steps"](b * 16 + i + 1))
                        dve.tensor_scalar(nmax[:, n, h:h + 1], nmax[:, n, h:h + 1], -K ** -0.5, None,
                                          ALU.mult).then_inc(sig["max_ready"].sem, 1)
                        if i >= 2:
                            scale_by_sum(i - 2)
                    scale_by_sum(2 * H - 2)
                    scale_by_sum(2 * H - 1)
                    dve.wait_ge(*sig["mixed_ready"](b + 1))
                    xs = x_tok[:, bass.ds(b * TPB, TPB), :]
                    dve.tensor_tensor(xs, xs, ps[:, 5, 0:TPB * P].rearrange("p (t f) -> p t f", t=TPB),
                                      ALU.add).then_inc(sig["mixed_taken"].sem, 1)


def two_way_mamba(core, w):
    nc, ps, x_tok = core.nc, core.ps, core.x_tok
    N, T, PAD, R = 16, 4, 3, 8
    HALVES, WAYS = 2, 2
    names = ("norm_steps rooted tile_ready tile_turned norm_ready weights_scaled a_exp a_ready diag_ready conv_ready z_ready "
             "xc_tanh xc_half xc_ready sz_tanh sz_half sz_ready half_ready bc_ready dt_ready dt_taken bc_taken bc_steps pre_ready abs_ready pos_ready exp_ready "
             "log_ready log_joined soft_steps delta_ready du_ready restart b_ready b_taken c_ready da_ready dbu_ready scanned "
             "hc_ready y_added y_gated join_ready join_taken out_ready act_held zeroed doubled").split()
    sig = {n: core.counter("mb_" + n) for n in names}
    loaded = core.counter("mb_loaded")
    with ExitStack() as ctx:
        def sb(name, shape, dt=FP32):
            return core.tensor(ctx, "mb_" + name, shape, dt)

        cols = sb("cols", [P, 2 + 4 * WAYS * HALVES])
        in_w = sb("in_w", [P, WAYS, 4 * P])
        taps = sb("taps", [P, WAYS, T, 2 * P])
        a = sb("a", [P, WAYS, HALVES, N])
        xp_bc = sb("xp_bc", [P, WAYS, HALVES, 96])
        xp_dt = sb("xp_dt", [P, WAYS, HALVES, R])
        dt_w = sb("dt_w", [R, WAYS, 2 * P])
        out_w = sb("out_w", [P, WAYS, 2 * P])
        fus = sb("fus", [P, WAYS, P])
        fus_b = sb("fus_b", [P, P])
        sel = sb("sel", [P, 2 * N * P], BF16)
        norm = TokenNorm(core, ctx, "mb", 1e-5, sig["norm_steps"], sig["rooted"])
        half_b = sb("half_b", [P, WAYS * HALVES])
        xn = sb("xn", [P, NT, P])
        xn_feat = sb("xn_feat", [P, B, S + 2 * PAD])
        conv_w = sb("conv_w", [P, WAYS, T, 2 * P])
        diag = sb("diag", [P, WAYS, HALVES, P])
        xc, sz, delta, du = (sb(n, [P, WAYS, HALVES, TOK]) for n in ("xc", "sz", "delta", "du"))
        dts = sb("dts", [R, WAYS, TOK])
        parts = sb("parts", [P, WAYS, TOK], BF16)
        da, dbu, hs, hc = (sb(n, [P, HALVES, TOK]) for n in ("da", "dbu", "hs", "hc"))
        bs = sb("bs", [P, 2, TOK])
        join = sb("join", [P, WAYS, HALVES, P])
        high = hc[:, 0, 0:TOK // 2].bitcast(BF16)
        middle = hc[:, 0, TOK // 2:TOK].bitcast(BF16)
        rest = hs[:, 0, :]

        SERIES = [1 / 7, -1 / 6, 1 / 5, -1 / 4, 1 / 3, -1 / 2, 1.0]
        SOFT = len(SERIES) + 2

        def col_of(r, h, n):
            c = 2 + 4 * (HALVES * r + h) + n
            return cols[:, c:c + 1]

        CONV_B, DT_B, D = 0, 1, 2

        def pair(n):
            return ps[:, 2 * n:2 * n + 2, :]

        def two(t):
            return t.rearrange("p (n c) -> p n c", n=2)

        loads = [(cols[:, :], "cols"), (in_w[:, :, :], "in_w"), (taps[:, :, :, :], "taps"), (a[:, :, :, :], "a_log"),
                 (xp_bc[:, :, :, :], "xp_bc"), (xp_dt[:, :, :, :], "xp_dt"), (dt_w[:, :, :], "dt_w"),
                 (out_w[:, :, :], "out_w"), (fus[:, :, :], "fus"), (fus_b[:, :], "fus_b"), (sel[:, :], "sel")]
        ALL = 16 * len(loads)

        with nc.Block(no_gpsimd_drain=True) as block:
            @block.sync
            def _(sp):
                for dst, name in loads:
                    src = w[name].partition_broadcast(P) if name in ("taps", "fus_b") else w[name]
                    sp.dma_start(dst, src).then_inc(loaded.sem, 16)

            @block.gpsimd
            def _(pool):
                pool.memset(xn_feat[:, :, 0:PAD], 0.0).then_inc(sig["zeroed"].sem, 1)
                pool.memset(xn_feat[:, :, PAD + S:], 0.0).then_inc(sig["zeroed"].sem, 1)
                pool.wait_ge(*sig["zeroed"](2))
                pool.memset(parts[96:P, :, :], 0.0).then_inc(sig["zeroed"].sem, 1)
                pool.wait_ge(*sig["zeroed"](3))
                pool.wait_ge(*loaded(ALL))
                for r in range(WAYS):
                    pool.tensor_tensor(conv_w[:, r, :, :], taps[:, r, :, :],
                                       in_w[:, r, 0:2 * P].unsqueeze(1).to_broadcast([P, T, 2 * P]),
                                       ALU.mult).then_inc(sig["weights_scaled"].sem, 1)
                for r in range(WAYS):
                    for h in range(HALVES):
                        pool.tensor_scalar(diag[:, r, h, :], core.ident[:, :], col_of(r, h, D), None, ALU.mult)\
                            .then_inc(sig["diag_ready"].sem, 1)
                for r in range(WAYS):
                    for h in range(HALVES):
                        n = HALVES * r + h
                        pool.wait_ge(*sig["soft_steps"](SOFT * n + SOFT))
                        pool.tensor_tensor(bs[:, h, :], bs[:, h, :], dbu[:, h, :], ALU.add)\
                            .then_inc(sig["log_joined"].sem, 1)
                        pool.wait_ge(*sig["log_joined"](n + 1))
                        pool.wait_ge(*sig["pos_ready"](n + 1))
                        pool.tensor_tensor(delta[:, r, h, :], delta[:, r, h, :], bs[:, h, :], ALU.add)\
                            .then_inc(sig["delta_ready"].sem, 1)
                        pool.wait_ge(*sig["delta_ready"](n + 1))
                        pool.tensor_tensor(du[:, r, h, :], delta[:, r, h, :], xc[:, r, h, :], ALU.mult)\
                            .then_inc(sig["du_ready"].sem, 1)
                pool.wait_ge(*sig["du_ready"](WAYS * HALVES))
                for r in range(WAYS):
                    if r:
                        pool.wait_ge(*sig["scanned"](2 + 2 * N * r))
                    edge = 0 if r == 0 else S - 1
                    for h in range(HALVES):
                        pool.memset(da[:, h, :].rearrange("p (b s) -> p b s", s=S)[:, :, edge:edge + 1], 0.0)\
                            .then_inc(sig["restart"].sem, 1)
                    with pool.Fori(0, N // 2) as i:
                        for u in range(2):
                            n = N * r + 2 * i + u
                            for h in range(HALVES):
                                pool.wait_ge(*sig["b_taken"](n + 2))
                                pool.wait_ge(*sig["scanned"](2 * n + h + 1))
                                pool.tensor_tensor(dbu[:, h, :], du[:, r, h, :], bs[:, u, :], ALU.mult)\
                                    .then_inc(sig["dbu_ready"].sem, 1)

            @block.tensor
            def _(pe):
                pe.wait_ge(*loaded(ALL))
                for t in range(NT):
                    pe.wait_ge(*sig["tile_ready"](t + 1))
                    pe.transpose(ps[:, t // 4, t % 4 * P:(t % 4 + 1) * P], xn[:, t, :], core.ident[:, :])\
                      .then_inc(sig["tile_turned"].sem, 1)
                pe.wait_ge(*sig["norm_ready"](2))
                pe.wait_ge(*sig["zeroed"](3))
                for r in range(WAYS):
                    pe.wait_ge(*sig["weights_scaled"](r + 1))
                    if r:
                        pe.wait_ge(*sig["bc_taken"](r))
                        pe.wait_ge(*sig["dt_taken"](r))
                        pe.wait_ge(*sig["pos_ready"](HALVES * r))
                    for h in range(HALVES):
                        for n in range(2):
                            for j in range(T):
                                at = j if r == 0 else 2 * PAD - j
                                last = pe.matmul(ps[:, 2 * h + n, :], conv_w[:, r, j, h * P:(h + 1) * P],
                                                 xn_feat[:, 2 * n:2 * n + 2, at:at + S], start=j == 0, stop=j == T - 1)
                        last.then_inc(sig["conv_ready"].sem, 1)
                    for h in range(HALVES):
                        for n in range(2):
                            last = pe.matmul(ps[:, 4 + 2 * h + n, :], in_w[:, r, (2 + h) * P:(3 + h) * P],
                                             xn_feat[:, 2 * n:2 * n + 2, PAD:PAD + S], start=True, stop=True)
                        last.then_inc(sig["z_ready"].sem, 1)
                    pe.wait_ge(*sig["xc_ready"](HALVES * (r + 1)))
                    for out, mat, bank, done in ((96, xp_bc, 0, "bc_ready"), (R, xp_dt, 2, "dt_ready")):
                        for n in range(2):
                            for h in range(HALVES):
                                last = pe.matmul(ps[0:out, bank + n, :], mat[:, r, h, :],
                                                 xc[:, r, h, n * HALF:(n + 1) * HALF], start=h == 0, stop=h == 1)
                        last.then_inc(sig[done].sem, 1)
                    pe.wait_ge(*sig["dt_taken"](r + 1))
                    pe.wait_ge(*sig["sz_ready"](HALVES * (r + 1)))
                    for h in range(HALVES):
                        for n in range(2):
                            last = pe.matmul(ps[:, 4 + 2 * h + n, :], dt_w[:, r, h * P:(h + 1) * P],
                                             dts[:, r, n * HALF:(n + 1) * HALF], start=True, stop=True)
                        last.then_inc(sig["pre_ready"].sem, 1)
                pe.wait_ge(*sig["bc_taken"](WAYS))
                pe.wait_ge(*sig["pos_ready"](WAYS * HALVES))
                pe.wait_ge(*sig["diag_ready"](WAYS * HALVES))

                def spread(r, s, bank, row, done):
                    for n in range(2):
                        last = pe.matmul(ps[:, bank + n, :], sel[:, bass.ds(row * P, P)],
                                         parts[:, r, n * HALF:(n + 1) * HALF], start=True, stop=True)
                    last.then_inc(sig[done].sem, 1)

                def spread_b(r, s):
                    pe.wait_ge(*sig["b_taken"](N * r + s + 1))
                    spread(r, s, 0, s, "b_ready")

                def spread_c(r, s):
                    pe.wait_ge(*sig["hc_ready"](2 * (N * r + s) + 2))
                    spread(r, s, 2, s + N, "c_ready")

                def add_state(r, s, last_state=False):
                    for h in range(HALVES):
                        pe.wait_ge(*sig["hc_ready"](2 * (N * r + s) + h + 3))
                        for n in range(2):
                            last = pe.matmul(ps[:, 4 + 2 * h + n, :], core.ident[:, :],
                                             hc[:, h, n * HALF:(n + 1) * HALF], start=False, stop=last_state)
                        last.then_inc(sig["y_added"].sem, 1)

                for r in range(WAYS):
                    if r:
                        pe.wait_ge(*sig["y_gated"](HALVES * r))
                    for h in range(HALVES):
                        for n in range(2):
                            pe.matmul(ps[:, 4 + 2 * h + n, :], diag[:, r, h, :],
                                      xc[:, r, h, n * HALF:(n + 1) * HALF], start=True, stop=False)
                    spread_b(r, 0)
                    spread_c(r, 0)
                    with pe.Fori(0, N // 2 - 1) as i:
                        for u in range(2):
                            spread_b(r, 2 * i + u + 1)
                            add_state(r, 2 * i + u)
                            spread_c(r, 2 * i + u + 1)
                    spread_b(r, N - 1)
                    add_state(r, N - 2)
                    spread_c(r, N - 1)
                    add_state(r, N - 1, last_state=True)
                for r in range(WAYS):
                    for h in range(HALVES):
                        if r == h == 0:
                            pe.wait_ge(*sig["b_taken"](WAYS * N + 1))
                        c = (HALVES * r + h) * P
                        last = pe.matmul(ps[:, 0, c:c + P], out_w[:, r, h * P:(h + 1) * P], fus[:, r, :],
                                         start=True, stop=True)
                last.then_inc(sig["join_ready"].sem, 1)
                pe.wait_ge(*sig["join_taken"](1))
                pe.wait_ge(*sig["y_gated"](WAYS * HALVES))
                pe.wait_ge(*sig["hc_ready"](2 * WAYS * N + 2))
                for t in range(NT):
                    for r in range(WAYS):
                        for h in range(HALVES):
                            last = pe.matmul(ps[:, 2 + t // 4, t % 4 * P:(t % 4 + 1) * P],
                                             sz[:, r, h, t * P:(t + 1) * P], join[:, r, h, :],
                                             start=r == h == 0, stop=r == h == 1)
                    if t % 4 == 3:
                        last.then_inc(sig["out_ready"].sem, 1)

            @block.scalar
            def _(act):
                norm.on_scalar(act)
                act.wait_ge(*loaded(ALL))
                act.activation(a[:, :, :, :], a[:, :, :, :], ACT.Exp).then_inc(sig["a_exp"].sem, 1)
                act.wait_ge(*sig["a_exp"](1))
                act.mul(a[:, :, :, :], a[:, :, :, :], -1.0).then_inc(sig["a_ready"].sem, 1)
                for n in range(WAYS * HALVES):
                    c = 2 + 4 * n
                    act.mul(half_b[:, n:n + 1], cols[:, c:c + 1], 0.5).then_inc(sig["half_ready"].sem, 1)
                for n in range(2):
                    act.wait_ge(*sig["tile_turned"](4 * n + 4))
                    act.activation(xn_feat[:, 2 * n:2 * n + 2, PAD:PAD + S],
                                   ps[:, n, :].rearrange("p (b s) -> p b s", s=S), ACT.Identity,
                                   scale=cols[:, 0:1], bias=cols[:, 1:2]).then_inc(sig["norm_ready"].sem, 1)
                act.wait_ge(*sig["half_ready"](WAYS * HALVES))
                for r in range(WAYS):
                    for h in range(HALVES):
                        act.wait_ge(*sig["conv_ready"](HALVES * r + h + 1))
                        act.activation(two(xc[:, r, h, :]), pair(h), ACT.Tanh, scale=0.5,
                                       bias=half_b[:, HALVES * r + h:HALVES * r + h + 1])\
                           .then_inc(sig["xc_tanh"].sem, 1)
                    for h in range(HALVES):
                        act.wait_ge(*sig["z_ready"](HALVES * r + h + 1))
                        act.activation(two(sz[:, r, h, :]), pair(2 + h), ACT.Tanh, scale=0.5)\
                           .then_inc(sig["sz_tanh"].sem, 1)
                    for h in range(HALVES):
                        n = HALVES * r + h
                        e = da[:, h, :]
                        act.wait_ge(*sig["pre_ready"](n + 1))
                        if r:
                            act.wait_ge(*sig["soft_steps"](SOFT * (n - 2) + SOFT))
                        act.activation(two(e), pair(2 + h), ACT.Abs, bias=col_of(r, h, DT_B))\
                           .then_inc(sig["abs_ready"].sem, 1)
                    for h in range(HALVES):
                        n = HALVES * r + h
                        e = da[:, h, :]
                        act.wait_ge(*sig["abs_ready"](n + 1))
                        act.activation(e, e, ACT.Exp, scale=-1.0).then_inc(sig["exp_ready"].sem, 1)
                    for h in range(HALVES):
                        n = HALVES * r + h
                        act.wait_ge(*sig["exp_ready"](n + 1))
                        if r:
                            act.wait_ge(*sig["log_joined"](n - 1))
                        act.activation(dbu[:, h, :], da[:, h, :], ACT.Ln, bias=1.0).then_inc(sig["log_ready"].sem, 1)
                act.sem_inc(sig["b_taken"].sem, 1)
                act.wait_ge(*sig["a_ready"](1))
                act.wait_ge(*sig["du_ready"](WAYS * HALVES))
                for r in range(WAYS):
                    act.wait_ge(*sig["restart"](HALVES * (r + 1)))
                    with act.Fori(0, N // 2) as i:
                        for u in range(2):
                            s = 2 * i + u
                            n = N * r + s
                            act.wait_ge(*sig["b_ready"](n + 1))
                            act.wait_ge(*sig["dbu_ready"](2 * n + 2))
                            act.copy(two(bs[:, u, :]), pair(0)).then_inc(sig["b_taken"].sem, 1)
                            for h in range(HALVES):
                                act.wait_ge(*sig["scanned"](2 * n + h + 1))
                                act.sem_inc(sig["act_held"].sem, 1)
                                lo = 1 - r
                                act.activation(da[:, h, :].rearrange("p (b s) -> p b s", s=S)[:, :, lo:lo + S - 1],
                                               delta[:, r, h, :].rearrange("p (b s) -> p b s", s=S)[:, :, lo:lo + S - 1],
                                               ACT.Exp, scale=a[:, r, h, bass.ds(s, 1)])\
                                   .then_inc(sig["da_ready"].sem, 1)

            def softplus_tail(r, h):
                dve, n, steps = nc.vector, HALVES * r + h, sig["soft_steps"]
                e, series, log = da[:, h, :], bs[:, h, :], dbu[:, h, :]
                dve.wait_ge(*sig["exp_ready"](n + 1))
                if r:
                    dve.wait_ge(*sig["delta_ready"](n - 1))
                dve.tensor_scalar(series, e, SERIES[0], None, ALU.mult).then_inc(steps.sem, 1)
                for m, c in enumerate(SERIES[1:]):
                    dve.wait_ge(*steps(SOFT * n + m + 1))
                    dve.scalar_tensor_tensor(series, series, c, e, ALU.add, ALU.mult).then_inc(steps.sem, 1)
                dve.wait_ge(*steps(SOFT * n + len(SERIES)))
                dve.wait_ge(*sig["log_ready"](n + 1))
                dve.tensor_tensor(log, log, series, ALU.subtract).then_inc(steps.sem, 1)
                dve.wait_ge(*steps(SOFT * n + len(SERIES) + 1))
                dve.scalar_tensor_tensor(log, e, 1 / 16, log, ALU.is_ge, ALU.mult).then_inc(steps.sem, 1)

            @block.vector
            def _(dve):
                norm.on_vector(dve)
                for t in range(NT):
                    norm.normalise(dve, xn[:, t, :], t).then_inc(sig["tile_ready"].sem, 1)
                dve.wait_ge(*loaded(ALL))
                dve.wait_ge(*sig["tile_ready"](NT))
                dve.scalar_tensor_tensor(x_tok[:, :, :], x_tok[:, :, :], 2.0,
                                         fus_b[:, :].unsqueeze(1).to_broadcast([P, NT, P]), ALU.mult, ALU.add)\
                   .then_inc(sig["doubled"].sem, 1)
                for r in range(WAYS):
                    for name, dst, first, bias in (("xc", xc, 0, True), ("sz", sz, 2, False)):
                        for h in range(HALVES):
                            n = HALVES * r + h
                            half = hs[:, h, :]
                            dve.wait_ge(*sig[name + "_tanh"](n + 1))
                            if name == "sz":
                                dve.wait_ge(*sig["xc_ready"](n + 1))
                            elif r:
                                dve.wait_ge(*sig["sz_ready"](n - 1))
                                dve.wait_ge(*sig["bc_taken"](r))
                            dve.tensor_scalar(two(half), pair(first + h), col_of(r, h, CONV_B) if bias else 0.0,
                                              0.5, ALU.add, ALU.mult).then_inc(sig[name + "_half"].sem, 1)
                            dve.wait_ge(*sig[name + "_half"](n + 1))
                            dve.scalar_tensor_tensor(dst[:, r, h, :], dst[:, r, h, :], 1.0, half, ALU.add,
                                                     ALU.mult).then_inc(sig[name + "_ready"].sem, 1)
                    dve.wait_ge(*sig["sz_ready"](HALVES * (r + 1)))
                    dve.wait_ge(*sig["dt_ready"](r + 1))
                    dve.tensor_copy(two(dts[:, r, :]), ps[0:R, 2:4, :]).then_inc(sig["dt_taken"].sem, 1)
                    dve.wait_ge(*sig["bc_ready"](r + 1))
                    bc, steps = ps[0:96, 0:2, :], sig["bc_steps"]
                    if r:
                        dve.wait_ge(*sig["bc_taken"](r))
                    dve.tensor_copy(two(high[0:96, :]), bc).then_inc(steps.sem, 1)
                    dve.wait_ge(*steps(4 * r + 1))
                    dve.tensor_tensor(two(rest[0:96, :]), bc, two(high[0:96, :]), ALU.subtract).then_inc(steps.sem, 1)
                    dve.tensor_copy(parts[0:32, r, :], high[0:32, :]).then_inc(steps.sem, 1)
                    dve.wait_ge(*steps(4 * r + 3))
                    dve.tensor_copy(middle[0:96, :], rest[0:96, :]).then_inc(steps.sem, 1)
                    dve.wait_ge(*steps(4 * r + 4))
                    dve.tensor_copy(parts[32:64, r, :], middle[32:64, :])
                    dve.tensor_tensor(parts[64:96, r, :], rest[64:96, :], middle[64:96, :], ALU.subtract)\
                       .then_inc(sig["bc_taken"].sem, 1)
                    for h in range(HALVES):
                        n = HALVES * r + h
                        dve.wait_ge(*sig["abs_ready"](n + 1))
                        dve.tensor_scalar(two(delta[:, r, h, :]), pair(2 + h), col_of(r, h, DT_B), 0.0,
                                          ALU.add, ALU.max).then_inc(sig["pos_ready"].sem, 1)
                    for h in range(HALVES):
                        softplus_tail(r, h)
                dve.sem_inc(sig["scanned"].sem, 2)
                dve.sem_inc(sig["hc_ready"].sem, 2)
                dve.sem_inc(sig["y_added"].sem, 2)
                dve.sem_inc(sig["dbu_ready"].sem, 4)

                def way(t, r):
                    return t if r == 0 else t[:, ::-1]

                dve.wait_ge(*sig["bc_taken"](WAYS))
                for r in range(WAYS):
                    with dve.Fori(0, N) as s:
                        n = N * r + s
                        for h in range(HALVES):
                            dve.wait_ge(*sig["da_ready"](2 * n + h + 1))
                            dve.wait_ge(*sig["dbu_ready"](2 * n + h + 5))
                            dve.wait_ge(*sig["hc_ready"](2 * n + h + 1))
                            dve.tensor_tensor_scan(way(hs[:, h, :], r), way(da[:, h, :], r), way(dbu[:, h, :], r), 0.0,
                                                   ALU.mult, ALU.add).then_inc(sig["scanned"].sem, 1)
                        for h in range(HALVES):
                            dve.wait_ge(*sig["scanned"](2 * n + h + 3))
                            dve.wait_ge(*sig["c_ready"](n + 1))
                            dve.wait_ge(*sig["y_added"](2 * n + h + 1))
                            dve.tensor_tensor(two(hc[:, h, :]), two(hs[:, h, :]), pair(1), ALU.mult)\
                               .then_inc(sig["hc_ready"].sem, 1)
                    dve.wait_ge(*sig["y_added"](2 + 2 * N * (r + 1)))
                    dve.wait_ge(*sig["sz_ready"](WAYS * HALVES))
                    for h in range(HALVES):
                        dve.tensor_tensor(two(sz[:, r, h, :]), pair(2 + h), two(sz[:, r, h, :]), ALU.mult)\
                           .then_inc(sig["y_gated"].sem, 1)
                dve.wait_ge(*sig["join_ready"](1))
                dve.tensor_copy(join[:, :, :, :].rearrange("p r h f -> p (r h f)"), ps[:, 0, :])\
                   .then_inc(sig["join_taken"].sem, 1)
                dve.wait_ge(*sig["doubled"](1))
                for n in range(2):
                    dve.wait_ge(*sig["out_ready"](n + 1))
                    xs = x_tok[:, 4 * n:4 * n + 4, :]
                    dve.tensor_tensor(xs, xs, ps[:, 2 + n, :].rearrange("p (t f) -> p t f", f=P), ALU.add)


def selector(parts, n, rows=None):
    t = np.zeros((rows or parts * n, n, P), "bfloat16")
    for r in range(parts * n):
        t[r, r % n, :] = 1
    return t.reshape(-1, n * P)


def layout(i):
    a = {k: np.asarray(v) for k, v in i.items()}
    d = {"x": a["x"].reshape(TOK, P), "context": a["ctx_1024"].reshape(TOK, P),
         "ident": np.eye(P, dtype=np.float32), "ident16": np.eye(P, dtype="bfloat16")}
    for s, dim, q, k, v, o in (("L0x", 8, "L0_xattn_Wq", "L0_xattn_Wk", "L0_xattn_Wv", "L0_xattn_Wo"),
                               ("L1x", 8, "L1_xattn_Wq", "L1_xattn_Wk", "L1_xattn_Wv", "L1_xattn_Wo"),
                               ("L2x", 8, "L2_xattn_w_q", "L2_xattn_w_k", "L2_xattn_w_v", "L2_xattn_w_o")):
        d[s + "_wq"], d[s + "_wk"] = a[q].T, a[k].T
        d[s + "_wv"], d[s + "_wo"] = a[v].T, a[o].T
        d[s + "_sel"] = selector(2, 4)
        d[s + "_rows"] = np.repeat(np.eye(HEADS, dtype=np.float32), dim, axis=0)
    for s in ("L0", "L1"):
        d[s + "x_bq"], d[s + "x_bk"] = a[s + "_xattn_bq"].reshape(P, 1), a[s + "_xattn_bk"].reshape(P, 1)
        d[s + "x_bv"], d[s + "x_bo"] = a[s + "_xattn_bv"], a[s + "_xattn_bo"]
    d["L1x_mask"] = a["mask_1x1xSxS2_ik0"].reshape(S, S)

    def heads64(w):
        return w.transpose(1, 0, 2).reshape(P, HEADS * 64)

    d["L3x_wq"], d["L3x_wk"], d["L3x_wv"] = (heads64(a["L3_xattn_" + n]) for n in ("WQ", "WK", "WV"))
    d["L3x_wo"] = a["L3_xattn_WO"].reshape(8, P, P).transpose(1, 0, 2).reshape(P, 8 * P)
    d["L3x_sel"] = selector(2, 2)
    d["L3x_rows"] = np.repeat(np.eye(2, dtype=np.float32), 64, axis=0)
    d["L3x_mask"] = np.tril(np.ones((S, S), np.int32))

    def units(gate, up, down):
        return np.concatenate([gate, up, down], axis=2)

    def cut(w):
        e, m, n = w.shape
        return w.reshape(e, m, n // P, P).transpose(0, 2, 1, 3).reshape(-1, m, P)

    gu, dn = a["L0_ffn_gate_up_w"], a["L0_ffn_down_w"]
    sg, su, sd = (a["L0_ffn_shared_" + n] for n in ("gate_w", "up_w", "down_w"))
    d["L0f_units"] = np.concatenate([
        units(gu[:, :, :P], gu[:, :, P:], dn),
        units(cut(sg.T[None]), cut(su.T[None]), sd.T.reshape(2, P, P))])
    d["L0f_router"], d["L0f_sel"] = a["L0_ffn_router_w"].T, selector(3, 18, P)
    w13, w2 = a["L2_ffn_w13"], a["L2_ffn_w2"]
    d["L2f_units"] = units(cut(w13[:, :, :256]), cut(w13[:, :, 256:]), w2.reshape(16, P, P))
    d["L2f_router"], d["L2f_sel"] = a["L2_ffn_router_w"].T, selector(3, 8, P)
    e1, e2, e3, s1, s2, s3 = (a["L3_ffn_" + n] for n in ("ew1", "ew2", "ew3", "sw1", "sw2", "sw3"))
    d["L3f_units"] = np.concatenate([units(cut(e1), cut(e2), e3.reshape(16, P, P)),
                                     units(cut(s1[None]), cut(s2[None]), s3.reshape(2, P, P))])
    d["L3f_router"], d["L3f_sel"] = a["L3_ffn_gate_w"], selector(3, 9, P)
    d["L0a_mats"] = np.stack([a["L0_attn_" + n].T for n in ("Wq", "Wk", "Wv", "Wo")], axis=1)
    d["L0a_bq"] = a["L0_attn_bq"].reshape(P, 1)
    d["L0a_rows"] = np.stack([a["L0_attn_" + n] for n in ("bk", "bv", "bo")])
    d["L3a_mq"], d["L3a_mk"], d["L3a_mv"] = a["L3_attn_Mq"], a["L3_attn_Mk"], a["L3_attn_Mv"]
    w1, w2 = a["L1_ffn_W1"], a["L1_ffn_W2"]
    d["L1f_mats"] = np.concatenate([w1, w2.reshape(8, 4, P, P).transpose(0, 2, 1, 3).reshape(8, P, 4 * P)], axis=2)
    d["L1f_router"], d["L1f_sel"] = a["L1_ffn_Wg"], selector(3, 8, P)
    d["L1f_gamma"], d["L1f_beta"] = a["L1_ffn_gamma"].T, a["L1_ffn_beta"].T
    d["L1f_b1"], d["L1f_b2"] = a["L1_ffn_b1"].reshape(32, P).T, a["L1_ffn_b2"]
    d["L2a_mats"] = np.stack([a["L2_attn_" + n].T for n in ("Wk", "Wv", "Wr", "Wo")], axis=1)
    d["L2a_cols"] = np.stack([a["L2_attn_" + n].reshape(P) for n in
                              ("time_mix_k", "time_mix_v", "time_mix_r", "w", "u")], axis=1)
    ways = [{n[len("L1_attn_f_"):]: v for n, v in a.items() if n.startswith(f"L1_attn_{way}_")} for way in "fb"]
    cols = [a["L1_attn_ln_g"], a["L1_attn_ln_b"]]
    for m in ways:
        for h in range(2):
            cols += [m[n][h * P:(h + 1) * P] for n in ("conv_b", "dt_b", "D", "D")]
    d["L1a_cols"] = np.stack(cols, axis=1)

    def both(f):
        return np.stack([f(m) for m in ways], axis=1)

    def halved(t):
        return t.reshape(2, P, -1).transpose(1, 0, 2)

    d["L1a_in_w"] = both(lambda m: m["in_w"].T)
    d["L1a_taps"] = np.stack([m["conv_w"][:, 0, :].T for m in ways])
    d["L1a_a_log"] = both(lambda m: halved(m["A_log"]))
    d["L1a_xp_bc"] = both(lambda m: halved(np.tile(m["xproj_w"][8:].T, (1, 3))))
    d["L1a_xp_dt"] = both(lambda m: halved(m["xproj_w"][:8].T))
    d["L1a_dt_w"] = both(lambda m: m["dt_w"].T)
    d["L1a_out_w"] = both(lambda m: m["out_w"])
    d["L1a_fus"] = a["L1_attn_fus_w"].T.reshape(2, P, P).transpose(1, 0, 2)
    d["L1a_fus_b"] = a["L1_attn_fus_b"]
    d["L1a_sel"] = selector(3, 32, P)
    return {k: np.ascontiguousarray(v) for k, v in d.items()}


STAGES = (0, 12)


def build(nc, d, out):
    ctx = ExitStack()
    with ctx:
        core = Core(ctx, nc)

        def of(stage):
            return {n[len(stage) + 1:]: v for n, v in d.items() if n.startswith(stage + "_")}

        stages = [
            lambda: linear_attention(core, of("L0a")),
            lambda: cross_attention(core, of("L0x"), dim=8, scale=8 ** -0.5, biased=True, masked=False),
            lambda: gated_experts(core, of("L0f"), units=18, per_expert=1, scores=16, rule="sigmoid"),
            lambda: two_way_mamba(core, of("L1a")),
            lambda: cross_attention(core, of("L1x"), dim=8, scale=8 ** -0.5, biased=True, masked=True),
            lambda: normed_experts(core, of("L1f")),
            lambda: rwkv_mixer(core, of("L2a")),
            lambda: cross_attention(core, of("L2x"), dim=8, scale=8 ** -0.5, biased=False, masked=False),
            lambda: gated_experts(core, of("L2f"), units=16, per_expert=2, scores=8, rule="renormalised"),
            lambda: reshaped_attention(core, of("L3a")),
            lambda: cross_attention(core, of("L3x"), dim=64, scale=64 ** -0.5, biased=False, masked=True),
            lambda: gated_experts(core, of("L3f"), units=18, per_expert=2, scores=8, rule="softmax"),
        ]
        load_stage(core, d["x"], d["context"], d["ident"], d["ident16"])
        for n in range(*STAGES):
            with ExitStack() as stage:
                core.new_stage(stage)
                stages[n]()
                post_norm(core, out if n == STAGES[1] - 1 else None)


def kernel(**inputs):
    import concourse.bacc as _bacc
    from concourse.bass_utils import run_bass_kernel_spmd as _run

    nc = _bacc.Bacc("TRN2", target_bir_lowering=False, num_devices=1)
    arrays, d = {}, {}
    for name, a in layout(inputs).items():
        arrays[f"in_{name}"] = a
        d[name] = nc.dram_tensor(f"in_{name}", a.shape, mybir.dt.from_np(a.dtype), kind="ExternalInput").ap()
    out = nc.dram_tensor("out_x", (TOK, P), FP32, kind="ExternalOutput").ap()
    build(nc, d, out)
    r = _run(nc, [arrays], core_ids=[0])
    return r.results[0]["out_x"].reshape(B, S, P)
```

```python
import numpy as np

import concourse.bass as bass
from concourse import mybir
from contextlib import ExitStack

FP32 = mybir.dt.float32
BF16 = mybir.dt.bfloat16
I32 = mybir.dt.int32
ALU = mybir.AluOpType
ACT = mybir.ActivationFunctionType
AX = mybir.AxisListType

P = 128
B, S = 4, 256
TOK = B * S
NT = TOK // P
TPB = S // P
HALF = 512
HEADS = 16


class Signal:

    def __init__(self, ctx, nc, name):
        self.sem = ctx.enter_context(nc.semaphore(name))
        self.base = 0

    def __call__(self, n):
        return self.sem, n + self.base

    def past(self, total):
        self.base += total


class Steps:

    def __init__(self, signal, start=0):
        self.counter, self.count = signal, start

    def done(self, ins):
        self.count = self.count + 1
        ins.then_inc(self.counter.sem, 1)

    def last(self):
        return self.counter(self.count)


class Core:

    def __init__(self, ctx, nc):
        self.nc = nc

        def sb(name, shape, dt):
            return ctx.enter_context(nc.sbuf_tensor(name, shape, dt))

        self.x_tok = sb("x_tok", [P, NT, P], FP32)
        self.x_feat = sb("x_feat", [P, TOK], FP32)
        self.c_feat = sb("c_feat", [P, TOK], FP32)
        self.ident = sb("ident", [P, P], FP32)
        self.ident16 = sb("ident16", [P, P], BF16)
        self.ps = ctx.enter_context(nc.psum_tensor("ps", [P, 8, HALF], FP32))
        self.kept, self.number = {}, 0
        self.named = {}
        self.ctx = ctx

    def tensor(self, ctx, name, shape, dt):
        self.named[name] = self.named.get(name, 0) + 1
        return ctx.enter_context(self.nc.sbuf_tensor(f"{name}_{self.named[name]}", shape, dt))

    def counter(self, name, kept=False):
        if kept:
            if name not in self.kept:
                self.kept[name] = Signal(self.ctx, self.nc, name)
            return self.kept[name]
        signal = Signal(self.stage, self.nc, f"{name}_{self.number}")
        self.to_clear.append(signal.sem)
        return signal

    def new_stage(self, ctx):
        self.stage, self.number, self.to_clear = ctx, self.number + 1, []


class TokenNorm:

    STEPS = 2 * NT + 7

    def __init__(self, core, ctx, name, eps, steps, rooted):
        self.core, self.eps, self.steps, self.rooted = core, eps, steps, rooted
        self.stats = core.tensor(ctx, name + "_stats", [P, NT * 6], FP32)
        self.mv = core.tensor(ctx, name + "_mv", [P, NT, 2], FP32)
        self.var = core.tensor(ctx, name + "_var", [P, NT], FP32)
        self.rstd = core.tensor(ctx, name + "_rstd", [P, NT], FP32)
        self.root = core.tensor(ctx, name + "_root", [P, NT], FP32)

    def on_scalar(self, act):
        act.wait_ge(*self.steps(2 * NT + 1))
        act.activation(self.root[:, :], self.var[:, :], ACT.Sqrt).then_inc(self.rooted.sem, 1)

    def on_vector(self, dve):
        steps, stats, mv, var, rstd, root = self.steps, self.stats, self.mv, self.var, self.rstd, self.root
        for t in range(NT):
            dve.bn_stats(stats[:, 6 * t:6 * t + 6], self.core.x_tok[:, t, :]).then_inc(steps.sem, 1)
        for t in range(NT):
            dve.wait_ge(*steps(t + 1))
            dve.bn_aggr(mv[:, t, :], stats[:, 6 * t:6 * t + 6]).then_inc(steps.sem, 1)
        dve.wait_ge(*steps(2 * NT))
        dve.tensor_scalar(var[:, :], mv[:, :, 1], self.eps, None, ALU.add).then_inc(steps.sem, 1)
        dve.wait_ge(*self.rooted(1))
        dve.reciprocal(rstd[:, :], root[:, :]).then_inc(steps.sem, 1)
        dve.wait_ge(*steps(2 * NT + 2))
        dve.tensor_tensor(root[:, :], rstd[:, :], rstd[:, :], ALU.mult).then_inc(steps.sem, 1)
        dve.wait_ge(*steps(2 * NT + 3))
        dve.tensor_tensor(root[:, :], root[:, :], var[:, :], ALU.mult).then_inc(steps.sem, 1)
        dve.wait_ge(*steps(2 * NT + 4))
        dve.tensor_scalar(root[:, :], root[:, :], 1.0, -0.5, ALU.subtract, ALU.mult).then_inc(steps.sem, 1)
        dve.wait_ge(*steps(2 * NT + 5))
        dve.tensor_tensor(root[:, :], root[:, :], rstd[:, :], ALU.mult).then_inc(steps.sem, 1)
        dve.wait_ge(*steps(2 * NT + 6))
        dve.tensor_tensor(rstd[:, :], rstd[:, :], root[:, :], ALU.add).then_inc(steps.sem, 1)
        dve.wait_ge(*steps(2 * NT + 7))

    def normalise(self, dve, out, t):
        return dve.tensor_scalar(out, self.core.x_tok[:, t, :], self.mv[:, t, 0:1], self.rstd[:, t:t + 1],
                                 ALU.subtract, ALU.mult)


def load_stage(core, x, context, ident, ident16, next_loads):
    nc = core.nc
    loaded = core.counter("io_loaded", kept=True)
    turned = core.counter("io_turned", kept=True)
    copied = core.counter("io_copied", kept=True)
    with ExitStack() as ctx:
        c_tok = core.tensor(ctx, "c_tok", [P, NT, P], FP32)
        with nc.Block(no_gpsimd_drain=True) as block:
            @block.sync
            def _(sp):
                sp.dma_start(core.x_tok[:, :, :], x.rearrange("(t p) d -> p t d", p=P)).then_inc(loaded.sem, 16)
                sp.dma_start(c_tok[:, :, :], context.rearrange("(t p) d -> p t d", p=P)).then_inc(loaded.sem, 16)
                sp.dma_start(core.ident[:, :], ident).then_inc(loaded.sem, 16)
                sp.dma_start(core.ident16[:, :], ident16).then_inc(loaded.sem, 16)
                for dst, src, done in next_loads:
                    sp.dma_start(dst, src).then_inc(done.sem, 16)

            @block.tensor
            def _(pe):
                pe.wait_ge(*loaded(64))
                for n, src in enumerate((core.x_tok, c_tok)):
                    for t in range(NT):
                        pe.transpose(core.ps[:, 2 * n + t // 4, t % 4 * P:(t % 4 + 1) * P], src[:, t, :],
                                     core.ident[:, :]).then_inc(turned.sem, 1)

            @block.scalar
            def _(act):
                for n, dst in enumerate((core.x_feat, core.c_feat)):
                    act.wait_ge(*turned(NT * (n + 1)))
                    act.copy(dst[:, :].rearrange("p (k c) -> p k c", k=2),
                             core.ps[:, 2 * n:2 * n + 2, :]).then_inc(copied.sem, 1)


def post_norm(core, to_clear, next_loads, out=None):
    nc, x_tok, x_feat, ps = core.nc, core.x_tok, core.x_feat, core.ps
    steps = core.counter("norm_steps", kept=True)
    normed = core.counter("norm_tile_ready", kept=True)
    turned = core.counter("norm_tile_turned", kept=True)
    copied = core.counter("norm_copied", kept=True)
    rooted = core.counter("norm_rooted", kept=True)
    with ExitStack() as ctx:
        norm = TokenNorm(core, ctx, "norm", 1e-5, steps, rooted)
        with nc.Block(no_gpsimd_drain=True) as block:
            @block.gpsimd
            def _(pool):
                for sem in to_clear:
                    pool.sem_clear(sem)

            @block.vector
            def _(dve):
                norm.on_vector(dve)
                for t in range(NT):
                    norm.normalise(dve, x_tok[:, t, :], t).then_inc(normed.sem, 1)

            if out is None:
                @block.sync
                def _(sp):
                    for dst, src, done in next_loads:
                        sp.dma_start(dst, src).then_inc(done.sem, 16)

                @block.tensor
                def _(pe):
                    for t in range(NT):
                        pe.wait_ge(*normed(t + 1))
                        pe.transpose(ps[:, t // 4, t % 4 * P:(t % 4 + 1) * P], x_tok[:, t, :],
                                     core.ident[:, :]).then_inc(turned.sem, 1)

                @block.scalar
                def _(act):
                    norm.on_scalar(act)
                    for k in range(2):
                        act.wait_ge(*turned(4 * k + 4))
                        act.copy(x_feat[:, k * HALF:(k + 1) * HALF], ps[:, k, :]).then_inc(copied.sem, 1)
            else:
                @block.scalar
                def _(act):
                    norm.on_scalar(act)

                @block.sync
                def _(sp):
                    dst = out.rearrange("(t p) d -> p t d", p=P)
                    for k in range(2):
                        sp.wait_ge(*normed(4 * k + 4))
                        sp.dma_start(dst[:, 4 * k:4 * k + 4, :], x_tok[:, 4 * k:4 * k + 4, :]).then_inc(copied.sem, 16)
                    sp.wait_ge(*copied(32))
    for s, total in ((steps, TokenNorm.STEPS), (rooted, 1), (normed, NT), (turned, NT), (copied, 2)):
        s.past(total)


def causal_attention(core, w, dim):
    nc, ps = core.nc, core.ps
    HT = P // dim
    NQ = HEADS // HT
    HG = min(HT, 4)
    NG = HEADS // HG
    VD = HEADS * dim
    VW = min(HALF, VD)
    VB = VD // VW
    NC = VD // P
    DV = dim + 1
    MS = TPB
    KS = 4
    RING = 6
    PS_MAX, PS_MIX, PS_OUT = 4, 6, 7
    names = ("item_ready q_taken kv_taken k_laid k_cast max_ready max_taken high_ready shift_ready "
             "shift_turned shift_taken scores_ready probs_ready mixed_ready sums_inverted mixed_taken mixed_turned "
             "turned_taken y_ready y_taken consts mask_turned pe_held").split()
    sig = {n: core.counter("xa_" + n) for n in names}
    loaded = core.counter("xa_loaded")
    items = [(kind, n, half) for half in range(2) for n in range(NQ) for kind in "qk"]
    items += [("v", n, t) for t in range(NT) for n in range(VB)]

    def taken(i):
        q = sum(kind == "q" for kind, _, _ in items[:i])
        return 2 * q, i - q

    with ExitStack() as ctx:
        def sb(name, shape, dt=FP32):
            return core.tensor(ctx, "xa_" + name, shape, dt)

        wq_s, wk_s = sb("wq", [P, NQ * P]), sb("wk", [P, NQ * P])
        head_rows = sb("head_rows", [P, HT])
        wv_s, wo_s = sb("wv", [P, VD]), sb("wo", [P, NC * P])
        sel = sb("sel", [2 * HG, HG * P], BF16)
        qT, k_raw = sb("qT", [P, NQ, TOK]), sb("k_raw", [P, NQ, TOK])
        q16 = sb("q16", [P, NQ, TOK], BF16)
        kT, k16 = sb("kT", [P, KS, HG, S]), sb("k16", [P, 2, HG, S], BF16)
        v = sb("v", [P, NT * HEADS * DV])
        mx = sb("mx", [P, TPB, HG])
        shift = sb("shift", [P, TPB, 2, HG], BF16)
        shiftT = sb("shiftT", [2 * HG, S], BF16)
        probs = sb("probs", [P, 2, TPB, HG, S])
        rec = sb("rec", [P, 2, TPB, HG])
        mixed = sb("mixed", [P, TPB, VD])
        mixedT = sb("mixedT", [P, TPB, NC, P])
        mask_i, mask_f = sb("mask_i", [P, P], I32), sb("mask_f", [P, P])
        mask_q = sb("mask_q", [P, P], BF16)
        mask_k = sb("mask_k", [P, P], BF16)
        loads = [(wq_s[:, :], w["wq"]), (wk_s[:, :], w["wk"]), (wv_s[:, :], w["wv"]), (wo_s[:, :], w["wo"]),
                 (sel[:, :], w["sel"]), (head_rows[:, :], w["rows"]), (mask_i[:, :], w["mask"])]
        ALL = 16 * len(loads)
        v5 = v[:, :].rearrange("p (t h d) -> p t h d", t=NT, h=HEADS)
        turned_mask = ps[:, PS_OUT, :].bitcast(BF16)
        mixed_ps = ps[:, PS_MIX, 0:TPB * HG * DV].rearrange("p (q h d) -> p q h d", q=TPB, h=HG)

        def after(b, g, ahead):
            b, g = b + (g + ahead) // NG, (g + ahead) % NG
            return None if isinstance(b, int) and b >= B else (b, g, b * NG + g)

        yield [(dst, src, loaded) for dst, src in loads]
        with nc.Block(no_gpsimd_drain=True) as block:
            @block.gpsimd
            def _(pool):
                pool.memset(v5[:, :, :, dim:DV], 1.0).then_inc(sig["consts"].sem, 1)
                pool.wait_ge(*loaded(ALL))
                pool.tensor_copy(mask_f[:, :], mask_i[:, :]).then_inc(sig["consts"].sem, 1)

            @block.tensor
            def _(pe):
                pe.sem_inc(sig["max_ready"].sem, 3)
                pe.sem_inc(sig["mixed_ready"].sem, 2)
                pe.wait_ge(*loaded(ALL))
                for i, (kind, n, part) in enumerate(items):
                    if i >= RING:
                        q_count, kv_count = taken(i - RING + 1)
                        pe.wait_ge(*sig["q_taken"](q_count))
                        if kv_count:
                            pe.wait_ge(*sig["kv_taken"](kv_count))
                    if kind == "v":
                        ins = pe.matmul(ps[:, i % RING, 0:VW], core.c_feat[:, part * P:(part + 1) * P],
                                        wv_s[:, n * VW:(n + 1) * VW], start=True, stop=True)
                    else:
                        wt, src = (wq_s, core.x_feat) if kind == "q" else (wk_s, core.c_feat)
                        ins = pe.matmul(ps[:, i % RING, :], wt[:, n * P:(n + 1) * P],
                                        src[:, part * HALF:(part + 1) * HALF], start=True, stop=True)
                    ins.then_inc(sig["item_ready"].sem, 1)
                pe.wait_ge(*sig["consts"](3))
                pe.transpose(turned_mask[:, 0:P], mask_q[:, :], core.ident16[:, :]).then_inc(sig["mask_turned"].sem, 1)
                pe.wait_ge(*sig["consts"](4))
                pe.wait_ge(*sig["q_taken"](taken(len(items))[0]))
                pe.wait_ge(*sig["kv_taken"](taken(len(items))[1]))

                def max_scores(unit, t):
                    if unit is None:
                        return
                    b, g, u = unit
                    if t == 0:
                        pe.wait_ge(*sig["k_cast"](u + 1))
                    pe.wait_ge(*sig["max_taken"](u * TPB + t + 1))
                    pe.sem_inc(sig["pe_held"].sem, 1)
                    q_tile = q16[:, g * HG // HT, bass.ds(b * S + t * P, P)]
                    seen = (t + 1) * P
                    dst = ps[:, PS_MAX + t, 0:HG * seen].rearrange("p (h s) -> p h s", h=HG)
                    pe.matmul(dst, q_tile, k16[:, g % 2, :, 0:seen], start=True, stop=False)
                    last = pe.matmul(dst[:, :, t * P:seen], core.ident16[:, :],
                                     mask_q[:, :].unsqueeze(1).to_broadcast([P, HG, P]), start=False, stop=True)
                    last.then_inc(sig["max_ready"].sem, 1)

                def turn_shift(unit):
                    if unit is None:
                        return
                    b, g, u = unit
                    pe.wait_ge(*sig["shift_ready"](u + 1))
                    pe.wait_ge(*sig["shift_taken"](u + 1))
                    if g == 2:
                        pe.wait_ge(*sig["y_taken"](b + 1))
                    for t in range(TPB):
                        last = pe.transpose(ps[0:2 * HG, PS_OUT, :].bitcast(BF16)[:, t * P:(t + 1) * P],
                                            shift[:, t, :, :].rearrange("p a h -> p (a h)"), core.ident16[:, :])
                    last.then_inc(sig["shift_turned"].sem, 1)

                def scores(unit, t):
                    if unit is None:
                        return
                    b, g, u = unit
                    pe.wait_ge(*sig["probs_ready"](u * TPB + t + 1))
                    if t == 0:
                        pe.wait_ge(*sig["shift_taken"](u + 2))
                    pe.sem_inc(sig["pe_held"].sem, 1)
                    queries = qT[:, g * HG // HT, bass.ds(b * S + t * P, S - t * P)]
                    for h in range(HG):
                        dst = ps[:, t, h * S + t * P:(h + 1) * S]
                        pe.matmul(dst, kT[:, g % KS, h, t * P:(t + 1) * P], queries, start=True, stop=False)
                        pe.matmul(dst[:, 0:P], core.ident16[:, :], mask_k[:, :], start=False, stop=False)
                        last = pe.matmul(dst, sel[:, h * P:(h + 1) * P], shiftT[:, t * P:S], start=False, stop=True)
                    last.then_inc(sig["scores_ready"].sem, 1)

                def mix(unit):
                    b, g, u = unit
                    pe.wait_ge(*sig["probs_ready"](u * TPB + 2 * TPB))
                    pe.wait_ge(*sig["mixed_taken"](u + 1))
                    pe.sem_inc(sig["pe_held"].sem, 1)
                    values = v[:, bass.ds(b * (TPB * HEADS * DV), TPB * HEADS * DV)]
                    for q in range(TPB):
                        for h in range(HG):
                            for t in range(q + 1):
                                o = (t * HEADS + g * HG + h) * DV
                                last = pe.matmul(mixed_ps[:, q, h, :], probs[:, g % 2, t, h, q * P:(q + 1) * P],
                                                 values[:, o:o + DV],
                                                 start=t == 0, stop=t == q)
                    last.then_inc(sig["mixed_ready"].sem, 1)

                def turn_mixed(b, q):
                    if q == 0:
                        pe.wait_ge(*sig["mixed_taken"](b * NG + NG + 1))
                    else:
                        pe.wait_ge(*sig["turned_taken"](TPB * b + q))
                    for c in range(NC):
                        bank, o = 2 + c // 4, c % 4 * P
                        last = pe.transpose(ps[:, bank, o:o + P], mixed[:, q, c * P:(c + 1) * P], core.ident[:, :])
                    last.then_inc(sig["mixed_turned"].sem, 1)

                def output(b):
                    pe.wait_ge(*sig["turned_taken"](TPB * b + TPB))
                    for q in range(TPB):
                        for c in range(NC):
                            last = pe.matmul(ps[:, PS_OUT, q * P:(q + 1) * P], mixedT[:, q, c, :],
                                             wo_s[:, c * P:(c + 1) * P], start=c == 0, stop=c == NC - 1)
                    last.then_inc(sig["y_ready"].sem, 1)

                def step(b, g):
                    turn_shift(after(b, g, 1))
                    for t in range(TPB):
                        max_scores(after(b, g, 2), t)
                        scores(after(b, g, 1), t)
                        if g == NG:
                            turn_mixed(b, t)
                    mix(after(b, g, 0))
                    if g == NG:
                        output(b)

                for t in range(TPB):
                    max_scores((0, 0, 0), t)
                max_scores((0, 1, 1), 0)
                turn_shift((0, 0, 0))
                max_scores((0, 1, 1), 1)
                for t in range(TPB):
                    scores((0, 0, 0), t)
                step(0, 0)
                with pe.Fori(0, B - 1) as b:
                    for g in range(1, NG + 1):
                        step(b, g)
                for g in range(1, NG):
                    step(B - 1, g)
                for q in range(TPB):
                    turn_mixed(B - 1, q)
                output(B - 1)

            @block.scalar
            def _(act):
                act.sem_inc(sig["probs_ready"].sem, TPB)
                act.wait_ge(*loaded(ALL))
                for i, (kind, n, half) in enumerate(items):
                    if kind == "q":
                        act.wait_ge(*sig["item_ready"](i + 1))
                        o = half * HALF
                        for dst in (qT[:, n, o:o + HALF], q16[:, n, o:o + HALF]):
                            ins = act.copy(dst, ps[:, i % RING, :])
                            ins.then_inc(sig["q_taken"].sem, 1)

                def cast_keys(unit):
                    if unit is None:
                        return
                    b, g, u = unit
                    act.wait_ge(*sig["k_laid"](u + 1))
                    act.wait_ge(*sig["max_ready"](u * TPB + 1))
                    act.copy(k16[:, g % 2, :, :], kT[:, g % KS, :, :]).then_inc(sig["k_cast"].sem, 1)

                def exps(unit, t):
                    if unit is None:
                        return
                    b, g, u = unit
                    act.wait_ge(*sig["scores_ready"](u * TPB + t + 1))
                    act.wait_ge(*sig["mixed_ready"](u + 1))
                    act.activation(probs[:, g % 2, t, :, t * P:S],
                                   ps[:, t, :].rearrange("p (h s) -> p h s", h=HG)[:, :, t * P:S], ACT.Exp,
                                   scale=dim ** -0.5).then_inc(sig["probs_ready"].sem, 1)

                def take_turned(b, q):
                    act.wait_ge(*sig["mixed_turned"](TPB * b + q + 1))
                    act.copy(mixedT[:, q, :, :].rearrange("p c f -> p (c f)").rearrange("p (n c) -> p n c", n=NC // 4),
                             ps[:, 2:2 + NC // 4, :]).then_inc(sig["turned_taken"].sem, 1)

                def step(b, g):
                    for t in range(TPB):
                        exps(after(b, g, 1), t)
                        if g == NG:
                            take_turned(b, t)
                        if t == 0:
                            cast_keys(after(b, g, 3))

                cast_keys((0, 0, 0))
                cast_keys((0, 1, 1))
                for t in range(TPB):
                    exps((0, 0, 0), t)
                cast_keys((0, 2, 2))
                step(0, 0)
                with act.Fori(0, B - 1) as b:
                    for g in range(1, NG + 1):
                        step(b, g)
                for g in range(1, NG):
                    step(B - 1, g)
                for q in range(TPB):
                    take_turned(B - 1, q)

            @block.vector
            def _(dve):
                dve.sem_inc(sig["max_taken"].sem, MS)
                dve.sem_inc(sig["shift_taken"].sem, 1)
                dve.sem_inc(sig["mixed_taken"].sem, 1)
                dve.sem_inc(sig["y_taken"].sem, 1)
                dve.wait_ge(*loaded(ALL))
                dve.wait_ge(*sig["consts"](2))
                dve.tensor_scalar(mask_q[:, :], mask_f[:, :], 0.0, -1e30, ALU.is_equal, ALU.mult)\
                   .then_inc(sig["consts"].sem, 1)
                dve.wait_ge(*sig["consts"](1))
                for i, (kind, n, part) in enumerate(items):
                    if kind == "q":
                        continue
                    dve.wait_ge(*sig["item_ready"](i + 1))
                    if kind == "k":
                        o = part * HALF
                        ins = dve.tensor_copy(k_raw[:, n, o:o + HALF], ps[:, i % RING, :])
                    else:
                        heads = VW // dim
                        dst = v5[:, part, n * heads:(n + 1) * heads, 0:dim]
                        src = ps[:, i % RING, 0:VW].rearrange("p (h d) -> p h d", d=dim)
                        ins = dve.tensor_copy(dst, src)
                    ins.then_inc(sig["kv_taken"].sem, 1)
                dve.wait_ge(*sig["mask_turned"](1))
                dve.tensor_copy(mask_k[:, :], turned_mask[:, 0:P]).then_inc(sig["consts"].sem, 1)
                dve.wait_ge(*sig["kv_taken"](taken(len(items))[1]))

                def lay_keys(unit):
                    if unit is None:
                        return
                    b, g, u = unit
                    if not isinstance(u, int) or u >= KS:
                        dve.wait_ge(*sig["scores_ready"]((u - KS) * TPB + TPB))
                    n, h0 = g * HG // HT, g * HG % HT
                    src = k_raw[:, n, bass.ds(b * S, S)].unsqueeze(1).to_broadcast([P, HG, S])
                    rows = head_rows[:, h0:h0 + HG].unsqueeze(2).to_broadcast([P, HG, S])
                    dve.tensor_tensor(kT[:, g % KS, :, :], src, rows, ALU.mult).then_inc(sig["k_laid"].sem, 1)

                def reduce(unit, t):
                    if unit is None:
                        return
                    b, g, u = unit
                    if t == 0 and (not isinstance(u, int) or u > 0):
                        dve.wait_ge(*sig["shift_ready"](u))
                    dve.wait_ge(*sig["max_ready"](u * TPB + t + 4))
                    dve.tensor_reduce(mx[:, t, :], ps[:, PS_MAX + t, 0:HG * (t + 1) * P]
                                      .rearrange("p (h s) -> p h s", h=HG), AX.X, ALU.max)\
                       .then_inc(sig["max_taken"].sem, 1)

                def make_shift(unit):
                    if unit is None:
                        return
                    b, g, u = unit
                    dve.wait_ge(*sig["max_taken"](u * TPB + TPB + MS))
                    dve.tensor_scalar(shift[:, :, 0, :], mx[:, :, :], -1.0, None, ALU.mult)\
                       .then_inc(sig["high_ready"].sem, 1)
                    dve.wait_ge(*sig["high_ready"](u + 1))
                    dve.scalar_tensor_tensor(shift[:, :, 1, :], mx[:, :, :], -1.0, shift[:, :, 0, :],
                                             ALU.mult, ALU.subtract).then_inc(sig["shift_ready"].sem, 1)

                def take_shift(unit):
                    if unit is None:
                        return
                    b, g, u = unit
                    dve.wait_ge(*sig["shift_turned"](u + 1))
                    dve.tensor_copy(shiftT[:, :], ps[0:2 * HG, PS_OUT, :].bitcast(BF16)[:, 0:S])\
                       .then_inc(sig["shift_taken"].sem, 1)

                def take_mixed(unit):
                    b, g, u = unit
                    dve.wait_ge(*sig["mixed_ready"](u + 3))
                    dve.wait_ge(*sig["mixed_taken"](u + 1))
                    dve.reciprocal(rec[:, g % 2, :, :], mixed_ps[:, :, :, dim]).then_inc(sig["sums_inverted"].sem, 1)
                    dve.wait_ge(*sig["sums_inverted"](u + 1))
                    dve.tensor_tensor(mixed[:, :, g * HG * dim:(g + 1) * HG * dim].rearrange("p q (h d) -> p q h d", h=HG),
                                      mixed_ps[:, :, :, 0:dim],
                                      rec[:, g % 2, :, :].unsqueeze(3).to_broadcast([P, TPB, HG, dim]),
                                      ALU.mult).then_inc(sig["mixed_taken"].sem, 1)

                def add_output(b):
                    dve.wait_ge(*sig["y_ready"](b + 1))
                    xs = core.x_tok[:, bass.ds(b * TPB, TPB), :]
                    dve.tensor_tensor(xs, xs, ps[:, PS_OUT, 0:TPB * P].rearrange("p (q f) -> p q f", q=TPB),
                                      ALU.add).then_inc(sig["y_taken"].sem, 1)

                def step(b, g):
                    if g == NG:
                        add_output(b)
                    take_shift(after(b, g, 2))
                    take_mixed(after(b, g, 0))
                    reduce(after(b, g, 3), 0)
                    lay_keys(after(b, g, 4))
                    reduce(after(b, g, 3), 1)
                    make_shift(after(b, g, 3))

                lay_keys((0, 0, 0))
                lay_keys((0, 1, 1))
                for u in range(3):
                    reduce((0, u, u), 0)
                    reduce((0, u, u), 1)
                    make_shift((0, u, u))
                    if u == 0:
                        lay_keys((0, 2, 2))
                        lay_keys((0, 3, 3))
                    if u < 2:
                        take_shift((0, u, u))
                step(0, 0)
                with dve.Fori(0, B - 1) as b:
                    for g in range(1, NG + 1):
                        step(b, g)
                for g in range(1, NG):
                    step(B - 1, g)
                add_output(B - 1)


def stacked_attention(core, w, biased, masked):
    nc, ps = core.nc, core.ps
    DIM, SCALE = 8, 8 ** -0.5
    HG = 4
    NG = HEADS // HG
    PAIRS = HEADS // 2
    NB = HG * S // HALF
    RING = 6
    WIDE = 2 * HG * DIM
    STEP = WIDE + DIM
    PS_MAX, PS_MIX, PS_TURN = 4, 6, 7
    names = ("item_ready q_taken kv_taken bias_added max_ready max_taken high_ready shift_ready shift_turned "
             "shift_taken scores_ready probs_ready mixed_ready mixed_taken sums_inverted mixed_normed values_laid "
             "y_ready consts mask_turned held high_cast rest_ready middle_ready low_ready rows_ready rows_by_act "
             "rows_by_dve").split()
    sig = {n: core.counter("sa_" + n) for n in names}
    loaded, route_loaded = core.counter("sa_loaded"), core.counter("sa_route_loaded")
    items = [("q", 0), ("k", 0), ("q", 1), ("k", 1), ("v", 0), ("v", 1)]
    fills = [(side, pair, half) for side in range(2) for pair in range(PAIRS) for half in range(2)]

    with ExitStack() as ctx:
        def sb(name, shape, dt=FP32):
            return core.tensor(ctx, "sa_" + name, shape, dt)

        wq_s, wk_s, wv_s, wo_s = sb("wq", [P, P]), sb("wk", [P, P]), sb("wv", [P, P]), sb("wo", [P, P])
        head_rows = sb("head_rows", [P, 2])
        sel = sb("sel", [2 * HG, HG * P], BF16)
        full = sb("full", [P, 2, TOK])
        route = sb("route", [P, 2, PAIRS, 3, P], BF16)
        parts = sb("parts", [P, 2, 3, TOK], BF16)
        rest = sb("rest", [P, 2, TOK])
        q_rows = sb("q_rows", [P, PAIRS, TOK], BF16)
        k_rows = sb("k_rows", [P, B * HEADS * S], BF16)
        v = sb("v", [P, NT * P])
        blocks = sb("blocks", [P, 2 * TPB * HG * STEP])
        mx = sb("mx", [P, TPB, HG])
        shift = sb("shift", [P, TPB, 2, HG], BF16)
        shiftT = sb("shiftT", [2 * HG, S], BF16)
        probs = sb("probs", [P, 2, TPB, HG, S])
        mixed = sb("mixed", [WIDE, 2, S])
        rec = sb("rec", [WIDE // 2, S])
        mixedT = sb("mixedT", [P, TOK])
        if biased:
            bq, bk = sb("bq", [P, 1]), sb("bk", [P, 1])
            bv, bo = sb("bv", [P, P]), sb("bo", [P, P])
        if masked:
            mask_i = sb("mask_i", [P, TPB, S], I32)
            mask_f = sb("mask_f", [P, TPB, S])
            mask_q = sb("mask_q", [P, TPB, S], BF16)
            mask_k = sb("mask_k", [P, TPB, S], BF16)
        loads = [(wq_s[:, :], w["wq"]), (wk_s[:, :], w["wk"]), (wv_s[:, :], w["wv"]), (wo_s[:, :], w["wo"]),
                 (sel[:, :], w["sel"]), (head_rows[:, :], w["rows"])]
        if biased:
            loads += [(bq[:, :], w["bq"]), (bk[:, :], w["bk"]), (bv[:, :], w["bv"].partition_broadcast(P)),
                      (bo[:, :], w["bo"].partition_broadcast(P))]
        if masked:
            loads += [(mask_i[:, :, :], w["mask"].rearrange("(t p) k -> p t k", p=P))]
        ALL = 16 * len(loads)
        k_rows4 = k_rows[:, :].rearrange("p (b h s) -> p b h s", b=B, h=HEADS)
        blocks5 = blocks[:, :].rearrange("p (u t h e) -> p u t h e", u=2, t=TPB, h=HG)
        turned_mask = ps[:, PS_TURN, :].bitcast(BF16)

        def after(b, g, ahead):
            b, g = b + (g + ahead) // NG, (g + ahead) % NG
            return None if isinstance(b, int) and b >= B else (b, g, b * NG + g)

        yield [(dst, src, loaded) for dst, src in loads] + [(route[:, :, :, :, :], w["route"], route_loaded)]
        with nc.Block(no_gpsimd_drain=True) as block:
            @block.gpsimd
            def _(pool):
                pool.memset(blocks[:, :], 0.0).then_inc(sig["consts"].sem, 1)
                pool.wait_ge(*sig["consts"](1))
                pool.memset(blocks5[:, :, :, :, WIDE // 2:WIDE // 2 + DIM], 1.0).then_inc(sig["consts"].sem, 1)
                if masked:
                    pool.wait_ge(*loaded(ALL))
                    pool.tensor_copy(mask_f[:, :, :], mask_i[:, :, :]).then_inc(sig["consts"].sem, 1)
                pool.wait_ge(*sig["consts"](2))
                pool.wait_ge(*sig["kv_taken"](4))

                def lay_values(unit):
                    if unit is None:
                        return
                    b, g, u = unit
                    pool.wait_ge(*sig["mixed_ready"](u + 1))
                    pool.sem_inc(sig["held"].sem, 1)
                    batch = v[:, bass.ds(b * (TPB * P), TPB * P)].rearrange("p (t g h d) -> p t g h d", t=TPB, g=NG, h=HG)
                    pool.tensor_copy(blocks5[:, g % 2, :, :, 0:DIM], batch[:, :, g, :, :])\
                        .then_inc(sig["values_laid"].sem, 1)

                lay_values((0, 0, 0))
                lay_values((0, 1, 1))
                with pool.Fori(0, B - 1) as b:
                    for g in range(1, NG + 1):
                        lay_values(after(b, g, 1))
                for g in range(1, NG):
                    lay_values(after(B - 1, g, 1))

            @block.tensor
            def _(pe):
                pe.sem_inc(sig["mixed_ready"].sem, 2)
                pe.wait_ge(*loaded(ALL))
                for i, (kind, half) in enumerate(items):
                    if kind == "v":
                        for t in range(4):
                            ins = pe.matmul(ps[:, i, t * P:(t + 1) * P],
                                            core.c_feat[:, (4 * half + t) * P:(4 * half + t + 1) * P],
                                            wv_s[:, :], start=True, stop=True)
                    else:
                        wt, src = (wq_s, core.x_feat) if kind == "q" else (wk_s, core.c_feat)
                        ins = pe.matmul(ps[:, i, :], wt[:, :], src[:, half * HALF:(half + 1) * HALF], start=True, stop=True)
                    ins.then_inc(sig["item_ready"].sem, 1)
                if masked:
                    pe.wait_ge(*sig["consts"](4))
                    for t in range(TPB):
                        for k in range(TPB):
                            pe.transpose(turned_mask[:, (t * TPB + k) * P:(t * TPB + k + 1) * P],
                                         mask_q[:, t, k * P:(k + 1) * P],
                                         core.ident16[:, :]).then_inc(sig["mask_turned"].sem, 1)
                pe.wait_ge(*sig["q_taken"](4))
                pe.wait_ge(*sig["kv_taken"](2))
                pe.wait_ge(*route_loaded(16))
                for i, (side, pair, half) in enumerate(fills):
                    if i % (2 * PAIRS) == 0:
                        pe.wait_ge(*sig["low_ready"](side + 1))
                    if i == items.index(("v", 0)):
                        pe.wait_ge(*sig["kv_taken"](4))
                    if i >= RING:
                        pe.wait_ge(*sig["rows_by_dve" if i % 2 else "rows_by_act"]((i - RING) // 2 + 1))
                    for part in range(3):
                        last = pe.matmul(ps[:, i % RING, :], route[:, side, pair, part, :],
                                         parts[:, side, part, half * HALF:(half + 1) * HALF],
                                         start=part == 0, stop=part == 2)
                    last.then_inc(sig["rows_ready"].sem, 1)
                pe.wait_ge(*sig["rows_by_act"](len(fills) // 2))
                pe.wait_ge(*sig["rows_by_dve"](len(fills) // 2))
                if masked:
                    pe.wait_ge(*sig["consts"](5))

                def max_scores(unit, t):
                    if unit is None:
                        return
                    b, g, u = unit
                    pe.wait_ge(*sig["max_taken"](u * TPB + t + 1))
                    pe.sem_inc(sig["held"].sem, 1)
                    keys = k_rows[:, bass.ds(b * (HEADS * S) + g * HG * S, HG * S)]
                    for n in range(NB):
                        dst = ps[:, PS_MAX + n, :]
                        last = pe.matmul(dst, q_rows[:, g * HG // 2 + n, bass.ds(b * S + t * P, P)],
                                         keys[:, 2 * n * S:2 * (n + 1) * S], start=True, stop=not masked)
                        if masked:
                            last = pe.matmul(dst.rearrange("p (h s) -> p h s", h=2), core.ident16[:, :],
                                             mask_q[:, t, :].unsqueeze(1).to_broadcast([P, 2, S]),
                                             start=False, stop=True)
                    last.then_inc(sig["max_ready"].sem, 1)

                def turn_shift(unit):
                    if unit is None:
                        return
                    b, g, u = unit
                    pe.wait_ge(*sig["shift_ready"](u + 1))
                    pe.wait_ge(*sig["shift_taken"](u + 1))
                    for t in range(TPB):
                        last = pe.transpose(ps[0:2 * HG, PS_TURN, :].bitcast(BF16)[:, t * P:(t + 1) * P],
                                            shift[:, t, :, :].rearrange("p a h -> p (a h)"), core.ident16[:, :])
                    last.then_inc(sig["shift_turned"].sem, 1)

                def scores(unit, t):
                    if unit is None:
                        return
                    b, g, u = unit
                    pe.wait_ge(*sig["probs_ready"](u * TPB + t + 1))
                    if t == 0:
                        pe.wait_ge(*sig["shift_taken"](u + 2))
                    pe.sem_inc(sig["held"].sem, 1)
                    keys = k_rows[:, bass.ds(b * (HEADS * S) + g * HG * S, HG * S)]
                    for h in range(HG):
                        dst = ps[:, NB * t + h // 2, h % 2 * S:(h % 2 + 1) * S]
                        if h % 2 == 0:
                            queries = q_rows[:, (g * HG + h) // 2, bass.ds(b * S, S)]
                        pe.matmul(dst, keys[:, h * S + t * P:h * S + (t + 1) * P], queries, start=True, stop=False)
                        if masked:
                            pe.matmul(dst, core.ident16[:, :], mask_k[:, t, :], start=False, stop=False)
                        last = pe.matmul(dst, sel[:, h * P:(h + 1) * P], shiftT[:, :], start=False, stop=True)
                    last.then_inc(sig["scores_ready"].sem, 1)

                def mix(unit):
                    b, g, u = unit
                    pe.wait_ge(*sig["probs_ready"](u * TPB + 2 * TPB))
                    pe.wait_ge(*sig["mixed_taken"](u + 1))
                    pe.wait_ge(*sig["values_laid"](u + 1))
                    for h in range(HG):
                        for t in range(TPB):
                            o = (g % 2 * TPB + t) * HG * STEP + h * WIDE
                            last = pe.matmul(ps[0:WIDE, PS_MIX, 0:S], blocks[:, o:o + WIDE], probs[:, g % 2, t, h, :],
                                             start=h == 0 and t == 0, stop=h == HG - 1 and t == TPB - 1)
                    last.then_inc(sig["mixed_ready"].sem, 1)

                def step(b, g):
                    turn_shift(after(b, g, 1))
                    for t in range(TPB):
                        max_scores(after(b, g, 2), t)
                        scores(after(b, g, 1), t)
                    mix(after(b, g, 0))

                for t in range(TPB):
                    max_scores((0, 0, 0), t)
                max_scores((0, 1, 1), 0)
                turn_shift((0, 0, 0))
                max_scores((0, 1, 1), 1)
                for t in range(TPB):
                    scores((0, 0, 0), t)
                step(0, 0)
                with pe.Fori(0, B - 1) as b:
                    for g in range(1, NG + 1):
                        step(b, g)
                for g in range(1, NG):
                    step(B - 1, g)
                pe.wait_ge(*sig["mixed_normed"](B * NG + 1))
                for t in range(NT):
                    pe.matmul(ps[:, t // 4, t % 4 * P:(t % 4 + 1) * P], mixedT[:, t * P:(t + 1) * P], wo_s[:, :],
                              start=True, stop=True).then_inc(sig["y_ready"].sem, 1)

            @block.scalar
            def _(act):
                act.sem_inc(sig["probs_ready"].sem, TPB)
                act.sem_inc(sig["mixed_taken"].sem, 1)
                act.wait_ge(*loaded(ALL))
                for i, (kind, half) in enumerate(items):
                    if kind == "q":
                        act.wait_ge(*sig["item_ready"](i + 1))
                        o = half * HALF
                        for dst in (full[:, 0, o:o + HALF], parts[:, 0, 0, o:o + HALF]):
                            if biased:
                                ins = act.activation(dst, ps[:, i, :], ACT.Identity, bias=bq[:, :])
                            else:
                                ins = act.copy(dst, ps[:, i, :])
                            ins.then_inc(sig["q_taken"].sem, 1)
                act.wait_ge(*sig["kv_taken"](2))
                act.copy(parts[:, 1, 0, :], full[:, 1, :]).then_inc(sig["high_cast"].sem, 1)
                for side in range(2):
                    act.wait_ge(*sig["rest_ready"](side + 1))
                    act.copy(parts[:, side, 1, :], rest[:, side, :]).then_inc(sig["middle_ready"].sem, 1)
                for i in range(0, len(fills), 2):
                    side, pair, half = fills[i]
                    act.wait_ge(*sig["rows_ready"](i + 1))
                    if side == 0:
                        ins = act.copy(q_rows[:, pair, half * HALF:(half + 1) * HALF], ps[:, i % RING, :])
                    else:
                        for a in range(2):
                            ins = act.activation(k_rows4[:, 2 * half:2 * half + 2, 2 * pair + a, :],
                                                 ps[:, i % RING, :].rearrange("p (b s) -> p b s", b=2),
                                                 ACT.Identity, scale=head_rows[:, a:a + 1])
                    ins.then_inc(sig["rows_by_act"].sem, 1)

                def exps(unit, t):
                    if unit is None:
                        return
                    b, g, u = unit
                    act.wait_ge(*sig["scores_ready"](u * TPB + t + 1))
                    act.wait_ge(*sig["mixed_ready"](u + 1))
                    act.activation(probs[:, g % 2, t, :, :].rearrange("p h s -> p (h s)")
                                   .rearrange("p (n c) -> p n c", n=NB),
                                   ps[:, NB * t:NB * t + NB, :], ACT.Exp,
                                   scale=SCALE).then_inc(sig["probs_ready"].sem, 1)

                def take_mixed(unit):
                    b, g, u = unit
                    act.wait_ge(*sig["mixed_ready"](u + 3))
                    act.wait_ge(*sig["mixed_normed"](u + 1))
                    act.copy(mixed[:, g % 2, :], ps[0:WIDE, PS_MIX, 0:S]).then_inc(sig["mixed_taken"].sem, 1)

                def step(b, g):
                    for t in range(TPB):
                        exps(after(b, g, 1), t)
                    take_mixed(after(b, g, 0))

                for t in range(TPB):
                    exps((0, 0, 0), t)
                step(0, 0)
                with act.Fori(0, B - 1) as b:
                    for g in range(1, NG + 1):
                        step(b, g)
                for g in range(1, NG):
                    step(B - 1, g)

            @block.vector
            def _(dve):
                dve.sem_inc(sig["max_taken"].sem, 1)
                dve.sem_inc(sig["shift_taken"].sem, 1)
                dve.sem_inc(sig["mixed_normed"].sem, 1)
                dve.wait_ge(*loaded(ALL))
                if biased:
                    dve.tensor_tensor(core.x_tok[:, :, :], core.x_tok[:, :, :],
                                      bo[:, :].unsqueeze(1).to_broadcast([P, NT, P]), ALU.add)\
                       .then_inc(sig["bias_added"].sem, 1)
                if masked:
                    dve.wait_ge(*sig["consts"](3))
                    dve.tensor_scalar(mask_q[:, :, :], mask_f[:, :, :], 0.0, -1e30, ALU.is_equal, ALU.mult)\
                       .then_inc(sig["consts"].sem, 1)
                for half, i in enumerate((1, 3)):
                    dve.wait_ge(*sig["item_ready"](i + 1))
                    dst = full[:, 1, half * HALF:(half + 1) * HALF]
                    if biased:
                        ins = dve.tensor_scalar(dst, ps[:, i, :], bk[:, :], None, ALU.add)
                    else:
                        ins = dve.tensor_copy(dst, ps[:, i, :])
                    ins.then_inc(sig["kv_taken"].sem, 1)
                dve.wait_ge(*sig["q_taken"](4))
                dve.tensor_tensor(rest[:, 0, :], full[:, 0, :], parts[:, 0, 0, :], ALU.subtract)\
                   .then_inc(sig["rest_ready"].sem, 1)
                dve.wait_ge(*sig["high_cast"](1))
                dve.tensor_tensor(rest[:, 1, :], full[:, 1, :], parts[:, 1, 0, :], ALU.subtract)\
                   .then_inc(sig["rest_ready"].sem, 1)
                for side in range(2):
                    dve.wait_ge(*sig["middle_ready"](side + 1))
                    dve.wait_ge(*sig["rest_ready"](side + 1))
                    dve.tensor_tensor(parts[:, side, 2, :], rest[:, side, :], parts[:, side, 1, :], ALU.subtract)\
                       .then_inc(sig["low_ready"].sem, 1)
                for half, i in enumerate((4, 5)):
                    dve.wait_ge(*sig["item_ready"](i + 1))
                    dst = v[:, half * HALF:(half + 1) * HALF]
                    if biased:
                        ins = dve.tensor_tensor(dst.rearrange("p (t f) -> p t f", t=4),
                                                ps[:, i, :].rearrange("p (t f) -> p t f", t=4),
                                                bv[:, :].unsqueeze(1).to_broadcast([P, 4, P]), ALU.add)
                    else:
                        ins = dve.tensor_copy(dst, ps[:, i, :])
                    ins.then_inc(sig["kv_taken"].sem, 1)
                for i in range(1, len(fills), 2):
                    side, pair, half = fills[i]
                    dve.wait_ge(*sig["rows_ready"](i + 1))
                    if side == 0:
                        ins = dve.tensor_copy(q_rows[:, pair, half * HALF:(half + 1) * HALF], ps[:, i % RING, :])
                    else:
                        for a in range(2):
                            ins = dve.tensor_scalar(k_rows4[:, 2 * half:2 * half + 2, 2 * pair + a, :],
                                                    ps[:, i % RING, :].rearrange("p (b s) -> p b s", b=2),
                                                    head_rows[:, a:a + 1], None, ALU.mult)
                    ins.then_inc(sig["rows_by_dve"].sem, 1)
                if masked:
                    dve.wait_ge(*sig["mask_turned"](TPB * TPB))
                    dve.tensor_copy(mask_k[:, :, :].rearrange("p k (t q) -> p k t q", t=TPB),
                                    turned_mask[:, 0:TPB * TPB * P].rearrange("p (t k q) -> p k t q", t=TPB, k=TPB))\
                       .then_inc(sig["consts"].sem, 1)
                def reduce(unit):
                    if unit is None:
                        return
                    b, g, u = unit
                    if not isinstance(u, int) or u > 0:
                        dve.wait_ge(*sig["shift_ready"](u))
                    for t in range(TPB):
                        dve.wait_ge(*sig["max_ready"](u * TPB + t + 1))
                        dve.tensor_reduce(mx[:, t, :], ps[:, PS_MAX:PS_MAX + NB, :].rearrange("p n (h s) -> p (n h) s", s=S), AX.X, ALU.max)\
                           .then_inc(sig["max_taken"].sem, 1)
                    dve.wait_ge(*sig["max_taken"](u * TPB + TPB + 1))
                    dve.tensor_scalar(shift[:, :, 0, :], mx[:, :, :], -1.0, None, ALU.mult)\
                       .then_inc(sig["high_ready"].sem, 1)
                    dve.wait_ge(*sig["high_ready"](u + 1))
                    dve.scalar_tensor_tensor(shift[:, :, 1, :], mx[:, :, :], -1.0, shift[:, :, 0, :],
                                             ALU.mult, ALU.subtract).then_inc(sig["shift_ready"].sem, 1)

                def take_shift(unit):
                    if unit is None:
                        return
                    b, g, u = unit
                    dve.wait_ge(*sig["shift_turned"](u + 1))
                    dve.tensor_copy(shiftT[:, :], ps[0:2 * HG, PS_TURN, :].bitcast(BF16)[:, 0:S])\
                       .then_inc(sig["shift_taken"].sem, 1)

                def normalise(unit):
                    b, g, u = unit
                    dve.wait_ge(*sig["mixed_taken"](u + 2))
                    dve.wait_ge(*sig["mixed_normed"](u + 1))
                    dve.reciprocal(rec[:, :], mixed[WIDE // 2:WIDE, g % 2, :]).then_inc(sig["sums_inverted"].sem, 1)
                    dve.wait_ge(*sig["sums_inverted"](u + 1))
                    dve.tensor_tensor(mixedT[g * HG * DIM:(g + 1) * HG * DIM, bass.ds(b * S, S)],
                                      mixed[0:WIDE // 2, g % 2, :], rec[:, :], ALU.mult)\
                       .then_inc(sig["mixed_normed"].sem, 1)

                def step(b, g):
                    take_shift(after(b, g, 2))
                    reduce(after(b, g, 3))
                    normalise(after(b, g, 0))

                reduce((0, 0, 0))
                take_shift((0, 0, 0))
                reduce((0, 1, 1))
                take_shift((0, 1, 1))
                reduce((0, 2, 2))
                step(0, 0)
                with dve.Fori(0, B - 1) as b:
                    for g in range(1, NG + 1):
                        step(b, g)
                for g in range(1, NG):
                    step(B - 1, g)
                if biased:
                    dve.wait_ge(*sig["bias_added"](1))
                for half in range(2):
                    dve.wait_ge(*sig["y_ready"](4 * half + 4))
                    xs = core.x_tok[:, 4 * half:4 * half + 4, :]
                    dve.tensor_tensor(xs, xs, ps[:, half, :].rearrange("p (t f) -> p t f", t=4), ALU.add)




ROUTE_SIGNALS = "logits_ready steps exps_ready parts_ready parts_turned parts_taken zeroed".split()


class Routing:

    def __init__(self, core, sb, sig, scores, NE, rule, bank=0):
        self.core, self.sig, self.scores, self.NE, self.rule = core, sig, scores, NE, rule
        self.K3, self.bank = 3 * NE, bank
        self.router = sb("router", [P, scores])
        self.sel = sb("sel", [P, NE * P], BF16)
        self.top = sb("top", [P, NT, 8])
        self.lg = sb("lg", [P, NT, scores])
        self.ex = sb("ex", [P, NT, scores])
        self.ch = sb("ch", [P, NT, scores])
        self.den = sb("den", [P, NT, 2])
        self.wt = sb("wt", [P, NT, NE])
        self.rest = sb("rest", [P, NT, NE])
        self.parts = sb("parts", [P, NT, 3, NE], BF16)
        self.partsT = sb("partsT", [P, TOK], BF16)

    def logits_on_tensor(self, pe):
        core, sig, ps = self.core, self.sig, self.core.ps
        for t in range(NT):
            last = pe.matmul(ps[:, self.bank, t * self.scores:(t + 1) * self.scores], core.x_feat[:, t * P:(t + 1) * P],
                             self.router[:, :], start=True, stop=True)
        last.then_inc(sig["logits_ready"].sem, 1)

    def parts_on_tensor(self, pe):
        sig, ps, core = self.sig, self.core.ps, self.core
        pe.wait_ge(*sig["parts_ready"](1))
        for t in range(NT):
            last = pe.transpose(ps[0:self.K3, self.bank + 1, :].bitcast(BF16)[:, t * P:(t + 1) * P],
                                self.parts[:, t, :, :].rearrange("p a e -> p (a e)"), core.ident16[:, :])
        last.then_inc(sig["parts_turned"].sem, 1)

    def on_scalar(self, act):
        act.wait_ge(*self.sig["steps"](2))
        act.activation(self.ex[:, :, :], self.lg[:, :, :], ACT.Exp, scale=-1.0 if self.rule == "sigmoid" else 1.0)\
           .then_inc(self.sig["exps_ready"].sem, 1)

    def on_vector(self, dve):
        sig, ps, scores, rule, NE, K3 = self.sig, self.core.ps, self.scores, self.rule, self.NE, self.K3
        top, lg, ex, ch, den, wt, rest = self.top, self.lg, self.ex, self.ch, self.den, self.wt, self.rest
        parts, partsT, shared = self.parts, self.partsT, NE > scores
        route = Steps(sig["steps"], 0)
        dve.wait_ge(*sig["logits_ready"](1))
        logits = ps[:, self.bank, 0:NT * scores].rearrange("p (t e) -> p t e", t=NT)
        for t in range(NT):
            last = dve.max(top[:, t, :], logits[:, t, :])
        route.done(last)
        dve.wait_ge(*route.last())
        first = top[:, :, 0:1].to_broadcast([P, NT, scores])
        second = top[:, :, 1:2].to_broadcast([P, NT, scores])
        if rule == "sigmoid":
            route.done(dve.tensor_copy(lg[:, :, :], logits))
        else:
            route.done(dve.tensor_tensor(lg[:, :, :], logits, first, ALU.subtract))
        route.done(dve.tensor_tensor(ch[:, :, :], logits, second, ALU.is_ge))
        dve.wait_ge(*sig["exps_ready"](1))
        dve.wait_ge(*route.last())
        if rule == "sigmoid":
            route.done(dve.tensor_scalar(ex[:, :, :], ex[:, :, :], 1.0, None, ALU.add))
            dve.wait_ge(*route.last())
            route.done(dve.reciprocal(ex[:, :, :], ex[:, :, :]))
            dve.wait_ge(*route.last())
            if shared:
                dve.wait_ge(*sig["zeroed"](3))
            route.done(dve.tensor_tensor(wt[:, :, 0:scores], ex[:, :, :], ch[:, :, :], ALU.mult))
        else:
            if rule == "renormalised":
                route.done(dve.tensor_reduce(den[:, :, 1], ex[:, :, :], AX.X, ALU.add))
            route.done(dve.tensor_tensor(ch[:, :, :], ex[:, :, :], ch[:, :, :], ALU.mult))
            dve.wait_ge(*route.last())
            route.done(dve.tensor_reduce(den[:, :, 0], ch[:, :, :], AX.X, ALU.add))
            dve.wait_ge(*route.last())
            if rule == "renormalised":
                route.done(dve.scalar_tensor_tensor(den[:, :, 0], den[:, :, 1], 1e-6, den[:, :, 0],
                                                    ALU.mult, ALU.add))
                dve.wait_ge(*route.last())
            route.done(dve.reciprocal(den[:, :, 0], den[:, :, 0]))
            dve.wait_ge(*route.last())
            if shared:
                dve.wait_ge(*sig["zeroed"](3))
            route.done(dve.tensor_tensor(wt[:, :, 0:scores], ch[:, :, :],
                                         den[:, :, 0:1].to_broadcast([P, NT, scores]), ALU.mult))
        dve.wait_ge(*route.last())
        route.done(dve.tensor_copy(parts[:, :, 0, :], wt[:, :, :]))
        dve.wait_ge(*route.last())
        route.done(dve.tensor_tensor(rest[:, :, :], wt[:, :, :], parts[:, :, 0, :], ALU.subtract))
        dve.wait_ge(*route.last())
        route.done(dve.tensor_copy(parts[:, :, 1, :], rest[:, :, :]))
        dve.wait_ge(*route.last())
        dve.tensor_tensor(parts[:, :, 2, :], rest[:, :, :], parts[:, :, 1, :], ALU.subtract)\
           .then_inc(sig["parts_ready"].sem, 1)
        dve.wait_ge(*sig["parts_turned"](1))
        dve.wait_ge(*sig["zeroed"](1))
        dve.tensor_copy(partsT[0:K3, :], ps[0:K3, self.bank + 1, :].bitcast(BF16)).then_inc(sig["parts_taken"].sem, 1)


def gated_experts(core, w, units, per_expert, scores, rule):
    nc, ps, x_tok, x_feat = core.nc, core.ps, core.x_tok, core.x_feat
    NE = units // per_expert
    shared = NE > scores
    names = ROUTE_SIGNALS + ("even_unit_loaded odd_unit_loaded even_down_loaded odd_down_loaded gate_ready gate_taken up_ready up_taken spread_ready hidden_ready "
                             "hidden_used y_copied y_turned").split()
    sig = {n: core.counter("ff_" + n) for n in names}
    unit_loaded = sig["even_unit_loaded"], sig["odd_unit_loaded"]
    down_loaded = sig["even_down_loaded"], sig["odd_down_loaded"]
    loaded = core.counter("ff_loaded")
    with ExitStack() as ctx:
        def sb(name, shape, dt=FP32):
            return core.tensor(ctx, "ff_" + name, shape, dt)

        GATE, UP, SPREAD, Y = 0, 2, 4, 6
        routing = Routing(core, sb, sig, scores, NE, rule, bank=SPREAD)
        ring = sb("ring", [P, 2, 3 * P])
        gate = sb("gate", [P, 2, 2, HALF])
        up = sb("up", [P, 2, 2, HALF])
        hid = sb("hid", [P, 2, 2, HALF])
        yT = sb("yT", [P, TOK])
        zero = sb("zero", [P, HALF], BF16)

        loads = [(routing.router[:, :], w["router"], loaded), (routing.sel[:, :], w["sel"], loaded)]
        for s in range(2):
            loads += [(ring[:, s, 0:2 * P], w["units"][s, :, 0:2 * P], unit_loaded[s]),
                      (ring[:, s, 2 * P:3 * P], w["units"][s, :, 2 * P:3 * P], down_loaded[s])]
        yield loads
        with nc.Block(no_gpsimd_drain=True) as block:
            @block.sync
            def _(sp):
                with sp.Fori(0, units // 2 - 1) as i:
                    for s in range(2):
                        sp.wait_ge(*sig["spread_ready"](4 * i + 2 * s + 2))
                        nxt = w["units"][bass.ds(2 * i + s + 2, 1), :, :].rearrange("u p n -> p (u n)")
                        sp.dma_start(ring[:, s, 0:2 * P], nxt[:, 0:2 * P]).then_inc(unit_loaded[s].sem, 16)
                        sp.wait_ge(*sig["hidden_used"](2 * i + s + 3))
                        sp.dma_start(ring[:, s, 2 * P:3 * P], nxt[:, 2 * P:3 * P]).then_inc(down_loaded[s].sem, 16)

            @block.gpsimd
            def _(pool):
                pool.memset(routing.partsT[:, :], 0.0).then_inc(sig["zeroed"].sem, 1)
                pool.memset(zero[:, :], 0.0).then_inc(sig["zeroed"].sem, 1)
                if shared:
                    pool.memset(routing.wt[:, :, scores:NE], 1.0).then_inc(sig["zeroed"].sem, 1)

            def gate_and_up(pe, n, s, turn):
                pe.wait_ge(*unit_loaded[s](16 * turn + 16))
                for h in range(2):
                    cols = x_feat[:, h * HALF:(h + 1) * HALF]
                    pe.wait_ge(*sig["gate_taken"](2 * n + h + 1))
                    pe.matmul(ps[:, GATE + h, :], ring[:, s, 0:P], cols, start=True, stop=True)\
                      .then_inc(sig["gate_ready"].sem, 1)
                    pe.wait_ge(*sig["up_taken"](2 * n + h + 3))
                    pe.matmul(ps[:, UP + h, :], ring[:, s, P:2 * P], cols, start=True, stop=True)\
                      .then_inc(sig["up_ready"].sem, 1)

            def spread_weights(pe, n, e):
                for h in range(2):
                    pe.wait_ge(*sig["hidden_ready"](2 * n + h + 1))
                    pe.matmul(ps[:, SPREAD + h, :], routing.sel[:, bass.ds(e * P, P)],
                              routing.partsT[:, h * HALF:(h + 1) * HALF],
                              start=True, stop=True).then_inc(sig["spread_ready"].sem, 1)

            def products_up(pe, n, s, turn, e):
                gate_and_up(pe, n, s, turn)
                spread_weights(pe, n, e)

            def products_down(pe, n, s, turn, last=False):
                pe.wait_ge(*down_loaded[s](16 * turn + 16))
                for h in range(2):
                    pe.wait_ge(*sig["hidden_ready"](2 * n + h + 3))
                    ins = pe.matmul(ps[:, Y + h, :], ring[:, s, 2 * P:3 * P], hid[:, s, h, :], start=False, stop=last)
                    if h == 1:
                        ins.then_inc(sig["hidden_used"].sem, 1)

            @block.tensor
            def _(pe):
                pe.sem_inc(sig["hidden_used"].sem, 2)
                pe.wait_ge(*loaded(32))
                pe.wait_ge(*sig["zeroed"](2))
                for h in range(2):
                    pe.matmul(ps[:, Y + h, :], zero[:, 0:P], zero[:, :], start=True, stop=False)
                routing.logits_on_tensor(pe)
                gate_and_up(pe, 0, 0, 0)
                routing.parts_on_tensor(pe)
                pe.wait_ge(*sig["parts_taken"](1))
                spread_weights(pe, 0, 0)
                with pe.Fori(0, units // 2 - 1) as i:
                    n = 2 * i
                    products_up(pe, n + 1, 1, i, n + 1 if per_expert == 1 else i)
                    products_down(pe, n, 0, i)
                    products_up(pe, n + 2, 0, i + 1, n + 2 if per_expert == 1 else i + 1)
                    products_down(pe, n + 1, 1, i)
                products_up(pe, units - 1, 1, units // 2 - 1, NE - 1)
                products_down(pe, units - 2, 0, units // 2 - 1)
                products_down(pe, units - 1, 1, units // 2 - 1, last=True)
                pe.wait_ge(*sig["y_copied"](1))
                for t in range(NT):
                    pe.transpose(ps[:, t // 4, t % 4 * P:(t % 4 + 1) * P], yT[:, t * P:(t + 1) * P],
                                 core.ident[:, :]).then_inc(sig["y_turned"].sem, 1)

            @block.scalar
            def _(act):
                act.sem_inc(sig["gate_taken"].sem, 2)
                routing.on_scalar(act)
                with act.Fori(0, units // 2) as i:
                    for s in range(2):
                        for h in range(2):
                            n = 2 * i + s
                            act.wait_ge(*sig["gate_ready"](2 * n + h + 1))
                            act.wait_ge(*sig["up_taken"](2 * n + h + 1))
                            act.activation(gate[:, s, h, :], ps[:, GATE + h, :], ACT.Silu)\
                               .then_inc(sig["gate_taken"].sem, 1)
                act.wait_ge(*sig["hidden_used"](units + 2))
                act.copy(yT[:, :].rearrange("p (n c) -> p n c", n=2), ps[:, Y:Y + 2, :]).then_inc(sig["y_copied"].sem, 1)

            @block.vector
            def _(dve):
                dve.sem_inc(sig["up_taken"].sem, 4)
                dve.sem_inc(sig["hidden_ready"].sem, 2)
                dve.wait_ge(*loaded(32))
                routing.on_vector(dve)
                with dve.Fori(0, units // 2) as i:
                    for s in range(2):
                        for h in range(2):
                            n = 2 * i + s
                            dve.wait_ge(*sig["gate_taken"](2 * n + h + 3))
                            dve.wait_ge(*sig["up_ready"](2 * n + h + 1))
                            dve.tensor_tensor(up[:, s, h, :], gate[:, s, h, :], ps[:, UP + h, :], ALU.mult)\
                               .then_inc(sig["up_taken"].sem, 1)
                        for h in range(2):
                            dve.wait_ge(*sig["up_taken"](2 * n + h + 5))
                            dve.wait_ge(*sig["hidden_used"](n + 1))
                            dve.wait_ge(*sig["spread_ready"](2 * n + h + 1))
                            dve.tensor_tensor(hid[:, s, h, :], up[:, s, h, :], ps[:, SPREAD + h, :], ALU.mult)\
                               .then_inc(sig["hidden_ready"].sem, 1)
                for t in range(2):
                    dve.wait_ge(*sig["y_turned"](4 * t + 4))
                    xs = x_tok[:, 4 * t:4 * t + 4, :]
                    dve.tensor_tensor(xs, xs, ps[:, t, :].rearrange("p (t f) -> p t f", t=4), ALU.add)


def normed_experts(core, w):
    nc, ps, x_tok, x_feat = core.nc, core.ps, core.x_tok, core.x_feat
    NE, U = 8, 4
    names = ROUTE_SIGNALS + ("even_loaded odd_loaded tile_ready tile_turned xhat_ready normed_ready hid_ready "
                             "relu_taken spread_ready spread_taken hidden_ready hidden_used wt_turned wt_taken "
                             "held own norm_steps rooted y_copied y_turned").split()
    sig = {n: core.counter("ne_" + n) for n in names}
    loaded = core.counter("ne_loaded")
    mats_loaded = sig["even_loaded"], sig["odd_loaded"]
    with ExitStack() as ctx:
        def sb(name, shape, dt=FP32):
            return core.tensor(ctx, "ne_" + name, shape, dt)

        routing = Routing(core, sb, sig, NE, NE, "softmax")
        ring = sb("ring", [P, 2, 2, U, P])
        gamma, beta, b1 = sb("gamma", [P, NE]), sb("beta", [P, NE]), sb("b1", [P, NE * U])
        b2 = sb("b2", [NE, P])
        norm = TokenNorm(core, ctx, "ne", 1e-6, sig["norm_steps"], sig["rooted"])
        xhat = sb("xhat", [P, NT, P])
        xhatT = sb("xhatT", [P, TOK])
        normed = sb("normed", [P, 2, TOK])
        relu = sb("relu", [P, 2, 2, HALF])
        hid = sb("hid", [P, 2, 2, HALF])
        spread = sb("spread", [P, 2, TOK])
        wtT = sb("wtT", [NE, TOK])
        total = sb("total", [P, NT])
        yT = sb("yT", [P, TOK])
        HID, SPREAD, Y = 0, 4, 6

        loads = [(dst[:, :], w[src], loaded) for dst, src in
                 ((routing.router, "router"), (routing.sel, "sel"), (gamma, "gamma"), (beta, "beta"), (b1, "b1"), (b2, "b2"))]
        for s in range(2):
            loads += [(ring[:, s, :, :, :].rearrange("p a u f -> p (a u f)"), w["mats"][s, :, :], mats_loaded[s])]
        yield loads
        with nc.Block(no_gpsimd_drain=True) as block:
            @block.sync
            def _(sp):
                with sp.Fori(0, NE // 2 - 1) as i:
                    for s in range(2):
                        sp.wait_ge(*sig["hidden_used"](U * (2 * i + s) + U + 2))
                        sp.dma_start(ring[:, s, :, :, :].rearrange("p a u f -> p (a u f)"),
                                     w["mats"][bass.ds(2 * i + s + 2, 1), :, :].rearrange("e p n -> p (e n)"))\
                          .then_inc(mats_loaded[s].sem, 16)

            @block.gpsimd
            def _(pool):
                pool.memset(routing.partsT[:, :], 0.0).then_inc(sig["zeroed"].sem, 1)

            def products_up(pe, n, s, u):
                for h in range(2):
                    pe.wait_ge(*sig["relu_taken"](2 * n + h + 1))
                    pe.matmul(ps[:, HID + 2 * (u % 2) + h, :], ring[:, s, 0, u, :],
                              normed[:, s, h * HALF:(h + 1) * HALF], start=True, stop=True)\
                      .then_inc(sig["hid_ready"].sem, 1)

            def enter_expert(pe, e, s, turn):
                for h in range(2):
                    pe.wait_ge(*sig["spread_taken"](2 * e + h + 1))
                    pe.matmul(ps[:, SPREAD + h, :], routing.sel[:, bass.ds(e * P, P)],
                              routing.partsT[:, h * HALF:(h + 1) * HALF], start=True, stop=True)\
                      .then_inc(sig["spread_ready"].sem, 1)
                pe.wait_ge(*mats_loaded[s](16 * turn + 16))
                pe.wait_ge(*sig["normed_ready"](e + 1))

            def products_down(pe, n, s, u, last=False):
                for h in range(2):
                    pe.wait_ge(*sig["hidden_ready"](2 * n + h + 5))
                    ins = pe.matmul(ps[:, Y + h, :], ring[:, s, 1, u, :], hid[:, u % 2, h, :], start=False, stop=last)
                    if h == 1:
                        ins.then_inc(sig["hidden_used"].sem, 1)

            @block.tensor
            def _(pe):
                pe.sem_inc(sig["hidden_used"].sem, 2)
                pe.wait_ge(*loaded(96))
                for t in range(NT):
                    pe.wait_ge(*sig["tile_ready"](t + 1))
                    pe.transpose(ps[:, 2 + t // 4, t % 4 * P:(t % 4 + 1) * P], xhat[:, t, :],
                                 core.ident[:, :]).then_inc(sig["tile_turned"].sem, 1)
                routing.logits_on_tensor(pe)
                routing.parts_on_tensor(pe)
                for t in range(NT):
                    last = pe.transpose(ps[0:NE, 4 + t // 4, t % 4 * P:(t % 4 + 1) * P], routing.wt[:, t, :],
                                        core.ident[:, :])
                last.then_inc(sig["wt_turned"].sem, 1)
                pe.wait_ge(*sig["wt_taken"](1))
                for h in range(2):
                    pe.matmul(ps[:, Y + h, :], b2[:, :], wtT[:, h * HALF:(h + 1) * HALF], start=True, stop=False)
                pe.wait_ge(*sig["parts_taken"](1))
                pe.wait_ge(*sig["xhat_ready"](2))
                enter_expert(pe, 0, 0, 0)
                products_up(pe, 0, 0, 0)

                def pair(i, final):
                    for k in range(2 * U):
                        n = 2 * U * i + k
                        if k + 1 == U:
                            enter_expert(pe, 2 * i + 1, 1, i)
                        if k + 1 == 2 * U and not final:
                            enter_expert(pe, 2 * i + 2, 0, i + 1)
                        if not (final and k + 1 == 2 * U):
                            products_up(pe, n + 1, (k + 1) // U % 2, (k + 1) % U)
                        products_down(pe, n, k // U, k % U, last=final and k + 1 == 2 * U)

                with pe.Fori(0, NE // 2 - 1) as i:
                    pair(i, False)
                pair(NE // 2 - 1, True)
                pe.wait_ge(*sig["y_copied"](1))
                for t in range(NT):
                    pe.transpose(ps[:, t // 4, t % 4 * P:(t % 4 + 1) * P], yT[:, t * P:(t + 1) * P],
                                 core.ident[:, :]).then_inc(sig["y_turned"].sem, 1)

            @block.scalar
            def _(act):
                norm.on_scalar(act)
                for h in range(2):
                    act.wait_ge(*sig["tile_turned"](4 * h + 4))
                    act.copy(xhatT[:, h * HALF:(h + 1) * HALF], ps[:, 2 + h, :]).then_inc(sig["xhat_ready"].sem, 1)
                act.sem_inc(sig["relu_taken"].sem, 4)
                act.sem_inc(sig["spread_taken"].sem, 2)
                routing.on_scalar(act)
                act.wait_ge(*loaded(96))
                with act.Fori(0, NE // 2) as i:
                    for k in range(2 * U):
                        n, s, u = 2 * U * i + k, k // U, k % U
                        if u == 0:
                            for h in range(2):
                                e = 2 * i + s
                                act.wait_ge(*sig["spread_ready"](2 * e + h + 1))
                                act.copy(spread[:, s, h * HALF:(h + 1) * HALF], ps[:, SPREAD + h, :])\
                                   .then_inc(sig["spread_taken"].sem, 1)
                        for h in range(2):
                            act.wait_ge(*sig["hid_ready"](2 * n + h + 1))
                            act.wait_ge(*sig["hidden_ready"](2 * n + h + 1))
                            act.sem_inc(sig["held"].sem, 1)
                            act.activation(relu[:, u % 2, h, :], ps[:, HID + 2 * (u % 2) + h, :], ACT.Relu,
                                           bias=b1[:, bass.ds(n, 1)]).then_inc(sig["relu_taken"].sem, 1)
                act.wait_ge(*sig["hidden_used"](NE * U + 2))
                act.copy(yT[:, :].rearrange("p (n c) -> p n c", n=2), ps[:, Y:Y + 2, :]).then_inc(sig["y_copied"].sem, 1)

            @block.vector
            def _(dve):
                norm.on_vector(dve)
                for t in range(NT):
                    norm.normalise(dve, xhat[:, t, :], t).then_inc(sig["tile_ready"].sem, 1)
                dve.wait_ge(*loaded(96))
                routing.on_vector(dve)
                own = sig["own"]
                dve.tensor_reduce(total[:, :], routing.wt[:, :, :], AX.X, ALU.add).then_inc(own.sem, 1)
                dve.wait_ge(*own(1))
                dve.tensor_scalar(total[:, :], total[:, :], 1.0, None, ALU.add).then_inc(own.sem, 1)
                dve.wait_ge(*own(2))
                dve.tensor_tensor(x_tok[:, :, :], x_tok[:, :, :], total[:, :].unsqueeze(2).to_broadcast([P, NT, P]),
                                  ALU.mult).then_inc(own.sem, 1)
                dve.wait_ge(*sig["wt_turned"](1))
                dve.tensor_copy(wtT[:, :].rearrange("e (n c) -> e n c", n=2), ps[0:NE, 4:6, :])\
                   .then_inc(sig["wt_taken"].sem, 1)
                dve.wait_ge(*sig["xhat_ready"](2))

                def normalise(e, s):
                    dve.tensor_scalar(normed[:, s, :], xhatT[:, :], gamma[:, bass.ds(e, 1)], beta[:, bass.ds(e, 1)],
                                      ALU.mult, ALU.add).then_inc(sig["normed_ready"].sem, 1)

                normalise(0, 0)
                dve.sem_inc(sig["hidden_ready"].sem, 4)

                def pair(i, final):
                    for k in range(2 * U):
                        n, s, u = 2 * U * i + k, k // U, k % U
                        if u == 1 and not (final and s == 1):
                            dve.wait_ge(*sig["hid_ready"](2 * (n - u) + 1))
                            normalise(2 * i + s + 1, 1 - s)
                        for h in range(2):
                            dve.wait_ge(*sig["relu_taken"](2 * n + h + 5))
                            dve.wait_ge(*sig["hidden_used"](n + 1))
                            dve.tensor_tensor(hid[:, u % 2, h, :], relu[:, u % 2, h, :],
                                              spread[:, s, h * HALF:(h + 1) * HALF], ALU.mult)\
                               .then_inc(sig["hidden_ready"].sem, 1)

                with dve.Fori(0, NE // 2 - 1) as i:
                    pair(i, False)
                pair(NE // 2 - 1, True)
                dve.wait_ge(*own(3))
                for t in range(2):
                    dve.wait_ge(*sig["y_turned"](4 * t + 4))
                    xs = x_tok[:, 4 * t:4 * t + 4, :]
                    dve.tensor_tensor(xs, xs, ps[:, t, :].rearrange("p (t f) -> p t f", t=4), ALU.add)


def linear_attention(core, w):
    nc, ps, x_tok, x_feat = core.nc, core.ps, core.x_tok, core.x_feat
    VW = P + 1
    names = ("steps q_ready k_ready v_ready q_under k_under q_exp k_exp q_mapped k_mapped v_taken kv_ready kv_taken "
             "mixed_ready mixed_taken mixed_turned turned_taken y_ready ones").split()
    sig = {n: core.counter("la_" + n) for n in names}
    loaded = core.counter("la_loaded")
    with ExitStack() as ctx:
        def sb(name, shape, dt=FP32):
            return core.tensor(ctx, "la_" + name, shape, dt)

        mats = sb("mats", [P, 4, P])
        bq = sb("bq", [P, 1])
        rows = sb("rows", [P, 3, P])
        q, q_min, q_max = sb("q", [P, TOK]), sb("q_min", [P, TOK]), sb("q_max", [P, TOK])
        k, k_min, k_max = sb("k", [P, NT, P]), sb("k_min", [P, NT, P]), sb("k_max", [P, NT, P])
        v = sb("v", [P, NT, VW])
        kv = sb("kv", [P, B, VW])
        rec = sb("rec", [P, NT])
        mixed = sb("mixed", [P, NT, P])
        mixedT = sb("mixedT", [P, NT, P])

        def halves(t):
            return t.rearrange("p (n c) -> p n c", n=2)

        yield [(mats[:, :, :], w["mats"], loaded), (bq[:, :], w["bq"], loaded),
               (rows[:, :, :], w["rows"].partition_broadcast(P), loaded)]
        with nc.Block(no_gpsimd_drain=True) as block:
            @block.gpsimd
            def _(pool):
                pool.memset(v[:, :, P:VW], 1.0).then_inc(sig["ones"].sem, 1)

            @block.tensor
            def _(pe):
                pe.wait_ge(*loaded(48))
                for n in range(2):
                    last = pe.matmul(ps[:, n, :], mats[:, 0, :], x_feat[:, n * HALF:(n + 1) * HALF],
                                     start=True, stop=True)
                last.then_inc(sig["q_ready"].sem, 1)
                for bank, m, done in ((2, 1, "k_ready"), (4, 2, "v_ready")):
                    for t in range(NT):
                        last = pe.matmul(ps[:, bank + t // 4, t % 4 * P:(t % 4 + 1) * P],
                                         x_feat[:, t * P:(t + 1) * P], mats[:, m, :], start=True, stop=True)
                    last.then_inc(sig[done].sem, 1)
                pe.wait_ge(*sig["k_mapped"](1))
                pe.wait_ge(*sig["v_taken"](1))
                for b in range(B):
                    for t in range(TPB):
                        last = pe.matmul(ps[:, 6 + b // 2, b % 2 * 256:b % 2 * 256 + VW], k[:, TPB * b + t, :],
                                         v[:, TPB * b + t, :], start=t == 0, stop=t == TPB - 1)
                last.then_inc(sig["kv_ready"].sem, 1)
                pe.wait_ge(*sig["kv_taken"](1))
                pe.wait_ge(*sig["q_mapped"](1))
                for t in range(NT):
                    last = pe.matmul(ps[:, t // 2, t % 2 * 256:t % 2 * 256 + VW], q[:, t * P:(t + 1) * P],
                                     kv[:, t // TPB, :], start=True, stop=True)
                last.then_inc(sig["mixed_ready"].sem, 1)
                pe.wait_ge(*sig["mixed_taken"](1))
                for t in range(NT):
                    last = pe.transpose(ps[:, 4 + t // 4, t % 4 * P:(t % 4 + 1) * P], mixed[:, t, :],
                                        core.ident[:, :])
                last.then_inc(sig["mixed_turned"].sem, 1)
                pe.wait_ge(*sig["turned_taken"](1))
                for t in range(NT):
                    last = pe.matmul(ps[:, 6 + t // 4, t % 4 * P:(t % 4 + 1) * P], mixedT[:, t, :], mats[:, 3, :],
                                     start=True, stop=True)
                last.then_inc(sig["y_ready"].sem, 1)

            @block.scalar
            def _(act):
                act.wait_ge(*sig["q_under"](1))
                act.activation(q_min[:, :], q_min[:, :], ACT.Exp).then_inc(sig["q_exp"].sem, 1)
                act.wait_ge(*sig["k_under"](1))
                act.activation(k_min[:, :, :], k_min[:, :, :], ACT.Exp).then_inc(sig["k_exp"].sem, 1)
                act.wait_ge(*sig["mixed_turned"](1))
                act.copy(halves(mixedT[:, :, :].rearrange("p t f -> p (t f)")), ps[:, 4:6, :])\
                   .then_inc(sig["turned_taken"].sem, 1)

            @block.vector
            def _(dve):
                own = Steps(sig["steps"])
                dve.wait_ge(*loaded(48))
                own.done(dve.tensor_tensor(x_tok[:, :, :], x_tok[:, :, :],
                                           rows[:, 2:3, :].to_broadcast([P, NT, P]), ALU.add))
                dve.wait_ge(*sig["q_ready"](1))
                dve.tensor_scalar(halves(q_min[:, :]), ps[:, 0:2, :], bq[:, 0:1], 0.0, ALU.add, ALU.min)\
                   .then_inc(sig["q_under"].sem, 1)
                own.done(dve.tensor_scalar(halves(q_max[:, :]), ps[:, 0:2, :], bq[:, 0:1], 0.0, ALU.add, ALU.max))
                dve.wait_ge(*sig["k_ready"](1))
                own.done(dve.tensor_tensor(k_max[:, :, :], ps[:, 2:4, :].rearrange("p n (t f) -> p (n t) f", f=P),
                                           rows[:, 0:1, :].to_broadcast([P, NT, P]), ALU.add))
                dve.wait_ge(*own.last())
                dve.tensor_scalar(k_min[:, :, :], k_max[:, :, :], 0.0, None, ALU.min).then_inc(sig["k_under"].sem, 1)
                dve.wait_ge(*sig["k_under"](1))
                own.done(dve.tensor_scalar(k_max[:, :, :], k_max[:, :, :], 0.0, None, ALU.max))
                dve.wait_ge(*sig["v_ready"](1))
                dve.tensor_tensor(v[:, :, 0:P], ps[:, 4:6, :].rearrange("p n (t f) -> p (n t) f", f=P),
                                  rows[:, 1:2, :].to_broadcast([P, NT, P]), ALU.add)\
                   .then_inc(sig["v_taken"].sem, 1)
                dve.wait_ge(*sig["ones"](1))
                dve.wait_ge(*sig["k_exp"](1))
                dve.wait_ge(*own.last())
                dve.tensor_tensor(k[:, :, :], k_min[:, :, :], k_max[:, :, :], ALU.add)\
                   .then_inc(sig["k_mapped"].sem, 1)
                dve.wait_ge(*sig["q_exp"](1))
                dve.tensor_tensor(q[:, :], q_min[:, :], q_max[:, :], ALU.add).then_inc(sig["q_mapped"].sem, 1)
                dve.wait_ge(*sig["kv_ready"](1))
                src = ps[:, 6:8, :].rearrange("p n (b c) -> p (n b) c", b=2)
                own.done(dve.tensor_copy(kv[:, :, 0:P], src[:, :, 0:P]))
                dve.tensor_scalar(kv[:, :, P:VW], src[:, :, P:VW], 1e-6, None, ALU.add)\
                   .then_inc(sig["kv_taken"].sem, 1)
                dve.wait_ge(*sig["mixed_ready"](1))
                src = ps[:, 0:4, :].rearrange("p n (t c) -> p (n t) c", t=2)
                own.done(dve.reciprocal(rec[:, :], src[:, :, P]))
                dve.wait_ge(*own.last())
                dve.tensor_tensor(mixed[:, :, :], src[:, :, 0:P], rec[:, :].unsqueeze(2).to_broadcast([P, NT, P]),
                                  ALU.mult).then_inc(sig["mixed_taken"].sem, 1)
                dve.wait_ge(*sig["y_ready"](1))
                dve.tensor_tensor(x_tok[:, :, :], x_tok[:, :, :],
                                  ps[:, 6:8, :].rearrange("p n (t f) -> p (n t) f", f=P), ALU.add)


def rwkv_mixer(core, w):
    nc, ps, x_tok, x_feat = core.nc, core.ps, core.x_tok, core.x_feat
    names = "own own_act k_ready v_ready r_ready mixed taken y_ready expo gated filled".split()
    sig = {n: core.counter("rw_" + n) for n in names}
    loaded = core.counter("rw_loaded")
    with ExitStack() as ctx:
        def sb(name, shape, dt=FP32):
            return core.tensor(ctx, "rw_" + name, shape, dt)

        mats = sb("mats", [P, 4, P])
        cols = sb("cols", [P, 5])
        keep = sb("keep", [P, 3])
        wn = sb("wn", [P, 1])
        xm = sb("xm", [P, 3, B, S])
        k, v = sb("k", [P, B, S]), sb("v", [P, B, S])
        pp, aa, bb = (sb(n, [P, B, S + 1]) for n in ("pp", "aa", "bb"))
        uk, top = sb("uk", [P, B, S]), sb("top", [P, B, S])
        e1, e2, e1b, e2b = (sb(n, [P, B, S]) for n in ("e1", "e2", "e1b", "e2b"))
        er = sb("er", [P, B, S])
        num, den = sb("num", [P, B, S]), sb("den", [P, B, S])

        def banks(n):
            return ps[:, n:n + 2, :].rearrange("p n (b s) -> p (n b) s", s=S)

        yield [(mats[:, :, :], w["mats"], loaded), (cols[:, :], w["cols"], loaded)]
        with nc.Block(no_gpsimd_drain=True) as block:
            @block.gpsimd
            def _(pool):
                pool.memset(pp[:, :, 0:1], -1e38).then_inc(sig["filled"].sem, 1)
                pool.memset(aa[:, :, 0:1], 0.0).then_inc(sig["filled"].sem, 1)
                pool.memset(bb[:, :, 0:1], 0.0).then_inc(sig["filled"].sem, 1)

            @block.tensor
            def _(pe):
                pe.wait_ge(*loaded(32))
                for m, done in enumerate(("k_ready", "v_ready", "r_ready")):
                    pe.wait_ge(*sig["mixed"](m + 1))
                    for n in range(2):
                        last = pe.matmul(ps[:, 2 * m + n, :], mats[:, m, :],
                                         xm[:, m, 2 * n:2 * n + 2, :].rearrange("p b s -> p (b s)"),
                                         start=True, stop=True)
                    last.then_inc(sig[done].sem, 1)
                for b in range(B):
                    pe.wait_ge(*sig["gated"](b + 1))
                    for t in range(TPB):
                        n = TPB * b + t
                        last = pe.matmul(ps[:, 6 + n // 4, n % 4 * P:(n % 4 + 1) * P], num[:, b, t * P:(t + 1) * P],
                                         mats[:, 3, :], start=True, stop=True)
                    if b % 2:
                        last.then_inc(sig["y_ready"].sem, 1)

            @block.scalar
            def _(act):
                act.wait_ge(*loaded(32))
                act.activation(wn[:, :], cols[:, 3:4], ACT.Exp).then_inc(sig["own_act"].sem, 1)
                act.wait_ge(*sig["own_act"](1))
                act.mul(wn[:, :], wn[:, :], -1.0).then_inc(sig["own_act"].sem, 1)
                act.wait_ge(*sig["v_ready"](1))
                act.copy(v[:, :, :], banks(2)).then_inc(sig["taken"].sem, 1)
                act.wait_ge(*sig["r_ready"](1))
                act.activation(er[:, :, :], banks(4), ACT.Exp, scale=-1.0).then_inc(sig["taken"].sem, 1)
                for n, e in enumerate((e1b, e2b, e1, e2)):
                    act.wait_ge(*sig["expo"](n + 1))
                    act.activation(e[:, :, :], e[:, :, :], ACT.Exp).then_inc(sig["own_act"].sem, 1)

            @block.vector
            def _(dve):
                own = Steps(sig["own"])
                dve.wait_ge(*loaded(32))
                own.done(dve.tensor_scalar(keep[:, :], cols[:, 0:3], -1.0, 1.0, ALU.mult, ALU.add))
                xb = x_feat[:, :].rearrange("p (b s) -> p b s", s=S)
                for m in range(3):
                    own.done(dve.tensor_scalar(xm[:, m, :, :], xb, cols[:, m:m + 1], None, ALU.mult))
                    dve.wait_ge(*own.last())
                    dve.scalar_tensor_tensor(xm[:, m, :, 1:S], xb[:, :, 0:S - 1], keep[:, m:m + 1],
                                             xm[:, m, :, 1:S], ALU.mult, ALU.add).then_inc(sig["mixed"].sem, 1)
                dve.wait_ge(*sig["k_ready"](1))
                own.done(dve.tensor_copy(k[:, :, :], banks(0)))
                dve.wait_ge(*own.last())
                dve.wait_ge(*sig["filled"](3))
                dve.wait_ge(*sig["own_act"](2))
                for b in range(B):
                    own.done(dve.tensor_tensor_scan(pp[:, b, 1:S + 1], wn[:, 0:1].to_broadcast([P, S]), k[:, b, :],
                                                    -1e38, ALU.add, ALU.max))
                own.done(dve.tensor_scalar(uk[:, :, :], k[:, :, :], cols[:, 4:5], None, ALU.add))
                dve.wait_ge(*own.last())
                old, new = pp[:, :, 0:S], pp[:, :, 1:S + 1]
                dve.scalar_tensor_tensor(e1b[:, :, :], old, wn[:, 0:1], new, ALU.add, ALU.subtract)\
                   .then_inc(sig["expo"].sem, 1)
                dve.tensor_tensor(e2b[:, :, :], k[:, :, :], new, ALU.subtract).then_inc(sig["expo"].sem, 1)
                own.done(dve.tensor_tensor(top[:, :, :], old, uk[:, :, :], ALU.max))
                dve.wait_ge(*own.last())
                dve.tensor_tensor(e1[:, :, :], old, top[:, :, :], ALU.subtract).then_inc(sig["expo"].sem, 1)
                dve.tensor_tensor(e2[:, :, :], uk[:, :, :], top[:, :, :], ALU.subtract).then_inc(sig["expo"].sem, 1)
                dve.wait_ge(*sig["taken"](1))
                dve.wait_ge(*sig["own_act"](4))
                dve.wait_ge(*sig["expo"](4))
                own.done(dve.tensor_tensor(top[:, :, :], e2b[:, :, :], v[:, :, :], ALU.mult))
                dve.wait_ge(*own.last())
                for b in range(B):
                    own.done(dve.tensor_tensor_scan(aa[:, b, 1:S + 1], e1b[:, b, :], top[:, b, :], 0.0,
                                                    ALU.mult, ALU.add))
                    own.done(dve.tensor_tensor_scan(bb[:, b, 1:S + 1], e1b[:, b, :], e2b[:, b, :], 0.0,
                                                    ALU.mult, ALU.add))
                dve.wait_ge(*sig["own_act"](6))
                dve.wait_ge(*own.last())
                own.done(dve.tensor_tensor(num[:, :, :], e1[:, :, :], aa[:, :, 0:S], ALU.mult))
                own.done(dve.tensor_tensor(den[:, :, :], e1[:, :, :], bb[:, :, 0:S], ALU.mult))
                own.done(dve.tensor_tensor(v[:, :, :], e2[:, :, :], v[:, :, :], ALU.mult))
                dve.wait_ge(*own.last())
                own.done(dve.tensor_tensor(num[:, :, :], num[:, :, :], v[:, :, :], ALU.add))
                own.done(dve.tensor_tensor(den[:, :, :], den[:, :, :], e2[:, :, :], ALU.add))
                dve.wait_ge(*sig["taken"](2))
                dve.wait_ge(*own.last())
                own.done(dve.scalar_tensor_tensor(den[:, :, :], er[:, :, :], 1.0, den[:, :, :], ALU.add, ALU.mult))
                dve.wait_ge(*own.last())
                for b in range(B):
                    own.done(dve.reciprocal(den[:, b, :], den[:, b, :]))
                    dve.wait_ge(*own.last())
                    dve.tensor_tensor(num[:, b, :], num[:, b, :], den[:, b, :], ALU.mult)\
                       .then_inc(sig["gated"].sem, 1)
                for n in range(2):
                    dve.wait_ge(*sig["y_ready"](n + 1))
                    xs = x_tok[:, 4 * n:4 * n + 4, :]
                    dve.tensor_tensor(xs, xs, ps[:, 6 + n, :].rearrange("p (t f) -> p t f", f=P), ALU.add)


def reshaped_attention(core, w):
    nc, ps, x_tok, x_feat = core.nc, core.ps, core.x_tok, core.x_feat
    H, K, V = 8, 64, 16
    BL = 8
    STEP = P + V
    names = ("steps qk_ready q_taken k_taken v_ready v_taken vt_ready vt_taken scores_ready max_ready scores_used "
             "rec_ready probs_ready mixed_ready mixed_taken held zeroed y_copied y_turned").split()
    sig = {n: core.counter("ra_" + n) for n in names}
    loaded = core.counter("ra_loaded")
    with ExitStack() as ctx:
        def sb(name, shape, dt=FP32):
            return core.tensor(ctx, "ra_" + name, shape, dt)

        mq, mk, mv = sb("mq", [P, BL * K]), sb("mk", [P, BL * K]), sb("mv", [P, P])
        qT, kT = sb("qT", [K, S, BL]), sb("kT", [K, S, BL])
        vT = sb("vT", [V, S, BL])
        v = sb("v", [P, 2 * H * STEP])
        yT = sb("yT", [P, S])
        probs = sb("probs", [P, 2, H, S])
        xb = sb("xb", [P, S])
        nmax = sb("nmax", [P, 2, H])
        sums = sb("sums", [P, 2, H])
        rec = sb("rec", [P, 2, H])
        yield [(mq[:, :], w["mq"], loaded), (mk[:, :], w["mk"], loaded), (mv[:, :], w["mv"], loaded)]
        with nc.Block(no_gpsimd_drain=True) as block:
            @block.gpsimd
            def _(pool):
                pool.memset(v[:, :], 0.0).then_inc(sig["zeroed"].sem, 1)
                with pool.Fori(0, B) as b:
                    for i in range(2 * H):
                        h, n = i // 2, i % 2
                        pool.wait_ge(*sig["rec_ready"](b * 16 + i + 1))
                        pool.sem_inc(sig["held"].sem, 1)
                        pool.tensor_scalar(probs[:, n, h, :], probs[:, n, h, :], rec[:, n, h:h + 1], None,
                                           ALU.mult).then_inc(sig["probs_ready"].sem, 1)

            @block.tensor
            def _(pe):
                pe.wait_ge(*loaded(48))
                with pe.Fori(0, B) as b:
                    pe.wait_ge(*sig["mixed_taken"](b + 1))
                    for j in range(BL):
                        pe.wait_ge(*sig["q_taken"](b * BL + j + 1))
                        pe.wait_ge(*sig["k_taken"](b * BL + j + 1))
                        pe.sem_inc(sig["held"].sem, 1)
                        xs = x_feat[:, bass.ds(b * S, S)]
                        pe.matmul(ps[0:K, j % 2, 0:S], mq[:, j * K:(j + 1) * K], xs, start=True, stop=True)
                        pe.matmul(ps[0:K, 2 + j % 2, 0:S], mk[:, j * K:(j + 1) * K], xs,
                                  start=True, stop=True).then_inc(sig["qk_ready"].sem, 1)
                    for j in range(BL):
                        last = pe.matmul(ps[0:V, 4 + j // 2, j % 2 * S:j % 2 * S + S], mv[:, j * V:(j + 1) * V], xs,
                                         start=True, stop=True)
                    last.then_inc(sig["v_ready"].sem, 1)
                    pe.wait_ge(*sig["q_taken"](b * BL + BL + 2))
                    pe.wait_ge(*sig["k_taken"](b * BL + BL + 2))
                    for h in range(H):
                        for n in range(2):
                            i = 2 * h + n
                            pe.wait_ge(*sig["scores_used"](b * 16 + i + 1))
                            ks = kT[:, h * 32 + n * 16:h * 32 + n * 16 + 16, :].rearrange("d t j -> d (t j)")
                            qs = qT[:, h * 32:h * 32 + 32, :].rearrange("d t j -> d (t j)")
                            pe.matmul(ps[:, i % 4, 0:S], ks, qs, start=True, stop=True)\
                              .then_inc(sig["scores_ready"].sem, 1)
                    pe.wait_ge(*sig["v_taken"](b + 1))
                    pe.sem_inc(sig["held"].sem, 1)
                    for n in range(2):
                        for h in range(H):
                            src = vT[:, h * 32 + n * 16:h * 32 + n * 16 + 16, :].rearrange("d t j -> d (t j)")
                            last = pe.transpose(ps[:, 4, (n * H + h) * V:(n * H + h + 1) * V], src,
                                                core.ident[0:V, 0:V])
                    last.then_inc(sig["vt_ready"].sem, 1)
                    pe.wait_ge(*sig["vt_taken"](b + 1))
                    pe.wait_ge(*sig["probs_ready"](16 * b + 16))
                    for r in range(BL):
                        for n in range(2):
                            src = probs[:, n, :, :].rearrange("c h (i r) -> c r (h i)", r=BL)
                            o = n * H * STEP + r * P
                            last = pe.matmul(ps[:, 5, 0:S], v[:, o:o + P], src[:, r, :], start=r == n == 0,
                                             stop=r == BL - 1 and n == 1)
                    last.then_inc(sig["mixed_ready"].sem, 1)
                    pe.wait_ge(*sig["y_copied"](b + 1))
                    for t in range(TPB):
                        last = pe.transpose(ps[:, 5, t * P:(t + 1) * P], yT[:, t * P:(t + 1) * P], core.ident[:, :])
                    last.then_inc(sig["y_turned"].sem, 1)

            @block.scalar
            def _(act):
                act.sem_inc(sig["q_taken"].sem, 2)
                act.sem_inc(sig["scores_used"].sem, 4)
                with act.Fori(0, B) as b:
                    for j in range(BL):
                        act.wait_ge(*sig["qk_ready"](b * BL + j + 1))
                        act.copy(qT[:, :, j], ps[0:K, j % 2, 0:S]).then_inc(sig["q_taken"].sem, 1)
                    act.wait_ge(*sig["v_ready"](b + 1))
                    act.copy(vT[:, :, :].rearrange("d t (n k) -> d n k t", n=4),
                             ps[0:V, 4:8, :].rearrange("d n (k t) -> d n k t", k=2)).then_inc(sig["v_taken"].sem, 1)
                    for h in range(H):
                        for n in range(2):
                            i = 2 * h + n
                            act.wait_ge(*sig["max_ready"](b * 16 + i + 1))
                            act.activation(probs[:, n, h, :], ps[:, i % 4, 0:S], ACT.Exp, bias=nmax[:, n, h:h + 1],
                                           scale=K ** -0.5, accum_out=sums[:, n, h:h + 1])\
                               .then_inc(sig["scores_used"].sem, 1)

            @block.vector
            def _(dve):
                dve.sem_inc(sig["k_taken"].sem, 2)
                dve.sem_inc(sig["mixed_taken"].sem, 1)
                dve.wait_ge(*sig["zeroed"](1))
                with dve.Fori(0, B) as b:
                    for j in range(BL):
                        dve.wait_ge(*sig["qk_ready"](b * BL + j + 1))
                        dve.tensor_copy(kT[:, :, j], ps[0:K, 2 + j % 2, 0:S]).then_inc(sig["k_taken"].sem, 1)
                    def invert_sum(i):
                        h, n = i // 2, i % 2
                        dve.wait_ge(*sig["scores_used"](b * 16 + i + 5))
                        dve.reciprocal(rec[:, n, h:h + 1], sums[:, n, h:h + 1]).then_inc(sig["rec_ready"].sem, 1)

                    for i in range(2 * H):
                        h, n = i // 2, i % 2
                        dve.wait_ge(*sig["scores_ready"](b * 16 + i + 1))
                        dve.tensor_reduce(nmax[:, n, h:h + 1], ps[:, i % 4, 0:S], AX.X, ALU.max)\
                           .then_inc(sig["steps"].sem, 1)
                        dve.wait_ge(*sig["steps"](b * 16 + i + 1))
                        dve.tensor_scalar(nmax[:, n, h:h + 1], nmax[:, n, h:h + 1], -K ** -0.5, None,
                                          ALU.mult).then_inc(sig["max_ready"].sem, 1)
                        if i >= 2:
                            invert_sum(i - 2)
                    invert_sum(2 * H - 2)
                    invert_sum(2 * H - 1)
                    dve.wait_ge(*sig["vt_ready"](b + 1))
                    dve.tensor_copy(v[:, :].rearrange("p (n h e) -> p n h e", n=2, h=H)[:, :, :, 0:V],
                                    ps[:, 4, 0:2 * H * V].rearrange("p (n h d) -> p n h d", n=2, h=H))\
                       .then_inc(sig["vt_taken"].sem, 1)
                    dve.wait_ge(*sig["mixed_ready"](b + 1))
                    dve.tensor_copy(yT[:, :], ps[:, 5, 0:S]).then_inc(sig["y_copied"].sem, 1)
                    dve.wait_ge(*sig["y_turned"](b + 1))
                    xs = x_tok[:, bass.ds(b * TPB, TPB), :]
                    dve.tensor_tensor(xs, xs, ps[:, 5, 0:TPB * P].rearrange("p (t f) -> p t f", t=TPB),
                                      ALU.add).then_inc(sig["mixed_taken"].sem, 1)


def two_way_mamba(core, w):
    nc, ps, x_tok = core.nc, core.ps, core.x_tok
    N, T, PAD, R = 16, 4, 3, 8
    HALVES, WAYS = 2, 2
    names = ("norm_steps rooted tile_ready tile_turned norm_ready weights_scaled a_exp a_ready diag_ready conv_ready z_ready "
             "xc_tanh xc_half xc_ready sz_tanh sz_half sz_ready half_ready bc_ready dt_ready dt_taken bc_taken bc_steps pre_ready abs_ready pos_ready exp_ready "
             "log_ready log_joined soft_steps delta_ready du_ready restart b_ready b_taken c_ready da_ready dbu_ready scanned "
             "hc_ready y_added y_gated join_ready join_taken out_ready act_held zeroed doubled").split()
    sig = {n: core.counter("mb_" + n) for n in names}
    loaded = core.counter("mb_loaded")
    with ExitStack() as ctx:
        def sb(name, shape, dt=FP32):
            return core.tensor(ctx, "mb_" + name, shape, dt)

        cols = sb("cols", [P, 2 + 4 * WAYS * HALVES])
        in_w = sb("in_w", [P, WAYS, 4 * P])
        taps = sb("taps", [P, WAYS, T, 2 * P])
        a = sb("a", [P, WAYS, HALVES, N])
        xp_bc = sb("xp_bc", [P, WAYS, HALVES, 96])
        xp_dt = sb("xp_dt", [P, WAYS, HALVES, R])
        dt_w = sb("dt_w", [R, WAYS, 2 * P])
        out_w = sb("out_w", [P, WAYS, 2 * P])
        fus = sb("fus", [P, WAYS, P])
        fus_b = sb("fus_b", [P, P])
        sel = sb("sel", [P, 2 * N * P], BF16)
        norm = TokenNorm(core, ctx, "mb", 1e-5, sig["norm_steps"], sig["rooted"])
        half_b = sb("half_b", [P, WAYS * HALVES])
        xn = sb("xn", [P, NT, P])
        xn_feat = sb("xn_feat", [P, B, S + 2 * PAD])
        conv_w = sb("conv_w", [P, WAYS, T, 2 * P])
        diag = sb("diag", [P, WAYS, HALVES, P])
        xc, sz, delta, du = (sb(n, [P, WAYS, HALVES, TOK]) for n in ("xc", "sz", "delta", "du"))
        dts = sb("dts", [R, WAYS, TOK])
        parts = sb("parts", [P, WAYS, TOK], BF16)
        da, dbu, hs, hc = (sb(n, [P, HALVES, TOK]) for n in ("da", "dbu", "hs", "hc"))
        bs = sb("bs", [P, 2, TOK])
        join = sb("join", [P, WAYS, HALVES, P])
        high = hc[:, 0, 0:TOK // 2].bitcast(BF16)
        middle = hc[:, 0, TOK // 2:TOK].bitcast(BF16)
        rest = hs[:, 0, :]

        SERIES = [1 / 7, -1 / 6, 1 / 5, -1 / 4, 1 / 3, -1 / 2, 1.0]
        SOFT = len(SERIES) + 2

        def col_of(r, h, n):
            c = 2 + 4 * (HALVES * r + h) + n
            return cols[:, c:c + 1]

        CONV_B, DT_B, D = 0, 1, 2

        def pair(n):
            return ps[:, 2 * n:2 * n + 2, :]

        def two(t):
            return t.rearrange("p (n c) -> p n c", n=2)

        loads = [(cols[:, :], "cols"), (in_w[:, :, :], "in_w"), (taps[:, :, :, :], "taps"), (a[:, :, :, :], "a_log"),
                 (xp_bc[:, :, :, :], "xp_bc"), (xp_dt[:, :, :, :], "xp_dt"), (dt_w[:, :, :], "dt_w"),
                 (out_w[:, :, :], "out_w"), (fus[:, :, :], "fus"), (fus_b[:, :], "fus_b"), (sel[:, :], "sel")]
        ALL = 16 * len(loads)

        yield [(dst, w[name].partition_broadcast(P) if name in ("taps", "fus_b") else w[name], loaded)
               for dst, name in loads]
        with nc.Block(no_gpsimd_drain=True) as block:
            @block.gpsimd
            def _(pool):
                pool.memset(xn_feat[:, :, 0:PAD], 0.0).then_inc(sig["zeroed"].sem, 1)
                pool.memset(xn_feat[:, :, PAD + S:], 0.0).then_inc(sig["zeroed"].sem, 1)
                pool.wait_ge(*sig["zeroed"](2))
                pool.memset(parts[96:P, :, :], 0.0).then_inc(sig["zeroed"].sem, 1)
                pool.wait_ge(*sig["zeroed"](3))
                pool.wait_ge(*loaded(ALL))
                for r in range(WAYS):
                    pool.tensor_tensor(conv_w[:, r, :, :], taps[:, r, :, :],
                                       in_w[:, r, 0:2 * P].unsqueeze(1).to_broadcast([P, T, 2 * P]),
                                       ALU.mult).then_inc(sig["weights_scaled"].sem, 1)
                for r in range(WAYS):
                    for h in range(HALVES):
                        pool.tensor_scalar(diag[:, r, h, :], core.ident[:, :], col_of(r, h, D), None, ALU.mult)\
                            .then_inc(sig["diag_ready"].sem, 1)
                for r in range(WAYS):
                    for h in range(HALVES):
                        n = HALVES * r + h
                        pool.wait_ge(*sig["soft_steps"](SOFT * n + SOFT))
                        pool.tensor_tensor(bs[:, h, :], bs[:, h, :], dbu[:, h, :], ALU.add)\
                            .then_inc(sig["log_joined"].sem, 1)
                        pool.wait_ge(*sig["log_joined"](n + 1))
                        pool.wait_ge(*sig["pos_ready"](n + 1))
                        pool.tensor_tensor(delta[:, r, h, :], delta[:, r, h, :], bs[:, h, :], ALU.add)\
                            .then_inc(sig["delta_ready"].sem, 1)
                        pool.wait_ge(*sig["delta_ready"](n + 1))
                        pool.tensor_tensor(du[:, r, h, :], delta[:, r, h, :], xc[:, r, h, :], ALU.mult)\
                            .then_inc(sig["du_ready"].sem, 1)
                pool.wait_ge(*sig["du_ready"](WAYS * HALVES))
                for r in range(WAYS):
                    if r:
                        pool.wait_ge(*sig["scanned"](2 + 2 * N * r))
                    edge = 0 if r == 0 else S - 1
                    for h in range(HALVES):
                        pool.memset(da[:, h, :].rearrange("p (b s) -> p b s", s=S)[:, :, edge:edge + 1], 0.0)\
                            .then_inc(sig["restart"].sem, 1)
                    with pool.Fori(0, N // 2) as i:
                        for u in range(2):
                            n = N * r + 2 * i + u
                            for h in range(HALVES):
                                pool.wait_ge(*sig["b_taken"](n + 2))
                                pool.wait_ge(*sig["scanned"](2 * n + h + 1))
                                pool.tensor_tensor(dbu[:, h, :], du[:, r, h, :], bs[:, u, :], ALU.mult)\
                                    .then_inc(sig["dbu_ready"].sem, 1)

            @block.tensor
            def _(pe):
                pe.wait_ge(*loaded(ALL))
                for t in range(NT):
                    pe.wait_ge(*sig["tile_ready"](t + 1))
                    pe.transpose(ps[:, t // 4, t % 4 * P:(t % 4 + 1) * P], xn[:, t, :], core.ident[:, :])\
                      .then_inc(sig["tile_turned"].sem, 1)
                pe.wait_ge(*sig["norm_ready"](2))
                pe.wait_ge(*sig["zeroed"](3))
                for r in range(WAYS):
                    pe.wait_ge(*sig["weights_scaled"](r + 1))
                    if r:
                        pe.wait_ge(*sig["bc_taken"](r))
                        pe.wait_ge(*sig["dt_taken"](r))
                        pe.wait_ge(*sig["pos_ready"](HALVES * r))
                    for h in range(HALVES):
                        for n in range(2):
                            for j in range(T):
                                at = j if r == 0 else 2 * PAD - j
                                last = pe.matmul(ps[:, 2 * h + n, :], conv_w[:, r, j, h * P:(h + 1) * P],
                                                 xn_feat[:, 2 * n:2 * n + 2, at:at + S], start=j == 0, stop=j == T - 1)
                        last.then_inc(sig["conv_ready"].sem, 1)
                    for h in range(HALVES):
                        for n in range(2):
                            last = pe.matmul(ps[:, 4 + 2 * h + n, :], in_w[:, r, (2 + h) * P:(3 + h) * P],
                                             xn_feat[:, 2 * n:2 * n + 2, PAD:PAD + S], start=True, stop=True)
                        last.then_inc(sig["z_ready"].sem, 1)
                    pe.wait_ge(*sig["xc_ready"](HALVES * (r + 1)))
                    for out, mat, bank, done in ((96, xp_bc, 0, "bc_ready"), (R, xp_dt, 2, "dt_ready")):
                        for n in range(2):
                            for h in range(HALVES):
                                last = pe.matmul(ps[0:out, bank + n, :], mat[:, r, h, :],
                                                 xc[:, r, h, n * HALF:(n + 1) * HALF], start=h == 0, stop=h == 1)
                        last.then_inc(sig[done].sem, 1)
                    pe.wait_ge(*sig["dt_taken"](r + 1))
                    pe.wait_ge(*sig["sz_ready"](HALVES * (r + 1)))
                    for h in range(HALVES):
                        for n in range(2):
                            last = pe.matmul(ps[:, 4 + 2 * h + n, :], dt_w[:, r, h * P:(h + 1) * P],
                                             dts[:, r, n * HALF:(n + 1) * HALF], start=True, stop=True)
                        last.then_inc(sig["pre_ready"].sem, 1)
                pe.wait_ge(*sig["bc_taken"](WAYS))
                pe.wait_ge(*sig["pos_ready"](WAYS * HALVES))
                pe.wait_ge(*sig["diag_ready"](WAYS * HALVES))

                def spread(r, s, bank, row, done):
                    for n in range(2):
                        last = pe.matmul(ps[:, bank + n, :], sel[:, bass.ds(row * P, P)],
                                         parts[:, r, n * HALF:(n + 1) * HALF], start=True, stop=True)
                    last.then_inc(sig[done].sem, 1)

                def spread_b(r, s):
                    pe.wait_ge(*sig["b_taken"](N * r + s + 1))
                    spread(r, s, 0, s, "b_ready")

                def spread_c(r, s):
                    pe.wait_ge(*sig["hc_ready"](2 * (N * r + s) + 2))
                    spread(r, s, 2, s + N, "c_ready")

                def add_state(r, s, h, last_state=False):
                    pe.wait_ge(*sig["hc_ready"](2 * (N * r + s) + h + 3))
                    for n in range(2):
                        last = pe.matmul(ps[:, 4 + 2 * h + n, :], core.ident[:, :],
                                         hc[:, h, n * HALF:(n + 1) * HALF], start=False, stop=last_state)
                    last.then_inc(sig["y_added"].sem, 1)

                for r in range(WAYS):
                    if r:
                        pe.wait_ge(*sig["y_gated"](HALVES * r))
                    for h in range(HALVES):
                        for n in range(2):
                            pe.matmul(ps[:, 4 + 2 * h + n, :], diag[:, r, h, :],
                                      xc[:, r, h, n * HALF:(n + 1) * HALF], start=True, stop=False)
                    spread_b(r, 0)
                    spread_c(r, 0)
                    spread_b(r, 1)
                    with pe.Fori(0, N // 2 - 1) as i:
                        for u in range(2):
                            s = 2 * i + u
                            spread_b(r, s + 2)
                            add_state(r, s, 0)
                            spread_c(r, s + 1)
                            add_state(r, s, 1)
                    add_state(r, N - 2, 0)
                    spread_c(r, N - 1)
                    add_state(r, N - 2, 1)
                    add_state(r, N - 1, 0, last_state=True)
                    add_state(r, N - 1, 1, last_state=True)
                for r in range(WAYS):
                    for h in range(HALVES):
                        if r == h == 0:
                            pe.wait_ge(*sig["b_taken"](WAYS * N + 1))
                        c = (HALVES * r + h) * P
                        last = pe.matmul(ps[:, 0, c:c + P], out_w[:, r, h * P:(h + 1) * P], fus[:, r, :],
                                         start=True, stop=True)
                last.then_inc(sig["join_ready"].sem, 1)
                pe.wait_ge(*sig["join_taken"](1))
                pe.wait_ge(*sig["y_gated"](WAYS * HALVES))
                pe.wait_ge(*sig["hc_ready"](2 * WAYS * N + 2))
                for t in range(NT):
                    for r in range(WAYS):
                        for h in range(HALVES):
                            last = pe.matmul(ps[:, 2 + t // 4, t % 4 * P:(t % 4 + 1) * P],
                                             sz[:, r, h, t * P:(t + 1) * P], join[:, r, h, :],
                                             start=r == h == 0, stop=r == h == 1)
                    if t % 4 == 3:
                        last.then_inc(sig["out_ready"].sem, 1)

            @block.scalar
            def _(act):
                norm.on_scalar(act)
                act.wait_ge(*loaded(ALL))
                act.activation(a[:, :, :, :], a[:, :, :, :], ACT.Exp).then_inc(sig["a_exp"].sem, 1)
                act.wait_ge(*sig["a_exp"](1))
                act.mul(a[:, :, :, :], a[:, :, :, :], -1.0).then_inc(sig["a_ready"].sem, 1)
                for n in range(WAYS * HALVES):
                    c = 2 + 4 * n
                    act.mul(half_b[:, n:n + 1], cols[:, c:c + 1], 0.5).then_inc(sig["half_ready"].sem, 1)
                for n in range(2):
                    act.wait_ge(*sig["tile_turned"](4 * n + 4))
                    act.activation(xn_feat[:, 2 * n:2 * n + 2, PAD:PAD + S],
                                   ps[:, n, :].rearrange("p (b s) -> p b s", s=S), ACT.Identity,
                                   scale=cols[:, 0:1], bias=cols[:, 1:2]).then_inc(sig["norm_ready"].sem, 1)
                act.wait_ge(*sig["half_ready"](WAYS * HALVES))
                for r in range(WAYS):
                    for h in range(HALVES):
                        act.wait_ge(*sig["conv_ready"](HALVES * r + h + 1))
                        act.activation(two(xc[:, r, h, :]), pair(h), ACT.Tanh, scale=0.5,
                                       bias=half_b[:, HALVES * r + h:HALVES * r + h + 1])\
                           .then_inc(sig["xc_tanh"].sem, 1)
                    for h in range(HALVES):
                        act.wait_ge(*sig["z_ready"](HALVES * r + h + 1))
                        act.activation(two(sz[:, r, h, :]), pair(2 + h), ACT.Tanh, scale=0.5)\
                           .then_inc(sig["sz_tanh"].sem, 1)
                    for h in range(HALVES):
                        n = HALVES * r + h
                        e = da[:, h, :]
                        act.wait_ge(*sig["pre_ready"](n + 1))
                        if r:
                            act.wait_ge(*sig["soft_steps"](SOFT * (n - 2) + SOFT))
                        act.activation(two(e), pair(2 + h), ACT.Abs, bias=col_of(r, h, DT_B))\
                           .then_inc(sig["abs_ready"].sem, 1)
                    for h in range(HALVES):
                        n = HALVES * r + h
                        e = da[:, h, :]
                        act.wait_ge(*sig["abs_ready"](n + 1))
                        act.activation(e, e, ACT.Exp, scale=-1.0).then_inc(sig["exp_ready"].sem, 1)
                    for h in range(HALVES):
                        n = HALVES * r + h
                        act.wait_ge(*sig["exp_ready"](n + 1))
                        if r:
                            act.wait_ge(*sig["log_joined"](n - 1))
                        act.activation(dbu[:, h, :], da[:, h, :], ACT.Ln, bias=1.0).then_inc(sig["log_ready"].sem, 1)

                def take_b(r, s, u):
                    n = N * r + s
                    act.wait_ge(*sig["b_ready"](n + 1))
                    act.wait_ge(*sig["dbu_ready"](2 * n + 2))
                    act.copy(two(bs[:, u, :]), pair(0)).then_inc(sig["b_taken"].sem, 1)

                def decays(r, s):
                    n = N * r + s
                    for h in range(HALVES):
                        act.wait_ge(*sig["scanned"](2 * n + h + 1))
                        act.sem_inc(sig["act_held"].sem, 1)
                        lo = 1 - r
                        act.activation(da[:, h, :].rearrange("p (b s) -> p b s", s=S)[:, :, lo:lo + S - 1],
                                       delta[:, r, h, :].rearrange("p (b s) -> p b s", s=S)[:, :, lo:lo + S - 1],
                                       ACT.Exp, scale=a[:, r, h, bass.ds(s, 1)])\
                           .then_inc(sig["da_ready"].sem, 1)

                act.sem_inc(sig["b_taken"].sem, 1)
                act.wait_ge(*sig["a_ready"](1))
                act.wait_ge(*sig["du_ready"](WAYS * HALVES))
                for r in range(WAYS):
                    act.wait_ge(*sig["restart"](HALVES * (r + 1)))
                    take_b(r, 0, 0)
                    with act.Fori(0, N // 4 - 1) as i:
                        for u in range(4):
                            take_b(r, 4 * i + u + 1, (u + 1) % 2)
                            decays(r, 4 * i + u)
                    for s in range(N - 4, N):
                        if s + 1 < N:
                            take_b(r, s + 1, (s + 1) % 2)
                        decays(r, s)

            def softplus_tail(r, h):
                dve, n, steps = nc.vector, HALVES * r + h, sig["soft_steps"]
                e, series, log = da[:, h, :], bs[:, h, :], dbu[:, h, :]
                dve.wait_ge(*sig["exp_ready"](n + 1))
                if r:
                    dve.wait_ge(*sig["delta_ready"](n - 1))
                dve.tensor_scalar(series, e, SERIES[0], None, ALU.mult).then_inc(steps.sem, 1)
                for m, c in enumerate(SERIES[1:]):
                    dve.wait_ge(*steps(SOFT * n + m + 1))
                    dve.scalar_tensor_tensor(series, series, c, e, ALU.add, ALU.mult).then_inc(steps.sem, 1)
                dve.wait_ge(*steps(SOFT * n + len(SERIES)))
                dve.wait_ge(*sig["log_ready"](n + 1))
                dve.tensor_tensor(log, log, series, ALU.subtract).then_inc(steps.sem, 1)
                dve.wait_ge(*steps(SOFT * n + len(SERIES) + 1))
                dve.scalar_tensor_tensor(log, e, 1 / 16, log, ALU.is_ge, ALU.mult).then_inc(steps.sem, 1)

            @block.vector
            def _(dve):
                norm.on_vector(dve)
                for t in range(NT):
                    norm.normalise(dve, xn[:, t, :], t).then_inc(sig["tile_ready"].sem, 1)
                dve.wait_ge(*loaded(ALL))
                dve.wait_ge(*sig["tile_ready"](NT))
                dve.scalar_tensor_tensor(x_tok[:, :, :], x_tok[:, :, :], 2.0,
                                         fus_b[:, :].unsqueeze(1).to_broadcast([P, NT, P]), ALU.mult, ALU.add)\
                   .then_inc(sig["doubled"].sem, 1)
                for r in range(WAYS):
                    for name, dst, first, bias in (("xc", xc, 0, True), ("sz", sz, 2, False)):
                        for h in range(HALVES):
                            n = HALVES * r + h
                            half = hs[:, h, :]
                            dve.wait_ge(*sig[name + "_tanh"](n + 1))
                            if name == "sz":
                                dve.wait_ge(*sig["xc_ready"](n + 1))
                            elif r:
                                dve.wait_ge(*sig["sz_ready"](n - 1))
                                dve.wait_ge(*sig["bc_taken"](r))
                            dve.tensor_scalar(two(half), pair(first + h), col_of(r, h, CONV_B) if bias else 0.0,
                                              0.5, ALU.add, ALU.mult).then_inc(sig[name + "_half"].sem, 1)
                            dve.wait_ge(*sig[name + "_half"](n + 1))
                            dve.scalar_tensor_tensor(dst[:, r, h, :], dst[:, r, h, :], 1.0, half, ALU.add,
                                                     ALU.mult).then_inc(sig[name + "_ready"].sem, 1)
                    dve.wait_ge(*sig["sz_ready"](HALVES * (r + 1)))
                    dve.wait_ge(*sig["dt_ready"](r + 1))
                    dve.tensor_copy(two(dts[:, r, :]), ps[0:R, 2:4, :]).then_inc(sig["dt_taken"].sem, 1)
                    dve.wait_ge(*sig["bc_ready"](r + 1))
                    bc, steps = ps[0:96, 0:2, :], sig["bc_steps"]
                    if r:
                        dve.wait_ge(*sig["bc_taken"](r))
                    dve.tensor_copy(two(high[0:96, :]), bc).then_inc(steps.sem, 1)
                    dve.wait_ge(*steps(4 * r + 1))
                    dve.tensor_tensor(two(rest[0:96, :]), bc, two(high[0:96, :]), ALU.subtract).then_inc(steps.sem, 1)
                    dve.tensor_copy(parts[0:32, r, :], high[0:32, :]).then_inc(steps.sem, 1)
                    dve.wait_ge(*steps(4 * r + 3))
                    dve.tensor_copy(middle[0:96, :], rest[0:96, :]).then_inc(steps.sem, 1)
                    dve.wait_ge(*steps(4 * r + 4))
                    dve.tensor_copy(parts[32:64, r, :], middle[32:64, :])
                    dve.tensor_tensor(parts[64:96, r, :], rest[64:96, :], middle[64:96, :], ALU.subtract)\
                       .then_inc(sig["bc_taken"].sem, 1)
                    for h in range(HALVES):
                        n = HALVES * r + h
                        dve.wait_ge(*sig["abs_ready"](n + 1))
                        dve.tensor_scalar(two(delta[:, r, h, :]), pair(2 + h), col_of(r, h, DT_B), 0.0,
                                          ALU.add, ALU.max).then_inc(sig["pos_ready"].sem, 1)
                    for h in range(HALVES):
                        softplus_tail(r, h)
                dve.sem_inc(sig["scanned"].sem, 2)
                dve.sem_inc(sig["hc_ready"].sem, 2)
                dve.sem_inc(sig["y_added"].sem, 2)
                dve.sem_inc(sig["dbu_ready"].sem, 4)

                def way(t, r):
                    return t if r == 0 else t[:, ::-1]

                dve.wait_ge(*sig["bc_taken"](WAYS))
                for r in range(WAYS):
                    with dve.Fori(0, N) as s:
                        n = N * r + s
                        for h in range(HALVES):
                            dve.wait_ge(*sig["da_ready"](2 * n + h + 1))
                            dve.wait_ge(*sig["dbu_ready"](2 * n + h + 5))
                            dve.wait_ge(*sig["hc_ready"](2 * n + h + 1))
                            dve.tensor_tensor_scan(way(hs[:, h, :], r), way(da[:, h, :], r), way(dbu[:, h, :], r), 0.0,
                                                   ALU.mult, ALU.add).then_inc(sig["scanned"].sem, 1)
                            dve.wait_ge(*sig["scanned"](2 * n + h + 3))
                            dve.wait_ge(*sig["c_ready"](n + 1))
                            dve.wait_ge(*sig["y_added"](2 * n + h + 1))
                            dve.tensor_tensor(two(hc[:, h, :]), two(hs[:, h, :]), pair(1), ALU.mult)\
                               .then_inc(sig["hc_ready"].sem, 1)
                    dve.wait_ge(*sig["y_added"](2 + 2 * N * (r + 1)))
                    dve.wait_ge(*sig["sz_ready"](WAYS * HALVES))
                    for h in range(HALVES):
                        dve.tensor_tensor(two(sz[:, r, h, :]), pair(2 + h), two(sz[:, r, h, :]), ALU.mult)\
                           .then_inc(sig["y_gated"].sem, 1)
                dve.wait_ge(*sig["join_ready"](1))
                dve.tensor_copy(join[:, :, :, :].rearrange("p r h f -> p (r h f)"), ps[:, 0, :])\
                   .then_inc(sig["join_taken"].sem, 1)
                dve.wait_ge(*sig["doubled"](1))
                for n in range(2):
                    dve.wait_ge(*sig["out_ready"](n + 1))
                    xs = x_tok[:, 4 * n:4 * n + 4, :]
                    dve.tensor_tensor(xs, xs, ps[:, 2 + n, :].rearrange("p (t f) -> p t f", f=P), ALU.add)


def selector(parts, n, rows=None):
    t = np.zeros((rows or parts * n, n, P), "bfloat16")
    for r in range(parts * n):
        t[r, r % n, :] = 1
    return t.reshape(-1, n * P)


Q_PARTS = (0, 0, 1, 0, 2, 1)
K_PARTS = (0, 1, 0, 2, 0, 1)


def routes():
    t = np.zeros((P, 2, HEADS // 2, 3, P), "bfloat16")
    for side, order in enumerate((Q_PARTS, K_PARTS)):
        for head in range(HEADS):
            for j, part in enumerate(order):
                for dd in range(8):
                    t[head * 8 + dd, side, head // 2, part, head % 2 * 64 + 8 * j + dd] = 1
    return t


def layout(i):
    a = {k: np.asarray(v) for k, v in i.items()}
    d = {"x": a["x"].reshape(TOK, P), "context": a["ctx_1024"].reshape(TOK, P),
         "ident": np.eye(P, dtype=np.float32), "ident16": np.eye(P, dtype="bfloat16")}
    for s, dim, q, k, v, o in (("L0x", 8, "L0_xattn_Wq", "L0_xattn_Wk", "L0_xattn_Wv", "L0_xattn_Wo"),
                               ("L1x", 8, "L1_xattn_Wq", "L1_xattn_Wk", "L1_xattn_Wv", "L1_xattn_Wo"),
                               ("L2x", 8, "L2_xattn_w_q", "L2_xattn_w_k", "L2_xattn_w_v", "L2_xattn_w_o")):
        d[s + "_wq"], d[s + "_wk"] = a[q].T, a[k].T
        d[s + "_wv"], d[s + "_wo"] = a[v].T, a[o].T
        d[s + "_sel"] = selector(2, 4)
        d[s + "_rows"] = np.repeat(np.eye(2, dtype=np.float32), 64, axis=0)
        d[s + "_route"] = routes()
    for s in ("L0", "L1"):
        d[s + "x_bq"], d[s + "x_bk"] = a[s + "_xattn_bq"].reshape(P, 1), a[s + "_xattn_bk"].reshape(P, 1)
        d[s + "x_bv"], d[s + "x_bo"] = a[s + "_xattn_bv"], a[s + "_xattn_bo"]
    d["L1x_mask"] = a["mask_1x1xSxS2_ik0"].reshape(S, S)

    def heads64(w):
        return w.transpose(1, 0, 2).reshape(P, HEADS * 64)

    d["L3x_wq"], d["L3x_wk"], d["L3x_wv"] = (heads64(a["L3_xattn_" + n]) for n in ("WQ", "WK", "WV"))
    d["L3x_wo"] = a["L3_xattn_WO"].reshape(8, P, P).transpose(1, 0, 2).reshape(P, 8 * P)
    d["L3x_sel"] = selector(2, 2)
    d["L3x_rows"] = np.repeat(np.eye(2, dtype=np.float32), 64, axis=0)
    d["L3x_mask"] = np.tril(np.ones((P, P), np.int32))

    def units(gate, up, down):
        return np.concatenate([gate, up, down], axis=2)

    def cut(w):
        e, m, n = w.shape
        return w.reshape(e, m, n // P, P).transpose(0, 2, 1, 3).reshape(-1, m, P)

    gu, dn = a["L0_ffn_gate_up_w"], a["L0_ffn_down_w"]
    sg, su, sd = (a["L0_ffn_shared_" + n] for n in ("gate_w", "up_w", "down_w"))
    d["L0f_units"] = np.concatenate([
        units(gu[:, :, :P], gu[:, :, P:], dn),
        units(cut(sg.T[None]), cut(su.T[None]), sd.T.reshape(2, P, P))])
    d["L0f_router"], d["L0f_sel"] = a["L0_ffn_router_w"].T, selector(3, 18, P)
    w13, w2 = a["L2_ffn_w13"], a["L2_ffn_w2"]
    d["L2f_units"] = units(cut(w13[:, :, :256]), cut(w13[:, :, 256:]), w2.reshape(16, P, P))
    d["L2f_router"], d["L2f_sel"] = a["L2_ffn_router_w"].T, selector(3, 8, P)
    e1, e2, e3, s1, s2, s3 = (a["L3_ffn_" + n] for n in ("ew1", "ew2", "ew3", "sw1", "sw2", "sw3"))
    d["L3f_units"] = np.concatenate([units(cut(e1), cut(e2), e3.reshape(16, P, P)),
                                     units(cut(s1[None]), cut(s2[None]), s3.reshape(2, P, P))])
    d["L3f_router"], d["L3f_sel"] = a["L3_ffn_gate_w"], selector(3, 9, P)
    d["L0a_mats"] = np.stack([a["L0_attn_" + n].T for n in ("Wq", "Wk", "Wv", "Wo")], axis=1)
    d["L0a_bq"] = a["L0_attn_bq"].reshape(P, 1)
    d["L0a_rows"] = np.stack([a["L0_attn_" + n] for n in ("bk", "bv", "bo")])
    d["L3a_mq"], d["L3a_mk"], d["L3a_mv"] = a["L3_attn_Mq"], a["L3_attn_Mk"], a["L3_attn_Mv"]
    w1, w2 = a["L1_ffn_W1"], a["L1_ffn_W2"]
    d["L1f_mats"] = np.concatenate([w1, w2.reshape(8, 4, P, P).transpose(0, 2, 1, 3).reshape(8, P, 4 * P)], axis=2)
    d["L1f_router"], d["L1f_sel"] = a["L1_ffn_Wg"], selector(3, 8, P)
    d["L1f_gamma"], d["L1f_beta"] = a["L1_ffn_gamma"].T, a["L1_ffn_beta"].T
    d["L1f_b1"], d["L1f_b2"] = a["L1_ffn_b1"].reshape(32, P).T, a["L1_ffn_b2"]
    d["L2a_mats"] = np.stack([a["L2_attn_" + n].T for n in ("Wk", "Wv", "Wr", "Wo")], axis=1)
    d["L2a_cols"] = np.stack([a["L2_attn_" + n].reshape(P) for n in
                              ("time_mix_k", "time_mix_v", "time_mix_r", "w", "u")], axis=1)
    ways = [{n[len("L1_attn_f_"):]: v for n, v in a.items() if n.startswith(f"L1_attn_{way}_")} for way in "fb"]
    cols = [a["L1_attn_ln_g"], a["L1_attn_ln_b"]]
    for m in ways:
        for h in range(2):
            cols += [m[n][h * P:(h + 1) * P] for n in ("conv_b", "dt_b", "D", "D")]
    d["L1a_cols"] = np.stack(cols, axis=1)

    def both(f):
        return np.stack([f(m) for m in ways], axis=1)

    def halved(t):
        return t.reshape(2, P, -1).transpose(1, 0, 2)

    d["L1a_in_w"] = both(lambda m: m["in_w"].T)
    d["L1a_taps"] = np.stack([m["conv_w"][:, 0, :].T for m in ways])
    d["L1a_a_log"] = both(lambda m: halved(m["A_log"]))
    d["L1a_xp_bc"] = both(lambda m: halved(np.tile(m["xproj_w"][8:].T, (1, 3))))
    d["L1a_xp_dt"] = both(lambda m: halved(m["xproj_w"][:8].T))
    d["L1a_dt_w"] = both(lambda m: m["dt_w"].T)
    d["L1a_out_w"] = both(lambda m: m["out_w"])
    d["L1a_fus"] = a["L1_attn_fus_w"].T.reshape(2, P, P).transpose(1, 0, 2)
    d["L1a_fus_b"] = a["L1_attn_fus_b"]
    d["L1a_sel"] = selector(3, 32, P)
    return {k: np.ascontiguousarray(v) for k, v in d.items()}


STAGES = (0, 12)


def build(nc, d, out):
    ctx = ExitStack()
    with ctx:
        core = Core(ctx, nc)

        def of(stage):
            return {n[len(stage) + 1:]: v for n, v in d.items() if n.startswith(stage + "_")}

        stages = [
            lambda: linear_attention(core, of("L0a")),
            lambda: stacked_attention(core, of("L0x"), biased=True, masked=False),
            lambda: gated_experts(core, of("L0f"), units=18, per_expert=1, scores=16, rule="sigmoid"),
            lambda: two_way_mamba(core, of("L1a")),
            lambda: stacked_attention(core, of("L1x"), biased=True, masked=True),
            lambda: normed_experts(core, of("L1f")),
            lambda: rwkv_mixer(core, of("L2a")),
            lambda: stacked_attention(core, of("L2x"), biased=False, masked=False),
            lambda: gated_experts(core, of("L2f"), units=16, per_expert=2, scores=8, rule="renormalised"),
            lambda: reshaped_attention(core, of("L3a")),
            lambda: causal_attention(core, of("L3x"), dim=64),
            lambda: gated_experts(core, of("L3f"), units=18, per_expert=2, scores=8, rule="softmax"),
        ]

        def begin(n):
            signals = ExitStack()
            core.new_stage(signals)
            stage = stages[n]()
            return signals, core.to_clear, stage, next(stage)

        first, last = STAGES
        present = begin(first)
        load_stage(core, d["x"], d["context"], d["ident"], d["ident16"], present[3])
        for n in range(first, last):
            signals, to_clear, stage, _ = present
            next(stage, None)
            if n + 1 < last:
                present = begin(n + 1)
                post_norm(core, to_clear, present[3])
            else:
                post_norm(core, to_clear, [], out)
            signals.close()


def kernel(**inputs):
    import concourse.bacc as _bacc
    from concourse.bass_utils import run_bass_kernel_spmd as _run

    nc = _bacc.Bacc("TRN2", target_bir_lowering=False, num_devices=1)
    arrays, d = {}, {}
    for name, a in layout(inputs).items():
        arrays[f"in_{name}"] = a
        d[name] = nc.dram_tensor(f"in_{name}", a.shape, mybir.dt.from_np(a.dtype), kind="ExternalInput").ap()
    out = nc.dram_tensor("out_x", (TOK, P), FP32, kind="ExternalOutput").ap()
    build(nc, d, out)
    r = _run(nc, [arrays], core_ids=[0])
    return r.results[0]["out_x"].reshape(B, S, P)
```
